# Optimizing a Trainium2 kernel written in Bass

```python
import numpy as np
import jax
import jax.numpy as jnp

def _softmax(x, axis=-1):
    return jax.nn.softmax(x, axis=axis)

def _gelu(x):
    return jax.nn.gelu(x, approximate=True)

def _silu(x):
    return jax.nn.silu(x)

def _sigmoid(x):
    return jax.nn.sigmoid(x)

def _layernorm(x, axis=-1, eps=1e-05):
    m = jnp.mean(x, axis=axis, keepdims=True)
    v = jnp.var(x, axis=axis, keepdims=True)
    return (x - m) / jnp.sqrt(v + eps)

def _scatter_add(tgt, idx, src, axis=0):
    return tgt.at[idx].add(src)

def _segment_sum(src, seg, n):
    return jax.ops.segment_sum(src, seg, n)
kernel_name = 'mk_adaln_d4_jaxref_r8_5d3a4a'

def setup_inputs(seed: int=0):
    np.random.seed(seed)
    _w = jnp.asarray

    def _L0_attn_setup():
        import jax, jax.numpy as jnp
        import numpy as np
        B, N, D = (2, 512, 256)
        H, DH, W = (8, 128, 64)
        SCALE = 8.0

        def _l2norm(t):
            return t / jnp.maximum(jnp.linalg.norm(t, axis=-1, keepdims=True), 1e-12)
        key = jax.random.key(seed)
        ks = jax.random.split(key, 5)
        return {'x': jax.random.normal(ks[0], (B, N, D), jnp.float32), 'Wq': jax.random.normal(ks[1], (H * DH, D), jnp.float32) * 0.02, 'Wkv': jax.random.normal(ks[2], (2 * H * DH, D), jnp.float32) * 0.02, 'q_scale': jnp.ones((DH,), jnp.float32), 'k_scale': jnp.ones((DH,), jnp.float32), 'Wg': jax.random.normal(ks[3], (H, D), jnp.float32) * 0.02, 'bg': jnp.zeros((H,), jnp.float32), 'Wo': jax.random.normal(ks[4], (D, H * DH), jnp.float32) * 0.02}
    _L0_attn_in = _L0_attn_setup()

    def _L0_ffn_setup():
        import jax, jax.numpy as jnp
        import numpy as np
        HIDDEN = 256
        INTER = 1024
        RETRIEVAL = 128
        NUM_EXPERTS = 512
        NUM_KEYS = 64
        TOP_K = 8
        B, S = (4, 256)
        key = jax.random.key(seed)
        ks = jax.random.split(key, 8)
        sc = 0.02
        return {'hidden_states': jax.random.normal(ks[0], (B, S, HIDDEN), jnp.float32), 'W_q': jax.random.normal(ks[1], (HIDDEN, RETRIEVAL), jnp.float32) * sc, 'keys': jax.random.normal(ks[2], (2, RETRIEVAL // 2, NUM_KEYS), jnp.float32) * sc, 'down_embed': jax.random.normal(ks[3], (NUM_EXPERTS, HIDDEN), jnp.float32) * sc, 'up_embed': jax.random.normal(ks[4], (NUM_EXPERTS, HIDDEN), jnp.float32) * sc, 'gate_w': jax.random.normal(ks[5], (HIDDEN, INTER), jnp.float32) * sc, 'up_w': jax.random.normal(ks[6], (HIDDEN, INTER), jnp.float32) * sc, 'down_w': jax.random.normal(ks[7], (INTER, HIDDEN), jnp.float32) * sc}
    _L0_ffn_in = _L0_ffn_setup()
    _L0_c = _w((lambda *s: np.random.randn(*s).astype(np.float32) * 0.05)(1, 256))
    _L0_wmod = _w((lambda *s: np.random.randn(*s).astype(np.float32) * 0.05)(256, 6 * 256) * 256 ** (-0.5))

    def _L1_attn_setup():
        import jax, jax.numpy as jnp
        import numpy as np
        DIM = 256
        HEAD_DIM = 128
        NH = DIM // HEAD_DIM
        CHUNK = 128

        def _forward(x, Wq, bq, Wk, bk, Wv, bv, Wbeta, bbeta, Walpha, balpha):
            B, T, D = x.shape
            H, S, C = (NH, HEAD_DIM, CHUNK)
            q = (x @ Wq + bq).reshape(B, T, H, S)
            k = (x @ Wk + bk).reshape(B, T, H, S)
            v = (x @ Wv + bv).reshape(B, T, H, S)
            k = k / jnp.maximum(jnp.linalg.norm(k, axis=-1, keepdims=True), 1e-12)
            alpha_val = jax.nn.sigmoid(x @ Walpha + balpha).reshape(B, T, H, 1)
            beta = jax.nn.softplus(x @ Wbeta + bbeta).reshape(B, T, H, 1)
            pad = -T % C

            def padt(t):
                return jnp.pad(t, ((0, 0), (0, pad), (0, 0), (0, 0))) if pad else t
            qp, kp, vp = (padt(q), padt(k), padt(v))
            ap, bp = (padt(alpha_val), padt(beta))
            Tp = T + pad
            n = Tp // C

            def ch(t):
                return t.reshape(B, n, C, H, t.shape[-1]).transpose(0, 1, 3, 2, 4)
            qc, kc, vc, bc = (ch(qp), ch(kp), ch(vp), ch(bp))
            cla = jnp.cumsum(jnp.log(ch(ap) + 1e-06), axis=3)
            decay = jnp.exp(cla - jnp.swapaxes(cla, -1, -2))
            causal = jnp.tril(jnp.ones((C, C), dtype=bool))
            decay = jnp.where(causal, decay, 0.0)
            attn = jnp.einsum('bnhcd,bnhed->bnhce', qc, kc) * jnp.swapaxes(bc, -1, -2) * decay
            y_local = jnp.einsum('bnhce,bnhed->bnhcd', attn, vc)
            chunk_decay = jnp.exp(cla)
            cla_end = cla[:, :, :, -1:, :]
            total_decay = jnp.exp(cla_end)
            decay_to_end = jnp.exp(cla_end - cla)
            kw = kc * bc * decay_to_end
            delta = jnp.einsum('bnhcd,bnhce->bnhde', vc, kw)
            state0 = jnp.zeros((B, H, S, S), x.dtype)

            def step(state, inp):
                q_i, yloc_i, cd_i, td_i, d_i = inp
                y_glob = jnp.einsum('bhce,bhde->bhcd', q_i, state) * cd_i
                new_state = state * td_i + d_i
                return (new_state, y_glob + yloc_i)
            xs = (jnp.moveaxis(qc, 1, 0), jnp.moveaxis(y_local, 1, 0), jnp.moveaxis(chunk_decay, 1, 0), jnp.moveaxis(total_decay, 1, 0), jnp.moveaxis(delta, 1, 0))
            final_state, y_chunks = jax.lax.scan(step, state0, xs)
            y = jnp.moveaxis(y_chunks, 0, 1)
            y = y.transpose(0, 1, 3, 2, 4).reshape(B, Tp, D)[:, :T, :]
            surprise = jnp.linalg.norm(y_local, axis=-1).mean(axis=-1)
            surprise = surprise.reshape(B, -1, 1).mean(axis=1, keepdims=True)
            return (y, final_state, surprise, alpha_val)

        def _reference_tuple_inner(x, Wq, bq, Wk, bk, Wv, bv, Wbeta, bbeta, Walpha, balpha):
            return _forward(x, Wq, bq, Wk, bk, Wv, bv, Wbeta, bbeta, Walpha, balpha)
        key = jax.random.key(seed)
        ks = jax.random.split(key, 6)
        B, T = (2, 512)
        s = 1.0 / np.sqrt(DIM)

        def lin(k, out_dim):
            k1, k2 = jax.random.split(k)
            W = jax.random.uniform(k1, (DIM, out_dim), minval=-s, maxval=s, dtype=jnp.float32)
            b = jax.random.uniform(k2, (out_dim,), minval=-s, maxval=s, dtype=jnp.float32)
            return (W, b)
        Wq, bq = lin(ks[0], NH * HEAD_DIM)
        Wk, bk = lin(ks[1], NH * HEAD_DIM)
        Wv, bv = lin(ks[2], NH * HEAD_DIM)
        Wbeta, bbeta = lin(ks[3], NH)
        Walpha, _ = lin(ks[4], NH)
        balpha = jnp.full((NH,), 2.0, dtype=jnp.float32)
        x = jax.random.normal(ks[5], (B, T, DIM), dtype=jnp.float32)
        return {'x': x, 'Wq': Wq, 'bq': bq, 'Wk': Wk, 'bk': bk, 'Wv': Wv, 'bv': bv, 'Wbeta': Wbeta, 'bbeta': bbeta, 'Walpha': Walpha, 'balpha': balpha}
    _L1_attn_in = _L1_attn_setup()

    def _L1_ffn_setup():
        import jax, jax.numpy as jnp
        import numpy as np
        from jax import lax
        E = 64
        TOP_K = 8
        SEL_K = 4
        THRESH = 0.5
        H = 256
        F_INT = 96
        B, S = (1, 256)
        key = jax.random.key(seed)
        k0, k1, k2, k3, k4 = jax.random.split(key, 5)
        return {'hidden_states': jax.random.normal(k0, (B, S, H), jnp.float32), 'gate_weight': jax.random.normal(k1, (E, H), jnp.float32) * 0.02, 'gate_up_proj': jax.random.normal(k2, (E, 2 * F_INT, H), jnp.float32) * 0.02, 'down_proj': jax.random.normal(k3, (E, H, F_INT), jnp.float32) * 0.02, 'similarity': jax.random.uniform(k4, (E, E), jnp.float32)}
    _L1_ffn_in = _L1_ffn_setup()
    _L1_c = _w((lambda *s: np.random.randn(*s).astype(np.float32) * 0.05)(1, 256))
    _L1_wmod = _w((lambda *s: np.random.randn(*s).astype(np.float32) * 0.05)(256, 6 * 256) * 256 ** (-0.5))

    def _L2_attn_setup():
        import jax, jax.numpy as jnp
        import numpy as np
        D_MODEL = 256
        N_HEADS = 16
        HEAD_DIM = D_MODEL // N_HEADS
        FF = 1024
        KCONV = 4
        EPS = 1e-05

        def _layernorm(x, w, b, eps=EPS):
            m = jnp.mean(x, axis=-1, keepdims=True)
            v = jnp.mean(jnp.square(x - m), axis=-1, keepdims=True)
            return (x - m) * jax.lax.rsqrt(v + eps) * w + b

        def _long_block(x, Wq, Wk, Wv, Wo, conv_w, conv_b, Wig, big, Wog, bog, Wg, bg, vnw, vnb, mnw, mnb, gnw, gnb, ln1w, ln1b, ln2w, ln2b, Wgate, Wval, Wout):
            B, T, C = x.shape
            H, D = (N_HEADS, HEAD_DIM)
            h = _layernorm(x, ln1w, ln1b)
            ht = jnp.transpose(h, (0, 2, 1))
            xc = jax.lax.conv_general_dilated(ht, conv_w, window_strides=(1,), padding=[(KCONV - 1, 0)], dimension_numbers=('NCH', 'OIH', 'NCH'), feature_group_count=C) + conv_b[None, :, None]
            x_conv = jax.nn.silu(jnp.transpose(xc, (0, 2, 1)))

            def l2norm(t):
                return t * jax.lax.rsqrt(jnp.sum(t * t, axis=-1, keepdims=True) + 1e-12)
            q = l2norm((h @ Wq).reshape(B, T, H, D))
            k = l2norm((h @ Wk).reshape(B, T, H, D))
            v = _layernorm((h @ Wv).reshape(B, T, H, D), vnw, vnb)
            i_gate = jax.nn.sigmoid(x_conv @ Wig + big).reshape(B, T, H, D)
            gamma = jax.nn.sigmoid(x_conv @ Wg + bg).reshape(B, T, H, 1)
            u = i_gate * k * v
            g = jnp.broadcast_to(gamma, u.shape)

            def combine(c1, c2):
                a1, b1 = c1
                a2, b2 = c2
                return (a1 * a2, a2 * b1 + b2)
            _, mem = jax.lax.associative_scan(combine, (g, u), axis=1)
            out = (_layernorm(mem, mnw, mnb) * q).reshape(B, T, C)
            og = out.reshape(B, T, H, D)
            m = jnp.mean(og, axis=-1, keepdims=True)
            var = jnp.mean(jnp.square(og - m), axis=-1, keepdims=True)
            og = (og - m) * jax.lax.rsqrt(var + EPS)
            out = (og * gnw.reshape(H, D) + gnb.reshape(H, D)).reshape(B, T, C)
            out = out * jax.nn.sigmoid(x_conv @ Wog + bog)
            h = x + out @ Wo
            h2 = _layernorm(h, ln2w, ln2b)
            mlp = jax.nn.silu(h2 @ Wgate) * (h2 @ Wval) @ Wout
            return h + mlp
        key = jax.random.key(seed)
        ks = jax.random.split(key, 32)
        B, T = (2, 512)
        s = lambda fan: 1.0 / np.sqrt(fan)
        inp = {'x': jax.random.normal(ks[0], (B, T, D_MODEL), jnp.float32), 'Wq': jax.random.normal(ks[1], (D_MODEL, D_MODEL), jnp.float32) * s(D_MODEL), 'Wk': jax.random.normal(ks[2], (D_MODEL, D_MODEL), jnp.float32) * s(D_MODEL), 'Wv': jax.random.normal(ks[3], (D_MODEL, D_MODEL), jnp.float32) * s(D_MODEL), 'Wo': jax.random.normal(ks[4], (D_MODEL, D_MODEL), jnp.float32) * s(D_MODEL), 'conv_w': jax.random.normal(ks[5], (D_MODEL, 1, KCONV), jnp.float32) * s(KCONV), 'conv_b': jnp.zeros((D_MODEL,), jnp.float32), 'Wig': jnp.zeros((D_MODEL, D_MODEL), jnp.float32), 'big': jnp.full((D_MODEL,), -3.0, jnp.float32), 'Wog': jax.random.normal(ks[6], (D_MODEL, D_MODEL), jnp.float32) * s(D_MODEL), 'bog': jnp.zeros((D_MODEL,), jnp.float32), 'Wg': jnp.zeros((D_MODEL, N_HEADS), jnp.float32), 'bg': jnp.asarray(np.log((lambda d: d / (1.0 - d))(1.0 - np.exp(np.linspace(np.log(1 - 0.9), np.log(1 - 0.999), N_HEADS)))), jnp.float32), 'vnw': jnp.ones((HEAD_DIM,), jnp.float32), 'vnb': jnp.zeros((HEAD_DIM,), jnp.float32), 'mnw': jnp.ones((HEAD_DIM,), jnp.float32), 'mnb': jnp.zeros((HEAD_DIM,), jnp.float32), 'gnw': jnp.ones((D_MODEL,), jnp.float32), 'gnb': jnp.zeros((D_MODEL,), jnp.float32), 'ln1w': jnp.ones((D_MODEL,), jnp.float32), 'ln1b': jnp.zeros((D_MODEL,), jnp.float32), 'ln2w': jnp.ones((D_MODEL,), jnp.float32), 'ln2b': jnp.zeros((D_MODEL,), jnp.float32), 'Wgate': jax.random.normal(ks[7], (D_MODEL, FF), jnp.float32) * s(D_MODEL), 'Wval': jax.random.normal(ks[8], (D_MODEL, FF), jnp.float32) * s(D_MODEL), 'Wout': jax.random.normal(ks[9], (FF, D_MODEL), jnp.float32) * s(FF)}
        return inp
    _L2_attn_in = _L2_attn_setup()

    def _L2_ffn_setup():
        import jax, jax.numpy as jnp
        import numpy as np
        N_EXPERTS = 8
        TOP_K = 2
        N_GROUP = 4
        TOPK_GROUP = 2
        ROUTED_SCALE = 1.0

        def _group_limited_topk(scores):
            T, N = scores.shape
            E = N // N_GROUP
            group_scores = scores.reshape(T, N_GROUP, E).max(axis=-1)
            _, gidx = jax.lax.top_k(group_scores, TOPK_GROUP)
            gmask = jax.nn.one_hot(gidx, N_GROUP, dtype=scores.dtype).sum(1)
            smask = jnp.repeat(gmask, E, axis=1)
            masked = jnp.where(smask > 0, scores, jnp.zeros((), scores.dtype))
            topk_w, topk_i = jax.lax.top_k(masked, TOP_K)
            return (topk_w, topk_i)
        key = jax.random.key(seed)
        ks = jax.random.split(key, 8)
        B, S, H, F, FS, N = (2, 128, 256, 176, 352, N_EXPERTS)
        std = jnp.float32(0.02)
        return {'hidden_states': jax.random.normal(ks[0], (B, S, H), jnp.float32), 'gate_weight': jax.random.normal(ks[1], (N, H), jnp.float32) * std, 'gate_w': jax.random.normal(ks[2], (N, F, H), jnp.float32) * std, 'up_w': jax.random.normal(ks[3], (N, F, H), jnp.float32) * std, 'down_w': jax.random.normal(ks[4], (N, H, F), jnp.float32) * std, 'sh_gate_w': jax.random.normal(ks[5], (FS, H), jnp.float32) * std, 'sh_up_w': jax.random.normal(ks[6], (FS, H), jnp.float32) * std, 'sh_down_w': jax.random.normal(ks[7], (H, FS), jnp.float32) * std}
    _L2_ffn_in = _L2_ffn_setup()
    _L2_c = _w((lambda *s: np.random.randn(*s).astype(np.float32) * 0.05)(1, 256))
    _L2_wmod = _w((lambda *s: np.random.randn(*s).astype(np.float32) * 0.05)(256, 6 * 256) * 256 ** (-0.5))

    def _L3_attn_setup():
        import jax, jax.numpy as jnp
        import numpy as np
        B, S, D = (2, 512, 256)
        H, DK, DV = (16, 128, 128)
        SEG = 64
        UPDATE = 'delta'
        CAUSAL = True
        key = jax.random.key(seed)
        ks = jax.random.split(key, 6)
        s = 0.02
        return {'x': jax.random.normal(ks[0], (B, S, D), jnp.float32), 'Wq': jax.random.normal(ks[1], (D, H * DK), jnp.float32) * s, 'Wk': jax.random.normal(ks[2], (D, H * DK), jnp.float32) * s, 'Wv': jax.random.normal(ks[3], (D, H * DV), jnp.float32) * s, 'Wo': jax.random.normal(ks[4], (H * DV, D), jnp.float32) * s, 'betas': jax.random.normal(ks[5], (1, H, 1, DV), jnp.float32)}
    _L3_attn_in = _L3_attn_setup()

    def _L3_ffn_setup():
        import jax, jax.numpy as jnp
        import numpy as np
        TOP_K = 2
        key = jax.random.key(seed)
        ks = jax.random.split(key, 7)
        B, S, H = (2, 256, 256)
        E, A, NS = (8, 64, 2048)
        x = jax.random.normal(ks[0], (B, S, H), jnp.float32)
        gate_w = jax.random.normal(ks[1], (E, H), jnp.float32) * 0.01
        W = jax.random.normal(ks[2], (H, H), jnp.float32) * 0.02
        atoms = jax.random.normal(ks[3], (A, NS), jnp.float32) * 0.02
        expert_atom_weights = jax.random.normal(ks[4], (E, A), jnp.float32) * 0.1
        importance = jax.random.normal(ks[5], (E, NS), jnp.float32) * 0.1
        mask_idx = jax.random.randint(ks[6], (NS,), 0, H * H, jnp.int32)
        return dict(x=x, gate_w=gate_w, W=W, atoms=atoms, expert_atom_weights=expert_atom_weights, importance=importance, mask_idx=mask_idx)
    _L3_ffn_in = _L3_ffn_setup()
    _L3_c = _w((lambda *s: np.random.randn(*s).astype(np.float32) * 0.05)(1, 256))
    _L3_wmod = _w((lambda *s: np.random.randn(*s).astype(np.float32) * 0.05)(256, 6 * 256) * 256 ** (-0.5))
    _d = {'L0_attn_x': _L0_attn_in['x'], 'L0_attn_Wq': _L0_attn_in['Wq'], 'L0_attn_Wkv': _L0_attn_in['Wkv'], 'L0_attn_q_scale': _L0_attn_in['q_scale'], 'L0_attn_k_scale': _L0_attn_in['k_scale'], 'L0_attn_Wg': _L0_attn_in['Wg'], 'L0_attn_bg': _L0_attn_in['bg'], 'L0_attn_Wo': _L0_attn_in['Wo'], 'L0_ffn_W_q': _L0_ffn_in['W_q'], 'L0_ffn_keys': _L0_ffn_in['keys'], 'L0_ffn_down_embed': _L0_ffn_in['down_embed'], 'L0_ffn_up_embed': _L0_ffn_in['up_embed'], 'L0_ffn_gate_w': _L0_ffn_in['gate_w'], 'L0_ffn_up_w': _L0_ffn_in['up_w'], 'L0_ffn_down_w': _L0_ffn_in['down_w'], 'L0_c': _L0_c, 'L0_wmod': _L0_wmod, 'L1_attn_Wq': _L1_attn_in['Wq'], 'L1_attn_bq': _L1_attn_in['bq'], 'L1_attn_Wk': _L1_attn_in['Wk'], 'L1_attn_bk': _L1_attn_in['bk'], 'L1_attn_Wv': _L1_attn_in['Wv'], 'L1_attn_bv': _L1_attn_in['bv'], 'L1_attn_Wbeta': _L1_attn_in['Wbeta'], 'L1_attn_bbeta': _L1_attn_in['bbeta'], 'L1_attn_Walpha': _L1_attn_in['Walpha'], 'L1_attn_balpha': _L1_attn_in['balpha'], 'L1_ffn_gate_weight': _L1_ffn_in['gate_weight'], 'L1_ffn_gate_up_proj': _L1_ffn_in['gate_up_proj'], 'L1_ffn_down_proj': _L1_ffn_in['down_proj'], 'L1_ffn_similarity': _L1_ffn_in['similarity'], 'L1_c': _L1_c, 'L1_wmod': _L1_wmod, 'L2_attn_Wq': _L2_attn_in['Wq'], 'L2_attn_Wk': _L2_attn_in['Wk'], 'L2_attn_Wv': _L2_attn_in['Wv'], 'L2_attn_Wo': _L2_attn_in['Wo'], 'L2_attn_conv_w': _L2_attn_in['conv_w'], 'L2_attn_conv_b': _L2_attn_in['conv_b'], 'L2_attn_Wig': _L2_attn_in['Wig'], 'L2_attn_big': _L2_attn_in['big'], 'L2_attn_Wog': _L2_attn_in['Wog'], 'L2_attn_bog': _L2_attn_in['bog'], 'L2_attn_Wg': _L2_attn_in['Wg'], 'L2_attn_bg': _L2_attn_in['bg'], 'L2_attn_vnw': _L2_attn_in['vnw'], 'L2_attn_vnb': _L2_attn_in['vnb'], 'L2_attn_mnw': _L2_attn_in['mnw'], 'L2_attn_mnb': _L2_attn_in['mnb'], 'L2_attn_gnw': _L2_attn_in['gnw'], 'L2_attn_gnb': _L2_attn_in['gnb'], 'L2_attn_ln1w': _L2_attn_in['ln1w'], 'L2_attn_ln1b': _L2_attn_in['ln1b'], 'L2_attn_ln2w': _L2_attn_in['ln2w'], 'L2_attn_ln2b': _L2_attn_in['ln2b'], 'L2_attn_Wgate': _L2_attn_in['Wgate'], 'L2_attn_Wval': _L2_attn_in['Wval'], 'L2_attn_Wout': _L2_attn_in['Wout'], 'L2_ffn_gate_weight': _L2_ffn_in['gate_weight'], 'L2_ffn_gate_w': _L2_ffn_in['gate_w'], 'L2_ffn_up_w': _L2_ffn_in['up_w'], 'L2_ffn_down_w': _L2_ffn_in['down_w'], 'L2_ffn_sh_gate_w': _L2_ffn_in['sh_gate_w'], 'L2_ffn_sh_up_w': _L2_ffn_in['sh_up_w'], 'L2_ffn_sh_down_w': _L2_ffn_in['sh_down_w'], 'L2_c': _L2_c, 'L2_wmod': _L2_wmod, 'L3_attn_Wq': _L3_attn_in['Wq'], 'L3_attn_Wk': _L3_attn_in['Wk'], 'L3_attn_Wv': _L3_attn_in['Wv'], 'L3_attn_Wo': _L3_attn_in['Wo'], 'L3_attn_betas': _L3_attn_in['betas'], 'L3_ffn_gate_w': _L3_ffn_in['gate_w'], 'L3_ffn_W': _L3_ffn_in['W'], 'L3_ffn_atoms': _L3_ffn_in['atoms'], 'L3_ffn_expert_atom_weights': _L3_ffn_in['expert_atom_weights'], 'L3_ffn_importance': _L3_ffn_in['importance'], 'L3_ffn_mask_idx': _L3_ffn_in['mask_idx'], 'L3_c': _L3_c, 'L3_wmod': _L3_wmod}
    _x0 = _d['L0_attn_x']
    _d['L0_attn_x'] = jax.random.normal(jax.random.fold_in(jax.random.key(seed), 1), (1, 1024, 256), dtype=_x0.dtype)
    del _x0
    return _d

def reference(L0_attn_x, L0_attn_Wq, L0_attn_Wkv, L0_attn_q_scale, L0_attn_k_scale, L0_attn_Wg, L0_attn_bg, L0_attn_Wo, L0_ffn_W_q, L0_ffn_keys, L0_ffn_down_embed, L0_ffn_up_embed, L0_ffn_gate_w, L0_ffn_up_w, L0_ffn_down_w, L0_c, L0_wmod, L1_attn_Wq, L1_attn_bq, L1_attn_Wk, L1_attn_bk, L1_attn_Wv, L1_attn_bv, L1_attn_Wbeta, L1_attn_bbeta, L1_attn_Walpha, L1_attn_balpha, L1_ffn_gate_weight, L1_ffn_gate_up_proj, L1_ffn_down_proj, L1_ffn_similarity, L1_c, L1_wmod, L2_attn_Wq, L2_attn_Wk, L2_attn_Wv, L2_attn_Wo, L2_attn_conv_w, L2_attn_conv_b, L2_attn_Wig, L2_attn_big, L2_attn_Wog, L2_attn_bog, L2_attn_Wg, L2_attn_bg, L2_attn_vnw, L2_attn_vnb, L2_attn_mnw, L2_attn_mnb, L2_attn_gnw, L2_attn_gnb, L2_attn_ln1w, L2_attn_ln1b, L2_attn_ln2w, L2_attn_ln2b, L2_attn_Wgate, L2_attn_Wval, L2_attn_Wout, L2_ffn_gate_weight, L2_ffn_gate_w, L2_ffn_up_w, L2_ffn_down_w, L2_ffn_sh_gate_w, L2_ffn_sh_up_w, L2_ffn_sh_down_w, L2_c, L2_wmod, L3_attn_Wq, L3_attn_Wk, L3_attn_Wv, L3_attn_Wo, L3_attn_betas, L3_ffn_gate_w, L3_ffn_W, L3_ffn_atoms, L3_ffn_expert_atom_weights, L3_ffn_importance, L3_ffn_mask_idx, L3_c, L3_wmod):

    def _L0_attn_ref(x, Wq, Wkv, q_scale, k_scale, Wg, bg, Wo):
        import jax, jax.numpy as jnp
        import numpy as np
        B, N, D = (2, 512, 256)
        H, DH, W = (8, 128, 64)
        SCALE = 8.0

        def _l2norm(t):
            return t / jnp.maximum(jnp.linalg.norm(t, axis=-1, keepdims=True), 1e-12)
        b, n, _ = x.shape
        inner = H * DH
        q = (x @ Wq.T).reshape(b, n, H, DH).transpose(0, 2, 1, 3)
        kv = x @ Wkv.T
        k = kv[..., :inner].reshape(b, n, H, DH).transpose(0, 2, 1, 3)
        v = kv[..., inner:].reshape(b, n, H, DH).transpose(0, 2, 1, 3)
        q = _l2norm(q) * q_scale
        k = _l2norm(k) * k_scale
        nb = n // W
        qb = q.reshape(b, H, nb, W, DH)
        kb = k.reshape(b, H, nb, W, DH)
        vb = v.reshape(b, H, nb, W, DH)

        def look_around(t):
            prev = jnp.concatenate([jnp.zeros_like(t[:, :, :1]), t[:, :, :-1]], axis=2)
            return jnp.concatenate([prev, t], axis=3)
        kw, vw = (look_around(kb), look_around(vb))
        pos = jnp.arange(n).reshape(nb, W)
        pos_prev = jnp.concatenate([jnp.full((1, W), -1), pos[:-1]], axis=0)
        posk = jnp.concatenate([pos_prev, pos], axis=1)
        dist = pos[:, :, None] - posk[:, None, :]
        mask = (posk[:, None, :] >= 0) & (dist >= 0) & (dist <= W)
        sim = jnp.einsum('bhnid,bhnjd->bhnij', qb * SCALE, kw)
        sim = jnp.where(mask, sim, jnp.finfo(sim.dtype).min)
        attn = jax.nn.softmax(sim, axis=-1)
        o = jnp.einsum('bhnij,bhnjd->bhnid', attn, vw).reshape(b, H, n, DH)
        gates = jax.nn.sigmoid(jnp.einsum('bnd,hd->bhn', x, Wg) + bg[None, :, None])
        o = o * gates[..., None]
        o = o.transpose(0, 2, 1, 3).reshape(b, n, inner)
        return o @ Wo.T

    def _L0_ffn_ref(hidden_states, W_q, keys, down_embed, up_embed, gate_w, up_w, down_w):
        import jax, jax.numpy as jnp
        import numpy as np
        HIDDEN = 256
        INTER = 1024
        RETRIEVAL = 128
        NUM_EXPERTS = 512
        NUM_KEYS = 64
        TOP_K = 8
        B, S = (4, 256)
        b, s, h = hidden_states.shape
        n = b * s
        queries = (hidden_states @ W_q).reshape(2, n, RETRIEVAL // 2)
        routing = jnp.einsum('tnd,tdk->tnk', queries, keys)
        scores2, idx2 = jax.lax.top_k(routing, TOP_K)
        sx, sy = (scores2[0], scores2[1])
        ix, iy = (idx2[0], idx2[1])
        all_scores = (sx[:, :, None] + sy[:, None, :]).reshape(n, TOP_K * TOP_K)
        all_idx = (ix[:, :, None] * NUM_KEYS + iy[:, None, :]).reshape(n, TOP_K * TOP_K)
        scores, pk = jax.lax.top_k(all_scores, TOP_K)
        indices = jnp.take_along_axis(all_idx, pk, axis=-1)
        de = down_embed[indices]
        ue = up_embed[indices]
        x = hidden_states.reshape(n, h)
        ew = jnp.einsum('nh,nkh->nk', x, de)
        ew = jax.nn.silu(ew) * jax.nn.softmax(scores, axis=-1)
        experts_states = jnp.einsum('nk,nkh->nh', ew, ue).reshape(b, s, h)
        mlp = jax.nn.silu(x @ gate_w) * (x @ up_w) @ down_w
        return mlp.reshape(b, s, h) + experts_states

    def _L1_attn_ref(x, Wq, bq, Wk, bk, Wv, bv, Wbeta, bbeta, Walpha, balpha):
        import jax, jax.numpy as jnp
        import numpy as np
        DIM = 256
        HEAD_DIM = 128
        NH = DIM // HEAD_DIM
        CHUNK = 128

        def _forward(x, Wq, bq, Wk, bk, Wv, bv, Wbeta, bbeta, Walpha, balpha):
            B, T, D = x.shape
            H, S, C = (NH, HEAD_DIM, CHUNK)
            q = (x @ Wq + bq).reshape(B, T, H, S)
            k = (x @ Wk + bk).reshape(B, T, H, S)
            v = (x @ Wv + bv).reshape(B, T, H, S)
            k = k / jnp.maximum(jnp.linalg.norm(k, axis=-1, keepdims=True), 1e-12)
            alpha_val = jax.nn.sigmoid(x @ Walpha + balpha).reshape(B, T, H, 1)
            beta = jax.nn.softplus(x @ Wbeta + bbeta).reshape(B, T, H, 1)
            pad = -T % C

            def padt(t):
                return jnp.pad(t, ((0, 0), (0, pad), (0, 0), (0, 0))) if pad else t
            qp, kp, vp = (padt(q), padt(k), padt(v))
            ap, bp = (padt(alpha_val), padt(beta))
            Tp = T + pad
            n = Tp // C

            def ch(t):
                return t.reshape(B, n, C, H, t.shape[-1]).transpose(0, 1, 3, 2, 4)
            qc, kc, vc, bc = (ch(qp), ch(kp), ch(vp), ch(bp))
            cla = jnp.cumsum(jnp.log(ch(ap) + 1e-06), axis=3)
            decay = jnp.exp(cla - jnp.swapaxes(cla, -1, -2))
            causal = jnp.tril(jnp.ones((C, C), dtype=bool))
            decay = jnp.where(causal, decay, 0.0)
            attn = jnp.einsum('bnhcd,bnhed->bnhce', qc, kc) * jnp.swapaxes(bc, -1, -2) * decay
            y_local = jnp.einsum('bnhce,bnhed->bnhcd', attn, vc)
            chunk_decay = jnp.exp(cla)
            cla_end = cla[:, :, :, -1:, :]
            total_decay = jnp.exp(cla_end)
            decay_to_end = jnp.exp(cla_end - cla)
            kw = kc * bc * decay_to_end
            delta = jnp.einsum('bnhcd,bnhce->bnhde', vc, kw)
            state0 = jnp.zeros((B, H, S, S), x.dtype)

            def step(state, inp):
                q_i, yloc_i, cd_i, td_i, d_i = inp
                y_glob = jnp.einsum('bhce,bhde->bhcd', q_i, state) * cd_i
                new_state = state * td_i + d_i
                return (new_state, y_glob + yloc_i)
            xs = (jnp.moveaxis(qc, 1, 0), jnp.moveaxis(y_local, 1, 0), jnp.moveaxis(chunk_decay, 1, 0), jnp.moveaxis(total_decay, 1, 0), jnp.moveaxis(delta, 1, 0))
            final_state, y_chunks = jax.lax.scan(step, state0, xs)
            y = jnp.moveaxis(y_chunks, 0, 1)
            y = y.transpose(0, 1, 3, 2, 4).reshape(B, Tp, D)[:, :T, :]
            surprise = jnp.linalg.norm(y_local, axis=-1).mean(axis=-1)
            surprise = surprise.reshape(B, -1, 1).mean(axis=1, keepdims=True)
            return (y, final_state, surprise, alpha_val)

        def _reference_tuple_inner(x, Wq, bq, Wk, bk, Wv, bv, Wbeta, bbeta, Walpha, balpha):
            return _forward(x, Wq, bq, Wk, bk, Wv, bv, Wbeta, bbeta, Walpha, balpha)
        return _reference_tuple_inner(x, Wq, bq, Wk, bk, Wv, bv, Wbeta, bbeta, Walpha, balpha)[0]

    def _L1_ffn_ref(hidden_states, gate_weight, gate_up_proj, down_proj, similarity):
        import jax, jax.numpy as jnp
        import numpy as np
        from jax import lax
        E = 64
        TOP_K = 8
        SEL_K = 4
        THRESH = 0.5
        H = 256
        F_INT = 96
        B, S = (1, 256)
        b, s, h = hidden_states.shape
        x = hidden_states.reshape(-1, h)
        logits = x @ gate_weight.T
        probs = jax.nn.softmax(logits.astype(jnp.float32), axis=-1).astype(logits.dtype)
        top_val, top_idx = lax.top_k(probs, TOP_K)
        top_val = top_val / jnp.clip(top_val.sum(-1, keepdims=True), 1e-12)
        sim = similarity.astype(jnp.float32)
        diag = jnp.arange(E)
        sim = sim.at[diag, diag].set(1.0)
        primary_mask = jnp.zeros((E,), bool).at[top_idx[:, :SEL_K].reshape(-1)].set(True)
        secondary_mask = jnp.zeros((E,), bool).at[top_idx[:, SEL_K:].reshape(-1)].set(True)
        cand = jnp.where(primary_mask[None, :], sim, -jnp.inf)
        best_primary = jnp.argmax(cand, axis=-1)
        best_sim = jnp.max(cand, axis=-1)
        replace = secondary_mask & ~primary_mask & (best_sim >= THRESH)
        mapping = jnp.where(replace, best_primary, jnp.arange(E))
        rerouted = mapping[top_idx]
        rerouted = rerouted.at[:, :SEL_K].set(top_idx[:, :SEL_K])
        flat_e = rerouted.reshape(-1)
        order = jnp.argsort(flat_e)
        tok = order // TOP_K
        xs = x[tok]
        group_sizes = jnp.zeros((E,), jnp.int32).at[flat_e].add(1)
        gu = lax.ragged_dot(xs, jnp.swapaxes(gate_up_proj, 1, 2), group_sizes)
        gate, up = jnp.split(gu, 2, axis=-1)
        hact = jax.nn.silu(gate) * up
        y = lax.ragged_dot(hact, jnp.swapaxes(down_proj, 1, 2), group_sizes)
        w = top_val.reshape(-1)[order]
        out = jnp.zeros_like(x).at[tok].add(y * w[:, None])
        return out.reshape(b, s, h)

    def _L2_attn_ref(x, Wq, Wk, Wv, Wo, conv_w, conv_b, Wig, big, Wog, bog, Wg, bg, vnw, vnb, mnw, mnb, gnw, gnb, ln1w, ln1b, ln2w, ln2b, Wgate, Wval, Wout):
        import jax, jax.numpy as jnp
        import numpy as np
        D_MODEL = 256
        N_HEADS = 16
        HEAD_DIM = D_MODEL // N_HEADS
        FF = 1024
        KCONV = 4
        EPS = 1e-05

        def _layernorm(x, w, b, eps=EPS):
            m = jnp.mean(x, axis=-1, keepdims=True)
            v = jnp.mean(jnp.square(x - m), axis=-1, keepdims=True)
            return (x - m) * jax.lax.rsqrt(v + eps) * w + b

        def _long_block(x, Wq, Wk, Wv, Wo, conv_w, conv_b, Wig, big, Wog, bog, Wg, bg, vnw, vnb, mnw, mnb, gnw, gnb, ln1w, ln1b, ln2w, ln2b, Wgate, Wval, Wout):
            B, T, C = x.shape
            H, D = (N_HEADS, HEAD_DIM)
            h = _layernorm(x, ln1w, ln1b)
            ht = jnp.transpose(h, (0, 2, 1))
            xc = jax.lax.conv_general_dilated(ht, conv_w, window_strides=(1,), padding=[(KCONV - 1, 0)], dimension_numbers=('NCH', 'OIH', 'NCH'), feature_group_count=C) + conv_b[None, :, None]
            x_conv = jax.nn.silu(jnp.transpose(xc, (0, 2, 1)))

            def l2norm(t):
                return t * jax.lax.rsqrt(jnp.sum(t * t, axis=-1, keepdims=True) + 1e-12)
            q = l2norm((h @ Wq).reshape(B, T, H, D))
            k = l2norm((h @ Wk).reshape(B, T, H, D))
            v = _layernorm((h @ Wv).reshape(B, T, H, D), vnw, vnb)
            i_gate = jax.nn.sigmoid(x_conv @ Wig + big).reshape(B, T, H, D)
            gamma = jax.nn.sigmoid(x_conv @ Wg + bg).reshape(B, T, H, 1)
            u = i_gate * k * v
            g = jnp.broadcast_to(gamma, u.shape)

            def combine(c1, c2):
                a1, b1 = c1
                a2, b2 = c2
                return (a1 * a2, a2 * b1 + b2)
            _, mem = jax.lax.associative_scan(combine, (g, u), axis=1)
            out = (_layernorm(mem, mnw, mnb) * q).reshape(B, T, C)
            og = out.reshape(B, T, H, D)
            m = jnp.mean(og, axis=-1, keepdims=True)
            var = jnp.mean(jnp.square(og - m), axis=-1, keepdims=True)
            og = (og - m) * jax.lax.rsqrt(var + EPS)
            out = (og * gnw.reshape(H, D) + gnb.reshape(H, D)).reshape(B, T, C)
            out = out * jax.nn.sigmoid(x_conv @ Wog + bog)
            h = x + out @ Wo
            h2 = _layernorm(h, ln2w, ln2b)
            mlp = jax.nn.silu(h2 @ Wgate) * (h2 @ Wval) @ Wout
            return h + mlp
        return _long_block(x, Wq, Wk, Wv, Wo, conv_w, conv_b, Wig, big, Wog, bog, Wg, bg, vnw, vnb, mnw, mnb, gnw, gnb, ln1w, ln1b, ln2w, ln2b, Wgate, Wval, Wout)

    def _L2_ffn_ref(hidden_states, gate_weight, gate_w, up_w, down_w, sh_gate_w, sh_up_w, sh_down_w):
        import jax, jax.numpy as jnp
        import numpy as np
        N_EXPERTS = 8
        TOP_K = 2
        N_GROUP = 4
        TOPK_GROUP = 2
        ROUTED_SCALE = 1.0

        def _group_limited_topk(scores):
            T, N = scores.shape
            E = N // N_GROUP
            group_scores = scores.reshape(T, N_GROUP, E).max(axis=-1)
            _, gidx = jax.lax.top_k(group_scores, TOPK_GROUP)
            gmask = jax.nn.one_hot(gidx, N_GROUP, dtype=scores.dtype).sum(1)
            smask = jnp.repeat(gmask, E, axis=1)
            masked = jnp.where(smask > 0, scores, jnp.zeros((), scores.dtype))
            topk_w, topk_i = jax.lax.top_k(masked, TOP_K)
            return (topk_w, topk_i)
        B, S, H = hidden_states.shape
        h = hidden_states.reshape(-1, H)
        logits = h.astype(jnp.float32) @ gate_weight.astype(jnp.float32).T
        scores = jax.nn.softmax(logits, axis=-1)
        topk_w, topk_i = _group_limited_topk(scores)
        topk_w = (topk_w * ROUTED_SCALE).astype(h.dtype)
        wmat = (jax.nn.one_hot(topk_i, N_EXPERTS, dtype=topk_w.dtype) * topk_w[..., None]).sum(axis=1)
        g = jnp.einsum('th,nfh->ntf', h, gate_w)
        u = jnp.einsum('th,nfh->ntf', h, up_w)
        e = jnp.einsum('ntf,nhf->nth', jax.nn.silu(g) * u, down_w)
        routed = jnp.einsum('nth,tn->th', e, wmat)
        sg = h @ sh_gate_w.T
        su = h @ sh_up_w.T
        shared = jax.nn.silu(sg) * su @ sh_down_w.T
        return (routed + shared).reshape(B, S, H)

    def _L3_attn_ref(x, Wq, Wk, Wv, Wo, betas):
        import jax, jax.numpy as jnp
        import numpy as np
        B, S, D = (2, 512, 256)
        H, DK, DV = (16, 128, 128)
        SEG = 64
        UPDATE = 'delta'
        CAUSAL = True
        Bsz, seq, _ = x.shape
        nseg = seq // SEG
        q = (x @ Wq).reshape(Bsz, seq, H, DK).transpose(0, 2, 1, 3)
        k = (x @ Wk).reshape(Bsz, seq, H, DK).transpose(0, 2, 1, 3)
        v = (x @ Wv).reshape(Bsz, seq, H, DV).transpose(0, 2, 1, 3)
        qs = q.reshape(Bsz, H, nseg, SEG, DK).transpose(2, 0, 1, 3, 4)
        ks_ = k.reshape(Bsz, H, nseg, SEG, DK).transpose(2, 0, 1, 3, 4)
        vs = v.reshape(Bsz, H, nseg, SEG, DV).transpose(2, 0, 1, 3, 4)
        causal_mask = jnp.tril(jnp.ones((SEG, SEG), bool))
        scale = DK ** 0.5
        beta = jax.nn.sigmoid(betas)

        def step(carry, seg):
            mem, z = carry
            qq, kk, vv = seg
            sigma_q = jax.nn.elu(qq) + 1.0
            scores = jnp.einsum('bhsk,bhtk->bhst', qq, kk) / scale
            if CAUSAL:
                scores = jnp.where(causal_mask, scores, -jnp.inf)
            att_dot = jax.nn.softmax(scores, axis=-1) @ vv
            att_mem = sigma_q @ mem / (sigma_q @ z)
            sigma_k = jax.nn.elu(kk) + 1.0
            if UPDATE == 'linear':
                mem_new = mem + jnp.einsum('bhsk,bhsv->bhkv', sigma_k, vv)
            else:
                delta = vv - sigma_k @ mem / (sigma_k @ z)
                mem_new = mem + jnp.einsum('bhsk,bhsv->bhkv', sigma_k, delta)
            z_new = z + sigma_k.sum(axis=-2, keepdims=True).transpose(0, 1, 3, 2)
            att = beta * att_mem + (1.0 - beta) * att_dot
            out = att.reshape(Bsz, SEG, H * DV) @ Wo
            return ((mem_new, z_new), out)
        mem0 = jnp.zeros((Bsz, H, DK, DV), x.dtype)
        z0 = jnp.ones((Bsz, H, DK, 1), x.dtype) / DK
        _, outs = jax.lax.scan(step, (mem0, z0), (qs, ks_, vs))
        return outs.transpose(1, 0, 2, 3).reshape(Bsz, seq, D)

    def _L3_ffn_ref(x, gate_w, W, atoms, expert_atom_weights, importance, mask_idx):
        import jax, jax.numpy as jnp
        import numpy as np
        TOP_K = 2
        B, S, H = x.shape
        xt = x.reshape(-1, H)
        logits = jnp.clip(xt @ gate_w.T, -50.0, 50.0)
        top_w, top_idx = jax.lax.top_k(logits, TOP_K)
        rw = jax.nn.softmax(top_w, axis=-1)
        deltas = jax.nn.softmax(expert_atom_weights, axis=-1) @ atoms
        weighted = deltas * jax.nn.sigmoid(importance)
        rows = mask_idx // H
        cols = mask_idx % H
        vals = jnp.einsum('tk,tks->ts', rw, weighted[top_idx])
        xg = xt[:, cols]
        contrib = jax.ops.segment_sum((xg * vals).T, rows, num_segments=H)
        out = xt @ W.T + contrib.T
        return out.reshape(B, S, H)
    x = L0_attn_x
    mod = (_silu(L0_c) @ L0_wmod).reshape(L0_c.shape[0], 6, 1, -1)
    sa, ca, ga, sb, cb, gb = (mod[:, 0], mod[:, 1], mod[:, 2], mod[:, 3], mod[:, 4], mod[:, 5])
    ga = (2 * (ga >= 0) - 1) * jnp.maximum(jnp.abs(ga), 0.25)
    gb = (2 * (gb >= 0) - 1) * jnp.maximum(jnp.abs(gb), 0.25)
    h = _layernorm(x, axis=-1) * (1 + ca) + sa
    x = x + ga * _L0_attn_ref(h, L0_attn_Wq, L0_attn_Wkv, L0_attn_q_scale, L0_attn_k_scale, L0_attn_Wg, L0_attn_bg, L0_attn_Wo)
    h = _layernorm(x, axis=-1) * (1 + cb) + sb
    x = x + gb * _L0_ffn_ref(h, L0_ffn_W_q, L0_ffn_keys, L0_ffn_down_embed, L0_ffn_up_embed, L0_ffn_gate_w, L0_ffn_up_w, L0_ffn_down_w)
    mod = (_silu(L1_c) @ L1_wmod).reshape(L1_c.shape[0], 6, 1, -1)
    sa, ca, ga, sb, cb, gb = (mod[:, 0], mod[:, 1], mod[:, 2], mod[:, 3], mod[:, 4], mod[:, 5])
    ga = (2 * (ga >= 0) - 1) * jnp.maximum(jnp.abs(ga), 0.25)
    gb = (2 * (gb >= 0) - 1) * jnp.maximum(jnp.abs(gb), 0.25)
    h = _layernorm(x, axis=-1) * (1 + ca) + sa
    x = x + ga * _L1_attn_ref(h, L1_attn_Wq, L1_attn_bq, L1_attn_Wk, L1_attn_bk, L1_attn_Wv, L1_attn_bv, L1_attn_Wbeta, L1_attn_bbeta, L1_attn_Walpha, L1_attn_balpha)
    h = _layernorm(x, axis=-1) * (1 + cb) + sb
    x = x + gb * _L1_ffn_ref(h, L1_ffn_gate_weight, L1_ffn_gate_up_proj, L1_ffn_down_proj, L1_ffn_similarity)
    mod = (_silu(L2_c) @ L2_wmod).reshape(L2_c.shape[0], 6, 1, -1)
    sa, ca, ga, sb, cb, gb = (mod[:, 0], mod[:, 1], mod[:, 2], mod[:, 3], mod[:, 4], mod[:, 5])
    ga = (2 * (ga >= 0) - 1) * jnp.maximum(jnp.abs(ga), 0.25)
    gb = (2 * (gb >= 0) - 1) * jnp.maximum(jnp.abs(gb), 0.25)
    h = _layernorm(x, axis=-1) * (1 + ca) + sa
    x = x + ga * _L2_attn_ref(h, L2_attn_Wq, L2_attn_Wk, L2_attn_Wv, L2_attn_Wo, L2_attn_conv_w, L2_attn_conv_b, L2_attn_Wig, L2_attn_big, L2_attn_Wog, L2_attn_bog, L2_attn_Wg, L2_attn_bg, L2_attn_vnw, L2_attn_vnb, L2_attn_mnw, L2_attn_mnb, L2_attn_gnw, L2_attn_gnb, L2_attn_ln1w, L2_attn_ln1b, L2_attn_ln2w, L2_attn_ln2b, L2_attn_Wgate, L2_attn_Wval, L2_attn_Wout)
    h = _layernorm(x, axis=-1) * (1 + cb) + sb
    x = x + gb * _L2_ffn_ref(h, L2_ffn_gate_weight, L2_ffn_gate_w, L2_ffn_up_w, L2_ffn_down_w, L2_ffn_sh_gate_w, L2_ffn_sh_up_w, L2_ffn_sh_down_w)
    mod = (_silu(L3_c) @ L3_wmod).reshape(L3_c.shape[0], 6, 1, -1)
    sa, ca, ga, sb, cb, gb = (mod[:, 0], mod[:, 1], mod[:, 2], mod[:, 3], mod[:, 4], mod[:, 5])
    ga = (2 * (ga >= 0) - 1) * jnp.maximum(jnp.abs(ga), 0.25)
    gb = (2 * (gb >= 0) - 1) * jnp.maximum(jnp.abs(gb), 0.25)
    h = _layernorm(x, axis=-1) * (1 + ca) + sa
    x = x + ga * _L3_attn_ref(h, L3_attn_Wq, L3_attn_Wk, L3_attn_Wv, L3_attn_Wo, L3_attn_betas)
    h = _layernorm(x, axis=-1) * (1 + cb) + sb
    x = x + gb * _L3_ffn_ref(h, L3_ffn_gate_w, L3_ffn_W, L3_ffn_atoms, L3_ffn_expert_atom_weights, L3_ffn_importance, L3_ffn_mask_idx)
    return x

_drawn_inputs = setup_inputs


def setup_inputs(seed=0):
    import zlib

    import numpy as np

    out = dict(_drawn_inputs(seed))
    spreads = {'L0_attn_q_scale': (1.0, 0.6),
     'L0_attn_k_scale': (1.0, 0.6),
     'L0_attn_bg': (0.0, 0.8),
     'L1_attn_balpha': (2.0, 0.6),
     'L2_attn_conv_b': (0.0, 0.628),
     'L2_attn_Wig': (0.0, 0.1),
     'L2_attn_big': (-3.0, 0.2),
     'L2_attn_bog': (0.0, 0.8),
     'L2_attn_Wg': (0.0, 0.1),
     'L2_attn_vnw': (1.0, 0.6),
     'L2_attn_vnb': (0.0, 0.46),
     'L2_attn_mnw': (1.0, 0.573),
     'L2_attn_mnb': (0.0, 0.455),
     'L2_attn_gnw': (1.0, 0.557),
     'L2_attn_gnb': (0.0, 0.46),
     'L2_attn_ln1w': (1.0, 0.2),
     'L2_attn_ln1b': (0.0, 0.1),
     'L2_attn_ln2w': (1.0, 0.2),
     'L2_attn_ln2b': (0.0, 0.423)}
    factors = {'L0_attn_Wq': 8.0,
     'L0_attn_Wkv': 8.0,
     'L0_attn_Wg': 8.0,
     'L0_attn_Wo': 8.0,
     'L0_ffn_W_q': 27.963,
     'L0_ffn_keys': 25.895,
     'L0_ffn_down_embed': 8.0,
     'L0_ffn_up_embed': 8.0,
     'L0_ffn_gate_w': 6.243,
     'L0_ffn_up_w': 6.186,
     'L0_ffn_down_w': 6.173,
     'L0_c': 5.491,
     'L0_wmod': 5.364,
     'L1_attn_bq': 5.919,
     'L1_attn_bk': 6.628,
     'L1_attn_bv': 5.903,
     'L1_attn_bbeta': 8.0,
     'L1_attn_Walpha': 3.058,
     'L1_ffn_gate_weight': 8.0,
     'L1_ffn_gate_up_proj': 8.0,
     'L1_ffn_down_proj': 8.0,
     'L2_ffn_gate_weight': 8.0,
     'L2_ffn_gate_w': 8.0,
     'L2_ffn_up_w': 8.0,
     'L2_ffn_down_w': 8.0,
     'L2_ffn_sh_gate_w': 8.0,
     'L2_ffn_sh_up_w': 8.0,
     'L2_ffn_sh_down_w': 8.0,
     'L3_attn_Wq': 8.0,
     'L3_attn_Wk': 8.0,
     'L3_attn_Wv': 5.43,
     'L3_attn_Wo': 5.426,
     'L3_attn_betas': 8.0,
     'L3_ffn_gate_w': 64.0,
     'L3_ffn_atoms': 64.0,
     'L3_ffn_expert_atom_weights': 64.0,
     'L3_ffn_importance': 64.0,
     'L3_ffn_W': 3.536}
    for name, (base, spread) in spreads.items():
        noise = np.random.default_rng([zlib.crc32(name.encode()), seed]).standard_normal(out[name].shape)
        drawn = base * np.exp(spread * noise) if base else spread * noise
        out[name] = jnp.asarray(drawn.astype(out[name].dtype))
    for name, factor in factors.items():
        out[name] = (out[name] * factor).astype(out[name].dtype)
    return out
```

```python
from contextlib import ExitStack, contextmanager

import numpy as np

import concourse.bass as bass
import concourse.mybir as mybir

F32 = mybir.dt.float32
I32 = mybir.dt.int32
ACT = mybir.ActivationFunctionType
ALU = mybir.AluOpType
AX = mybir.AxisListType

P = 128
T = 1024
D = 256
DB = D // P
CH = 512
NCH = T // CH
TT = T // P
NEG = -1.0e30
EXP_LN = "natural_log_exp_and_others"

SHIFT_A, SCALE_A, GATE_A, SHIFT_B, SCALE_B, GATE_B = range(0, 6 * DB, DB)


class Chain:

    def __init__(self, sem):
        self.sem, self.done, self.turn, self.each, self.k = sem, 0, None, 0, 0

    def link(self, eng, ins):
        ins.then_inc(self.sem, 1)
        self.k += 1
        if self.turn is None:
            self.done, self.k = self.done + 1, 0
            eng.wait_ge(self.sem, self.done)
        else:
            eng.wait_ge(self.sem, self.turn * self.each + (self.done + self.k))

    def enter(self, turn, each):
        self.turn, self.each, self.k = turn, each, 0

    def leave(self, turns):
        assert self.k == self.each, (self.k, self.each)
        self.done, self.turn, self.k = self.done + turns * self.each, None, 0


class Core:

    def __init__(self, nc, ctx, dram):
        self.nc, self.ctx, self.dram, self.local = nc, ctx, dram, None
        self.x = ctx.enter_context(nc.sbuf_tensor("x_stream", [P, DB, T], F32))
        self.h = ctx.enter_context(nc.sbuf_tensor("h_modulated", [P, DB, T], F32))
        self.mod = ctx.enter_context(nc.sbuf_tensor("modulation", [P, 4, 6 * DB], F32))
        self.ident = ctx.enter_context(nc.sbuf_tensor("ident", [P, P], F32))
        self.ones = ctx.enter_context(nc.sbuf_tensor("ones", [P, P], F32))
        self.zeros = ctx.enter_context(nc.sbuf_tensor("zeros", [P, CH], F32))
        self.mean_w = ctx.enter_context(nc.sbuf_tensor("mean_w", [P, P], F32))
        self.eps = ctx.enter_context(nc.sbuf_tensor("eps", [P, 4], F32))
        self.bank = ctx.enter_context(nc.psum_tensor("bank", [P, 8, CH], F32))
        self.dve_chain = Chain(self.sem("dve_step"))
        self.act_chain = Chain(self.sem("act_step"))
        self.pool_chain = Chain(self.sem("pool_step"))
        self.calls = {}

    def sem(self, name):
        if self.local is None:
            return self.ctx.enter_context(self.nc.semaphore(name))
        self.local.append(self.nc.alloc_semaphore(name=name))
        return self.local[-1]

    @contextmanager
    def stage(self):
        self.local = []
        yield
        self.nc.clear_and_free_semaphores(self.local)
        self.nc.all_engine_barrier()
        self.local = None

    def shared(self, name):
        if name not in self.calls:
            self.calls[name] = self.ctx.enter_context(self.nc.semaphore(name))
        return self.calls[name]


def over(ap, n, axis=1):
    a = ap.unsqueeze(axis)
    shape = list(a.shape)
    shape[axis] = n
    return a.to_broadcast(shape)


def chunk(c):
    return slice(c * CH, (c + 1) * CH)


def tile(t):
    return slice(t * P, (t + 1) * P)


EPS_LN, EPS_L2 = 1.0e-5, 1.0e-12


def constants(k):
    nc = k.nc
    with nc.Block() as block:
        @block.gpsimd
        def _(pool):
            step = k.pool_chain
            pool.memset(k.ones[:], 1.0)
            pool.memset(k.zeros[:], 0.0)
            pool.memset(k.mean_w[:], 1.0 / D)
            pool.memset(k.eps[:, 0:1], EPS_LN)
            pool.memset(k.eps[:, 1:2], EPS_L2)
            pool.memset(k.eps[:, 2:3], 1.0)
            pool.memset(k.eps[:, 3:4], 1.0e-6)
            step.link(pool, pool.memset(k.ident[:], 0.0))
            step.link(pool, pool.affine_select(out=k.ident[:], in_=k.ident[:], compare_op=ALU.not_equal, fill=1.0,
                                               base=0, pattern=[[-1, P]], channel_multiplier=1))


def modulations(k):
    nc, d = k.nc, k.dram
    x_in, row_ready, row_copied, col_ready, c_ready = (
        k.sem(n) for n in ("x_in", "mod_row_ready", "mod_row_copied", "mod_col_ready", "silu_c_ready"))
    w_in = [k.sem(f"wmod_in{n}") for n in range(2)]
    with ExitStack() as ctx:
        cs = ctx.enter_context(nc.sbuf_tensor("cs", [P, 4 * DB], F32))
        w = ctx.enter_context(nc.sbuf_tensor("wmod", [P, 2, DB, 6 * D], F32))
        row = ctx.enter_context(nc.sbuf_tensor("mod_row", [1, 2, 6 * D], F32))
        tmp = ctx.enter_context(nc.sbuf_tensor("mod_tmp", [P, 4, DB], F32))
        with nc.Block() as block:
            @block.sync
            def _(sp):
                sp.dma_start(cs[:], d["cs"]).then_inc(c_ready, 16)
                for layer in range(4):
                    if layer >= 2:
                        sp.wait_ge(row_ready, layer - 1)
                    sp.dma_start(w[:, layer % 2], d["wmod"][layer].rearrange("(b p) n -> p b n", p=P)
                                 ).then_inc(w_in[layer % 2], 16)
                sp.dma_start(k.x[:], d["x"].rearrange("(b p) t -> p b t", p=P)).then_inc(x_in, 16)
                sp.wait_ge(x_in, 16)

            @block.scalar
            def _(act):
                act.wait_ge(c_ready, 16)
                act.activation(cs[:], cs[:], ACT.Silu).then_inc(c_ready, 1)
                for layer in range(4):
                    act.wait_ge(row_ready, layer + 1)
                    if layer >= 2:
                        act.wait_ge(col_ready, layer - 1)
                    act.activation(row[0:1, layer % 2].rearrange("p (n c) -> p n c", n=3), k.bank[0:1, 0:3, :],
                                   ACT.Identity).then_inc(row_copied, 1)

            @block.tensor
            def _(pe):
                pe.wait_ge(c_ready, 17)
                for layer in range(4):
                    pe.wait_ge(w_in[layer % 2], 16 * (layer // 2 + 1))
                    if layer:
                        pe.wait_ge(row_copied, layer)
                    for n in range(3):
                        for b in range(DB):
                            last = pe.matmul(k.bank[0:1, n, :], cs[:, layer * DB + b:layer * DB + b + 1],
                                             w[:, layer % 2, b, chunk(n)], start=(b == 0), stop=(b == DB - 1))
                    last.then_inc(row_ready, 1)
                    pe.wait_ge(row_copied, layer + 1)
                    for j in range(6 * DB):
                        last = pe.matmul(k.bank[:, 4, layer * 16 + j:layer * 16 + j + 1],
                                         row[0:1, layer % 2, tile(j)], k.ones[0:1, 0:1], start=True, stop=True)
                    last.then_inc(col_ready, 1)

            @block.vector
            def _(dve):
                step = k.dve_chain
                dve.wait_ge(col_ready, 4)
                cols = k.bank[:, 4, 0:64].rearrange("p (l j) -> p l j", l=4)
                step.link(dve, dve.tensor_copy(k.mod[:], cols[:, :, 0:6 * DB]))
                for at in (SCALE_A, SCALE_B):
                    s = k.mod[:, :, at:at + DB]
                    step.link(dve, dve.tensor_scalar(s, s, 1.0, None, ALU.add))
                for at in (GATE_A, GATE_B):
                    g = k.mod[:, :, at:at + DB]
                    step.link(dve, dve.tensor_scalar(tmp[:], g, 0.0, 2.0, ALU.is_ge, ALU.mult))
                    step.link(dve, dve.tensor_scalar(tmp[:], tmp[:], -1.0, None, ALU.add))
                    step.link(dve, dve.tensor_tensor(g, g, tmp[:], ALU.mult))
                    step.link(dve, dve.tensor_scalar(g, g, 0.25, None, ALU.max))
                    step.link(dve, dve.tensor_tensor(g, g, tmp[:], ALU.mult))


def layernorm(k, src, dst, scale, shift):
    nc = k.nc
    mean_ready, centered, squared, var_ready, root_ready, normed, out_ready = (
        k.shared("ln_" + n) for n in ("mean_ready", "centered", "squared", "var_ready", "root_ready", "normed", "out"))
    at = NCH * k.calls.setdefault("layernorms", 0)
    k.calls["layernorms"] += 1
    with ExitStack() as ctx:
        xc = ctx.enter_context(nc.sbuf_tensor(f"ln_centered{at}", [P, DB, T], F32))
        sq = ctx.enter_context(nc.sbuf_tensor(f"ln_square{at}", [P, DB, T], F32))
        rs = ctx.enter_context(nc.sbuf_tensor(f"ln_rstd{at}", [P, T], F32))
        with nc.Block() as block:
            @block.tensor
            def _(pe):
                for c in range(NCH):
                    for b in range(DB):
                        last = pe.matmul(k.bank[:, c, :], k.mean_w[:], src[:, b, chunk(c)],
                                         start=(b == 0), stop=(b == DB - 1))
                    last.then_inc(mean_ready, 1)
                for c in range(NCH):
                    pe.wait_ge(squared, at + c + 1)
                    for b in range(DB):
                        last = pe.matmul(k.bank[:, 2 + c, :], k.mean_w[:], sq[:, b, chunk(c)],
                                         start=(b == 0), stop=(b == DB - 1))
                    last.then_inc(var_ready, 1)

            @block.vector
            def _(dve):
                for c in range(NCH):
                    dve.wait_ge(mean_ready, at + c + 1)
                    dve.tensor_tensor(xc[:, :, chunk(c)], src[:, :, chunk(c)], over(k.bank[:, c, :], DB),
                                      ALU.subtract).then_inc(centered, 1)
                for c in range(NCH):
                    dve.wait_ge(root_ready, at + c + 1)
                    dve.tensor_tensor(xc[:, :, chunk(c)], xc[:, :, chunk(c)], over(rs[:, chunk(c)], DB),
                                      ALU.mult).then_inc(normed, 1)
                    dve.wait_ge(normed, at + c + 1)
                    for b in range(DB):
                        last = dve.tensor_scalar(dst[:, b, chunk(c)], xc[:, b, chunk(c)], scale[:, b:b + 1],
                                                 shift[:, b:b + 1], ALU.mult, ALU.add)
                    last.then_inc(out_ready, 1)

            @block.scalar
            def _(act):
                act.preload_act_table_set(EXP_LN)
                for c in range(NCH):
                    act.wait_ge(centered, at + c + 1)
                    act.activation(sq[:, :, chunk(c)], xc[:, :, chunk(c)], ACT.Square).then_inc(squared, 1)
                for c in range(NCH):
                    act.wait_ge(var_ready, at + c + 1)
                    k.act_chain.link(act, act.activation(rs[:, chunk(c)], k.bank[:, 2 + c, :], ACT.Ln,
                                                         bias=k.eps[:, 0:1]))
                    act.activation(rs[:, chunk(c)], rs[:, chunk(c)], ACT.Exp, scale=-0.5).then_inc(root_ready, 1)


def adaln(k, layer, shift, scale):
    layernorm(k, k.x, k.h, k.mod[:, layer, scale:scale + DB], k.mod[:, layer, shift:shift + DB])


def gated_units(k, name, units, f, w_in, w_out, gate, src=None, row_of=None, rows=None, extra=None):
    nc = k.nc
    src = k.h if src is None else src
    pairs = units // 2
    loads = 2 if rows is None else 3
    loaded = [k.sem(f"{name}_w_in{n}") for n in range(2)]
    up_ready, act_ready, gated, summed, done = (
        k.sem(f"{name}_{n}") for n in ("up_ready", "act_ready", "gated", "summed", "done"))
    with ExitStack() as ctx:
        wi = ctx.enter_context(nc.sbuf_tensor(f"{name}_wi", [P, 2, DB, 2 * f], F32))
        wo = ctx.enter_context(nc.sbuf_tensor(f"{name}_wo", [P, 2, D], F32))
        s = ctx.enter_context(nc.sbuf_tensor(f"{name}_s", [P, NCH, CH], F32))
        a = ctx.enter_context(nc.sbuf_tensor(f"{name}_a", [P, NCH, CH], F32))
        wr = ctx.enter_context(nc.sbuf_tensor(f"{name}_wr", [P, 2, T], F32)) if rows is not None else None
        with nc.Block() as block:
            @block.sync
            def _(sp):
                def load(i, half):
                    u = i * 2 + half
                    sp.dma_start(wi[:, half], w_in[bass.ds(u, 1)].rearrange("u p (b n) -> p (u b) n", b=DB)
                                 ).then_inc(loaded[half], 16)
                    sp.dma_start(wo[0:f, half], w_out[bass.ds(u, 1)].rearrange("u f n -> f (u n)")
                                 ).then_inc(loaded[half], 16)
                    if rows is not None:
                        r = row_of(i, half)
                        sp.dma_start(wr[:, half], rows[bass.ds(r, 1)].to_broadcast([P, T])).then_inc(loaded[half], 16)

                for half in range(2):
                    load(0, half)
                with sp.Fori(1, pairs) as i:
                    for half in range(2):
                        sp.wait_ge(summed, i * 4 + (2 * half - 2))
                        load(i, half)

            @block.tensor
            def _(pe):
                for m in range(DB):
                    for c in range(NCH):
                        pe.matmul(k.bank[:, 4 + 2 * m + c, :], k.zeros[:, 0:P], k.zeros[:], start=True, stop=False,
                                  skip_group_check=True)
                for n, (lhs_t, rhs) in enumerate(extra or []):
                    for m in range(DB):
                        for c in range(NCH):
                            pe.matmul(k.bank[:, 4 + 2 * m + c, :], lhs_t[:, tile(m)], rhs[:, chunk(c)], start=False,
                                      stop=False, skip_group_check=True)

                def up(i, half, c):
                    if c == 0:
                        pe.wait_ge(loaded[half], (i + 1) * (16 * loads))
                    for part in range(2):
                        for b in range(DB):
                            last = pe.matmul(k.bank[0:f, 2 * c + part, :], wi[:, half, b, part * f:(part + 1) * f],
                                             src[:, b, chunk(c)], start=(b == 0), stop=(b == DB - 1))
                    last.then_inc(up_ready, 1)

                def down(i, half, c):
                    pe.wait_ge(gated, i * 4 + (2 * half + c + 1))
                    for m in range(DB):
                        last = pe.matmul(k.bank[:, 4 + 2 * m + c, :], wo[0:f, half, tile(m)], a[0:f, c, :],
                                         start=False, stop=False, skip_group_check=True)
                    last.then_inc(summed, 1)

                def pair(i, last):
                    up(i, 0, 1)
                    down(i, 0, 0)
                    up(i, 1, 0)
                    down(i, 0, 1)
                    up(i, 1, 1)
                    down(i, 1, 0)
                    if not last:
                        up(i + 1, 0, 0)
                    down(i, 1, 1)

                up(0, 0, 0)
                with pe.Fori(0, pairs - 1) as i:
                    pair(i, False)
                pair(pairs - 1, True)

            @block.scalar
            def _(act):
                act.preload_act_table(ACT.Silu)
                with act.Fori(0, pairs) as i:
                    for n in range(4):
                        c = n % 2
                        act.wait_ge(up_ready, i * 4 + (n + 1))
                        act.activation(s[0:f, c, :], k.bank[0:f, 2 * c, :], ACT.Silu).then_inc(act_ready, 1)

            @block.vector
            def _(dve):
                step = k.dve_chain
                with dve.Fori(0, pairs) as i:
                    step.enter(i, 0 if rows is None else 4)
                    for n in range(4):
                        half, c = n // 2, n % 2
                        dve.wait_ge(act_ready, i * 4 + (n + 1))
                        if rows is None:
                            dve.tensor_tensor(a[0:f, c, :], s[0:f, c, :], k.bank[0:f, 2 * c + 1, :], ALU.mult
                                              ).then_inc(gated, 1)
                        else:
                            step.link(dve, dve.tensor_tensor(a[0:f, c, :], s[0:f, c, :], k.bank[0:f, 2 * c + 1, :],
                                                             ALU.mult))
                            dve.tensor_tensor(a[0:f, c, :], a[0:f, c, :], wr[0:f, half, chunk(c)], ALU.mult
                                              ).then_inc(gated, 1)
                step.leave(pairs)
                dve.wait_ge(summed, 4 * pairs)
                for m in range(DB):
                    for c in range(NCH):
                        last = dve.scalar_tensor_tensor(k.x[:, m, chunk(c)], k.bank[:, 4 + 2 * m + c, :],
                                                        gate[:, m:m + 1], k.x[:, m, chunk(c)], ALU.mult, ALU.add)
                last.then_inc(done, 1)


def l0_attention(k):
    nc, d = k.nc, k.dram
    H, W, KW = 8, 64, 192
    SCALE = 8.0
    w_in = k.sem("l0_w_in")
    v_w_in, v_ready, v_copied, g_ready, gate_exp, gate_one, gates_ready, mask_ready, qscale_in = (
        k.sem("l0_" + n) for n in ("v_w_in", "v_ready", "v_copied", "g_ready", "gate_exp", "gate_one", "gates_ready",
                                   "mask_ready", "qscale_in"))
    qk_ready, sq_ready, ss_ready, ss_clamped, rn_ready, qk_normed, scores_ready, shifted, probs_exp, probs_ready = (
        k.sem("l0_" + n) for n in ("qk_ready", "sq_ready", "ss_ready", "ss_clamped", "rn_ready", "qk_normed",
                                   "scores_ready", "shifted", "probs_exp", "probs_ready"))
    pt_ready, pt_copied, o_ready, o_copied, vh_ready, y_ready, y_done = (
        k.sem("l0_" + n) for n in ("pt_ready", "pt_copied", "o_ready", "o_copied", "vh_ready", "y_ready", "y_done"))
    with ExitStack() as ctx:
        def sb(n, shape):
            return ctx.enter_context(nc.sbuf_tensor("l0_" + n, shape, F32))
        wv = sb("wv", [P, DB, H * P])
        wo = sb("wo", [P, H, D])
        wg = sb("wg", [P, DB, H])
        bg = sb("bg", [P, H])
        scales = sb("scales", [P, 2])
        wqk = sb("wqk", [P, DB, 2 * P])
        v = sb("v", [P, TT, H * P])
        vh = sb("vh", [P, TT, P])
        gates = sb("gates", [P, TT, H])
        qk = sb("qk", [P, 2, W + T])
        sq = sb("sq", [P, 2, CH])
        rn = sb("rn", [P, 2, CH])
        mask = sb("mask", [P, 2, KW])
        sc = sb("sc", [P, TT, P + P])
        st = sb("st", [P, 3, TT])
        pt = sb("pt", [P, TT, 2, P])
        o = sb("o", [P, H, T])
        with nc.Block() as block:
            @block.sync
            def _(sp):
                sp.dma_start(wv[:], d["l0_wv"].rearrange("(b p) n -> p b n", p=P)).then_inc(v_w_in, 16)
                sp.dma_start(wg[:], d["l0_wg"].rearrange("(b p) n -> p b n", p=P)).then_inc(v_w_in, 16)
                sp.dma_start(bg[:], d["l0_bg"].to_broadcast([P, H])).then_inc(v_w_in, 16)
                sp.dma_start(scales[:], d["l0_scales"]).then_inc(qscale_in, 16)
                sp.dma_start(wqk[:], d["l0_wqk"][0].rearrange("(b p) n -> p b n", p=P)).then_inc(w_in, 16)
                sp.dma_start(wo[:], d["l0_wo"].rearrange("(h p) n -> p h n", p=P)).then_inc(qscale_in, 16)
                with sp.Fori(1, H) as h:
                    sp.wait_ge(qk_ready, h * 4)
                    sp.dma_start(wqk[:], d["l0_wqk"][bass.ds(h, 1)].rearrange("u (b p) n -> p (u b) n", p=P)
                                 ).then_inc(w_in, 16)

            @block.gpsimd
            def _(pool):
                step = k.pool_chain
                pool.memset(qk[:, :, 0:W], 0.0)
                pool.memset(sc[:, :, 0:W], 0.0)
                step.link(pool, pool.memset(mask[:], 0.0))
                m0, m1 = mask[:, 0, :], mask[:, 1, :]
                for m in (m0, m1):
                    step.link(pool, pool.affine_select(out=m, in_=m, compare_op=ALU.is_ge, fill=NEG, base=W,
                                                       pattern=[[-1, KW]], channel_multiplier=1))
                    step.link(pool, pool.affine_select(out=m, in_=m, compare_op=ALU.is_ge, fill=NEG, base=0,
                                                       pattern=[[1, KW]], channel_multiplier=-1))
                pool.memset(mask[:, 0, 0:W], NEG).then_inc(mask_ready, 1)
                with pool.Fori(0, H) as h:
                    pool.wait_ge(v_copied, 2 * TT)
                    pool.wait_ge(o_ready, h * 2)
                    pool.tensor_copy(vh[:], v[:, :, bass.ds(h * P, P)]).then_inc(vh_ready, 1)

            @block.tensor
            def _(pe):
                pe.wait_ge(v_w_in, 48)
                for t in range(TT):
                    for n in range(2):
                        j = 2 * t + n
                        if j >= 2:
                            pe.wait_ge(v_copied, j - 1)
                        for b in range(DB):
                            last = pe.matmul(k.bank[:, j % 2, :], k.h[:, b, tile(t)], wv[:, b, chunk(n)],
                                             start=(b == 0), stop=(b == DB - 1))
                        last.then_inc(v_ready, 1)
                for t in range(TT):
                    for b in range(DB):
                        last = pe.matmul(k.bank[:, 2, t * H:(t + 1) * H], k.h[:, b, tile(t)], wg[:, b, :],
                                         start=(b == 0), stop=(b == DB - 1))
                last.then_inc(g_ready, 1)
                pe.wait_ge(v_copied, 2 * TT)
                pe.wait_ge(gates_ready, 1)
                with pe.Fori(0, H) as h:
                    pe.wait_ge(w_in, (h + 1) * 16)
                    pe.wait_ge(o_copied, h * 2)
                    for j in range(4):
                        for b in range(DB):
                            last = pe.matmul(k.bank[:, j, :], wqk[:, b, tile(j // 2)], k.h[:, b, chunk(j % 2)],
                                             start=(b == 0), stop=(b == DB - 1))
                        last.then_inc(qk_ready, 1)
                    for j in range(4):
                        pe.wait_ge(sq_ready, h * 4 + (j + 1))
                        pe.matmul(k.bank[:, 4 + j, :], k.ones[:], sq[:, j % 2, :], start=True, stop=True
                                  ).then_inc(ss_ready, 1)
                    pe.wait_ge(qk_normed, h * 4 + 4)
                    for t in range(TT):
                        last = pe.matmul(k.bank[:, t // 2, (t % 2) * 256:(t % 2) * 256 + KW],
                                         qk[:, 0, W + t * P:W + (t + 1) * P], qk[:, 1, t * P:t * P + KW],
                                         start=True, stop=True)
                    last.then_inc(scores_ready, 1)
                    pe.wait_ge(probs_ready, h + 1)
                    for t in range(TT):
                        for part in range(2):
                            last = pe.transpose(k.bank[:, 4 + t // 2, (t % 2) * 256 + part * P:
                                                       (t % 2) * 256 + (part + 1) * P],
                                                sc[:, t, tile(part)], k.ident[:])
                        if t % 2:
                            last.then_inc(pt_ready, 1)
                    pe.wait_ge(vh_ready, h + 1)
                    for t in range(TT):
                        if t % 2 == 0:
                            pe.wait_ge(pt_copied, h * 4 + (t // 2 + 1))
                        out = k.bank[:, t // 4, (t % 4) * P:(t % 4 + 1) * P]
                        if t:
                            pe.matmul(out, vh[:, t - 1, :], pt[:, t, 0, :], start=True, stop=False)
                        last = pe.matmul(out, vh[:, t, :], pt[:, t, 1, :], start=(t == 0), stop=True)
                        if t % 4 == 3:
                            last.then_inc(o_ready, 1)
                pe.wait_ge(qscale_in, 32)
                pe.wait_ge(o_copied, 2 * H)
                for m in range(DB):
                    for c in range(NCH):
                        for h in range(H):
                            last = pe.matmul(k.bank[:, 2 * m + c, :], wo[:, h, tile(m)], o[:, h, chunk(c)],
                                             start=(h == 0), stop=(h == H - 1))
                        last.then_inc(y_ready, 1)

            @block.scalar
            def _(act):
                step = k.act_chain
                act.preload_act_table_set(EXP_LN)
                for j in range(2 * TT):
                    act.wait_ge(v_ready, j + 1)
                    act.activation(v[:, j // 2, chunk(j % 2)], k.bank[:, j % 2, :], ACT.Identity
                                   ).then_inc(v_copied, 1)
                act.wait_ge(gate_one, 1)
                act.activation(gates[:], gates[:], ACT.Exp, scale=-1.0).then_inc(gate_exp, 1)
                with act.Fori(0, H) as h:
                    step.enter(h, 4)
                    for j in range(4):
                        act.wait_ge(qk_ready, h * 4 + (j + 1))
                        if j >= 2:
                            act.wait_ge(ss_ready, h * 4 + (j - 1))
                        act.activation(sq[:, j % 2, :], k.bank[:, j, :], ACT.Square).then_inc(sq_ready, 1)
                    for j in range(4):
                        act.wait_ge(ss_clamped, h * 4 + (j + 1))
                        step.link(act, act.activation(rn[:, j % 2, :], rn[:, j % 2, :], ACT.Ln, scale=65536.0))
                        act.activation(rn[:, j % 2, :], rn[:, j % 2, :], ACT.Exp, scale=-0.5).then_inc(rn_ready, 1)
                    act.wait_ge(shifted, h + 1)
                    act.activation(sc[:, :, W:W + KW], sc[:, :, W:W + KW], ACT.Exp).then_inc(probs_exp, 1)
                    for j in range(4):
                        act.wait_ge(pt_ready, h * 4 + (j + 1))
                        act.activation(pt[:, 2 * j:2 * j + 2], k.bank[:, 4 + j, :].rearrange(
                            "p (t a q) -> p t a q", t=2, a=2), ACT.Identity).then_inc(pt_copied, 1)
                    for c in range(2):
                        act.wait_ge(o_ready, h * 2 + (c + 1))
                        act.activation(o[:, bass.ds(h, 1), chunk(c)], k.bank[:, c:c + 1, :], ACT.Identity
                                       ).then_inc(o_copied, 1)
                step.leave(H)

            @block.vector
            def _(dve):
                step = k.dve_chain
                dve.wait_ge(v_w_in, 48)
                dve.wait_ge(g_ready, 1)
                dve.tensor_tensor(gates[:], k.bank[:, 2, 0:TT * H].rearrange("p (t h) -> p t h", t=TT),
                                  over(bg[:], TT), ALU.add).then_inc(gate_one, 1)
                dve.wait_ge(gate_exp, 1)
                step.link(dve, dve.tensor_scalar(gates[:], gates[:], 1.0, None, ALU.add))
                dve.reciprocal(gates[:], gates[:]).then_inc(gates_ready, 1)
                dve.wait_ge(gates_ready, 1)
                dve.wait_ge(qscale_in, 32)
                step.link(dve, dve.tensor_scalar(scales[:], scales[:], 256.0, None, ALU.mult))
                step.link(dve, dve.tensor_scalar(scales[:, 0:1], scales[:, 0:1], SCALE, None, ALU.mult))
                dve.wait_ge(mask_ready, 1)
                with dve.Fori(0, H) as h:
                    step.enter(h, 6)
                    for j in range(4):
                        dve.wait_ge(ss_ready, h * 4 + (j + 1))
                        if j >= 2:
                            dve.wait_ge(qk_normed, h * 4 + (j - 1))
                        dve.tensor_scalar(rn[:, j % 2, :], k.bank[:, 4 + j, :], 1.0e-24, None, ALU.max
                                          ).then_inc(ss_clamped, 1)
                        if j >= 1:
                            i = j - 1
                            dve.wait_ge(rn_ready, h * 4 + j)
                            dve.scalar_tensor_tensor(qk[:, i // 2, W + (i % 2) * CH:W + (i % 2 + 1) * CH],
                                                     k.bank[:, i, :], scales[:, i // 2:i // 2 + 1], rn[:, i % 2, :],
                                                     ALU.mult, ALU.mult).then_inc(qk_normed, 1)
                    dve.wait_ge(rn_ready, h * 4 + 4)
                    dve.scalar_tensor_tensor(qk[:, 1, W + CH:W + 2 * CH], k.bank[:, 3, :], scales[:, 1:2],
                                             rn[:, 1, :], ALU.mult, ALU.mult).then_inc(qk_normed, 1)
                    dve.wait_ge(scores_ready, h + 1)
                    banks = k.bank[:, 0:4, :].rearrange("p n (a q) -> p (n a) q", a=2)
                    s = sc[:, :, W:W + KW]
                    dve.tensor_tensor(s[:, 0:1], banks[:, 0:1, 0:KW], mask[:, 0:1], ALU.add)
                    step.link(dve, dve.tensor_tensor(s[:, 1:TT], banks[:, 1:TT, 0:KW], over(mask[:, 1, :], TT - 1),
                                                     ALU.add))
                    step.link(dve, dve.tensor_reduce(st[:, 0, :], s, AX.X, ALU.max))
                    dve.tensor_tensor(s, s, over(st[:, 0, :], KW, 2), ALU.subtract).then_inc(shifted, 1)
                    dve.wait_ge(probs_exp, h + 1)
                    step.link(dve, dve.tensor_reduce(st[:, 1, :], s, AX.X, ALU.add))
                    step.link(dve, dve.reciprocal(st[:, 2, :], st[:, 1, :]))
                    step.link(dve, dve.tensor_copy(st[:, 0, :], gates[:, :, bass.ds(h, 1)].rearrange(
                        "p t h -> p (t h)")))
                    step.link(dve, dve.tensor_tensor(st[:, 2, :], st[:, 2, :], st[:, 0, :], ALU.mult))
                    dve.tensor_tensor(s, s, over(st[:, 2, :], KW, 2), ALU.mult).then_inc(probs_ready, 1)
                step.leave(H)
                for j in range(4):
                    dve.wait_ge(y_ready, j + 1)
                    m, c = j // 2, j % 2
                    last = dve.scalar_tensor_tensor(k.x[:, m, chunk(c)], k.bank[:, j, :],
                                                    k.mod[:, 0, GATE_A + m:GATE_A + m + 1], k.x[:, m, chunk(c)],
                                                    ALU.mult, ALU.add)
                last.then_inc(y_done, 1)


def l0_ffn(k):
    nc, d = k.nc, k.dram
    TOP, KEYS, E, EB = 8, 64, 512, 4
    w_in, q_ready, q_copied, route_ready, route_copied = (
        k.sem("l0f_" + n) for n in ("w_in", "q_ready", "q_copied", "route_ready", "route_copied"))
    best_ready, best_exp, sums_ready, pair_exp, weights_ready, wt_ready, wt_copied, s_ready, s_act, s_gated = (
        k.sem("l0f_" + n) for n in ("best_ready", "best_exp", "sums_ready", "pair_exp", "weights_ready", "wt_ready",
                                    "wt_copied", "s_ready", "s_act", "s_gated"))
    with ExitStack() as outer:
        ar = outer.enter_context(nc.sbuf_tensor("l0f_ar", [P, EB, T], F32))
        ue = outer.enter_context(nc.sbuf_tensor("l0f_ue", [P, EB, D], F32))
        with ExitStack() as ctx:
            def sb(n, shape):
                return ctx.enter_context(nc.sbuf_tensor("l0f_" + n, shape, F32))
            wq = sb("wq", [P, DB, P])
            keys = sb("keys", [KEYS, 2, KEYS])
            de = sb("de", [P, DB, E])
            q = sb("q", [KEYS, 2, T])
            r = sb("r", [P, TT, 2, KEYS])
            s8 = sb("s8", [P, 2, TT, TOP])
            pairs = sb("pairs", [P, TT, TOP, TOP])
            best = sb("best", [P, TT, TOP])
            be = sb("be", [P, TT, TOP])
            st = sb("st", [P, 4, TT])
            f = sb("f", [P, 2, TOP, KEYS])
            fe = sb("fe", [P, 2, E])
            w = sb("w", [P, 2, E])
            wt = sb("wt", [P, EB, T])
            sa = sb("sa", [P, 2, CH])
            with nc.Block() as block:
                @block.sync
                def _(sp):
                    sp.dma_start(wq[:], d["l0f_wq"].rearrange("(b p) n -> p b n", p=P)).then_inc(w_in, 16)
                    sp.dma_start(keys[:], d["l0f_keys"].rearrange("g p n -> p g n")).then_inc(w_in, 16)
                    sp.dma_start(de[:], d["l0f_de"].rearrange("(b p) n -> p b n", p=P)).then_inc(w_in, 16)
                    sp.dma_start(ue[:], d["l0f_ue"].rearrange("(b p) n -> p b n", p=P)).then_inc(w_in, 16)

                @block.tensor
                def _(pe):
                    pe.wait_ge(w_in, 64)
                    for g in range(2):
                        for b in range(DB):
                            last = pe.matmul(k.bank[:, g, :], wq[:, b, :], k.h[:, b, chunk(g)],
                                             start=(b == 0), stop=(b == DB - 1))
                        last.then_inc(q_ready, 1)
                    pe.wait_ge(q_copied, 2)
                    for t in range(TT):
                        for g in range(2):
                            last = pe.matmul(k.bank[:, 2 + t // 4, (t % 4) * P + g * KEYS:(t % 4) * P + (g + 1) * KEYS],
                                             q[:, g, tile(t)], keys[:, g, :], start=True, stop=True)
                    last.then_inc(route_ready, 1)
                    for t in range(TT):
                        pe.wait_ge(weights_ready, t + 1)
                        if t >= 2:
                            pe.wait_ge(wt_copied, t - 1)
                        for e in range(EB):
                            last = pe.transpose(k.bank[:, 4 + t % 2, tile(e)], w[:, t % 2, tile(e)], k.ident[:])
                        last.then_inc(wt_ready, 1)
                    for n in range(2 * EB):
                        e, c = n // 2, n % 2
                        if n >= 2:
                            pe.wait_ge(s_act, n - 1)
                        for b in range(DB):
                            last = pe.matmul(k.bank[:, 6 + c, :], de[:, b, tile(e)], k.h[:, b, chunk(c)],
                                             start=(b == 0), stop=(b == DB - 1))
                        last.then_inc(s_ready, 1)

                @block.scalar
                def _(act):
                    act.preload_act_table_set(EXP_LN)
                    act.wait_ge(route_ready, 1)
                    act.activation(r[:].rearrange("p t g e -> p (t g e)"),
                                   k.bank[:, 2:4, :].rearrange("p b n -> p (b n)"), ACT.Identity
                                   ).then_inc(route_copied, 1)
                    act.wait_ge(best_ready, 1)
                    act.activation(be[:], be[:], ACT.Exp).then_inc(best_exp, 1)
                    for t in range(TT):
                        act.wait_ge(sums_ready, t + 1)
                        act.activation(fe[:, t % 2, :], f[:, t % 2].rearrange("p i j -> p (i j)"), ACT.Exp,
                                       bias=st[:, 0, t:t + 1]).then_inc(pair_exp, 1)
                        if t >= 1:
                            act.wait_ge(wt_ready, t)
                            act.activation(wt[:, :, tile(t - 1)], k.bank[:, 4 + (t - 1) % 2, :].rearrange(
                                "p (e q) -> p e q", e=EB), ACT.Identity).then_inc(wt_copied, 1)
                    act.wait_ge(wt_ready, TT)
                    act.activation(wt[:, :, tile(TT - 1)], k.bank[:, 5, :].rearrange("p (e q) -> p e q", e=EB),
                                   ACT.Identity).then_inc(wt_copied, 1)
                    for n in range(2 * EB):
                        act.wait_ge(s_ready, n + 1)
                        if n >= 2:
                            act.wait_ge(s_gated, n - 1)
                        act.activation(sa[:, n % 2, :], k.bank[:, 6 + n % 2, :], ACT.Silu).then_inc(s_act, 1)

                @block.vector
                def _(dve):
                    step = k.dve_chain
                    for g in range(2):
                        dve.wait_ge(q_ready, g + 1)
                        view = q[:, g, :].rearrange("p (t o) -> p t o", o=2)
                        dve.tensor_copy(view[:, :, 0], k.bank[0:KEYS, g, :])
                        dve.tensor_copy(view[:, :, 1], k.bank[KEYS:P, g, :]).then_inc(q_copied, 1)
                    dve.wait_ge(route_copied, 1)
                    for t in range(TT):
                        for g in range(2):
                            last = dve.max(s8[:, g, t, :], r[:, t, g, :])
                    step.link(dve, last)
                    step.link(dve, dve.tensor_tensor(pairs[:], over(s8[:, 0], TOP, 3), over(s8[:, 1], TOP, 2), ALU.add))
                    for t in range(TT):
                        last = dve.max(best[:, t, :], pairs[:, t].rearrange("p i j -> p (i j)"))
                    step.link(dve, last)
                    dve.tensor_tensor(be[:], best[:], over(best[:, :, 0], TOP, 2), ALU.subtract
                                      ).then_inc(best_ready, 1)
                    step.link(dve, dve.tensor_scalar(st[:, 0, :], best[:, :, 0], -1.0, None, ALU.mult))
                    dve.wait_ge(best_exp, 1)
                    step.link(dve, dve.tensor_reduce(st[:, 1, :], be[:], AX.X, ALU.add))
                    step.link(dve, dve.reciprocal(st[:, 2, :], st[:, 1, :]))
                    for t in range(TT):
                        if t >= 2:
                            dve.wait_ge(pair_exp, t - 1)
                        step.link(dve, dve.tensor_tensor(f[:, t % 2], over(r[:, t, 0, 0:TOP], KEYS, 2),
                                                         over(r[:, t, 1, :], TOP, 1), ALU.add))
                        dve.sem_inc(sums_ready, 1)
                        dve.wait_ge(pair_exp, t + 1)
                        if t >= 2:
                            dve.wait_ge(wt_ready, t - 1)
                        wv = w[:, t % 2, :]
                        step.link(dve, dve.scalar_tensor_tensor(wv, f[:, t % 2].rearrange("p i j -> p (i j)"),
                                                                best[:, t, TOP - 1:TOP], fe[:, t % 2, :],
                                                                ALU.is_ge, ALU.mult))
                        step.link(dve, dve.tensor_scalar(wv, wv, st[:, 2, t:t + 1], None, ALU.mult))
                        step.link(dve, dve.tensor_reduce(st[:, 3, t:t + 1], wv[:, 0:E - 1], AX.X, ALU.add))
                        dve.tensor_scalar(wv[:, E - 1:E], st[:, 3, t:t + 1], -1.0, 1.0, ALU.mult, ALU.add
                                          ).then_inc(weights_ready, 1)
                    dve.wait_ge(wt_copied, TT)
                    for n in range(2 * EB):
                        e, c = n // 2, n % 2
                        dve.wait_ge(s_act, n + 1)
                        dve.tensor_tensor(ar[:, e, chunk(c)], sa[:, c, :], wt[:, e, chunk(c)], ALU.mult
                                          ).then_inc(s_gated, 1)
        gated_units(k, "l0m", 8, P, d["l0f_win"], d["l0f_wout"], gate_col(k, 0, GATE_B),
                    extra=[(ue[:, e, :], ar[:, e, :]) for e in range(EB)])


def l1_attention(k):
    nc, d = k.nc, k.dram
    H = 2
    names = ("w_in", "z_ready", "z_biased", "z_abs_ready", "z_exp", "one_plus_ready", "z_ln", "gates_ready",
             "alpha_ready", "alpha_ln", "cla_ready", "h_copied", "qkv_ready", "qkv_biased", "k_squared", "k_sum_ready",
             "k_rn_ready", "k_normed", "la_tri_ready", "row_ready", "row_exp", "dt_ready", "dt_exp", "to_end_ready",
             "to_end_exp", "kw_ready", "qk_turned", "qt_copied", "qg_ready", "st_ready", "attn_ready", "y_ready",
             "delta_ready", "state_ready", "x_added", "const_ready")
    s = {n: k.sem("l1_" + n) for n in names}
    with ExitStack() as ctx:
        def sb(n, shape):
            return ctx.enter_context(nc.sbuf_tensor("l1_" + n, shape, F32))
        w = sb("w", [P, DB, 3 * D])
        wz = sb("wz", [P, DB, 4])
        bias = sb("bias", [P, 3 * D])
        bz = sb("bz", [P, 4])
        tri = sb("tri", [P, P])
        late = sb("late", [P, P])
        z = sb("z", [P, TT, 4])
        zt = sb("zt", [P, 2, TT, 4])
        la = sb("la", [P, TT, H])
        cla = sb("cla", [P, TT, H])
        hc = sb("hc", [P, DB, P])
        qkv = sb("qkv", [P, 3, H, P])
        sq = sb("sq", [P, H, P])
        rn = sb("rn", [P, H])
        la_tri = sb("la_tri", [P, H, P])
        dt = sb("dt", [P, H, P])
        ecr = sb("ecr", [P, H, P])
        te = sb("te", [P, H])
        kw = sb("kw", [P, H, P])
        qkt = sb("qkt", [P, 2, H, P])
        qg = sb("qg", [P, H, P])
        at = sb("at", [P, H, P])
        state = sb("state", [P, H, P])
        with nc.Block() as block:
            @block.sync
            def _(sp):
                sp.dma_start(wz[:], d["l1_wz"].rearrange("(b p) n -> p b n", p=P)).then_inc(s["w_in"], 16)
                sp.dma_start(bz[:], d["l1_bz"].to_broadcast([P, 4])).then_inc(s["w_in"], 16)
                sp.dma_start(w[:], d["l1_w"].rearrange("(b p) n -> p b n", p=P)).then_inc(s["w_in"], 16)
                sp.dma_start(bias[:], d["l1_b"].to_broadcast([P, 3 * D])).then_inc(s["w_in"], 16)

            @block.gpsimd
            def _(pool):
                step = k.pool_chain
                pool.memset(state[:], 0.0)
                pool.memset(tri[:], 1.0)
                step.link(pool, pool.memset(late[:], 0.0))
                pool.affine_select(out=tri[:], in_=tri[:], compare_op=ALU.is_ge, fill=0.0, base=0, pattern=[[1, P]],
                                   channel_multiplier=-1)
                pool.affine_select(out=late[:], in_=late[:], compare_op=ALU.is_ge, fill=NEG, base=0,
                                   pattern=[[1, P]], channel_multiplier=-1).then_inc(s["const_ready"], 1)
                with pool.Fori(0, TT) as i:
                    pool.wait_ge(s["qkv_ready"], i)
                    pool.tensor_copy(hc[:], k.h[:, :, bass.ds(i * P, P)]).then_inc(s["h_copied"], 1)

            @block.tensor
            def _(pe):
                pe.wait_ge(s["w_in"], 64)
                for t in range(TT):
                    for b in range(DB):
                        last = pe.matmul(k.bank[:, 7, t * 4:t * 4 + 4], k.h[:, b, tile(t)], wz[:, b, :],
                                         start=(b == 0), stop=(b == DB - 1))
                last.then_inc(s["z_ready"], 1)
                pe.wait_ge(s["const_ready"], 1)
                pe.wait_ge(s["alpha_ln"], 1)
                pe.matmul(k.bank[:, 7, 64:64 + TT * H], tri[:], la[:].rearrange("p t h -> p (t h)"), start=True,
                          stop=True).then_inc(s["cla_ready"], 1)
                with pe.Fori(0, TT) as i:
                    pe.wait_ge(s["h_copied"], i + 1)
                    pe.wait_ge(s["qkv_biased"], i)
                    for b in range(DB):
                        pe.matmul(k.bank[:, 0, :], hc[:, b, :], w[:, b, 0:2 * D], start=(b == 0), stop=(b == 1))
                    for b in range(DB):
                        last = pe.matmul(k.bank[:, 1, 0:D], hc[:, b, :], w[:, b, 2 * D:], start=(b == 0), stop=(b == 1))
                    last.then_inc(s["qkv_ready"], 1)
                    pe.wait_ge(s["la_tri_ready"], i + 1)
                    pe.matmul(k.bank[:, 2, 0:H * P], k.ones[:], la_tri[:].rearrange("p h q -> p (h q)"), start=True,
                              stop=True).then_inc(s["row_ready"], 1)
                    pe.wait_ge(s["k_normed"], i + 1)
                    for a in range(2):
                        for h in range(H):
                            last = pe.transpose(k.bank[:, 3, tile(2 * a + h)], qkv[:, a, h, :], k.ident[:])
                    last.then_inc(s["qk_turned"], 1)
                    pe.wait_ge(s["qt_copied"], i + 1)
                    for h in range(H):
                        last = pe.matmul(k.bank[:, 4, tile(h)], qkt[:, 1, h, :], qkt[:, 0, h, :], start=True, stop=True)
                    last.then_inc(s["st_ready"], 1)
                    pe.wait_ge(s["attn_ready"], i + 1)
                    pe.wait_ge(s["qg_ready"], i + 1)
                    pe.wait_ge(s["state_ready"], i)
                    for h in range(H):
                        pe.matmul(k.bank[:, 5, tile(h)], qkv[:, 2, h, :], at[:, h, :], start=True, stop=False)
                        last = pe.matmul(k.bank[:, 5, tile(h)], state[:, h, :], qg[:, h, :], start=False, stop=True)
                    last.then_inc(s["y_ready"], 1)
                    pe.wait_ge(s["kw_ready"], i + 1)
                    for h in range(H):
                        last = pe.matmul(k.bank[:, 6, tile(h)], kw[:, h, :], qkv[:, 2, h, :], start=True, stop=True)
                    last.then_inc(s["delta_ready"], 1)

            @block.scalar
            def _(act):
                step = k.act_chain
                act.preload_act_table_set(EXP_LN)
                act.wait_ge(s["z_abs_ready"], 1)
                act.activation(zt[:, 0], zt[:, 0], ACT.Exp, scale=-1.0).then_inc(s["z_exp"], 1)
                act.wait_ge(s["one_plus_ready"], 1)
                act.activation(zt[:, 1, :, 0:H], zt[:, 0, :, 0:H], ACT.Ln).then_inc(s["z_ln"], 1)
                act.wait_ge(s["alpha_ready"], 1)
                act.activation(la[:], zt[:, 0, :, H:2 * H], ACT.Ln, bias=k.eps[:, 3:4]).then_inc(s["alpha_ln"], 1)
                act.wait_ge(s["gates_ready"], 1)
                with act.Fori(0, TT) as i:
                    step.enter(i, 2)
                    act.wait_ge(s["qkv_biased"], i + 1)
                    act.activation(sq[:], qkv[:, 1], ACT.Square).then_inc(s["k_squared"], 1)
                    act.wait_ge(s["row_ready"], i + 1)
                    act.activation(ecr[:].rearrange("p h q -> p (h q)"), k.bank[:, 2, 0:H * P], ACT.Exp
                                   ).then_inc(s["row_exp"], 1)
                    act.wait_ge(s["k_sum_ready"], i + 1)
                    step.link(act, act.activation(rn[:], rn[:], ACT.Ln, scale=65536.0))
                    act.activation(rn[:], rn[:], ACT.Exp, scale=-0.5).then_inc(s["k_rn_ready"], 1)
                    act.wait_ge(s["to_end_ready"], i + 1)
                    act.activation(te[:], te[:], ACT.Exp).then_inc(s["to_end_exp"], 1)
                    act.wait_ge(s["dt_ready"], i + 1)
                    act.activation(dt[:], dt[:], ACT.Exp).then_inc(s["dt_exp"], 1)
                    act.wait_ge(s["qk_turned"], i + 1)
                    step.link(act, act.activation(qkt[:].rearrange("p a h q -> p (a h q)"), k.bank[:, 3, :],
                                                  ACT.Identity))
                    act.sem_inc(s["qt_copied"], 1)
                step.leave(TT)

            @block.vector
            def _(dve):
                step = k.dve_chain
                dve.wait_ge(s["w_in"], 64)
                dve.wait_ge(s["z_ready"], 1)
                step.link(dve, dve.tensor_tensor(z[:], k.bank[:, 7, 0:TT * 4].rearrange("p (t n) -> p t n", t=TT),
                                                 over(bz[:], TT), ALU.add))
                step.link(dve, dve.tensor_scalar(zt[:, 1], z[:], -1.0, None, ALU.mult))
                dve.tensor_tensor(zt[:, 0, :, 0:H], z[:, :, 0:H], zt[:, 1, :, 0:H], ALU.max)
                dve.tensor_copy(zt[:, 0, :, H:], z[:, :, H:]).then_inc(s["z_abs_ready"], 1)
                dve.wait_ge(s["z_exp"], 1)
                dve.tensor_scalar(zt[:, 0], zt[:, 0], 1.0, None, ALU.add).then_inc(s["one_plus_ready"], 1)
                dve.wait_ge(s["one_plus_ready"], 1)
                dve.reciprocal(zt[:, 0, :, H:], zt[:, 0, :, H:]).then_inc(s["alpha_ready"], 1)
                dve.wait_ge(s["z_ln"], 1)
                step.link(dve, dve.scalar_tensor_tensor(z[:, :, 0:H], z[:, :, 0:H], 0.0, zt[:, 1, :, 0:H], ALU.max,
                                                        ALU.add))
                dve.wait_ge(s["cla_ready"], 1)
                dve.tensor_copy(cla[:].rearrange("p t h -> p (t h)"), k.bank[:, 7, 64:64 + TT * H]
                                ).then_inc(s["gates_ready"], 1)
                dve.wait_ge(s["gates_ready"], 1)
                dve.wait_ge(s["const_ready"], 1)
                with dve.Fori(0, TT) as i:
                    step.enter(i, 4)
                    dve.wait_ge(s["qkv_ready"], i + 1)
                    dve.wait_ge(s["delta_ready"], i)
                    dve.tensor_tensor(qkv[:].rearrange("p a h q -> p (a h q)"),
                                      k.bank[:, 0:2, :].rearrange("p n q -> p (n q)")[:, 0:3 * D], bias[:], ALU.add
                                      ).then_inc(s["qkv_biased"], 1)
                    for h in range(H):
                        last = dve.tensor_scalar(la_tri[:, h, :], tri[:], la[:, bass.ds(i, 1), h], None, ALU.mult)
                    last.then_inc(s["la_tri_ready"], 1)
                    dve.wait_ge(s["k_squared"], i + 1)
                    step.link(dve, dve.tensor_reduce(rn[:], sq[:], AX.X, ALU.add))
                    dve.tensor_scalar(rn[:], rn[:], 1.0e-24, None, ALU.max).then_inc(s["k_sum_ready"], 1)
                    dve.wait_ge(s["row_exp"], i + 1)
                    row = k.bank[:, 2, 0:H * P].rearrange("p (h q) -> p h q", h=H)
                    dve.tensor_tensor(te[:], row[:, :, P - 1], cla[:, bass.ds(i, 1), :].rearrange("p t h -> p (t h)"),
                                      ALU.subtract).then_inc(s["to_end_ready"], 1)
                    for h in range(H):
                        last = dve.scalar_tensor_tensor(dt[:, h, :], row[:, h, :], cla[:, bass.ds(i, 1), h], late[:],
                                                        ALU.subtract, ALU.add)
                    last.then_inc(s["dt_ready"], 1)
                    dve.wait_ge(s["k_rn_ready"], i + 1)
                    for h in range(H):
                        last = dve.tensor_scalar(qkv[:, 1, h, :], qkv[:, 1, h, :], rn[:, h:h + 1], 256.0, ALU.mult,
                                                 ALU.mult)
                    last.then_inc(s["k_normed"], 1)
                    dve.wait_ge(s["to_end_exp"], i + 1)
                    step.link(dve, dve.tensor_tensor(te[:], te[:], z[:, bass.ds(i, 1), 0:H].rearrange(
                        "p t h -> p (t h)"), ALU.mult))
                    dve.wait_ge(s["k_normed"], i + 1)
                    for h in range(H):
                        last = dve.tensor_scalar(kw[:, h, :], qkv[:, 1, h, :], te[:, h:h + 1], None, ALU.mult)
                    last.then_inc(s["kw_ready"], 1)
                    dve.wait_ge(s["qt_copied"], i + 1)
                    dve.tensor_tensor(qg[:], qkt[:, 0], ecr[:], ALU.mult).then_inc(s["qg_ready"], 1)
                    dve.wait_ge(s["dt_exp"], i + 1)
                    dve.wait_ge(s["st_ready"], i + 1)
                    for h in range(H):
                        last = dve.scalar_tensor_tensor(at[:, h, :], k.bank[:, 4, tile(h)], z[:, bass.ds(i, 1), h],
                                                        dt[:, h, :], ALU.mult, ALU.mult)
                    last.then_inc(s["attn_ready"], 1)
                    dve.wait_ge(s["y_ready"], i + 1)
                    for h in range(H):
                        xs = k.x[:, h, bass.ds(i * P, P)]
                        last = dve.scalar_tensor_tensor(xs, k.bank[:, 5, tile(h)], k.mod[:, 1, GATE_A + h:GATE_A + h + 1],
                                                        xs, ALU.mult, ALU.add)
                    step.link(dve, last)
                    dve.wait_ge(s["delta_ready"], i + 1)
                    for h in range(H):
                        last = dve.scalar_tensor_tensor(state[:, h, :], state[:, h, :], ecr[:, h, P - 1:P],
                                                        k.bank[:, 6, tile(h)], ALU.mult, ALU.add)
                    step.link(dve, last)
                    dve.sem_inc(s["state_ready"], 1)
                step.leave(TT)


def l1_ffn(k):
    nc, d = k.nc, k.dram
    E, TOP, SEL, THRESH = 64, 8, 4, 0.5
    names = ("w_in", "sim_in", "logits_ready", "shifted", "probs_exp", "weights_ready", "masks_ready", "wt_ready",
             "wt_copied", "counts_ready", "sim_ready", "map_ready", "eff_ready", "eff_copied", "stored")
    s = {n: k.sem("l1f_" + n) for n in names}
    rows = nc.dram_tensor("l1f_token_weights", (E, T), F32, kind="Internal").ap()
    with ExitStack() as ctx:
        def sb(n, shape, dt=F32):
            return ctx.enter_context(nc.sbuf_tensor("l1f_" + n, shape, dt))
        gw = sb("gw", [P, DB, E])
        sim = sb("sim", [E, E])
        iota = sb("iota", [E, E])
        p = sb("p", [P, TT, E])
        st = sb("st", [P, 2, TT])
        v8 = sb("v8", [P, TT, TOP])
        w = sb("w", [P, 2, TT, E])
        mask = sb("mask", [P, 2, TT, E])
        wt = sb("wt", [E, 2, T])
        cnt = sb("cnt", [E, 2])
        m8 = sb("m8", [E, TOP])
        i8 = sb("i8", [E, TOP], mybir.dt.uint32)
        bi = sb("bi", [E, 2])
        mp = sb("mp", [E, E])
        eff = sb("eff", [E, T])
        with nc.Block() as block:
            @block.sync
            def _(sp):
                sp.dma_start(gw[:], d["l1f_gw"].rearrange("(b p) n -> p b n", p=P)).then_inc(s["w_in"], 16)
                sp.dma_start(sim[:], d["l1f_sim"]).then_inc(s["sim_in"], 16)
                sp.wait_ge(s["eff_copied"], 2)
                sp.dma_start(rows, eff[:]).then_inc(s["stored"], 16)
                sp.wait_ge(s["stored"], 16)

            @block.gpsimd
            def _(pool):
                pool.iota(iota[:], pattern=[[1, E]], base=0, channel_multiplier=0,
                          allow_small_or_imprecise_dtypes=True)
                pool.wait_ge(s["sim_in"], 16)
                pool.affine_select(out=sim[:], in_=sim[:], compare_op=ALU.not_equal, fill=1.0, base=0,
                                   pattern=[[-1, E]], channel_multiplier=1).then_inc(s["sim_ready"], 1)

            @block.tensor
            def _(pe):
                pe.wait_ge(s["w_in"], 16)
                for t in range(TT):
                    for b in range(DB):
                        last = pe.matmul(k.bank[:, 0, t * E:(t + 1) * E], k.h[:, b, tile(t)], gw[:, b, :],
                                         start=(b == 0), stop=(b == DB - 1))
                last.then_inc(s["logits_ready"], 1)
                pe.wait_ge(s["masks_ready"], 1)
                for a in range(2):
                    for t in range(TT):
                        pe.matmul(k.bank[0:E, 1, a:a + 1], mask[:, a, t, :], k.ones[:, 0:1], start=(t == 0),
                                  stop=(t == TT - 1))
                for t in range(TT):
                    last = pe.matmul(k.bank[0:E, 1, E:2 * E], k.ones[:, 0:E], mask[:, 0, t, :], start=(t == 0),
                                     stop=(t == TT - 1))
                last.then_inc(s["counts_ready"], 1)
                pe.wait_ge(s["weights_ready"], 1)
                for a in range(2):
                    for t in range(TT):
                        last = pe.transpose(k.bank[0:E, 2 + 2 * a + t // 4, (t % 4) * P:(t % 4 + 1) * P],
                                            w[:, a, t, :], k.ident[:])
                    last.then_inc(s["wt_ready"], 1)
                pe.wait_ge(s["wt_copied"], 2)
                pe.wait_ge(s["map_ready"], 1)
                for c in range(NCH):
                    pe.matmul(k.bank[0:E, 6 + c, :], k.ident[0:E, 0:E], wt[:, 0, chunk(c)], start=True, stop=False)
                    pe.matmul(k.bank[0:E, 6 + c, :], mp[:], wt[:, 1, chunk(c)], start=False, stop=True
                              ).then_inc(s["eff_ready"], 1)

            @block.scalar
            def _(act):
                act.preload_act_table_set(EXP_LN)
                act.wait_ge(s["shifted"], 1)
                act.activation(p[:], p[:], ACT.Exp).then_inc(s["probs_exp"], 1)
                for a in range(2):
                    act.wait_ge(s["wt_ready"], a + 1)
                    act.activation(wt[:, a, :], k.bank[0:E, 2 + 2 * a:4 + 2 * a, :].rearrange("p n q -> p (n q)"),
                                   ACT.Identity).then_inc(s["wt_copied"], 1)
                for c in range(NCH):
                    act.wait_ge(s["eff_ready"], c + 1)
                    act.activation(eff[:, chunk(c)], k.bank[0:E, 6 + c, :], ACT.Identity).then_inc(s["eff_copied"], 1)

            @block.vector
            def _(dve):
                step = k.dve_chain
                dve.wait_ge(s["logits_ready"], 1)
                logits = k.bank[:, 0, :].rearrange("p (t e) -> p t e", t=TT)
                step.link(dve, dve.tensor_reduce(st[:, 0, :], logits, AX.X, ALU.max))
                dve.tensor_tensor(p[:], logits, over(st[:, 0, :], E, 2), ALU.subtract).then_inc(s["shifted"], 1)
                dve.wait_ge(s["probs_exp"], 1)
                step.link(dve, dve.tensor_reduce(st[:, 0, :], p[:], AX.X, ALU.add))
                step.link(dve, dve.reciprocal(st[:, 1, :], st[:, 0, :]))
                step.link(dve, dve.tensor_tensor(p[:], p[:], over(st[:, 1, :], E, 2), ALU.mult))
                for t in range(TT):
                    last = dve.max(v8[:, t, :], p[:, t, :])
                step.link(dve, last)
                step.link(dve, dve.tensor_reduce(st[:, 0, :], v8[:], AX.X, ALU.add))
                step.link(dve, dve.tensor_scalar(st[:, 0, :], st[:, 0, :], 1.0e-12, None, ALU.max))
                step.link(dve, dve.reciprocal(st[:, 1, :], st[:, 0, :]))
                dve.tensor_tensor(mask[:, 0], p[:], over(v8[:, :, SEL - 1], E, 2), ALU.is_ge)
                step.link(dve, dve.tensor_tensor(mask[:, 1], p[:], over(v8[:, :, TOP - 1], E, 2), ALU.is_ge))
                step.link(dve, dve.tensor_tensor(mask[:, 1], mask[:, 1], mask[:, 0], ALU.subtract))
                dve.sem_inc(s["masks_ready"], 1)
                step.link(dve, dve.tensor_tensor(p[:], p[:], over(st[:, 1, :], E, 2), ALU.mult))
                for a in range(2):
                    last = dve.tensor_tensor(w[:, a], p[:], mask[:, a], ALU.mult)
                last.then_inc(s["weights_ready"], 1)
                dve.wait_ge(s["counts_ready"], 1)
                dve.wait_ge(s["sim_ready"], 1)
                step.link(dve, dve.tensor_scalar(mp[:], k.bank[0:E, 1, E:2 * E], 0.5, NEG, ALU.is_lt, ALU.mult))
                step.link(dve, dve.tensor_tensor(mp[:], mp[:], sim[:], ALU.add))
                step.link(dve, dve.max(m8[:], mp[:]))
                step.link(dve, dve.max_index(i8[:], m8[:], mp[:]))
                step.link(dve, dve.tensor_copy(bi[:, 0:1], i8[:, 0:1]))
                step.link(dve, dve.tensor_scalar(cnt[:, 0:1], k.bank[0:E, 1, 0:1], 0.5, None, ALU.is_lt))
                step.link(dve, dve.tensor_scalar(cnt[:, 1:2], k.bank[0:E, 1, 1:2], 0.5, None, ALU.is_ge))
                step.link(dve, dve.tensor_tensor(cnt[:, 0:1], cnt[:, 0:1], cnt[:, 1:2], ALU.mult))
                step.link(dve, dve.tensor_scalar(cnt[:, 1:2], m8[:, 0:1], THRESH, None, ALU.is_ge))
                step.link(dve, dve.tensor_tensor(cnt[:, 0:1], cnt[:, 0:1], cnt[:, 1:2], ALU.mult))
                step.link(dve, dve.scalar_tensor_tensor(mp[:], iota[:], bi[:, 0:1], k.ident[0:E, 0:E], ALU.is_equal,
                                                        ALU.subtract))
                dve.scalar_tensor_tensor(mp[:], mp[:], cnt[:, 0:1], k.ident[0:E, 0:E], ALU.mult, ALU.add
                                         ).then_inc(s["map_ready"], 1)
    gated_units(k, "l1m", E, 96, d["l1f_win"], d["l1f_wout"], gate_col(k, 1, GATE_B),
                row_of=lambda pair, half: pair * 2 + half, rows=rows)


def head_norm(k, buf, group, eps, center, scale=None, shift=None):
    nc = k.nc
    tiles = [(b, c) for b in range(DB) for c in range(NCH)]
    N = len(tiles)
    mean_ready, centered, squared, var_ready, root_ready, normed, out_ready = (
        k.shared("hn_" + n) for n in ("mean_ready", "centered", "squared", "var_ready", "root_ready", "normed", "out"))
    call = k.calls.setdefault("head_norms", 0)
    k.calls["head_norms"] += 1
    at = N * call
    cen = N * k.calls.setdefault("head_norms_centered", 0)
    k.calls["head_norms_centered"] += center
    with ExitStack() as ctx:
        sq = ctx.enter_context(nc.sbuf_tensor(f"hn_square{call}", [P, DB, T], F32))
        rs = ctx.enter_context(nc.sbuf_tensor(f"hn_rstd{call}", [P, DB, T], F32))
        with nc.Block() as block:
            @block.tensor
            def _(pe):
                if center:
                    for n, (b, c) in enumerate(tiles):
                        pe.matmul(k.bank[:, n, :], group[:], buf[:, b, chunk(c)], start=True, stop=True
                                  ).then_inc(mean_ready, 1)
                for n, (b, c) in enumerate(tiles):
                    pe.wait_ge(squared, at + n + 1)
                    pe.matmul(k.bank[:, 4 + n, :], group[:], sq[:, b, chunk(c)], start=True, stop=True
                              ).then_inc(var_ready, 1)

            @block.vector
            def _(dve):
                if center:
                    for n, (b, c) in enumerate(tiles):
                        dve.wait_ge(mean_ready, cen + n + 1)
                        dve.tensor_tensor(buf[:, b, chunk(c)], buf[:, b, chunk(c)], k.bank[:, n, :], ALU.subtract
                                          ).then_inc(centered, 1)
                for n, (b, c) in enumerate(tiles):
                    dve.wait_ge(root_ready, at + n + 1)
                    xs = buf[:, b, chunk(c)]
                    dve.tensor_tensor(xs, xs, rs[:, b, chunk(c)], ALU.mult).then_inc(normed, 1)
                if center:
                    for n, (b, c) in enumerate(tiles):
                        dve.wait_ge(normed, at + n + 1)
                        xs = buf[:, b, chunk(c)]
                        last = dve.tensor_scalar(xs, xs, scale[:, b:b + 1], shift[:, b:b + 1], ALU.mult, ALU.add)
                    last.then_inc(out_ready, 1)

            @block.scalar
            def _(act):
                act.preload_act_table_set(EXP_LN)
                for n, (b, c) in enumerate(tiles):
                    if center:
                        act.wait_ge(centered, cen + n + 1)
                    act.activation(sq[:, b, chunk(c)], buf[:, b, chunk(c)], ACT.Square).then_inc(squared, 1)
                for n, (b, c) in enumerate(tiles):
                    act.wait_ge(var_ready, at + n + 1)
                    r = rs[:, b, chunk(c)]
                    k.act_chain.link(act, act.activation(r, k.bank[:, 4 + n, :], ACT.Ln, bias=k.eps[:, eps:eps + 1]))
                    act.activation(r, r, ACT.Exp, scale=-0.5).then_inc(root_ready, 1)


def l2_attention(k):
    nc, d = k.nc, k.dram
    HD, TAPS, PROJ = 16, 4, 6
    Q, K, V, IG, G, OG = range(PROJ)
    names = ("cols_in", "w_in", "wo_in", "pad_ready", "sum_w", "mean_w", "conv_ready", "silu_ready", "proj_ready",
             "proj_copied", "u_ready", "scanned", "mixed", "gated", "y_ready", "res_ready", "x_added")
    s = {n: k.sem("l2_" + n) for n in names}
    with ExitStack() as outer:
        h2 = outer.enter_context(nc.sbuf_tensor("l2_h2", [P, DB, T], F32))
        COLS = ["ln1w", "ln1b", "ln2w", "ln2b", "vnw", "vnb", "mnw", "mnb", "gnw", "gnb", "conv_b", "tap0", "tap1",
                "tap2", "tap3", "big", "bg", "bog"]
        cols = outer.enter_context(nc.sbuf_tensor("l2_cols", [P, len(COLS), DB], F32))

        def col(name):
            return cols[:, COLS.index(name), :]

        with ExitStack() as ctx:
            def sb(n, shape):
                return ctx.enter_context(nc.sbuf_tensor("l2_" + n, shape, F32))
            w = sb("w", [P, DB, PROJ * D])
            wo = sb("wo", [P, DB, D])
            hp = sb("hp", [P, DB, TAPS - 1 + T])
            xc = sb("xc", [P, DB, T])
            pr = sb("pr", [P, PROJ, DB, T])
            hsum = sb("hsum", [P, P])
            hmean = sb("hmean", [P, P])
            with nc.Block() as block:
                @block.sync
                def _(sp):
                    sp.dma_start(cols[:], d["l2_cols"]).then_inc(s["cols_in"], 16)
                    sp.dma_start(w[:], d["l2_w"].rearrange("(b p) n -> p b n", p=P)).then_inc(s["w_in"], 16)
                    sp.dma_start(wo[:], d["l2_wo"].rearrange("(b p) n -> p b n", p=P)).then_inc(s["wo_in"], 16)
                    sp.wait_ge(s["cols_in"], 16)

                @block.gpsimd
                def _(pool):
                    step = k.pool_chain
                    pool.memset(hp[:, :, 0:TAPS - 1], 0.0).then_inc(s["pad_ready"], 1)
                    for m, v in ((hsum, 1.0), (hmean, 1.0 / HD)):
                        groups = m[:].rearrange("p (g e) -> p g e", e=HD)
                        step.link(pool, pool.memset(m[:], v))
                        step.link(pool, pool.affine_select(out=groups, in_=groups, compare_op=ALU.is_ge, fill=0.0,
                                                           base=0, pattern=[[-HD, P // HD], [0, HD]],
                                                           channel_multiplier=1))
                        step.link(pool, pool.affine_select(out=groups, in_=groups, compare_op=ALU.is_ge, fill=0.0,
                                                           base=HD - 1, pattern=[[HD, P // HD], [0, HD]],
                                                           channel_multiplier=-1))
            layernorm(k, k.h, hp[:, :, TAPS - 1:], col("ln1w"), col("ln1b"))
            with nc.Block() as block:
                @block.tensor
                def _(pe):
                    pe.wait_ge(s["w_in"], 16)
                    for n in range(PROJ * 4):
                        j, m, c = n // 4, n // 2 % 2, n % 2
                        if n == IG * 4:
                            pe.wait_ge(s["silu_ready"], DB)
                        if n >= 8:
                            pe.wait_ge(s["proj_copied"], n - 7)
                        for b in range(DB):
                            src = (hp[:, b, TAPS - 1 + c * CH:TAPS - 1 + (c + 1) * CH] if j < IG
                                   else xc[:, b, chunk(c)])
                            last = pe.matmul(k.bank[:, n % 8, :], w[:, b, j * D + m * P:j * D + (m + 1) * P], src,
                                             start=(b == 0), stop=(b == DB - 1))
                        last.then_inc(s["proj_ready"], 1)

                @block.vector
                def _(dve):
                    step = k.dve_chain
                    for b in range(DB):
                        step.link(dve, dve.tensor_scalar(xc[:, b, :], hp[:, b, TAPS - 1:TAPS - 1 + T],
                                                         col("tap3")[:, b:b + 1], col("conv_b")[:, b:b + 1],
                                                         ALU.mult, ALU.add))
                        for j in range(TAPS - 1):
                            step.link(dve, dve.scalar_tensor_tensor(xc[:, b, :], hp[:, b, j:j + T],
                                                                    col(f"tap{j}")[:, b:b + 1], xc[:, b, :],
                                                                    ALU.mult, ALU.add))
                        dve.sem_inc(s["conv_ready"], 1)

                @block.scalar
                def _(act):
                    act.preload_act_table(ACT.Silu)
                    for b in range(DB):
                        act.wait_ge(s["conv_ready"], b + 1)
                        act.activation(xc[:, b, :], xc[:, b, :], ACT.Silu).then_inc(s["silu_ready"], 1)
                    for n in range(PROJ * 4):
                        j, m, c = n // 4, n // 2 % 2, n % 2
                        act.wait_ge(s["proj_ready"], n + 1)
                        if j < IG:
                            act.activation(pr[:, j, m, chunk(c)], k.bank[:, n % 8, :], ACT.Identity
                                           ).then_inc(s["proj_copied"], 1)
                        else:
                            bias = col(("big", "bg", "bog")[j - IG])[:, m:m + 1]
                            act.activation(pr[:, j, m, chunk(c)], k.bank[:, n % 8, :], ACT.Sigmoid, bias=bias
                                           ).then_inc(s["proj_copied"], 1)
            head_norm(k, pr[:, Q], hsum, 1, False)
            head_norm(k, pr[:, K], hsum, 1, False)
            head_norm(k, pr[:, V], hmean, 0, True, col("vnw"), col("vnb"))
            with nc.Block() as block:
                @block.vector
                def _(dve):
                    step = k.dve_chain
                    step.link(dve, dve.tensor_tensor(pr[:, K], pr[:, K], pr[:, IG], ALU.mult))
                    step.link(dve, dve.tensor_tensor(pr[:, K], pr[:, K], pr[:, V], ALU.mult))
                    for b in range(DB):
                        step.link(dve, dve.tensor_tensor_scan(pr[:, V, b, :], pr[:, G, b, :], pr[:, K, b, :], 0.0,
                                                              ALU.mult, ALU.add))
            head_norm(k, pr[:, V], hmean, 0, True, col("mnw"), col("mnb"))
            with nc.Block() as block:
                @block.vector
                def _(dve):
                    k.dve_chain.link(dve, dve.tensor_tensor(pr[:, V], pr[:, V], pr[:, Q], ALU.mult))
            head_norm(k, pr[:, V], hmean, 0, True, col("gnw"), col("gnb"))
            with nc.Block() as block:
                @block.vector
                def _(dve):
                    dve.tensor_tensor(pr[:, V], pr[:, V], pr[:, OG], ALU.mult).then_inc(s["gated"], 1)
                    for n in range(4):
                        m, c = n // 2, n % 2
                        dve.wait_ge(s["y_ready"], n + 1)
                        r, x = k.h[:, m, chunk(c)], k.x[:, m, chunk(c)]
                        k.dve_chain.link(dve, dve.tensor_tensor(r, r, k.bank[:, n, :], ALU.add))
                        last = dve.scalar_tensor_tensor(x, r, gate_col(k, 2, GATE_A)[:, m:m + 1], x, ALU.mult, ALU.add)
                    last.then_inc(s["x_added"], 1)

                @block.tensor
                def _(pe):
                    pe.wait_ge(s["wo_in"], 16)
                    pe.wait_ge(s["gated"], 1)
                    for n in range(4):
                        m, c = n // 2, n % 2
                        for b in range(DB):
                            last = pe.matmul(k.bank[:, n, :], wo[:, b, tile(m)], pr[:, V, b, chunk(c)],
                                             start=(b == 0), stop=(b == DB - 1))
                        last.then_inc(s["y_ready"], 1)
        layernorm(k, k.h, h2, col("ln2w"), col("ln2b"))
        gated_units(k, "l2m", 8, P, d["l2_win"], d["l2_wout"], gate_col(k, 2, GATE_A), src=h2)


def l2_ffn(k):
    nc, d = k.nc, k.dram
    E, GROUPS, FU = 8, 4, 88
    names = ("w_in", "logits_ready", "shifted", "probs_exp", "weights_ready", "wt_ready", "wt_copied", "stored")
    s = {n: k.sem("l2f_" + n) for n in names}
    rows = nc.dram_tensor("l2f_token_weights", (E + 2, T), F32, kind="Internal").ap()
    with ExitStack() as ctx:
        def sb(n, shape):
            return ctx.enter_context(nc.sbuf_tensor("l2f_" + n, shape, F32))
        gw = sb("gw", [P, DB, E])
        p = sb("p", [P, TT, E])
        g = sb("g", [P, 2, TT, GROUPS])
        m = sb("m", [P, 2, TT, E])
        st = sb("st", [P, 2, TT])
        w = sb("w", [P, TT, E + 2])
        wt = sb("wt", [E + 2, T])
        with nc.Block() as block:
            @block.sync
            def _(sp):
                sp.dma_start(gw[:], d["l2f_gw"].rearrange("(b p) n -> p b n", p=P)).then_inc(s["w_in"], 16)
                sp.wait_ge(s["wt_copied"], 1)
                sp.dma_start(rows, wt[:]).then_inc(s["stored"], 16)
                sp.wait_ge(s["stored"], 16)

            @block.tensor
            def _(pe):
                pe.wait_ge(s["w_in"], 16)
                for t in range(TT):
                    for b in range(DB):
                        last = pe.matmul(k.bank[:, 0, t * E:(t + 1) * E], k.h[:, b, tile(t)], gw[:, b, :],
                                         start=(b == 0), stop=(b == DB - 1))
                last.then_inc(s["logits_ready"], 1)
                pe.wait_ge(s["weights_ready"], 1)
                for t in range(TT):
                    last = pe.transpose(k.bank[0:E + 2, 1 + t // 4, (t % 4) * P:(t % 4 + 1) * P], w[:, t, :],
                                        k.ident[:])
                last.then_inc(s["wt_ready"], 1)

            @block.scalar
            def _(act):
                act.preload_act_table_set(EXP_LN)
                act.wait_ge(s["shifted"], 1)
                act.activation(p[:], p[:], ACT.Exp).then_inc(s["probs_exp"], 1)
                act.wait_ge(s["wt_ready"], 1)
                act.activation(wt[:], k.bank[0:E + 2, 1:3, :].rearrange("p n q -> p (n q)"), ACT.Identity
                               ).then_inc(s["wt_copied"], 1)

            @block.vector
            def _(dve):
                step = k.dve_chain
                dve.memset(w[:, :, E:], 1.0)
                dve.wait_ge(s["logits_ready"], 1)
                logits = k.bank[:, 0, 0:TT * E].rearrange("p (t e) -> p t e", t=TT)
                step.link(dve, dve.tensor_reduce(st[:, 0, :], logits, AX.X, ALU.max))
                dve.tensor_tensor(p[:], logits, over(st[:, 0, :], E, 2), ALU.subtract).then_inc(s["shifted"], 1)
                dve.wait_ge(s["probs_exp"], 1)
                step.link(dve, dve.tensor_reduce(st[:, 0, :], p[:], AX.X, ALU.add))
                step.link(dve, dve.reciprocal(st[:, 1, :], st[:, 0, :]))
                step.link(dve, dve.tensor_tensor(p[:], p[:], over(st[:, 1, :], E, 2), ALU.mult))

                def second_best(of, n, tmp):
                    step.link(dve, dve.tensor_reduce(st[:, 0, :], of, AX.X, ALU.max))
                    step.link(dve, dve.tensor_tensor(tmp, of, over(st[:, 0, :], n, 2), ALU.is_ge))
                    step.link(dve, dve.scalar_tensor_tensor(tmp, tmp, -4.0, of, ALU.mult, ALU.add))
                    step.link(dve, dve.tensor_reduce(st[:, 1, :], tmp, AX.X, ALU.max))

                step.link(dve, dve.tensor_reduce(g[:, 0], p[:].rearrange("p t (g e) -> p t g e", g=GROUPS), AX.X,
                                                 ALU.max))
                second_best(g[:, 0], GROUPS, g[:, 1])
                step.link(dve, dve.tensor_tensor(g[:, 1], g[:, 0], over(st[:, 1, :], GROUPS, 2), ALU.is_ge))
                by_group = m[:, 0].rearrange("p t (g e) -> p t g e", g=GROUPS)
                step.link(dve, dve.tensor_tensor(by_group, p[:].rearrange("p t (g e) -> p t g e", g=GROUPS),
                                                 over(g[:, 1], E // GROUPS, 3), ALU.mult))
                second_best(m[:, 0], E, m[:, 1])
                step.link(dve, dve.tensor_tensor(m[:, 1], m[:, 0], over(st[:, 1, :], E, 2), ALU.is_ge))
                dve.tensor_tensor(w[:, :, 0:E], m[:, 0], m[:, 1], ALU.mult).then_inc(s["weights_ready"], 1)
    gated_units(k, "l2e", 2 * (E + 2), FU, d["l2f_win"], d["l2f_wout"], gate_col(k, 2, GATE_B),
                row_of=lambda pair, half: pair, rows=rows)


def l3_attention(k):
    nc, d = k.nc, k.dram
    H, HP, S, MZ = 16, 2, 64, P + 1
    PAIRS, NS = H // HP, T // S
    INV_SCALE = float(P) ** -0.5
    names = ("betas_in", "betas_ready", "wo_in", "w_in", "const_ready", "v_ready", "vp_ready", "vs_copied", "qk_ready",
             "qk_copied", "neg_ready", "neg_exp", "sigma_ready", "scores_ready", "shifted", "probs_exp", "probs_ready",
             "pt_ready", "pt_copied", "dot_ready", "kt_ready", "kt_copied", "read_ready", "rden_ready", "delta_ready",
             "query_read", "mem_ready", "mem_copied", "am_scaled", "att_ready", "attt_ready", "attt_copied", "y_ready",
             "x_added")
    s = {n: k.sem("l3_" + n) for n in names}
    with ExitStack() as ctx:
        def sb(n, shape):
            return ctx.enter_context(nc.sbuf_tensor("l3_" + n, shape, F32))
        beta = sb("beta", [P, H * P])
        omb = sb("omb", [P, HP * P])
        mask = sb("mask", [P, P])
        zrow = sb("zrow", [1, MZ])
        w = sb("w", [P, DB, 3 * HP * P])
        wo = sb("wo", [P, H, D])
        att = sb("att", [P, H, T])
        vp = sb("vp", [P, TT, HP, P])
        vs = sb("vs", [P, TT, HP, P])
        qk = sb("qk", [P, HP, 2, T])
        neg = sb("neg", [P, 2, CH])
        sg = sb("sg", [P, HP, TT, 4, S])
        sc = sb("sc", [P, HP, TT, P])
        st = sb("st", [P, HP, 2, TT])
        pt = sb("pt", [P, HP, TT, P])
        kt = sb("kt", [P, HP, TT, P])
        rd = sb("rd", [P, HP])
        nd = sb("nd", [P, HP, MZ])
        mem = sb("mem", [P, HP, MZ])
        am = sb("am", [P, HP, TT, P])
        with nc.Block() as block:
            @block.sync
            def _(sp):
                sp.dma_start(beta[:], d["l3_betas"].to_broadcast([P, H * P])).then_inc(s["betas_in"], 16)

                def load(i):
                    sp.dma_start(w[:], d["l3_w"][bass.ds(i, 1)].rearrange("u (b p) n -> p (u b) n", p=P)
                                 ).then_inc(s["w_in"], 16)

                load(0)
                sp.dma_start(wo[:], d["l3_wo"].rearrange("(j p) n -> p j n", p=P)).then_inc(s["wo_in"], 16)
                with sp.Fori(1, PAIRS) as i:
                    sp.wait_ge(s["qk_ready"], i * 8)
                    load(i)

            @block.gpsimd
            def _(pool):
                step = k.pool_chain
                step.link(pool, pool.memset(mask[:], 0.0))
                step.link(pool, pool.affine_select(out=mask[:], in_=mask[:], compare_op=ALU.is_ge, fill=NEG, base=0,
                                                   pattern=[[-1, P]], channel_multiplier=1))
                step.link(pool, pool.memset(mask[S:P, 0:S], NEG))
                pool.memset(nd[:], -1.0)
                step.link(pool, pool.memset(zrow[:], 0.0))
                pool.memset(zrow[:, P:], 1.0 / P).then_inc(s["const_ready"], 1)
                with pool.Fori(0, PAIRS) as i:
                    pool.wait_ge(s["betas_ready"], 1)
                    for a in range(HP):
                        pool.wait_ge(s["query_read"], i * (HP * NS) + HP * NS)
                        pool.tensor_tensor(am[:, a], am[:, a],
                                           over(beta[:, bass.ds(i * (HP * P) + a * P, P)], TT), ALU.mult
                                           ).then_inc(s["am_scaled"], 1)

            @block.tensor
            def _(pe):
                pe.wait_ge(s["const_ready"], 1)
                with pe.Fori(0, PAIRS) as i:
                    pe.wait_ge(s["w_in"], i * 16 + 16)
                    pe.wait_ge(s["attt_copied"], i * HP)
                    for t in range(TT):
                        for b in range(DB):
                            last = pe.matmul(k.bank[:, t // 2, (t % 2) * 256:(t % 2 + 1) * 256], k.h[:, b, tile(t)],
                                             w[:, b, 4 * P:6 * P], start=(b == 0), stop=(b == DB - 1))
                        if t % 2:
                            last.then_inc(s["v_ready"], 1)
                    for a in range(HP):
                        for n in range(4):
                            if a:
                                pe.wait_ge(s["sigma_ready"], i * 8 + (n + 1))
                                pe.wait_ge(s["qk_copied"], i * 8 + (n + 1))
                            for b in range(DB):
                                last = pe.matmul(k.bank[:, 4 + n, :], w[:, b, tile(2 * a + n // 2)],
                                                 k.h[:, b, chunk(n % 2)], start=(b == 0), stop=(b == DB - 1))
                            last.then_inc(s["qk_ready"], 1)
                    pe.wait_ge(s["vp_ready"], i + 1)
                    pe.wait_ge(s["vs_copied"], i * 2 + 2)
                    pe.wait_ge(s["qk_copied"], i * 8 + 8)
                    for a in range(HP):
                        for t in range(TT):
                            last = pe.matmul(k.bank[:, 2 * a + t // 4, (t % 4) * P:(t % 4 + 1) * P],
                                             qk[:, a, 0, tile(t)], qk[:, a, 1, tile(t)], start=True, stop=True)
                        last.then_inc(s["scores_ready"], 1)
                    pe.wait_ge(s["sigma_ready"], i * 8 + 8)
                    for a in range(HP):
                        for t in range(TT):
                            last = pe.transpose(k.bank[:, 4 + 2 * a + t // 4, (t % 4) * P:(t % 4 + 1) * P],
                                                sg[:, a, t, 1:3, :].rearrange("p a q -> p (a q)"), k.ident[:])
                        last.then_inc(s["kt_ready"], 1)
                    for a in range(HP):
                        pe.wait_ge(s["probs_ready"], i * HP + (a + 1))
                        for t in range(TT):
                            last = pe.transpose(k.bank[:, 2 * a + t // 4, (t % 4) * P:(t % 4 + 1) * P],
                                                sc[:, a, t, :], k.ident[:])
                        last.then_inc(s["pt_ready"], 1)
                    pe.wait_ge(s["kt_copied"], i * 4 + 4)
                    for a in range(HP):
                        pe.wait_ge(s["pt_copied"], i * HP + (a + 1))
                        for t in range(TT):
                            last = pe.matmul(k.bank[:, 4 + 2 * a + t // 4, (t % 4) * P:(t % 4 + 1) * P],
                                             pt[:, a, t, :], vp[:, t, a, :], start=True, stop=True)
                        last.then_inc(s["dot_ready"], 1)
                    for a in range(HP):
                        pe.matmul(k.bank[:, a, 0:MZ], k.ones[0:1, :], zrow[:], start=True, stop=False,
                                  skip_group_check=True).then_inc(s["mem_ready"], 1)
                    for n in range(NS):
                        t, odd = n // 2, n % 2
                        for a in range(HP):
                            step = HP * n + a
                            pe.wait_ge(s["mem_copied"], i * (HP * NS) + (step + 1))
                            if n:
                                pe.wait_ge(s["query_read"], i * (HP * NS) + (step - 1))
                            pe.matmul(k.bank[:, 2 + a, 0:MZ], sg[:, a, t, 2 * odd:2 * odd + 2, :].rearrange(
                                "p a q -> p (a q)"), mem[:, a, :], start=True, stop=True
                                ).then_inc(s["read_ready"], 1)
                        if n == NS - 1:
                            break
                        for a in range(HP):
                            half = slice(0, S) if odd else slice(S, P)
                            pe.wait_ge(s["delta_ready"], i * (HP * (NS - 1)) + (HP * n + a + 1))
                            pe.matmul(k.bank[:, a, 0:MZ], kt[half, a, t, :], nd[half, a, :], start=False,
                                      stop=False, skip_group_check=True).then_inc(s["mem_ready"], 1)
                    for a in range(HP):
                        pe.wait_ge(s["att_ready"], i * HP + (a + 1))
                        for t in range(TT):
                            last = pe.transpose(k.bank[:, 2 * a + t // 4, (t % 4) * P:(t % 4 + 1) * P],
                                                am[:, a, t, :], k.ident[:])
                        last.then_inc(s["attt_ready"], 1)
                pe.wait_ge(s["wo_in"], 16)
                pe.wait_ge(s["attt_copied"], H)
                for n in range(4):
                    m, c = n // 2, n % 2
                    for j in range(H):
                        last = pe.matmul(k.bank[:, 4 + n, :], wo[:, j, tile(m)], att[:, j, chunk(c)],
                                         start=(j == 0), stop=(j == H - 1))
                    last.then_inc(s["y_ready"], 1)

            @block.scalar
            def _(act):
                act.preload_act_table(ACT.Sigmoid)
                act.wait_ge(s["betas_in"], 16)
                act.activation(beta[:], beta[:], ACT.Sigmoid).then_inc(s["betas_ready"], 1)
                act.preload_act_table_set(EXP_LN)
                with act.Fori(0, PAIRS) as i:
                    act.wait_ge(s["vp_ready"], i + 1)
                    banks = k.bank[:, 0:4, :].rearrange("p n q -> p (n q)")
                    flat = vs[:].rearrange("p t a q -> p (t a q)")
                    act.activation(flat[S:P], banks[0:S], ACT.Identity).then_inc(s["vs_copied"], 1)
                    act.activation(flat[0:S], banks[S:P], ACT.Identity).then_inc(s["vs_copied"], 1)
                    for a in range(HP):
                        for n in range(4):
                            act.wait_ge(s["neg_ready"], i * 8 + (4 * a + n + 1))
                            act.activation(qk[:, a, n // 2, chunk(n % 2)], k.bank[:, 4 + n, :], ACT.Identity
                                           ).then_inc(s["qk_copied"], 1)
                            act.activation(neg[:, n % 2, :], neg[:, n % 2, :], ACT.Exp).then_inc(s["neg_exp"], 1)
                    for a in range(HP):
                        act.wait_ge(s["kt_ready"], i * HP + (a + 1))
                        banks = k.bank[:, 4 + 2 * a:6 + 2 * a, :].rearrange("p n q -> p (n q)")
                        flat = kt[:, a].rearrange("p t q -> p (t q)")
                        act.activation(flat[S:P], banks[0:S], ACT.Identity, scale=-1.0).then_inc(s["kt_copied"], 1)
                        act.activation(flat[0:S], banks[S:P], ACT.Identity, scale=-1.0).then_inc(s["kt_copied"], 1)
                        act.wait_ge(s["shifted"], i * HP + (a + 1))
                        act.activation(sc[:, a], sc[:, a], ACT.Exp).then_inc(s["probs_exp"], 1)
                    for a in range(HP):
                        act.wait_ge(s["pt_ready"], i * HP + (a + 1))
                        act.activation(pt[:, a].rearrange("p t q -> p (t q)"),
                                       k.bank[:, 2 * a:2 * a + 2, :].rearrange("p n q -> p (n q)"), ACT.Identity
                                       ).then_inc(s["pt_copied"], 1)
                    for n in range(NS):
                        t, odd = n // 2, n % 2
                        half = slice(S, P) if odd else slice(0, S)
                        for a in range(HP):
                            act.wait_ge(s["rden_ready"], i * (HP * NS) + (HP * n + a + 1))
                            act.activation(am[half, a, t, :], k.bank[half, 2 + a, 0:P], ACT.Identity,
                                           scale=rd[half, a:a + 1]).then_inc(s["query_read"], 1)
                    for a in range(HP):
                        act.wait_ge(s["attt_ready"], i * HP + (a + 1))
                        act.activation(att[:].rearrange("p j (g q) -> p j g q", q=S)[
                            :, :, :, bass.ds(i * (4 * HP) + 4 * a, 4)].rearrange("p j g n -> p g n j"),
                            k.bank[:, 2 * a:2 * a + 2, :].rearrange("p n q -> p (n q)").rearrange(
                                "p (g n j) -> p g n j", g=NS, n=4), ACT.Identity).then_inc(s["attt_copied"], 1)

            @block.vector
            def _(dve):
                step = k.dve_chain
                dve.wait_ge(s["const_ready"], 1)
                dve.wait_ge(s["betas_ready"], 1)
                with dve.Fori(0, PAIRS) as i:
                    step.enter(i, 9)
                    step.link(dve, dve.tensor_scalar(omb[:], beta[:, bass.ds(i * (HP * P), HP * P)], -1.0, 1.0,
                                                     ALU.mult, ALU.add))
                    dve.wait_ge(s["v_ready"], i * 4 + 4)
                    dve.tensor_tensor(vp[:].rearrange("p t a q -> p t (a q)"),
                                      k.bank[:, 0:4, :].rearrange("p n (t q) -> p (n t) q", t=2),
                                      over(omb[:], TT), ALU.mult
                                      ).then_inc(s["vp_ready"], 1)

                    def sigma(j):
                        a, n = j // 4, j % 4
                        dve.wait_ge(s["neg_exp"], i * 8 + (j + 1))
                        slots = (0, 3) if n < 2 else (1, 2)
                        for odd in range(2):
                            src = k.bank[:, 4 + n, :].rearrange("p (t o q) -> p t o q", o=2, q=S)[:, :, odd, :]
                            e = neg[:, n % 2, :].rearrange("p (t o q) -> p t o q", o=2, q=S)[:, :, odd, :]
                            c = n % 2
                            last = dve.scalar_tensor_tensor(sg[:, a, 4 * c:4 * c + 4, slots[odd], :], src, 0.0, e,
                                                            ALU.max, ALU.add)
                        last.then_inc(s["sigma_ready"], 1)

                    for j in range(8):
                        a, n = j // 4, j % 4
                        dve.wait_ge(s["qk_ready"], i * 8 + (j + 1))
                        if j >= 2:
                            dve.wait_ge(s["sigma_ready"], i * 8 + (j - 1))
                        dve.tensor_scalar(neg[:, n % 2, :], k.bank[:, 4 + n, :], 0.0, None, ALU.min
                                          ).then_inc(s["neg_ready"], 1)
                        dve.wait_ge(s["qk_copied"], i * 8 + (j + 1))
                        sigma(j)
                    for a in range(HP):
                        dve.wait_ge(s["scores_ready"], i * HP + (a + 1))
                        banks = k.bank[:, 2 * a:2 * a + 2, :].rearrange("p n (t q) -> p (n t) q", q=P)
                        step.link(dve, dve.scalar_tensor_tensor(sc[:, a], banks, INV_SCALE, over(mask[:], TT),
                                                                ALU.mult, ALU.add))
                        step.link(dve, dve.tensor_reduce(st[:, a, 0, :], sc[:, a], AX.X, ALU.max))
                        dve.tensor_tensor(sc[:, a], sc[:, a], over(st[:, a, 0, :], P, 2), ALU.subtract
                                          ).then_inc(s["shifted"], 1)
                    for a in range(HP):
                        dve.wait_ge(s["probs_exp"], i * HP + (a + 1))
                        step.link(dve, dve.tensor_reduce(st[:, a, 0, :], sc[:, a], AX.X, ALU.add))
                        step.link(dve, dve.reciprocal(st[:, a, 1, :], st[:, a, 0, :]))
                        dve.tensor_tensor(sc[:, a], sc[:, a], over(st[:, a, 1, :], P, 2), ALU.mult
                                          ).then_inc(s["probs_ready"], 1)
                    for n in range(NS):
                        t, odd = n // 2, n % 2
                        half = slice(0, S) if odd else slice(S, P)
                        for a in range(HP):
                            m = HP * n + a
                            dve.wait_ge(s["mem_ready"], i * (HP * NS) + (m + 1))
                            dve.tensor_copy(mem[:, a, :], k.bank[:, a, 0:MZ]).then_inc(s["mem_copied"], 1)
                        for a in range(HP):
                            m = HP * n + a
                            dve.wait_ge(s["read_ready"], i * (HP * NS) + (m + 1))
                            dve.reciprocal(rd[:, a:a + 1], k.bank[:, 2 + a, P:MZ]).then_inc(s["rden_ready"], 1)
                        if n == NS - 1:
                            break
                        for a in range(HP):
                            m = HP * n + a
                            dve.wait_ge(s["rden_ready"], i * (HP * NS) + (m + 1))
                            dve.scalar_tensor_tensor(nd[half, a, 0:P], k.bank[half, 2 + a, 0:P], rd[half, a:a + 1],
                                                     vs[half, t, a, :], ALU.mult, ALU.subtract
                                                     ).then_inc(s["delta_ready"], 1)
                    for a in range(HP):
                        dve.wait_ge(s["am_scaled"], i * HP + (a + 1))
                        dve.wait_ge(s["dot_ready"], i * HP + (a + 1))
                        dve.tensor_tensor(am[:, a], am[:, a], k.bank[:, 4 + 2 * a:6 + 2 * a, :].rearrange(
                            "p n (t q) -> p (n t) q", q=P), ALU.add).then_inc(s["att_ready"], 1)
                step.leave(PAIRS)
                for n in range(4):
                    m, c = n // 2, n % 2
                    dve.wait_ge(s["y_ready"], n + 1)
                    xs = k.x[:, m, chunk(c)]
                    dve.scalar_tensor_tensor(xs, k.bank[:, 4 + n, :], gate_col(k, 3, GATE_A)[:, m:m + 1], xs,
                                             ALU.mult, ALU.add).then_inc(s["x_added"], 1)


def l3_ffn(k):
    nc, d = k.nc, k.dram
    E, A, N = 8, 64, 2048
    UNITS = N // P
    PAIRS = UNITS // 2
    names = ("w_in", "idx_in", "ea_in", "iota_ready", "logits_ready", "shifted", "probs_exp", "weights_ready",
             "rt_ready", "rt_copied", "ea_shifted", "ea_exp", "ea_ready", "eat_ready", "eat_copied", "imp_ready",
             "delta_ready", "values_ready", "index_ready", "made", "up_ready", "copied", "gated", "summed", "done")
    s = {n: k.sem("l3f_" + n) for n in names}
    with ExitStack() as ctx:
        def sb(n, shape, dt=F32):
            return ctx.enter_context(nc.sbuf_tensor("l3f_" + n, shape, dt))
        gw = sb("gw", [P, DB, E])
        wt = sb("wt", [P, DB, D])
        ea = sb("ea", [E, A])
        est = sb("est", [E, 2])
        eat = sb("eat", [A, E])
        atoms = sb("atoms", [A, N])
        imp = sb("imp", [E, N])
        idx = sb("idx", [P, N], I32)
        idx_s = sb("idx_s", [P, UNITS], I32)
        colf = sb("colf", [P, N])
        rowf = sb("rowf", [P, UNITS])
        feature = sb("feature", [P, DB])
        iota = sb("iota", [P, D])
        p = sb("p", [P, TT, E])
        m = sb("m", [P, TT, E])
        v8 = sb("v8", [P, TT, 8])
        st = sb("st", [P, 2, TT])
        rt = sb("rt", [E, T])
        pick = sb("pick", [P, 2, DB, P])
        val = sb("val", [E, 2, P])
        put = sb("put", [P, 2, D])
        g = sb("g", [P, NCH, CH])
        a = sb("a", [P, NCH, CH])
        with nc.Block() as block:
            @block.sync
            def _(sp):
                sp.dma_start(gw[:], d["l3f_gw"].rearrange("(b p) n -> p b n", p=P)).then_inc(s["w_in"], 16)
                sp.dma_start(wt[:], d["l3f_w"].rearrange("(b p) n -> p b n", p=P)).then_inc(s["w_in"], 16)
                sp.dma_start(ea[:], d["l3f_ea"]).then_inc(s["ea_in"], 16)
                sp.dma_start(atoms[:], d["l3f_atoms"]).then_inc(s["ea_in"], 16)
                sp.dma_start(imp[:], d["l3f_imp"]).then_inc(s["ea_in"], 16)
                sp.dma_start(idx[:], d["l3f_idx"].to_broadcast([P, N])).then_inc(s["idx_in"], 16)
                sp.dma_start(idx_s[:], d["l3f_idx_s"]).then_inc(s["idx_in"], 16)

            @block.gpsimd
            def _(pool):
                pool.iota(iota[:], pattern=[[1, D]], base=0, channel_multiplier=0,
                          allow_small_or_imprecise_dtypes=True)
                pool.iota(feature[:], pattern=[[P, DB]], base=0, channel_multiplier=1,
                          allow_small_or_imprecise_dtypes=True).then_inc(s["iota_ready"], 1)

            @block.tensor
            def _(pe):
                pe.wait_ge(s["w_in"], 32)
                for t in range(TT):
                    for b in range(DB):
                        last = pe.matmul(k.bank[:, 0, t * E:(t + 1) * E], k.h[:, b, tile(t)], gw[:, b, :],
                                         start=(b == 0), stop=(b == DB - 1))
                last.then_inc(s["logits_ready"], 1)
                for mm in range(DB):
                    for c in range(NCH):
                        for b in range(DB):
                            pe.matmul(k.bank[:, 4 + 2 * mm + c, :], wt[:, b, tile(mm)], k.h[:, b, chunk(c)],
                                      start=(b == 0), stop=False, skip_group_check=True)
                pe.wait_ge(s["ea_ready"], 1)
                pe.transpose(k.bank[0:A, 1, 0:E], ea[:], k.ident[0:E, 0:E]).then_inc(s["eat_ready"], 1)
                pe.wait_ge(s["weights_ready"], 1)
                for t in range(TT):
                    last = pe.transpose(k.bank[0:E, 2 + t // 4, (t % 4) * P:(t % 4 + 1) * P], m[:, t, :], k.ident[:])
                last.then_inc(s["rt_ready"], 1)
                pe.wait_ge(s["eat_copied"], 1)
                for n in range(N // CH):
                    if n >= 2:
                        pe.wait_ge(s["values_ready"], n - 1)
                    pe.matmul(k.bank[0:E, n % 2, :], eat[:], atoms[:, chunk(n)], start=True, stop=True
                              ).then_inc(s["delta_ready"], 1)
                pe.wait_ge(s["values_ready"], N // CH)
                pe.wait_ge(s["rt_copied"], 1)

                def up(i, half, c):
                    if c == 0:
                        pe.wait_ge(s["made"], i * 2 + (half + 1))
                    for b in range(DB):
                        pe.matmul(k.bank[:, 2 * c, :], pick[:, half, b, :], k.h[:, b, chunk(c)], start=(b == 0),
                                  stop=(b == DB - 1))
                    pe.matmul(k.bank[:, 2 * c + 1, :], val[:, half, :], rt[:, chunk(c)], start=True, stop=True
                              ).then_inc(s["up_ready"], 1)

                def down(i, half, c):
                    pe.wait_ge(s["gated"], i * 4 + (2 * half + c + 1))
                    for mm in range(DB):
                        last = pe.matmul(k.bank[:, 4 + 2 * mm + c, :], put[:, half, tile(mm)], a[:, c, :],
                                         start=False, stop=False, skip_group_check=True)
                    last.then_inc(s["summed"], 1)

                def pair(i, last):
                    up(i, 0, 1)
                    down(i, 0, 0)
                    up(i, 1, 0)
                    down(i, 0, 1)
                    up(i, 1, 1)
                    down(i, 1, 0)
                    if not last:
                        up(i + 1, 0, 0)
                    down(i, 1, 1)

                up(0, 0, 0)
                with pe.Fori(0, PAIRS - 1) as i:
                    pair(i, False)
                pair(PAIRS - 1, True)

            @block.scalar
            def _(act):
                act.preload_act_table_set(EXP_LN)
                act.wait_ge(s["ea_shifted"], 1)
                act.activation(ea[:], ea[:], ACT.Exp).then_inc(s["ea_exp"], 1)
                act.wait_ge(s["shifted"], 1)
                act.activation(p[:], p[:], ACT.Exp).then_inc(s["probs_exp"], 1)
                act.wait_ge(s["eat_ready"], 1)
                act.activation(eat[:], k.bank[0:A, 1, 0:E], ACT.Identity).then_inc(s["eat_copied"], 1)
                act.wait_ge(s["rt_ready"], 1)
                act.activation(rt[:], k.bank[0:E, 2:4, :].rearrange("p n q -> p (n q)"), ACT.Identity
                               ).then_inc(s["rt_copied"], 1)
                act.wait_ge(s["ea_in"], 48)
                act.activation(imp[:], imp[:], ACT.Sigmoid).then_inc(s["imp_ready"], 1)
                with act.Fori(0, PAIRS) as i:
                    for n in range(4):
                        c = n % 2
                        act.wait_ge(s["up_ready"], i * 4 + (n + 1))
                        act.activation(g[:, c, :], k.bank[:, 2 * c, :], ACT.Identity).then_inc(s["copied"], 1)

            @block.vector
            def _(dve):
                step = k.dve_chain
                dve.wait_ge(s["ea_in"], 48)
                step.link(dve, dve.tensor_reduce(est[:, 0:1], ea[:], AX.X, ALU.max))
                dve.tensor_scalar(ea[:], ea[:], est[:, 0:1], None, ALU.subtract).then_inc(s["ea_shifted"], 1)
                dve.wait_ge(s["logits_ready"], 1)
                step.link(dve, dve.tensor_scalar(p[:], k.bank[:, 0, 0:TT * E].rearrange("p (t e) -> p t e", t=TT),
                                                 -50.0, 50.0, ALU.max, ALU.min))
                for t in range(TT):
                    last = dve.max(v8[:, t, :], p[:, t, :])
                step.link(dve, last)
                step.link(dve, dve.tensor_tensor(m[:], p[:], over(v8[:, :, 1], E, 2), ALU.is_ge))
                dve.tensor_tensor(p[:], p[:], over(v8[:, :, 0], E, 2), ALU.subtract).then_inc(s["shifted"], 1)
                dve.wait_ge(s["ea_exp"], 1)
                step.link(dve, dve.tensor_reduce(est[:, 0:1], ea[:], AX.X, ALU.add))
                step.link(dve, dve.reciprocal(est[:, 1:2], est[:, 0:1]))
                dve.tensor_scalar(ea[:], ea[:], est[:, 1:2], None, ALU.mult).then_inc(s["ea_ready"], 1)
                dve.wait_ge(s["probs_exp"], 1)
                step.link(dve, dve.tensor_tensor(m[:], m[:], p[:], ALU.mult))
                step.link(dve, dve.tensor_reduce(st[:, 0, :], m[:], AX.X, ALU.add))
                step.link(dve, dve.reciprocal(st[:, 1, :], st[:, 0, :]))
                dve.tensor_tensor(m[:], m[:], over(st[:, 1, :], E, 2), ALU.mult).then_inc(s["weights_ready"], 1)
                dve.wait_ge(s["idx_in"], 32)
                step.link(dve, dve.tensor_single_scalar(idx[:], idx[:], D - 1, ALU.bitwise_and))
                step.link(dve, dve.tensor_single_scalar(idx_s[:], idx_s[:], 8, ALU.logical_shift_right))
                dve.tensor_copy(colf[:], idx[:])
                step.link(dve, dve.tensor_copy(rowf[:], idx_s[:]))
                dve.wait_ge(s["imp_ready"], 1)
                for n in range(N // CH):
                    dve.wait_ge(s["delta_ready"], n + 1)
                    dve.tensor_tensor(imp[:, chunk(n)], imp[:, chunk(n)], k.bank[0:E, n % 2, :], ALU.mult
                                      ).then_inc(s["values_ready"], 1)
                dve.wait_ge(s["values_ready"], N // CH)
                dve.wait_ge(s["iota_ready"], 1)

                def make(i, half):
                    at = i * (2 * P) + half * P
                    for b in range(DB):
                        dve.tensor_scalar(pick[:, half, b, :], colf[:, bass.ds(at, P)], feature[:, b:b + 1], None,
                                          ALU.is_equal)
                    dve.tensor_copy(val[:, half, :], imp[:, bass.ds(at, P)])
                    dve.tensor_scalar(put[:, half, :], iota[:], rowf[:, bass.ds(i * 2 + half, 1)], None,
                                      ALU.is_equal).then_inc(s["made"], 1)

                def mix(i, n):
                    c = n % 2
                    dve.wait_ge(s["copied"], i * 4 + (n + 1))
                    dve.tensor_tensor(a[:, c, :], g[:, c, :], k.bank[:, 2 * c + 1, :], ALU.mult
                                      ).then_inc(s["gated"], 1)

                make(0, 0)
                make(0, 1)
                with dve.Fori(0, PAIRS - 1) as i:
                    for n in range(4):
                        mix(i, n)
                    for half in range(2):
                        dve.wait_ge(s["summed"], i * 4 + (2 * half + 2))
                        make(i + 1, half)
                for n in range(4):
                    mix(PAIRS - 1, n)
                dve.wait_ge(s["summed"], 4 * PAIRS)
                for mm in range(DB):
                    for c in range(NCH):
                        xs = k.x[:, mm, chunk(c)]
                        last = dve.scalar_tensor_tensor(xs, k.bank[:, 4 + 2 * mm + c, :],
                                                        gate_col(k, 3, GATE_B)[:, mm:mm + 1], xs, ALU.mult, ALU.add)
                last.then_inc(s["done"], 1)


def store(k, out):
    nc = k.nc
    stored = k.sem("x_stored")
    with nc.Block() as block:
        @block.sync
        def _(sp):
            sp.dma_start(out.rearrange("(b p) t -> p b t", p=P), k.x[:]).then_inc(stored, 16)
            sp.wait_ge(stored, 16)


def gate_col(k, layer, at):
    return k.mod[:, layer, at:at + DB]


def build(nc, dram, out, only=None):
    halves = ((0, l0_attention, l0_ffn), (1, l1_attention, l1_ffn), (2, l2_attention, l2_ffn), (3, l3_attention, l3_ffn))
    steps = [(layer, part, half) for layer, *parts in halves for half, part in enumerate(parts)]
    with ExitStack() as ctx:
        k = Core(nc, ctx, dram)
        with k.stage():
            constants(k)
            modulations(k)
        for n, (layer, part, half) in enumerate(steps):
            if only is not None and n not in only:
                continue
            with k.stage():
                if half:
                    adaln(k, layer, SHIFT_B, SCALE_B)
                else:
                    adaln(k, layer, SHIFT_A, SCALE_A)
                part(k)
        store(k, out)


def laid_out(i):
    def t(a):
        return np.swapaxes(np.asarray(a), -1, -2)

    def cat(*a, axis=-1):
        return np.concatenate([np.asarray(x) for x in a], axis=axis)

    H0 = 8
    wq = t(i["L0_attn_Wq"]).reshape(D, H0, P).transpose(1, 0, 2)
    wkv = t(i["L0_attn_Wkv"])
    wk = wkv[:, :H0 * P].reshape(D, H0, P).transpose(1, 0, 2)
    a = {
        "x": t(np.asarray(i["L0_attn_x"])[0]),
        "cs": np.stack([np.asarray(i[f"L{n}_c"]).reshape(DB, P).T for n in range(4)], 1).reshape(P, 4 * DB),
        "wmod": np.stack([np.asarray(i[f"L{n}_wmod"]) for n in range(4)]),
        "l0_wqk": cat(wq, wk),
        "l0_wv": wkv[:, H0 * P:],
        "l0_wg": t(i["L0_attn_Wg"]),
        "l0_bg": np.asarray(i["L0_attn_bg"])[None],
        "l0_scales": np.stack([np.asarray(i["L0_attn_q_scale"]), np.asarray(i["L0_attn_k_scale"])], 1),
        "l0_wo": t(i["L0_attn_Wo"]),
    }
    def units(gate, up, down):
        w = cat(gate, up)
        n, _, f = w.shape
        return w.reshape(n, DB, P, f).transpose(0, 2, 1, 3).reshape(n, P, DB * f), np.asarray(down)

    def blocks(gate, up, down, n):
        def cut(w):
            w = np.asarray(w)
            return w.reshape(D, n, -1).transpose(1, 0, 2)
        down = np.asarray(down)
        return units(cut(gate), cut(up), down.reshape(n, -1, D))

    a["l0f_wq"] = np.asarray(i["L0_ffn_W_q"])
    a["l0f_keys"] = np.asarray(i["L0_ffn_keys"])
    a["l0f_de"] = t(i["L0_ffn_down_embed"])
    a["l0f_ue"] = np.asarray(i["L0_ffn_up_embed"])
    a["l0f_win"], a["l0f_wout"] = blocks(i["L0_ffn_gate_w"], i["L0_ffn_up_w"], i["L0_ffn_down_w"], 8)
    a["l1_w"] = cat(i["L1_attn_Wq"], i["L1_attn_Wk"], i["L1_attn_Wv"])
    a["l1_b"] = cat(i["L1_attn_bq"], i["L1_attn_bk"], i["L1_attn_bv"])[None]
    a["l1_wz"] = cat(i["L1_attn_Wbeta"], i["L1_attn_Walpha"])
    a["l1_bz"] = cat(i["L1_attn_bbeta"], i["L1_attn_balpha"])[None]
    a["l1f_gw"] = t(i["L1_ffn_gate_weight"])
    a["l1f_sim"] = np.asarray(i["L1_ffn_similarity"])
    gu = t(i["L1_ffn_gate_up_proj"])
    F1 = gu.shape[-1] // 2
    a["l1f_win"], a["l1f_wout"] = units(gu[..., :F1], gu[..., F1:], t(i["L1_ffn_down_proj"]))
    def cols2(v):
        v = np.asarray(v)
        return np.tile(v, D // v.shape[0]).reshape(DB, P).T

    conv = np.asarray(i["L2_attn_conv_w"])[:, 0]
    two = [i["L2_attn_" + n] for n in ("ln1w", "ln1b", "ln2w", "ln2b", "vnw", "vnb", "mnw", "mnb", "gnw", "gnb",
                                       "conv_b")]
    two += [conv[:, j] for j in range(4)]
    two += [i["L2_attn_big"], np.repeat(np.asarray(i["L2_attn_bg"]), 16), i["L2_attn_bog"]]
    a["l2_cols"] = np.stack([cols2(v) for v in two], 1)
    a["l2_w"] = cat(i["L2_attn_Wq"], i["L2_attn_Wk"], i["L2_attn_Wv"], i["L2_attn_Wig"],
                    np.repeat(np.asarray(i["L2_attn_Wg"]), 16, axis=1), i["L2_attn_Wog"])
    a["l2_wo"] = np.asarray(i["L2_attn_Wo"])
    a["l2_win"], a["l2_wout"] = blocks(i["L2_attn_Wgate"], i["L2_attn_Wval"], i["L2_attn_Wout"], 8)
    a["l2f_gw"] = t(i["L2_ffn_gate_weight"])

    def halves(w):
        return w.reshape(8, D, 2, 88).transpose(0, 2, 1, 3).reshape(16, D, 88)

    wi, wo = units(halves(t(i["L2_ffn_gate_w"])), halves(t(i["L2_ffn_up_w"])),
                   t(i["L2_ffn_down_w"]).reshape(16, 88, D))
    si, so = blocks(t(i["L2_ffn_sh_gate_w"]), t(i["L2_ffn_sh_up_w"]), t(i["L2_ffn_sh_down_w"]), 4)
    a["l2f_win"], a["l2f_wout"] = cat(wi, si, axis=0), cat(wo, so, axis=0)
    PR3 = 8
    q3, k3, v3 = (np.asarray(i["L3_attn_" + n]).reshape(D, PR3, 2, P).transpose(1, 0, 2, 3) for n in ("Wq", "Wk", "Wv"))
    a["l3_w"] = cat(np.stack([q3, k3], 3).reshape(PR3, D, 4 * P), v3.reshape(PR3, D, 2 * P))
    a["l3_wo"] = np.asarray(i["L3_attn_Wo"])
    a["l3_betas"] = np.asarray(i["L3_attn_betas"]).reshape(1, 16 * P)
    idx = np.asarray(i["L3_ffn_mask_idx"])
    a["l3f_gw"], a["l3f_w"] = t(i["L3_ffn_gate_w"]), t(i["L3_ffn_W"])
    a["l3f_ea"], a["l3f_atoms"] = np.asarray(i["L3_ffn_expert_atom_weights"]), np.asarray(i["L3_ffn_atoms"])
    a["l3f_imp"] = np.asarray(i["L3_ffn_importance"])
    a["l3f_idx"], a["l3f_idx_s"] = idx[None], idx.reshape(-1, P).T
    return a


def kernel(**inputs):
    import concourse.bacc as _bacc
    from concourse.bass_utils import run_bass_kernel_spmd as _run

    arrays = {"in_" + n: np.ascontiguousarray(a) for n, a in laid_out(inputs).items()}
    nc = _bacc.Bacc("TRN2", target_bir_lowering=False, num_devices=1)
    dram = {n[3:]: nc.dram_tensor(n, a.shape, mybir.dt.from_np(a.dtype), kind="ExternalInput").ap()
            for n, a in arrays.items()}
    out = nc.dram_tensor("out", (D, T), F32, kind="ExternalOutput").ap()
    build(nc, dram, out)
    r = _run(nc, [arrays], core_ids=[0])
    return np.ascontiguousarray(r.results[0]["out"].T)[None]
```

```python
from contextlib import ExitStack, contextmanager

import numpy as np

import concourse.bass as bass
import concourse.mybir as mybir

F32 = mybir.dt.float32
F32R = mybir.dt.float32r
I32 = mybir.dt.int32
ACT = mybir.ActivationFunctionType
ALU = mybir.AluOpType
AX = mybir.AxisListType

P = 128
T = 1024
D = 256
DB = D // P
CH = 512
NCH = T // CH
TT = T // P
NEG = -1.0e30
EXP_LN = "natural_log_exp_and_others"

SHIFT_A, SCALE_A, GATE_A, SHIFT_B, SCALE_B, GATE_B = range(0, 6 * DB, DB)


class Chain:

    def __init__(self, sem):
        self.sem, self.done, self.turn, self.each, self.k = sem, 0, None, 0, 0

    def link(self, eng, ins):
        ins.then_inc(self.sem, 1)
        self.k += 1
        if self.turn is None:
            self.done, self.k = self.done + 1, 0
            eng.wait_ge(self.sem, self.done)
        else:
            eng.wait_ge(self.sem, self.turn * self.each + (self.done + self.k))

    def enter(self, turn, each):
        self.turn, self.each, self.k = turn, each, 0

    def leave(self, turns):
        assert self.k == self.each, (self.k, self.each)
        self.done, self.turn, self.k = self.done + turns * self.each, None, 0


class Core:

    def __init__(self, nc, ctx, dram):
        self.nc, self.ctx, self.dram, self.local = nc, ctx, dram, None
        self.x = ctx.enter_context(nc.sbuf_tensor("x_stream", [P, DB, T], F32))
        self.h = ctx.enter_context(nc.sbuf_tensor("h_modulated", [P, DB, T], F32))
        self.mod = ctx.enter_context(nc.sbuf_tensor("modulation", [P, 4, 6 * DB], F32))
        self.ident = ctx.enter_context(nc.sbuf_tensor("ident", [P, P], F32))
        self.ones = ctx.enter_context(nc.sbuf_tensor("ones", [P, P], F32))
        self.zeros = ctx.enter_context(nc.sbuf_tensor("zeros", [P, CH], F32))
        self.mean_w = ctx.enter_context(nc.sbuf_tensor("mean_w", [P, P], F32))
        self.eps = ctx.enter_context(nc.sbuf_tensor("eps", [P, 4], F32))
        self.bank = ctx.enter_context(nc.psum_tensor("bank", [P, 8, CH], F32))
        self.dve_chain = Chain(self.sem("dve_step"))
        self.act_chain = Chain(self.sem("act_step"))
        self.pool_chain = Chain(self.sem("pool_step"))
        self.calls = {}

    def sem(self, name):
        if self.local is None:
            return self.ctx.enter_context(self.nc.semaphore(name))
        self.local.append(self.nc.alloc_semaphore(name=name))
        return self.local[-1]

    @contextmanager
    def stage(self):
        self.local = []
        yield
        self.nc.clear_and_free_semaphores(self.local)
        self.nc.all_engine_barrier()
        self.local = None

    def shared(self, name):
        if name not in self.calls:
            self.calls[name] = self.ctx.enter_context(self.nc.semaphore(name))
        return self.calls[name]


def over(ap, n, axis=1):
    a = ap.unsqueeze(axis)
    shape = list(a.shape)
    shape[axis] = n
    return a.to_broadcast(shape)


def chunk(c):
    return slice(c * CH, (c + 1) * CH)


def tile(t):
    return slice(t * P, (t + 1) * P)


EPS_LN, EPS_L2 = 1.0e-5, 1.0e-12


def constants(k):
    nc = k.nc
    with nc.Block() as block:
        @block.gpsimd
        def _(pool):
            step = k.pool_chain
            pool.memset(k.ones[:], 1.0)
            pool.memset(k.zeros[:], 0.0)
            pool.memset(k.mean_w[:], 1.0 / D)
            pool.memset(k.eps[:, 0:1], EPS_LN)
            pool.memset(k.eps[:, 1:2], EPS_L2)
            pool.memset(k.eps[:, 2:3], 1.0)
            pool.memset(k.eps[:, 3:4], 1.0e-6)
            step.link(pool, pool.memset(k.ident[:], 0.0))
            step.link(pool, pool.affine_select(out=k.ident[:], in_=k.ident[:], compare_op=ALU.not_equal, fill=1.0,
                                               base=0, pattern=[[-1, P]], channel_multiplier=1))


class Modulations:

    def __init__(self, k, ctx):
        self.k = k
        self.cs = ctx.enter_context(k.nc.sbuf_tensor("cs", [P, 4 * DB], F32))
        self.w = [ctx.enter_context(k.nc.sbuf_tensor(f"wmod{n}", [P, DB, 6 * D], F32)) for n in range(4)]
        self.tmp = ctx.enter_context(k.nc.sbuf_tensor("mod_tmp", [P, 3, DB], F32))
        self.w_in = [k.shared(f"wmod_in{n}") for n in range(4)]
        self.scaled, self.added, self.summed = (k.shared("mod_" + n) for n in ("scaled", "added", "summed"))

    def on_scalar(self, act, layers):
        for n in layers:
            act.wait_ge(self.w_in[n], 16)
            act.activation(self.w[n][:, 0], self.w[n][:, 0], ACT.Identity, scale=self.cs[:, n * DB:n * DB + 1]
                           ).then_inc(self.scaled, 1)

    def add_blocks(self, dve, layers):
        for n in layers:
            w = self.w[n]
            dve.wait_ge(self.scaled, n + 1)
            dve.scalar_tensor_tensor(w[:, 0], w[:, 1], self.cs[:, n * DB + 1:n * DB + 2], w[:, 0], ALU.mult, ALU.add
                                     ).then_inc(self.added, 1)

    def on_tensor(self, pe, layers):
        for n in layers:
            pe.wait_ge(self.added, n + 1)
            for j in range(6 * DB):
                last = pe.matmul(self.k.bank[:, 3, n * 16 + j:n * 16 + j + 1], self.w[n][:, 0, tile(j)],
                                 self.k.ones[:, 0:1], start=True, stop=True)
            last.then_inc(self.summed, 1)

    def finish(self, dve, layers):
        k, step, first, count = self.k, self.k.dve_chain, layers[0], len(layers)
        mod, tmp = k.mod[:, first:first + count], self.tmp[:, 0:count]
        dve.wait_ge(self.summed, first + count)
        cols = k.bank[:, 3, 0:64].rearrange("p (l j) -> p l j", l=4)
        step.link(dve, dve.tensor_copy(mod, cols[:, first:first + count, 0:6 * DB]))
        for at in (SCALE_A, SCALE_B):
            s = mod[:, :, at:at + DB]
            step.link(dve, dve.tensor_scalar(s, s, 1.0, None, ALU.add))
        for at in (GATE_A, GATE_B):
            g = mod[:, :, at:at + DB]
            step.link(dve, dve.tensor_scalar(tmp, g, 0.0, 2.0, ALU.is_ge, ALU.mult))
            step.link(dve, dve.tensor_scalar(tmp, tmp, -1.0, None, ALU.add))
            step.link(dve, dve.tensor_tensor(g, g, tmp, ALU.mult))
            step.link(dve, dve.tensor_scalar(g, g, 0.25, None, ALU.max))
            step.link(dve, dve.tensor_tensor(g, g, tmp, ALU.mult))

    def start(self):
        k, nc, d = self.k, self.k.nc, self.k.dram
        x_in, c_in, c_ready = (k.sem(n) for n in ("x_in", "c_in", "silu_c_ready"))
        with nc.Block() as block:
            @block.sync
            def _(sp):
                def load(n):
                    sp.dma_start(self.w[n][:], d["wmod"][n].rearrange("(b p) n -> p b n", p=P)
                                 ).then_inc(self.w_in[n], 16)

                sp.dma_start(self.cs[:], d["cs"]).then_inc(c_in, 16)
                load(0)
                sp.dma_start(k.x[:], d["x"].rearrange("(b p) t -> p b t", p=P)).then_inc(x_in, 16)
                for n in range(1, 4):
                    load(n)
                sp.wait_ge(x_in, 16)

            @block.scalar
            def _(act):
                act.wait_ge(c_in, 16)
                act.activation(self.cs[:], self.cs[:], ACT.Silu).then_inc(c_ready, 1)
                act.wait_ge(c_ready, 1)
                self.on_scalar(act, [0])

            @block.tensor
            def _(pe):
                self.on_tensor(pe, [0])

            @block.vector
            def _(dve):
                dve.wait_ge(c_ready, 1)
                self.add_blocks(dve, [0])
                self.finish(dve, [0])


class LayerNorm:

    def __init__(self, k, ctx, src, dst, scale, shift):
        self.k, self.src, self.dst, self.scale, self.shift = k, src, dst, scale, shift
        self.at = NCH * k.calls.setdefault("layernorms", 0)
        k.calls["layernorms"] += 1
        self.s = {n: k.shared("ln_" + n) for n in ("mean_ready", "centered", "squared", "var_ready", "root_ready",
                                                   "normed", "out_ready")}
        self.sq = ctx.enter_context(k.nc.sbuf_tensor(f"ln_square{self.at}", [P, DB, T], F32))
        self.rs = ctx.enter_context(k.nc.sbuf_tensor(f"ln_rstd{self.at}", [P, T], F32))

    def wait(self, eng):
        eng.wait_ge(self.s["out_ready"], self.at + NCH)

    def on_tensor(self, pe):
        k, s = self.k, self.s
        for c in range(NCH):
            for b in range(DB):
                last = pe.matmul(k.bank[:, c, :], k.mean_w[:], self.src[:, b, chunk(c)], start=(b == 0),
                                 stop=(b == DB - 1))
            last.then_inc(s["mean_ready"], 1)
        for c in range(NCH):
            pe.wait_ge(s["squared"], self.at + c + 1)
            for b in range(DB):
                last = pe.matmul(k.bank[:, 2 + c, :], k.mean_w[:], self.sq[:, b, chunk(c)], start=(b == 0),
                                 stop=(b == DB - 1))
            last.then_inc(s["var_ready"], 1)

    def on_vector(self, dve):
        k, s, dst = self.k, self.s, self.dst
        for c in range(NCH):
            dve.wait_ge(s["mean_ready"], self.at + c + 1)
            dve.tensor_tensor(dst[:, :, chunk(c)], self.src[:, :, chunk(c)], over(k.bank[:, c, :], DB), ALU.subtract
                              ).then_inc(s["centered"], 1)
        for c in range(NCH):
            dve.wait_ge(s["root_ready"], self.at + c + 1)
            dve.tensor_tensor(dst[:, :, chunk(c)], dst[:, :, chunk(c)], over(self.rs[:, chunk(c)], DB), ALU.mult
                              ).then_inc(s["normed"], 1)
            dve.wait_ge(s["normed"], self.at + c + 1)
            for b in range(DB):
                last = dve.tensor_scalar(dst[:, b, chunk(c)], dst[:, b, chunk(c)], self.scale[:, b:b + 1],
                                         self.shift[:, b:b + 1], ALU.mult, ALU.add)
            last.then_inc(s["out_ready"], 1)

    def on_scalar(self, act):
        k, s, rs = self.k, self.s, self.rs
        act.preload_act_table_set(EXP_LN)
        for c in range(NCH):
            act.wait_ge(s["centered"], self.at + c + 1)
            act.activation(self.sq[:, :, chunk(c)], self.dst[:, :, chunk(c)], ACT.Square).then_inc(s["squared"], 1)
        for c in range(NCH):
            act.wait_ge(s["var_ready"], self.at + c + 1)
            k.act_chain.link(act, act.activation(rs[:, chunk(c)], k.bank[:, 2 + c, :], ACT.Ln, bias=k.eps[:, 0:1]))
            act.activation(rs[:, chunk(c)], rs[:, chunk(c)], ACT.Exp, scale=-0.5).then_inc(s["root_ready"], 1)


def layernorm(k, src, dst, scale, shift):
    with ExitStack() as ctx:
        norm = LayerNorm(k, ctx, src, dst, scale, shift)
        with k.nc.Block() as block:
            block.tensor(norm.on_tensor)
            block.vector(norm.on_vector)
            block.scalar(norm.on_scalar)


def adaln(k, ctx, layer, shift, scale):
    return LayerNorm(k, ctx, k.x, k.h, k.mod[:, layer, scale:scale + DB], k.mod[:, layer, shift:shift + DB])


def gated_units(k, name, units, w_in, w_out, gate, src=None, rows=None, turn=1, rows_per_turn=0, owner=None,
                extra=None):
    nc = k.nc
    src = k.h if src is None else src
    pairs = units // 2
    weighted = rows is not None
    loaded = [k.sem(f"{name}_w_in{n}") for n in range(2)]
    rows_in = [k.sem(f"{name}_rows_in{n}") for n in range(2)]
    src_hi_ready, src_split, in_hi_ready, in_split, out_hi_ready, out_split, up_ready, act_ready, up_used, gated, hi_ready, lo_ready, summed, done = (
        k.sem(f"{name}_{n}") for n in ("src_hi_ready", "src_split", "in_hi_ready", "in_split", "out_hi_ready",
                                       "out_split", "up_ready", "act_ready", "up_used", "gated", "hi_ready",
                                       "lo_ready", "summed", "done"))
    WI = DB * 2 * P
    WU = WI + D
    w_in_part, w_out_part = slice(0, WI), slice(WI, WU)
    with ExitStack() as ctx:
        def sb(n, shape, dt=F32):
            return ctx.enter_context(nc.sbuf_tensor(f"{name}_{n}", shape, dt))
        w = sb("w", [P, 2, WU])
        w_hi, w_lo = (sb("w_" + n, [P, 2, WU], F32R) for n in ("hi", "lo"))
        src_hi, src_lo = (sb("src_" + n, [P, DB, T], F32R) for n in ("hi", "lo"))
        s = sb("s", [P, NCH, CH])
        a = sb("a", [P, NCH, CH])
        a_hi, a_lo = (sb("a_" + n, [P, NCH, CH], F32R) for n in ("hi", "lo"))
        wr = sb("wr", [P, 2, T]) if weighted else None
        with nc.Block() as block:
            @block.sync
            def _(sp):
                def load_unit(g, j):
                    half = j % 2
                    u = g * turn + j
                    sp.dma_start(w[:, half, w_in_part], w_in[bass.ds(u, 1)].rearrange("u p n -> p (u n)")
                                 ).then_inc(loaded[half], 16)
                    sp.dma_start(w[:, half, w_out_part], w_out[bass.ds(u, 1)].rearrange("u f n -> f (u n)")
                                 ).then_inc(loaded[half], 16)

                def load_rows(g, j):
                    for p0, p1, r in owner(j):
                        sp.dma_start(wr[p0:p1, j % 2], rows[bass.ds(g * rows_per_turn + r, 1)].to_broadcast(
                            [p1 - p0, T])).then_inc(rows_in[j % 2], 16)

                def do_turn(g, first):
                    for j in range(turn):
                        if not (first and j < 2):
                            sp.wait_ge(out_split, g * turn + (j - 1))
                        load_unit(g, j)
                        if weighted:
                            if not (first and j < 2):
                                sp.wait_ge(gated, g * (2 * turn) + (2 * j - 2))
                            load_rows(g, j)

                do_turn(0, True)
                if units > turn:
                    with sp.Fori(1, units // turn) as g:
                        do_turn(g, False)

            @block.gpsimd
            def _(pool):
                def low_parts(i, half):
                    for part, hi_ready_, split_ in ((w_in_part, in_hi_ready, in_split),
                                                    (w_out_part, out_hi_ready, out_split)):
                        pool.wait_ge(hi_ready_, i * 2 + (half + 1))
                        pool.tensor_tensor(w_lo[:, half, part], w[:, half, part], w_hi[:, half, part].bitcast(F32),
                                           ALU.subtract).then_inc(split_, 1)

                with pool.Fori(0, pairs) as i:
                    for half in range(2):
                        low_parts(i, half)

            @block.tensor
            def _(pe):
                for m in range(DB):
                    for c in range(NCH):
                        pe.matmul(k.bank[:, 4 + 2 * m + c, :], k.zeros[:, 0:P], k.zeros[:], start=True, stop=False,
                                  skip_group_check=True)
                for n, (lhs_t, rhs) in enumerate(extra or []):
                    for m in range(DB):
                        for c in range(NCH):
                            pe.matmul(k.bank[:, 4 + 2 * m + c, :], lhs_t[:, tile(m)], rhs[:, chunk(c)], start=False,
                                      stop=False, skip_group_check=True)
                passes = ((w_hi, src_hi, a_hi), (w_hi, src_lo, a_lo), (w_lo, src_hi, a_hi))

                def up(i, n, first=False):
                    half, c = n // 2, n % 2
                    if c == 0:
                        pe.wait_ge(in_split, i * 2 + (half + 1))
                    if not (first and n < 2):
                        pe.wait_ge(up_used, i * 4 + (n - 1))
                    if first and n < 2:
                        pe.wait_ge(src_split, n + 1)
                    for part in range(2):
                        for b in range(DB):
                            at = b * 2 * P + part * P
                            for q, (wq, xq, _) in enumerate(passes):
                                last = pe.matmul(k.bank[:, 2 * c + part, :], wq[:, half, at:at + P],
                                                 xq[:, b, chunk(c)], start=(b == 0 and q == 0),
                                                 stop=(b == DB - 1 and q == 2))
                    last.then_inc(up_ready, 1)

                def down(i, n):
                    half, c = n // 2 % 2, n % 2
                    if c == 0:
                        pe.wait_ge(out_split, i * 2 + (n // 2 + 1))
                    pe.wait_ge(lo_ready, i * 4 + (n + 1))
                    for m in range(DB):
                        at = WI + m * P
                        for wq, _, aq in passes:
                            last = pe.matmul(k.bank[:, 4 + 2 * m + c, :], wq[:, half, at:at + P], aq[:, c, :],
                                             start=False, stop=False, skip_group_check=True)
                    last.then_inc(summed, 1)

                up(0, 0, True)
                up(0, 1, True)
                for n in range(2, 4):
                    up(0, n, True)
                    down(0, n - 2)
                with pe.Fori(1, pairs) as i:
                    for n in range(4):
                        up(i, n)
                        down(i, n - 2)
                down(pairs, -2)
                down(pairs, -1)

            @block.scalar
            def _(act):
                for c in range(NCH):
                    act.activation(src_hi[:, :, chunk(c)], src[:, :, chunk(c)], ACT.Identity
                                   ).then_inc(src_hi_ready, 1)
                act.preload_act_table(ACT.Silu)

                def high(i, unit, part, ready):
                    half = unit % 2
                    act.wait_ge(loaded[half], i * 32 + (32 + 32 * (unit // 2)))
                    act.activation(w_hi[:, half, part], w[:, half, part], ACT.Identity).then_inc(ready, 1)

                def pair(i, first, last):
                    for n in range(4):
                        half, c = n // 2, n % 2
                        if c == 0:
                            high(i, half, w_out_part, out_hi_ready)
                            if not (last and half):
                                high(i, half + 1, w_in_part, in_hi_ready)
                        act.wait_ge(up_ready, i * 4 + (n + 1))
                        act.activation(s[:, c, :], k.bank[:, 2 * c, :], ACT.Silu).then_inc(act_ready, 1)
                        act.wait_ge(gated, i * 4 + (n + 1))
                        if not (first and n < 2):
                            act.wait_ge(summed, i * 4 + (n - 1))
                        act.activation(a_hi[:, c, :], a[:, c, :], ACT.Identity).then_inc(hi_ready, 1)

                high(0, 0, w_in_part, in_hi_ready)
                pair(0, True, False)
                with act.Fori(1, pairs - 1) as i:
                    pair(i, False, False)
                pair(pairs - 1, False, True)

            @block.vector
            def _(dve):
                for c in range(NCH):
                    dve.wait_ge(src_hi_ready, c + 1)
                    dve.tensor_tensor(src_lo[:, :, chunk(c)], src[:, :, chunk(c)], src_hi[:, :, chunk(c)].bitcast(F32),
                                      ALU.subtract).then_inc(src_split, 1)

                def pair(i, first):
                    for n in range(4):
                        half, c = n // 2, n % 2
                        dve.wait_ge(act_ready, i * 4 + (n + 1))
                        last = dve.tensor_tensor(a[:, c, :], s[:, c, :], k.bank[:, 2 * c + 1, :], ALU.mult)
                        last.then_inc(up_used, 1)
                        if weighted:
                            dve.wait_ge(up_used, i * 4 + (n + 1))
                            if c == 0:
                                dve.wait_ge(rows_in[half], i * 32 + 32)
                            last = dve.tensor_tensor(a[:, c, :], a[:, c, :], wr[:, half, chunk(c)], ALU.mult)
                            last.then_inc(gated, 1)
                        else:
                            dve.wait_ge(up_used, i * 4 + (n + 1))
                            dve.sem_inc(gated, 1)
                        dve.wait_ge(hi_ready, i * 4 + (n + 1))
                        if not (first and n < 2):
                            dve.wait_ge(summed, i * 4 + (n - 1))
                        dve.tensor_tensor(a_lo[:, c, :], a[:, c, :], a_hi[:, c, :].bitcast(F32), ALU.subtract
                                          ).then_inc(lo_ready, 1)

                pair(0, True)
                with dve.Fori(1, pairs) as i:
                    pair(i, False)
                dve.wait_ge(summed, 4 * pairs)
                for m in range(DB):
                    for c in range(NCH):
                        last = dve.scalar_tensor_tensor(k.x[:, m, chunk(c)], k.bank[:, 4 + 2 * m + c, :],
                                                        gate[:, m:m + 1], k.x[:, m, chunk(c)], ALU.mult, ALU.add)
                last.then_inc(done, 1)


def owners(f, count=2):
    def pieces(j):
        out, at = [], j * P
        while at < (j + 1) * P:
            end = min((at // f + 1) * f, (j + 1) * P)
            out.append((at - j * P, end - j * P, at // f))
            at = end
        if len(out) == 1:
            out = [(0, P // 2, out[0][2]), (P // 2, P, out[0][2])]
        assert len(out) == count
        return out
    return pieces


def l0_attention(k, norm, mods):
    nc, d = k.nc, k.dram
    H, W, KW = 8, 64, 192
    SCALE = 8.0
    w_in = k.sem("l0_w_in")
    v_w_in, v_ready, v_copied, g_ready, gate_exp, gate_one, gates_ready, mask_ready, qscale_in = (
        k.sem("l0_" + n) for n in ("v_w_in", "v_ready", "v_copied", "g_ready", "gate_exp", "gate_one", "gates_ready",
                                   "mask_ready", "qscale_in"))
    qk_ready, sq_ready, ss_ready, ss_clamped, rn_ready, qk_normed, scores_ready, scores_read, best_ready, probs_exp, probs_ready = (
        k.sem("l0_" + n) for n in ("qk_ready", "sq_ready", "ss_ready", "ss_clamped", "rn_ready", "qk_normed",
                                   "scores_ready", "scores_read", "best_ready", "probs_exp", "probs_ready"))
    pt_ready, pt_copied, o_ready, o_copied, vh_ready, y_ready, y_done = (
        k.sem("l0_" + n) for n in ("pt_ready", "pt_copied", "o_ready", "o_copied", "vh_ready", "y_ready", "y_done"))
    with ExitStack() as ctx:
        def sb(n, shape):
            return ctx.enter_context(nc.sbuf_tensor("l0_" + n, shape, F32))
        wv = sb("wv", [P, DB, H * P])
        wo = sb("wo", [P, H, D])
        wg = sb("wg", [P, DB, H])
        bg = sb("bg", [P, H])
        scales = sb("scales", [P, 2])
        wqk = sb("wqk", [P, DB, 2 * P])
        v = sb("v", [P, TT, H * P])
        vh = sb("vh", [P, TT, P])
        gates = sb("gates", [P, TT, H])
        qk = sb("qk", [P, 2, W + T])
        sq = norm.sq[:].rearrange("p b (c q) -> p (b c) q", q=CH)
        rn = sb("rn", [P, 4, CH])
        mask = sb("mask", [P, 2, KW])
        sc = sb("sc", [P, TT, P + P])
        st = sb("st", [P, 4, TT])
        pt = sb("pt", [P, TT, 2, P])
        o = sb("o", [P, H, T])
        with nc.Block() as block:
            @block.sync
            def _(sp):
                sp.dma_start(wv[:], d["l0_wv"].rearrange("(b p) n -> p b n", p=P)).then_inc(v_w_in, 16)
                sp.dma_start(wg[:], d["l0_wg"].rearrange("(b p) n -> p b n", p=P)).then_inc(v_w_in, 16)
                sp.dma_start(bg[:], d["l0_bg"].to_broadcast([P, H])).then_inc(v_w_in, 16)
                sp.dma_start(scales[:], d["l0_scales"]).then_inc(qscale_in, 16)
                sp.dma_start(wqk[:], d["l0_wqk"][0].rearrange("(b p) n -> p b n", p=P)).then_inc(w_in, 16)
                sp.dma_start(wo[:], d["l0_wo"].rearrange("(h p) n -> p h n", p=P)).then_inc(qscale_in, 16)
                with sp.Fori(1, H) as h:
                    sp.wait_ge(qk_ready, h * 4)
                    sp.dma_start(wqk[:], d["l0_wqk"][bass.ds(h, 1)].rearrange("u (b p) n -> p (u b) n", p=P)
                                 ).then_inc(w_in, 16)

            @block.gpsimd
            def _(pool):
                step = k.pool_chain
                pool.memset(qk[:, :, 0:W], 0.0)
                pool.memset(sc[:, :, 0:W], 0.0)
                step.link(pool, pool.memset(mask[:], 0.0))
                m0, m1 = mask[:, 0, :], mask[:, 1, :]
                for m in (m0, m1):
                    step.link(pool, pool.affine_select(out=m, in_=m, compare_op=ALU.is_ge, fill=NEG, base=W,
                                                       pattern=[[-1, KW]], channel_multiplier=1))
                    step.link(pool, pool.affine_select(out=m, in_=m, compare_op=ALU.is_ge, fill=NEG, base=0,
                                                       pattern=[[1, KW]], channel_multiplier=-1))
                pool.memset(mask[:, 0, 0:W], NEG).then_inc(mask_ready, 1)

                def values(h):
                    pool.wait_ge(o_copied, h * 2 + 2)
                    pool.tensor_copy(vh[:], v[:, :, bass.ds(h * P, P)]).then_inc(vh_ready, 1)

                pool.wait_ge(v_copied, 2 * TT)
                with pool.Fori(0, H) as h:
                    values(h)

            @block.tensor
            def _(pe):
                norm.on_tensor(pe)
                norm.wait(pe)
                pe.wait_ge(v_w_in, 48)
                for t in range(TT):
                    for n in range(2):
                        j = 2 * t + n
                        if j >= 2:
                            pe.wait_ge(v_copied, j - 1)
                        for b in range(DB):
                            last = pe.matmul(k.bank[:, j % 2, :], k.h[:, b, tile(t)], wv[:, b, chunk(n)],
                                             start=(b == 0), stop=(b == DB - 1))
                        last.then_inc(v_ready, 1)
                for t in range(TT):
                    for b in range(DB):
                        last = pe.matmul(k.bank[:, 2, t * H:(t + 1) * H], k.h[:, b, tile(t)], wg[:, b, :],
                                         start=(b == 0), stop=(b == DB - 1))
                last.then_inc(g_ready, 1)
                mods.on_tensor(pe, range(1, 4))
                pe.wait_ge(v_copied, 2 * TT)
                pe.wait_ge(gates_ready, 1)

                def project(h):
                    pe.wait_ge(w_in, h * 16 + 16)
                    for j in range(4):
                        for b in range(DB):
                            last = pe.matmul(k.bank[:, 4 + j, :], wqk[:, b, tile(j // 2)], k.h[:, b, chunk(j % 2)],
                                             start=(b == 0), stop=(b == DB - 1))
                        last.then_inc(qk_ready, 1)

                def square_sums(h):
                    for j in range(4):
                        pe.wait_ge(sq_ready, h * 4 + (j + 1))
                        if j >= 2:
                            pe.wait_ge(ss_clamped, h * 4 + (j - 1))
                        pe.matmul(k.bank[:, j % 2, :], k.ones[:], sq[:, j, :], start=True, stop=True
                                  ).then_inc(ss_ready, 1)

                def turn_probs(h, part):
                    pe.wait_ge(probs_ready, h * 2 + (part + 1))
                    if part:
                        pe.wait_ge(pt_copied, h * 4 + 2)
                    for t in range(4 * part, 4 * part + 4):
                        for side in range(2):
                            at = (t % 2) * 256 + side * P
                            last = pe.transpose(k.bank[:, 2 + t // 2 % 2, at:at + P], sc[:, t, tile(side)],
                                                k.ident[:])
                        if t % 2:
                            last.then_inc(pt_ready, 1)

                def mix_values(h, part):
                    pe.wait_ge(pt_copied, h * 4 + (2 * part + 2))
                    for t in range(4 * part, 4 * part + 4):
                        out = k.bank[:, part, (t % 4) * P:(t % 4 + 1) * P]
                        if t:
                            pe.matmul(out, vh[:, t - 1, :], pt[:, t, 0, :], start=True, stop=False)
                        last = pe.matmul(out, vh[:, t, :], pt[:, t, 1, :], start=(t == 0), stop=True)
                    last.then_inc(o_ready, 1)

                def head(h, final):
                    pe.wait_ge(qk_normed, h * 4 + 4)
                    pe.wait_ge(ss_clamped, h * 4 + 4)
                    pe.wait_ge(o_copied, h * 2 + 2)
                    for t in range(TT):
                        last = pe.matmul(k.bank[:, t // 2, (t % 2) * 256:(t % 2) * 256 + KW],
                                         qk[:, 0, W + t * P:W + (t + 1) * P], qk[:, 1, t * P:t * P + KW],
                                         start=True, stop=True)
                    last.then_inc(scores_ready, 1)
                    if not final:
                        project(h + 1)
                        pe.wait_ge(scores_read, h + 1)
                        square_sums(h + 1)
                    turn_probs(h, 0)
                    turn_probs(h, 1)
                    if not final:
                        pe.wait_ge(ss_clamped, h * 4 + 8)
                    pe.wait_ge(vh_ready, h + 1)
                    mix_values(h, 0)
                    mix_values(h, 1)

                project(0)
                square_sums(0)
                with pe.Fori(0, H - 1) as h:
                    head(h, False)
                head(H - 1, True)
                pe.wait_ge(qscale_in, 32)
                pe.wait_ge(o_copied, 2 * H + 2)
                for m in range(DB):
                    for c in range(NCH):
                        for h in range(H):
                            last = pe.matmul(k.bank[:, 2 * m + c, :], wo[:, h, tile(m)], o[:, h, chunk(c)],
                                             start=(h == 0), stop=(h == H - 1))
                        last.then_inc(y_ready, 1)

            @block.scalar
            def _(act):
                norm.on_scalar(act)
                step = k.act_chain
                act.preload_act_table_set(EXP_LN)
                mods.on_scalar(act, range(1, 4))
                for j in range(2 * TT):
                    act.wait_ge(v_ready, j + 1)
                    act.activation(v[:, j // 2, chunk(j % 2)], k.bank[:, j % 2, :], ACT.Identity
                                   ).then_inc(v_copied, 1)
                act.wait_ge(gate_one, 1)
                act.activation(gates[:], gates[:], ACT.Exp, scale=-1.0).then_inc(gate_exp, 1)
                act.sem_inc(o_copied, 2)

                def square(h, j):
                    act.wait_ge(qk_ready, h * 4 + (j + 1))
                    act.activation(sq[:, j, :], k.bank[:, 4 + j, :], ACT.Square).then_inc(sq_ready, 1)

                def factors(h, parts):
                    for j in parts:
                        act.wait_ge(ss_clamped, h * 4 + (j + 1))
                        step.link(act, act.activation(rn[:, j, :], rn[:, j, :], ACT.Ln, scale=65536.0))
                        act.activation(rn[:, j, :], rn[:, j, :], ACT.Exp, scale=-0.5).then_inc(rn_ready, 1)

                def head(h, final):
                    for j in range(4):
                        if not final:
                            square(h + 1, j)
                        if j == 1:
                            act.wait_ge(best_ready, h + 1)
                            for t in range(TT):
                                act.activation(sc[:, t, W:W + KW], sc[:, t, W:W + KW], ACT.Exp, bias=st[:, 0, t:t + 1],
                                               accum_out=st[:, 1, t:t + 1]).then_inc(probs_exp, 1)
                    for j in range(4):
                        if not final and j in (0, 2):
                            factors(h + 1, (j // 2,))
                        act.wait_ge(pt_ready, h * 4 + (j + 1))
                        act.activation(pt[:, 2 * j:2 * j + 2], k.bank[:, 2 + j % 2, :].rearrange(
                            "p (t a q) -> p t a q", t=2, a=2), ACT.Identity).then_inc(pt_copied, 1)
                    if not final:
                        factors(h + 1, (2, 3))
                    for c in range(2):
                        act.wait_ge(o_ready, h * 2 + (c + 1))
                        act.activation(o[:, bass.ds(h, 1), chunk(c)], k.bank[:, c:c + 1, :], ACT.Identity
                                       ).then_inc(o_copied, 1)

                for j in range(4):
                    square(0, j)
                factors(0, range(4))
                with act.Fori(0, H - 1) as h:
                    step.enter(h, 4)
                    head(h, False)
                step.leave(H - 1)
                head(H - 1, True)

            @block.vector
            def _(dve):
                norm.on_vector(dve)
                step = k.dve_chain
                mods.add_blocks(dve, range(1, 4))
                dve.wait_ge(v_w_in, 48)
                dve.wait_ge(g_ready, 1)
                dve.tensor_tensor(gates[:], k.bank[:, 2, 0:TT * H].rearrange("p (t h) -> p t h", t=TT),
                                  over(bg[:], TT), ALU.add).then_inc(gate_one, 1)
                dve.wait_ge(gate_exp, 1)
                step.link(dve, dve.tensor_scalar(gates[:], gates[:], 1.0, None, ALU.add))
                dve.reciprocal(gates[:], gates[:]).then_inc(gates_ready, 1)
                dve.wait_ge(gates_ready, 1)
                dve.wait_ge(qscale_in, 32)
                step.link(dve, dve.tensor_scalar(scales[:], scales[:], 256.0, None, ALU.mult))
                step.link(dve, dve.tensor_scalar(scales[:, 0:1], scales[:, 0:1], SCALE, None, ALU.mult))
                mods.finish(dve, range(1, 4))
                dve.wait_ge(mask_ready, 1)

                def clamp(h):
                    for j in range(4):
                        dve.wait_ge(ss_ready, h * 4 + (j + 1))
                        dve.tensor_scalar(rn[:, j, :], k.bank[:, j % 2, :], 1.0e-24, None, ALU.max
                                          ).then_inc(ss_clamped, 1)

                def normalise(h):
                    for j in range(4):
                        dve.wait_ge(rn_ready, h * 4 + (j + 1))
                        n, c = j // 2, j % 2
                        dve.scalar_tensor_tensor(qk[:, n, W + c * CH:W + (c + 1) * CH], k.bank[:, 4 + j, :],
                                                 scales[:, n:n + 1], rn[:, j, :], ALU.mult, ALU.mult
                                                 ).then_inc(qk_normed, 1)

                def softmax(h):
                    dve.wait_ge(scores_ready, h + 1)
                    banks = k.bank[:, 0:4, :].rearrange("p n (a q) -> p (n a) q", a=2)
                    s = sc[:, :, W:W + KW]
                    dve.tensor_tensor(s[:, 0:1], banks[:, 0:1, 0:KW], mask[:, 0:1], ALU.add)
                    step.link(dve, dve.tensor_tensor(s[:, 1:TT], banks[:, 1:TT, 0:KW], over(mask[:, 1, :], TT - 1),
                                                     ALU.add))
                    dve.sem_inc(scores_read, 1)
                    step.link(dve, dve.tensor_reduce(st[:, 2, :], s, AX.X, ALU.max))
                    dve.tensor_scalar(st[:, 0, :], st[:, 2, :], -1.0, None, ALU.mult).then_inc(best_ready, 1)
                    step.link(dve, dve.tensor_copy(st[:, 3, :], gates[:, :, bass.ds(h, 1)].rearrange(
                        "p t h -> p (t h)")))
                    for part in range(2):
                        four = slice(4 * part, 4 * part + 4)
                        dve.wait_ge(probs_exp, h * TT + (4 * part + 4))
                        step.link(dve, dve.reciprocal(st[:, 2, four], st[:, 1, four]))
                        step.link(dve, dve.tensor_tensor(st[:, 2, four], st[:, 2, four], st[:, 3, four], ALU.mult))
                        dve.tensor_tensor(s[:, four], s[:, four], over(st[:, 2, four], KW, 2), ALU.mult
                                          ).then_inc(probs_ready, 1)

                clamp(0)
                normalise(0)
                with dve.Fori(0, H - 1) as h:
                    step.enter(h, 7)
                    softmax(h)
                    clamp(h + 1)
                    normalise(h + 1)
                step.leave(H - 1)
                softmax(H - 1)
                for j in range(4):
                    dve.wait_ge(y_ready, j + 1)
                    m, c = j // 2, j % 2
                    last = dve.scalar_tensor_tensor(k.x[:, m, chunk(c)], k.bank[:, j, :],
                                                    k.mod[:, 0, GATE_A + m:GATE_A + m + 1], k.x[:, m, chunk(c)],
                                                    ALU.mult, ALU.add)
                last.then_inc(y_done, 1)


def l0_ffn(k, norm):
    nc, d = k.nc, k.dram
    TOP, KEYS, E, EB = 8, 64, 512, 4
    w_in, q_ready, q_copied, route_ready, route_copied = (
        k.sem("l0f_" + n) for n in ("w_in", "q_ready", "q_copied", "route_ready", "route_copied"))
    best_ready, best_exp, sums_ready, pair_exp, weights_ready, wt_ready, wt_copied, s_ready, s_act, s_gated = (
        k.sem("l0f_" + n) for n in ("best_ready", "best_exp", "sums_ready", "pair_exp", "weights_ready", "wt_ready",
                                    "wt_copied", "s_ready", "s_act", "s_gated"))
    with ExitStack() as outer:
        ar = outer.enter_context(nc.sbuf_tensor("l0f_ar", [P, EB, T], F32))
        ue = outer.enter_context(nc.sbuf_tensor("l0f_ue", [P, EB, D], F32))
        with ExitStack() as ctx:
            def sb(n, shape):
                return ctx.enter_context(nc.sbuf_tensor("l0f_" + n, shape, F32))
            wq = sb("wq", [P, DB, P])
            keys = sb("keys", [KEYS, 2, KEYS])
            de = sb("de", [P, DB, E])
            q = sb("q", [KEYS, 2, T])
            r = sb("r", [P, TT, 2, KEYS])
            s8 = sb("s8", [P, 2, TT, TOP])
            pairs = sb("pairs", [P, TT, TOP, TOP])
            best = sb("best", [P, TT, TOP])
            be = sb("be", [P, TT, TOP])
            st = sb("st", [P, 4, TT])
            f = sb("f", [P, 2, TOP, KEYS])
            fe = sb("fe", [P, 2, E])
            w = sb("w", [P, 2, E])
            wt = sb("wt", [P, EB, T])
            sa = sb("sa", [P, 2, CH])
            with nc.Block() as block:
                @block.sync
                def _(sp):
                    sp.dma_start(wq[:], d["l0f_wq"].rearrange("(b p) n -> p b n", p=P)).then_inc(w_in, 16)
                    sp.dma_start(keys[:], d["l0f_keys"].rearrange("g p n -> p g n")).then_inc(w_in, 16)
                    sp.dma_start(de[:], d["l0f_de"].rearrange("(b p) n -> p b n", p=P)).then_inc(w_in, 16)
                    sp.dma_start(ue[:], d["l0f_ue"].rearrange("(b p) n -> p b n", p=P)).then_inc(w_in, 16)

                @block.tensor
                def _(pe):
                    norm.on_tensor(pe)
                    norm.wait(pe)
                    pe.wait_ge(w_in, 64)
                    for g in range(2):
                        for b in range(DB):
                            last = pe.matmul(k.bank[:, g, :], wq[:, b, :], k.h[:, b, chunk(g)],
                                             start=(b == 0), stop=(b == DB - 1))
                        last.then_inc(q_ready, 1)
                    pe.wait_ge(q_copied, 2)
                    for t in range(TT):
                        for g in range(2):
                            last = pe.matmul(k.bank[:, 2 + t // 4, (t % 4) * P + g * KEYS:(t % 4) * P + (g + 1) * KEYS],
                                             q[:, g, tile(t)], keys[:, g, :], start=True, stop=True)
                    last.then_inc(route_ready, 1)
                    for t in range(TT):
                        pe.wait_ge(weights_ready, t + 1)
                        if t >= 2:
                            pe.wait_ge(wt_copied, t - 1)
                        for e in range(EB):
                            last = pe.transpose(k.bank[:, 4 + t % 2, tile(e)], w[:, t % 2, tile(e)], k.ident[:])
                        last.then_inc(wt_ready, 1)
                    for n in range(2 * EB):
                        e, c = n // 2, n % 2
                        if n >= 2:
                            pe.wait_ge(s_act, n - 1)
                        for b in range(DB):
                            last = pe.matmul(k.bank[:, 6 + c, :], de[:, b, tile(e)], k.h[:, b, chunk(c)],
                                             start=(b == 0), stop=(b == DB - 1))
                        last.then_inc(s_ready, 1)

                @block.scalar
                def _(act):
                    norm.on_scalar(act)
                    act.preload_act_table_set(EXP_LN)
                    act.wait_ge(route_ready, 1)
                    act.activation(r[:].rearrange("p t g e -> p (t g e)"),
                                   k.bank[:, 2:4, :].rearrange("p b n -> p (b n)"), ACT.Identity
                                   ).then_inc(route_copied, 1)
                    act.wait_ge(best_ready, 1)
                    act.activation(be[:], be[:], ACT.Exp).then_inc(best_exp, 1)
                    for t in range(TT):
                        act.wait_ge(sums_ready, t + 1)
                        act.activation(fe[:, t % 2, :], f[:, t % 2].rearrange("p i j -> p (i j)"), ACT.Exp,
                                       bias=st[:, 0, t:t + 1]).then_inc(pair_exp, 1)
                        if t >= 1:
                            act.wait_ge(wt_ready, t)
                            act.activation(wt[:, :, tile(t - 1)], k.bank[:, 4 + (t - 1) % 2, :].rearrange(
                                "p (e q) -> p e q", e=EB), ACT.Identity).then_inc(wt_copied, 1)
                    act.wait_ge(wt_ready, TT)
                    act.activation(wt[:, :, tile(TT - 1)], k.bank[:, 5, :].rearrange("p (e q) -> p e q", e=EB),
                                   ACT.Identity).then_inc(wt_copied, 1)
                    for n in range(2 * EB):
                        act.wait_ge(s_ready, n + 1)
                        if n >= 2:
                            act.wait_ge(s_gated, n - 1)
                        act.activation(sa[:, n % 2, :], k.bank[:, 6 + n % 2, :], ACT.Silu).then_inc(s_act, 1)

                @block.vector
                def _(dve):
                    norm.on_vector(dve)
                    step = k.dve_chain
                    for g in range(2):
                        dve.wait_ge(q_ready, g + 1)
                        view = q[:, g, :].rearrange("p (t o) -> p t o", o=2)
                        dve.tensor_copy(view[:, :, 0], k.bank[0:KEYS, g, :])
                        dve.tensor_copy(view[:, :, 1], k.bank[KEYS:P, g, :]).then_inc(q_copied, 1)
                    dve.wait_ge(route_copied, 1)
                    for t in range(TT):
                        for g in range(2):
                            last = dve.max(s8[:, g, t, :], r[:, t, g, :])
                    step.link(dve, last)
                    step.link(dve, dve.tensor_tensor(pairs[:], over(s8[:, 0], TOP, 3), over(s8[:, 1], TOP, 2), ALU.add))
                    for t in range(TT):
                        last = dve.max(best[:, t, :], pairs[:, t].rearrange("p i j -> p (i j)"))
                    step.link(dve, last)
                    dve.tensor_tensor(be[:], best[:], over(best[:, :, 0], TOP, 2), ALU.subtract
                                      ).then_inc(best_ready, 1)
                    step.link(dve, dve.tensor_scalar(st[:, 0, :], best[:, :, 0], -1.0, None, ALU.mult))
                    dve.wait_ge(best_exp, 1)
                    step.link(dve, dve.tensor_reduce(st[:, 1, :], be[:], AX.X, ALU.add))
                    step.link(dve, dve.reciprocal(st[:, 2, :], st[:, 1, :]))
                    for t in range(TT):
                        if t >= 2:
                            dve.wait_ge(pair_exp, t - 1)
                        step.link(dve, dve.tensor_tensor(f[:, t % 2], over(r[:, t, 0, 0:TOP], KEYS, 2),
                                                         over(r[:, t, 1, :], TOP, 1), ALU.add))
                        dve.sem_inc(sums_ready, 1)
                        dve.wait_ge(pair_exp, t + 1)
                        if t >= 2:
                            dve.wait_ge(wt_ready, t - 1)
                        wv = w[:, t % 2, :]
                        step.link(dve, dve.scalar_tensor_tensor(wv, f[:, t % 2].rearrange("p i j -> p (i j)"),
                                                                best[:, t, TOP - 1:TOP], fe[:, t % 2, :],
                                                                ALU.is_ge, ALU.mult))
                        step.link(dve, dve.tensor_scalar(wv, wv, st[:, 2, t:t + 1], None, ALU.mult))
                        step.link(dve, dve.tensor_reduce(st[:, 3, t:t + 1], wv[:, 0:E - 1], AX.X, ALU.add))
                        dve.tensor_scalar(wv[:, E - 1:E], st[:, 3, t:t + 1], -1.0, 1.0, ALU.mult, ALU.add
                                          ).then_inc(weights_ready, 1)
                    dve.wait_ge(wt_copied, TT)
                    for n in range(2 * EB):
                        e, c = n // 2, n % 2
                        dve.wait_ge(s_act, n + 1)
                        dve.tensor_tensor(ar[:, e, chunk(c)], sa[:, c, :], wt[:, e, chunk(c)], ALU.mult
                                          ).then_inc(s_gated, 1)
        gated_units(k, "l0m", 8, d["l0f_win"], d["l0f_wout"], gate_col(k, 0, GATE_B), turn=2,
                    extra=[(ue[:, e, :], ar[:, e, :]) for e in range(EB)])


def l1_attention(k, norm):
    nc, d = k.nc, k.dram
    H = 2
    names = ("w_in", "z_ready", "z_biased", "z_abs_ready", "z_exp", "one_plus_ready", "z_ln", "gates_ready",
             "alpha_ready", "alpha_ln", "cla_ready", "h_copied", "qkv_ready", "qkv_biased", "k_squared", "k_sum_ready",
             "k_rn_ready", "k_normed", "la_tri_ready", "row_ready", "row_exp", "dt_ready", "dt_exp", "to_end_ready",
             "to_end_exp", "kw_ready", "qk_turned", "qt_copied", "qg_ready", "st_ready", "attn_ready", "y_ready",
             "delta_ready", "state_ready", "x_added", "const_ready")
    s = {n: k.sem("l1_" + n) for n in names}
    with ExitStack() as ctx:
        def sb(n, shape):
            return ctx.enter_context(nc.sbuf_tensor("l1_" + n, shape, F32))
        w = sb("w", [P, DB, 3 * D])
        wz = sb("wz", [P, DB, 4])
        bias = sb("bias", [P, 3 * D])
        bz = sb("bz", [P, 4])
        tri = sb("tri", [P, P])
        late = sb("late", [P, P])
        z = sb("z", [P, TT, 4])
        zt = sb("zt", [P, 2, TT, 4])
        la = sb("la", [P, TT, H])
        cla = sb("cla", [P, TT, H])
        hc = sb("hc", [P, DB, P])
        qkv = sb("qkv", [P, 3, H, P])
        sq = sb("sq", [P, H, P])
        rn = sb("rn", [P, H])
        la_tri = sb("la_tri", [P, H, P])
        dt = sb("dt", [P, H, P])
        ecr = sb("ecr", [P, H, P])
        te = sb("te", [P, H])
        kw = sb("kw", [P, H, P])
        qkt = sb("qkt", [P, 2, H, P])
        qg = sb("qg", [P, H, P])
        at = sb("at", [P, H, P])
        state = sb("state", [P, H, P])
        with nc.Block() as block:
            @block.sync
            def _(sp):
                sp.dma_start(wz[:], d["l1_wz"].rearrange("(b p) n -> p b n", p=P)).then_inc(s["w_in"], 16)
                sp.dma_start(bz[:], d["l1_bz"].to_broadcast([P, 4])).then_inc(s["w_in"], 16)
                sp.dma_start(w[:], d["l1_w"].rearrange("(b p) n -> p b n", p=P)).then_inc(s["w_in"], 16)
                sp.dma_start(bias[:], d["l1_b"].to_broadcast([P, 3 * D])).then_inc(s["w_in"], 16)

            @block.gpsimd
            def _(pool):
                step = k.pool_chain
                pool.memset(state[:], 0.0)
                pool.memset(tri[:], 1.0)
                step.link(pool, pool.memset(late[:], 0.0))
                pool.affine_select(out=tri[:], in_=tri[:], compare_op=ALU.is_ge, fill=0.0, base=0, pattern=[[1, P]],
                                   channel_multiplier=-1)
                pool.affine_select(out=late[:], in_=late[:], compare_op=ALU.is_ge, fill=NEG, base=0,
                                   pattern=[[1, P]], channel_multiplier=-1).then_inc(s["const_ready"], 1)
                norm.wait(pool)
                with pool.Fori(0, TT) as i:
                    pool.wait_ge(s["qkv_ready"], i)
                    pool.tensor_copy(hc[:], k.h[:, :, bass.ds(i * P, P)]).then_inc(s["h_copied"], 1)

            @block.tensor
            def _(pe):
                norm.on_tensor(pe)
                norm.wait(pe)
                pe.wait_ge(s["w_in"], 64)
                for t in range(TT):
                    for b in range(DB):
                        last = pe.matmul(k.bank[:, 7, t * 4:t * 4 + 4], k.h[:, b, tile(t)], wz[:, b, :],
                                         start=(b == 0), stop=(b == DB - 1))
                last.then_inc(s["z_ready"], 1)
                pe.wait_ge(s["const_ready"], 1)
                pe.wait_ge(s["alpha_ln"], 1)
                pe.matmul(k.bank[:, 7, 64:64 + TT * H], tri[:], la[:].rearrange("p t h -> p (t h)"), start=True,
                          stop=True).then_inc(s["cla_ready"], 1)
                with pe.Fori(0, TT) as i:
                    pe.wait_ge(s["h_copied"], i + 1)
                    pe.wait_ge(s["qkv_biased"], i)
                    for b in range(DB):
                        pe.matmul(k.bank[:, 0, :], hc[:, b, :], w[:, b, 0:2 * D], start=(b == 0), stop=(b == 1))
                    for b in range(DB):
                        last = pe.matmul(k.bank[:, 1, 0:D], hc[:, b, :], w[:, b, 2 * D:], start=(b == 0), stop=(b == 1))
                    last.then_inc(s["qkv_ready"], 1)
                    pe.wait_ge(s["la_tri_ready"], i + 1)
                    pe.matmul(k.bank[:, 2, 0:H * P], k.ones[:], la_tri[:].rearrange("p h q -> p (h q)"), start=True,
                              stop=True).then_inc(s["row_ready"], 1)
                    pe.wait_ge(s["k_normed"], i + 1)
                    for a in range(2):
                        for h in range(H):
                            last = pe.transpose(k.bank[:, 3, tile(2 * a + h)], qkv[:, a, h, :], k.ident[:])
                    last.then_inc(s["qk_turned"], 1)
                    pe.wait_ge(s["qt_copied"], i + 1)
                    for h in range(H):
                        last = pe.matmul(k.bank[:, 4, tile(h)], qkt[:, 1, h, :], qkt[:, 0, h, :], start=True, stop=True)
                    last.then_inc(s["st_ready"], 1)
                    pe.wait_ge(s["attn_ready"], i + 1)
                    pe.wait_ge(s["qg_ready"], i + 1)
                    pe.wait_ge(s["state_ready"], i)
                    for h in range(H):
                        pe.matmul(k.bank[:, 5, tile(h)], qkv[:, 2, h, :], at[:, h, :], start=True, stop=False)
                        last = pe.matmul(k.bank[:, 5, tile(h)], state[:, h, :], qg[:, h, :], start=False, stop=True)
                    last.then_inc(s["y_ready"], 1)
                    pe.wait_ge(s["kw_ready"], i + 1)
                    for h in range(H):
                        last = pe.matmul(k.bank[:, 6, tile(h)], kw[:, h, :], qkv[:, 2, h, :], start=True, stop=True)
                    last.then_inc(s["delta_ready"], 1)

            @block.scalar
            def _(act):
                norm.on_scalar(act)
                step = k.act_chain
                act.preload_act_table_set(EXP_LN)
                act.wait_ge(s["z_abs_ready"], 1)
                act.activation(zt[:, 0], zt[:, 0], ACT.Exp, scale=-1.0).then_inc(s["z_exp"], 1)
                act.wait_ge(s["one_plus_ready"], 1)
                act.activation(zt[:, 1, :, 0:H], zt[:, 0, :, 0:H], ACT.Ln).then_inc(s["z_ln"], 1)
                act.wait_ge(s["alpha_ready"], 1)
                act.activation(la[:], zt[:, 0, :, H:2 * H], ACT.Ln, bias=k.eps[:, 3:4]).then_inc(s["alpha_ln"], 1)
                act.wait_ge(s["gates_ready"], 1)
                with act.Fori(0, TT) as i:
                    step.enter(i, 2)
                    act.wait_ge(s["qkv_biased"], i + 1)
                    act.activation(sq[:], qkv[:, 1], ACT.Square).then_inc(s["k_squared"], 1)
                    act.wait_ge(s["row_ready"], i + 1)
                    act.activation(ecr[:].rearrange("p h q -> p (h q)"), k.bank[:, 2, 0:H * P], ACT.Exp
                                   ).then_inc(s["row_exp"], 1)
                    act.wait_ge(s["k_sum_ready"], i + 1)
                    step.link(act, act.activation(rn[:], rn[:], ACT.Ln, scale=65536.0))
                    act.activation(rn[:], rn[:], ACT.Exp, scale=-0.5).then_inc(s["k_rn_ready"], 1)
                    act.wait_ge(s["to_end_ready"], i + 1)
                    act.activation(te[:], te[:], ACT.Exp).then_inc(s["to_end_exp"], 1)
                    act.wait_ge(s["dt_ready"], i + 1)
                    act.activation(dt[:], dt[:], ACT.Exp).then_inc(s["dt_exp"], 1)
                    act.wait_ge(s["qk_turned"], i + 1)
                    step.link(act, act.activation(qkt[:].rearrange("p a h q -> p (a h q)"), k.bank[:, 3, :],
                                                  ACT.Identity))
                    act.sem_inc(s["qt_copied"], 1)
                step.leave(TT)

            @block.vector
            def _(dve):
                norm.on_vector(dve)
                step = k.dve_chain
                dve.wait_ge(s["w_in"], 64)
                dve.wait_ge(s["z_ready"], 1)
                step.link(dve, dve.tensor_tensor(z[:], k.bank[:, 7, 0:TT * 4].rearrange("p (t n) -> p t n", t=TT),
                                                 over(bz[:], TT), ALU.add))
                step.link(dve, dve.tensor_scalar(zt[:, 1], z[:], -1.0, None, ALU.mult))
                dve.tensor_tensor(zt[:, 0, :, 0:H], z[:, :, 0:H], zt[:, 1, :, 0:H], ALU.max)
                dve.tensor_copy(zt[:, 0, :, H:], z[:, :, H:]).then_inc(s["z_abs_ready"], 1)
                dve.wait_ge(s["z_exp"], 1)
                dve.tensor_scalar(zt[:, 0], zt[:, 0], 1.0, None, ALU.add).then_inc(s["one_plus_ready"], 1)
                dve.wait_ge(s["one_plus_ready"], 1)
                dve.reciprocal(zt[:, 0, :, H:], zt[:, 0, :, H:]).then_inc(s["alpha_ready"], 1)
                dve.wait_ge(s["z_ln"], 1)
                step.link(dve, dve.scalar_tensor_tensor(z[:, :, 0:H], z[:, :, 0:H], 0.0, zt[:, 1, :, 0:H], ALU.max,
                                                        ALU.add))
                dve.wait_ge(s["cla_ready"], 1)
                dve.tensor_copy(cla[:].rearrange("p t h -> p (t h)"), k.bank[:, 7, 64:64 + TT * H]
                                ).then_inc(s["gates_ready"], 1)
                dve.wait_ge(s["gates_ready"], 1)
                dve.wait_ge(s["const_ready"], 1)
                with dve.Fori(0, TT) as i:
                    step.enter(i, 4)
                    dve.wait_ge(s["qkv_ready"], i + 1)
                    dve.wait_ge(s["delta_ready"], i)
                    dve.tensor_tensor(qkv[:].rearrange("p a h q -> p (a h q)"),
                                      k.bank[:, 0:2, :].rearrange("p n q -> p (n q)")[:, 0:3 * D], bias[:], ALU.add
                                      ).then_inc(s["qkv_biased"], 1)
                    for h in range(H):
                        last = dve.tensor_scalar(la_tri[:, h, :], tri[:], la[:, bass.ds(i, 1), h], None, ALU.mult)
                    last.then_inc(s["la_tri_ready"], 1)
                    dve.wait_ge(s["k_squared"], i + 1)
                    step.link(dve, dve.tensor_reduce(rn[:], sq[:], AX.X, ALU.add))
                    dve.tensor_scalar(rn[:], rn[:], 1.0e-24, None, ALU.max).then_inc(s["k_sum_ready"], 1)
                    dve.wait_ge(s["row_exp"], i + 1)
                    row = k.bank[:, 2, 0:H * P].rearrange("p (h q) -> p h q", h=H)
                    dve.tensor_tensor(te[:], row[:, :, P - 1], cla[:, bass.ds(i, 1), :].rearrange("p t h -> p (t h)"),
                                      ALU.subtract).then_inc(s["to_end_ready"], 1)
                    for h in range(H):
                        last = dve.scalar_tensor_tensor(dt[:, h, :], row[:, h, :], cla[:, bass.ds(i, 1), h], late[:],
                                                        ALU.subtract, ALU.add)
                    last.then_inc(s["dt_ready"], 1)
                    dve.wait_ge(s["k_rn_ready"], i + 1)
                    for h in range(H):
                        last = dve.tensor_scalar(qkv[:, 1, h, :], qkv[:, 1, h, :], rn[:, h:h + 1], 256.0, ALU.mult,
                                                 ALU.mult)
                    last.then_inc(s["k_normed"], 1)
                    dve.wait_ge(s["to_end_exp"], i + 1)
                    step.link(dve, dve.tensor_tensor(te[:], te[:], z[:, bass.ds(i, 1), 0:H].rearrange(
                        "p t h -> p (t h)"), ALU.mult))
                    dve.wait_ge(s["k_normed"], i + 1)
                    for h in range(H):
                        last = dve.tensor_scalar(kw[:, h, :], qkv[:, 1, h, :], te[:, h:h + 1], None, ALU.mult)
                    last.then_inc(s["kw_ready"], 1)
                    dve.wait_ge(s["qt_copied"], i + 1)
                    dve.tensor_tensor(qg[:], qkt[:, 0], ecr[:], ALU.mult).then_inc(s["qg_ready"], 1)
                    dve.wait_ge(s["dt_exp"], i + 1)
                    dve.wait_ge(s["st_ready"], i + 1)
                    for h in range(H):
                        last = dve.scalar_tensor_tensor(at[:, h, :], k.bank[:, 4, tile(h)], z[:, bass.ds(i, 1), h],
                                                        dt[:, h, :], ALU.mult, ALU.mult)
                    last.then_inc(s["attn_ready"], 1)
                    dve.wait_ge(s["y_ready"], i + 1)
                    for h in range(H):
                        xs = k.x[:, h, bass.ds(i * P, P)]
                        last = dve.scalar_tensor_tensor(xs, k.bank[:, 5, tile(h)], k.mod[:, 1, GATE_A + h:GATE_A + h + 1],
                                                        xs, ALU.mult, ALU.add)
                    step.link(dve, last)
                    dve.wait_ge(s["delta_ready"], i + 1)
                    for h in range(H):
                        last = dve.scalar_tensor_tensor(state[:, h, :], state[:, h, :], ecr[:, h, P - 1:P],
                                                        k.bank[:, 6, tile(h)], ALU.mult, ALU.add)
                    step.link(dve, last)
                    dve.sem_inc(s["state_ready"], 1)
                step.leave(TT)


def l1_ffn(k, norm):
    nc, d = k.nc, k.dram
    E, TOP, SEL, THRESH = 64, 8, 4, 0.5
    names = ("w_in", "sim_in", "logits_ready", "shifted", "probs_exp", "weights_ready", "masks_ready", "wt_ready",
             "wt_copied", "counts_ready", "sim_ready", "map_ready", "eff_ready", "eff_copied", "stored")
    s = {n: k.sem("l1f_" + n) for n in names}
    rows = nc.dram_tensor("l1f_token_weights", (E, T), F32, kind="Internal").ap()
    with ExitStack() as ctx:
        def sb(n, shape, dt=F32):
            return ctx.enter_context(nc.sbuf_tensor("l1f_" + n, shape, dt))
        gw = sb("gw", [P, DB, E])
        sim = sb("sim", [E, E])
        iota = sb("iota", [E, E])
        p = sb("p", [P, TT, E])
        st = sb("st", [P, 2, TT])
        v8 = sb("v8", [P, TT, TOP])
        w = sb("w", [P, 2, TT, E])
        mask = sb("mask", [P, 2, TT, E])
        wt = sb("wt", [E, 2, T])
        cnt = sb("cnt", [E, 2])
        m8 = sb("m8", [E, TOP])
        i8 = sb("i8", [E, TOP], mybir.dt.uint32)
        bi = sb("bi", [E, 2])
        mp = sb("mp", [E, E])
        eff = sb("eff", [E, T])
        with nc.Block() as block:
            @block.sync
            def _(sp):
                sp.dma_start(gw[:], d["l1f_gw"].rearrange("(b p) n -> p b n", p=P)).then_inc(s["w_in"], 16)
                sp.dma_start(sim[:], d["l1f_sim"]).then_inc(s["sim_in"], 16)
                sp.wait_ge(s["eff_copied"], 2)
                sp.dma_start(rows, eff[:]).then_inc(s["stored"], 16)
                sp.wait_ge(s["stored"], 16)

            @block.gpsimd
            def _(pool):
                pool.iota(iota[:], pattern=[[1, E]], base=0, channel_multiplier=0,
                          allow_small_or_imprecise_dtypes=True)
                pool.wait_ge(s["sim_in"], 16)
                pool.affine_select(out=sim[:], in_=sim[:], compare_op=ALU.not_equal, fill=1.0, base=0,
                                   pattern=[[-1, E]], channel_multiplier=1).then_inc(s["sim_ready"], 1)

            @block.tensor
            def _(pe):
                norm.on_tensor(pe)
                norm.wait(pe)
                pe.wait_ge(s["w_in"], 16)
                for t in range(TT):
                    for b in range(DB):
                        last = pe.matmul(k.bank[:, 0, t * E:(t + 1) * E], k.h[:, b, tile(t)], gw[:, b, :],
                                         start=(b == 0), stop=(b == DB - 1))
                last.then_inc(s["logits_ready"], 1)
                pe.wait_ge(s["masks_ready"], 1)
                for a in range(2):
                    for t in range(TT):
                        pe.matmul(k.bank[0:E, 1, a:a + 1], mask[:, a, t, :], k.ones[:, 0:1], start=(t == 0),
                                  stop=(t == TT - 1))
                for t in range(TT):
                    last = pe.matmul(k.bank[0:E, 1, E:2 * E], k.ones[:, 0:E], mask[:, 0, t, :], start=(t == 0),
                                     stop=(t == TT - 1))
                last.then_inc(s["counts_ready"], 1)
                pe.wait_ge(s["weights_ready"], 1)
                for a in range(2):
                    for t in range(TT):
                        last = pe.transpose(k.bank[0:E, 2 + 2 * a + t // 4, (t % 4) * P:(t % 4 + 1) * P],
                                            w[:, a, t, :], k.ident[:])
                    last.then_inc(s["wt_ready"], 1)
                pe.wait_ge(s["wt_copied"], 2)
                pe.wait_ge(s["map_ready"], 1)
                for c in range(NCH):
                    pe.matmul(k.bank[0:E, 6 + c, :], k.ident[0:E, 0:E], wt[:, 0, chunk(c)], start=True, stop=False)
                    pe.matmul(k.bank[0:E, 6 + c, :], mp[:], wt[:, 1, chunk(c)], start=False, stop=True
                              ).then_inc(s["eff_ready"], 1)

            @block.scalar
            def _(act):
                norm.on_scalar(act)
                act.preload_act_table_set(EXP_LN)
                act.wait_ge(s["shifted"], 1)
                act.activation(p[:], p[:], ACT.Exp).then_inc(s["probs_exp"], 1)
                for a in range(2):
                    act.wait_ge(s["wt_ready"], a + 1)
                    act.activation(wt[:, a, :], k.bank[0:E, 2 + 2 * a:4 + 2 * a, :].rearrange("p n q -> p (n q)"),
                                   ACT.Identity).then_inc(s["wt_copied"], 1)
                for c in range(NCH):
                    act.wait_ge(s["eff_ready"], c + 1)
                    act.activation(eff[:, chunk(c)], k.bank[0:E, 6 + c, :], ACT.Identity).then_inc(s["eff_copied"], 1)

            @block.vector
            def _(dve):
                norm.on_vector(dve)
                step = k.dve_chain
                dve.wait_ge(s["logits_ready"], 1)
                logits = k.bank[:, 0, :].rearrange("p (t e) -> p t e", t=TT)
                step.link(dve, dve.tensor_reduce(st[:, 0, :], logits, AX.X, ALU.max))
                dve.tensor_tensor(p[:], logits, over(st[:, 0, :], E, 2), ALU.subtract).then_inc(s["shifted"], 1)
                dve.wait_ge(s["probs_exp"], 1)
                step.link(dve, dve.tensor_reduce(st[:, 0, :], p[:], AX.X, ALU.add))
                step.link(dve, dve.reciprocal(st[:, 1, :], st[:, 0, :]))
                step.link(dve, dve.tensor_tensor(p[:], p[:], over(st[:, 1, :], E, 2), ALU.mult))
                for t in range(TT):
                    last = dve.max(v8[:, t, :], p[:, t, :])
                step.link(dve, last)
                step.link(dve, dve.tensor_reduce(st[:, 0, :], v8[:], AX.X, ALU.add))
                step.link(dve, dve.tensor_scalar(st[:, 0, :], st[:, 0, :], 1.0e-12, None, ALU.max))
                step.link(dve, dve.reciprocal(st[:, 1, :], st[:, 0, :]))
                dve.tensor_tensor(mask[:, 0], p[:], over(v8[:, :, SEL - 1], E, 2), ALU.is_ge)
                step.link(dve, dve.tensor_tensor(mask[:, 1], p[:], over(v8[:, :, TOP - 1], E, 2), ALU.is_ge))
                step.link(dve, dve.tensor_tensor(mask[:, 1], mask[:, 1], mask[:, 0], ALU.subtract))
                dve.sem_inc(s["masks_ready"], 1)
                step.link(dve, dve.tensor_tensor(p[:], p[:], over(st[:, 1, :], E, 2), ALU.mult))
                for a in range(2):
                    last = dve.tensor_tensor(w[:, a], p[:], mask[:, a], ALU.mult)
                last.then_inc(s["weights_ready"], 1)
                dve.wait_ge(s["counts_ready"], 1)
                dve.wait_ge(s["sim_ready"], 1)
                step.link(dve, dve.tensor_scalar(mp[:], k.bank[0:E, 1, E:2 * E], 0.5, NEG, ALU.is_lt, ALU.mult))
                step.link(dve, dve.tensor_tensor(mp[:], mp[:], sim[:], ALU.add))
                step.link(dve, dve.max(m8[:], mp[:]))
                step.link(dve, dve.max_index(i8[:], m8[:], mp[:]))
                step.link(dve, dve.tensor_copy(bi[:, 0:1], i8[:, 0:1]))
                step.link(dve, dve.tensor_scalar(cnt[:, 0:1], k.bank[0:E, 1, 0:1], 0.5, None, ALU.is_lt))
                step.link(dve, dve.tensor_scalar(cnt[:, 1:2], k.bank[0:E, 1, 1:2], 0.5, None, ALU.is_ge))
                step.link(dve, dve.tensor_tensor(cnt[:, 0:1], cnt[:, 0:1], cnt[:, 1:2], ALU.mult))
                step.link(dve, dve.tensor_scalar(cnt[:, 1:2], m8[:, 0:1], THRESH, None, ALU.is_ge))
                step.link(dve, dve.tensor_tensor(cnt[:, 0:1], cnt[:, 0:1], cnt[:, 1:2], ALU.mult))
                step.link(dve, dve.scalar_tensor_tensor(mp[:], iota[:], bi[:, 0:1], k.ident[0:E, 0:E], ALU.is_equal,
                                                        ALU.subtract))
                dve.scalar_tensor_tensor(mp[:], mp[:], cnt[:, 0:1], k.ident[0:E, 0:E], ALU.mult, ALU.add
                                         ).then_inc(s["map_ready"], 1)
    gated_units(k, "l1m", E * 96 // P, d["l1f_win"], d["l1f_wout"], gate_col(k, 1, GATE_B), rows=rows, turn=6,
                rows_per_turn=8, owner=owners(96))


def head_norm(k, buf, group, eps, center, scale=None, shift=None):
    nc = k.nc
    tiles = [(b, c) for b in range(DB) for c in range(NCH)]
    N = len(tiles)
    mean_ready, centered, squared, var_ready, root_ready, normed, out_ready = (
        k.shared("hn_" + n) for n in ("mean_ready", "centered", "squared", "var_ready", "root_ready", "normed", "out"))
    call = k.calls.setdefault("head_norms", 0)
    k.calls["head_norms"] += 1
    at = N * call
    cen = N * k.calls.setdefault("head_norms_centered", 0)
    k.calls["head_norms_centered"] += center
    with ExitStack() as ctx:
        sq = ctx.enter_context(nc.sbuf_tensor(f"hn_square{call}", [P, DB, T], F32))
        rs = ctx.enter_context(nc.sbuf_tensor(f"hn_rstd{call}", [P, DB, T], F32))
        with nc.Block() as block:
            @block.tensor
            def _(pe):
                if center:
                    for n, (b, c) in enumerate(tiles):
                        pe.matmul(k.bank[:, n, :], group[:], buf[:, b, chunk(c)], start=True, stop=True
                                  ).then_inc(mean_ready, 1)
                for n, (b, c) in enumerate(tiles):
                    pe.wait_ge(squared, at + n + 1)
                    pe.matmul(k.bank[:, 4 + n, :], group[:], sq[:, b, chunk(c)], start=True, stop=True
                              ).then_inc(var_ready, 1)

            @block.vector
            def _(dve):
                if center:
                    for n, (b, c) in enumerate(tiles):
                        dve.wait_ge(mean_ready, cen + n + 1)
                        dve.tensor_tensor(buf[:, b, chunk(c)], buf[:, b, chunk(c)], k.bank[:, n, :], ALU.subtract
                                          ).then_inc(centered, 1)
                for n, (b, c) in enumerate(tiles):
                    dve.wait_ge(root_ready, at + n + 1)
                    xs = buf[:, b, chunk(c)]
                    dve.tensor_tensor(xs, xs, rs[:, b, chunk(c)], ALU.mult).then_inc(normed, 1)
                if center:
                    for n, (b, c) in enumerate(tiles):
                        dve.wait_ge(normed, at + n + 1)
                        xs = buf[:, b, chunk(c)]
                        last = dve.tensor_scalar(xs, xs, scale[:, b:b + 1], shift[:, b:b + 1], ALU.mult, ALU.add)
                    last.then_inc(out_ready, 1)

            @block.scalar
            def _(act):
                act.preload_act_table_set(EXP_LN)
                for n, (b, c) in enumerate(tiles):
                    if center:
                        act.wait_ge(centered, cen + n + 1)
                    act.activation(sq[:, b, chunk(c)], buf[:, b, chunk(c)], ACT.Square).then_inc(squared, 1)
                for n, (b, c) in enumerate(tiles):
                    act.wait_ge(var_ready, at + n + 1)
                    r = rs[:, b, chunk(c)]
                    k.act_chain.link(act, act.activation(r, k.bank[:, 4 + n, :], ACT.Ln, bias=k.eps[:, eps:eps + 1]))
                    act.activation(r, r, ACT.Exp, scale=-0.5).then_inc(root_ready, 1)


def l2_attention(k, norm):
    nc, d = k.nc, k.dram
    HD, TAPS, PROJ = 16, 4, 6
    Q, K, V, IG, G, OG = range(PROJ)
    names = ("cols_in", "w_in", "wo_in", "pad_ready", "sum_w", "mean_w", "conv_ready", "silu_ready", "proj_ready",
             "proj_copied", "u_ready", "scanned", "mixed", "gated", "y_ready", "res_ready", "x_added")
    s = {n: k.sem("l2_" + n) for n in names}
    with ExitStack() as outer:
        h2 = outer.enter_context(nc.sbuf_tensor("l2_h2", [P, DB, T], F32))
        COLS = ["ln1w", "ln1b", "ln2w", "ln2b", "vnw", "vnb", "mnw", "mnb", "gnw", "gnb", "conv_b", "tap0", "tap1",
                "tap2", "tap3", "big", "bg", "bog"]
        cols = outer.enter_context(nc.sbuf_tensor("l2_cols", [P, len(COLS), DB], F32))

        def col(name):
            return cols[:, COLS.index(name), :]

        with ExitStack() as ctx:
            def sb(n, shape):
                return ctx.enter_context(nc.sbuf_tensor("l2_" + n, shape, F32))
            w = sb("w", [P, DB, PROJ * D])
            wo = sb("wo", [P, DB, D])
            hp = sb("hp", [P, DB, TAPS - 1 + T])
            xc = sb("xc", [P, DB, T])
            pr = sb("pr", [P, PROJ, DB, T])
            hsum = sb("hsum", [P, P])
            hmean = sb("hmean", [P, P])
            with nc.Block() as block:
                @block.sync
                def _(sp):
                    sp.dma_start(cols[:], d["l2_cols"]).then_inc(s["cols_in"], 16)
                    sp.dma_start(w[:], d["l2_w"].rearrange("(b p) n -> p b n", p=P)).then_inc(s["w_in"], 16)
                    sp.dma_start(wo[:], d["l2_wo"].rearrange("(b p) n -> p b n", p=P)).then_inc(s["wo_in"], 16)
                    sp.wait_ge(s["cols_in"], 16)

                block.tensor(norm.on_tensor)
                block.vector(norm.on_vector)
                block.scalar(norm.on_scalar)

                @block.gpsimd
                def _(pool):
                    step = k.pool_chain
                    pool.memset(hp[:, :, 0:TAPS - 1], 0.0).then_inc(s["pad_ready"], 1)
                    for m, v in ((hsum, 1.0), (hmean, 1.0 / HD)):
                        groups = m[:].rearrange("p (g e) -> p g e", e=HD)
                        step.link(pool, pool.memset(m[:], v))
                        step.link(pool, pool.affine_select(out=groups, in_=groups, compare_op=ALU.is_ge, fill=0.0,
                                                           base=0, pattern=[[-HD, P // HD], [0, HD]],
                                                           channel_multiplier=1))
                        step.link(pool, pool.affine_select(out=groups, in_=groups, compare_op=ALU.is_ge, fill=0.0,
                                                           base=HD - 1, pattern=[[HD, P // HD], [0, HD]],
                                                           channel_multiplier=-1))
            layernorm(k, k.h, hp[:, :, TAPS - 1:], col("ln1w"), col("ln1b"))
            with nc.Block() as block:
                @block.tensor
                def _(pe):
                    pe.wait_ge(s["w_in"], 16)
                    for n in range(PROJ * 4):
                        j, m, c = n // 4, n // 2 % 2, n % 2
                        if n == IG * 4:
                            pe.wait_ge(s["silu_ready"], DB)
                        if n >= 8:
                            pe.wait_ge(s["proj_copied"], n - 7)
                        for b in range(DB):
                            src = (hp[:, b, TAPS - 1 + c * CH:TAPS - 1 + (c + 1) * CH] if j < IG
                                   else xc[:, b, chunk(c)])
                            last = pe.matmul(k.bank[:, n % 8, :], w[:, b, j * D + m * P:j * D + (m + 1) * P], src,
                                             start=(b == 0), stop=(b == DB - 1))
                        last.then_inc(s["proj_ready"], 1)

                @block.vector
                def _(dve):
                    step = k.dve_chain
                    for b in range(DB):
                        step.link(dve, dve.tensor_scalar(xc[:, b, :], hp[:, b, TAPS - 1:TAPS - 1 + T],
                                                         col("tap3")[:, b:b + 1], col("conv_b")[:, b:b + 1],
                                                         ALU.mult, ALU.add))
                        for j in range(TAPS - 1):
                            step.link(dve, dve.scalar_tensor_tensor(xc[:, b, :], hp[:, b, j:j + T],
                                                                    col(f"tap{j}")[:, b:b + 1], xc[:, b, :],
                                                                    ALU.mult, ALU.add))
                        dve.sem_inc(s["conv_ready"], 1)

                @block.scalar
                def _(act):
                    act.preload_act_table(ACT.Silu)
                    for b in range(DB):
                        act.wait_ge(s["conv_ready"], b + 1)
                        act.activation(xc[:, b, :], xc[:, b, :], ACT.Silu).then_inc(s["silu_ready"], 1)
                    for n in range(PROJ * 4):
                        j, m, c = n // 4, n // 2 % 2, n % 2
                        act.wait_ge(s["proj_ready"], n + 1)
                        if j < IG:
                            act.activation(pr[:, j, m, chunk(c)], k.bank[:, n % 8, :], ACT.Identity
                                           ).then_inc(s["proj_copied"], 1)
                        else:
                            bias = col(("big", "bg", "bog")[j - IG])[:, m:m + 1]
                            act.activation(pr[:, j, m, chunk(c)], k.bank[:, n % 8, :], ACT.Sigmoid, bias=bias
                                           ).then_inc(s["proj_copied"], 1)
            head_norm(k, pr[:, Q], hsum, 1, False)
            head_norm(k, pr[:, K], hsum, 1, False)
            head_norm(k, pr[:, V], hmean, 0, True, col("vnw"), col("vnb"))
            with nc.Block() as block:
                @block.vector
                def _(dve):
                    step = k.dve_chain
                    step.link(dve, dve.tensor_tensor(pr[:, K], pr[:, K], pr[:, IG], ALU.mult))
                    step.link(dve, dve.tensor_tensor(pr[:, K], pr[:, K], pr[:, V], ALU.mult))
                    for b in range(DB):
                        step.link(dve, dve.tensor_tensor_scan(pr[:, V, b, :], pr[:, G, b, :], pr[:, K, b, :], 0.0,
                                                              ALU.mult, ALU.add))
            head_norm(k, pr[:, V], hmean, 0, True, col("mnw"), col("mnb"))
            with nc.Block() as block:
                @block.vector
                def _(dve):
                    k.dve_chain.link(dve, dve.tensor_tensor(pr[:, V], pr[:, V], pr[:, Q], ALU.mult))
            head_norm(k, pr[:, V], hmean, 0, True, col("gnw"), col("gnb"))
            with nc.Block() as block:
                @block.vector
                def _(dve):
                    dve.tensor_tensor(pr[:, V], pr[:, V], pr[:, OG], ALU.mult).then_inc(s["gated"], 1)
                    for n in range(4):
                        m, c = n // 2, n % 2
                        dve.wait_ge(s["y_ready"], n + 1)
                        r, x = k.h[:, m, chunk(c)], k.x[:, m, chunk(c)]
                        k.dve_chain.link(dve, dve.tensor_tensor(r, r, k.bank[:, n, :], ALU.add))
                        last = dve.scalar_tensor_tensor(x, r, gate_col(k, 2, GATE_A)[:, m:m + 1], x, ALU.mult, ALU.add)
                    last.then_inc(s["x_added"], 1)

                @block.tensor
                def _(pe):
                    pe.wait_ge(s["wo_in"], 16)
                    pe.wait_ge(s["gated"], 1)
                    for n in range(4):
                        m, c = n // 2, n % 2
                        for b in range(DB):
                            last = pe.matmul(k.bank[:, n, :], wo[:, b, tile(m)], pr[:, V, b, chunk(c)],
                                             start=(b == 0), stop=(b == DB - 1))
                        last.then_inc(s["y_ready"], 1)
        layernorm(k, k.h, h2, col("ln2w"), col("ln2b"))
        gated_units(k, "l2m", 8, d["l2_win"], d["l2_wout"], gate_col(k, 2, GATE_A), src=h2, turn=2)


def l2_ffn(k, norm):
    nc, d = k.nc, k.dram
    E, GROUPS, F, UNITS = 8, 4, 176, 14
    names = ("w_in", "logits_ready", "shifted", "probs_exp", "weights_ready", "wt_ready", "wt_copied", "stored")
    s = {n: k.sem("l2f_" + n) for n in names}
    rows = nc.dram_tensor("l2f_token_weights", (E + 1, T), F32, kind="Internal").ap()
    with ExitStack() as ctx:
        def sb(n, shape):
            return ctx.enter_context(nc.sbuf_tensor("l2f_" + n, shape, F32))
        gw = sb("gw", [P, DB, E])
        p = sb("p", [P, TT, E])
        g = sb("g", [P, 2, TT, GROUPS])
        m = sb("m", [P, 2, TT, E])
        st = sb("st", [P, 2, TT])
        w = sb("w", [P, TT, E + 1])
        wt = sb("wt", [E + 1, T])
        with nc.Block() as block:
            @block.sync
            def _(sp):
                sp.dma_start(gw[:], d["l2f_gw"].rearrange("(b p) n -> p b n", p=P)).then_inc(s["w_in"], 16)
                sp.wait_ge(s["wt_copied"], 1)
                sp.dma_start(rows, wt[:]).then_inc(s["stored"], 16)
                sp.wait_ge(s["stored"], 16)

            @block.tensor
            def _(pe):
                norm.on_tensor(pe)
                norm.wait(pe)
                pe.wait_ge(s["w_in"], 16)
                for t in range(TT):
                    for b in range(DB):
                        last = pe.matmul(k.bank[:, 0, t * E:(t + 1) * E], k.h[:, b, tile(t)], gw[:, b, :],
                                         start=(b == 0), stop=(b == DB - 1))
                last.then_inc(s["logits_ready"], 1)
                pe.wait_ge(s["weights_ready"], 1)
                for t in range(TT):
                    last = pe.transpose(k.bank[0:E + 1, 1 + t // 4, (t % 4) * P:(t % 4 + 1) * P], w[:, t, :],
                                        k.ident[:])
                last.then_inc(s["wt_ready"], 1)

            @block.scalar
            def _(act):
                norm.on_scalar(act)
                act.preload_act_table_set(EXP_LN)
                act.wait_ge(s["shifted"], 1)
                act.activation(p[:], p[:], ACT.Exp).then_inc(s["probs_exp"], 1)
                act.wait_ge(s["wt_ready"], 1)
                act.activation(wt[:], k.bank[0:E + 1, 1:3, :].rearrange("p n q -> p (n q)"), ACT.Identity
                               ).then_inc(s["wt_copied"], 1)

            @block.vector
            def _(dve):
                norm.on_vector(dve)
                step = k.dve_chain
                dve.memset(w[:, :, E:], 1.0)
                dve.wait_ge(s["logits_ready"], 1)
                logits = k.bank[:, 0, 0:TT * E].rearrange("p (t e) -> p t e", t=TT)
                step.link(dve, dve.tensor_reduce(st[:, 0, :], logits, AX.X, ALU.max))
                dve.tensor_tensor(p[:], logits, over(st[:, 0, :], E, 2), ALU.subtract).then_inc(s["shifted"], 1)
                dve.wait_ge(s["probs_exp"], 1)
                step.link(dve, dve.tensor_reduce(st[:, 0, :], p[:], AX.X, ALU.add))
                step.link(dve, dve.reciprocal(st[:, 1, :], st[:, 0, :]))
                step.link(dve, dve.tensor_tensor(p[:], p[:], over(st[:, 1, :], E, 2), ALU.mult))

                def second_best(of, n, tmp):
                    step.link(dve, dve.tensor_reduce(st[:, 0, :], of, AX.X, ALU.max))
                    step.link(dve, dve.tensor_tensor(tmp, of, over(st[:, 0, :], n, 2), ALU.is_ge))
                    step.link(dve, dve.scalar_tensor_tensor(tmp, tmp, -4.0, of, ALU.mult, ALU.add))
                    step.link(dve, dve.tensor_reduce(st[:, 1, :], tmp, AX.X, ALU.max))

                step.link(dve, dve.tensor_reduce(g[:, 0], p[:].rearrange("p t (g e) -> p t g e", g=GROUPS), AX.X,
                                                 ALU.max))
                second_best(g[:, 0], GROUPS, g[:, 1])
                step.link(dve, dve.tensor_tensor(g[:, 1], g[:, 0], over(st[:, 1, :], GROUPS, 2), ALU.is_ge))
                by_group = m[:, 0].rearrange("p t (g e) -> p t g e", g=GROUPS)
                step.link(dve, dve.tensor_tensor(by_group, p[:].rearrange("p t (g e) -> p t g e", g=GROUPS),
                                                 over(g[:, 1], E // GROUPS, 3), ALU.mult))
                second_best(m[:, 0], E, m[:, 1])
                step.link(dve, dve.tensor_tensor(m[:, 1], m[:, 0], over(st[:, 1, :], E, 2), ALU.is_ge))
                dve.tensor_tensor(w[:, :, 0:E], m[:, 0], m[:, 1], ALU.mult).then_inc(s["weights_ready"], 1)
    routed, shared = owners(F), [(0, P // 2, E), (P // 2, P, E)]
    gated_units(k, "l2e", UNITS, d["l2f_win"], d["l2f_wout"], gate_col(k, 2, GATE_B), rows=rows, turn=UNITS,
                owner=lambda j: routed(j) if j * P < E * F else shared)


def l3_attention(k, norm):
    nc, d = k.nc, k.dram
    H, HP, S, PAD = 16, 2, 64, 8
    PAIRS, NS, LAG = H // HP, T // S, 4
    INV_SCALE = float(P) ** -0.5
    EVEN, ODD = slice(0, S), slice(S, P)
    A_BANKS = (0, 1, 4, 7)
    GROUPS = [(a, g) for a in range(HP) for g in range(4)]
    names = ("betas_in", "betas_ready", "wo_in", "w_in", "const_ready", "zeroed", "v_ready", "v_even_copied",
             "v_odd_copied", "qk_ready", "qk_copied", "neg_ready", "neg_exp", "sigma_ready", "z_ready", "dk_ready", "dk_read",
             "kt_ready", "kt_copied", "xk_ready", "a_ready", "a_copied", "scores_ready", "scores_read", "shifted",
             "probs_exp", "probs_ready", "pt_ready", "pt_copied", "qz_ready", "dq_ready", "dq_ln", "rd_ready",
             "q_normed", "mem_ready", "mem_copied", "read_ready", "dot_ready", "dot_scaled", "att_ready", "y_ready",
             "x_added", "h_hi_ready", "h_split", "w_hi_ready", "w_split", "v_whole")
    s = {n: k.sem("l3_" + n) for n in names}
    with ExitStack() as ctx:
        def sb(n, shape, dt=F32):
            return ctx.enter_context(nc.sbuf_tensor("l3_" + n, shape, dt))
        beta = sb("beta", [P, H])
        bt = sb("bt", [P, 2, HP])
        mask = sb("mask", [P, P])
        w = sb("w", [P, DB, 3 * HP * P])
        w_hi, w_lo = (sb("w_" + n, [P, DB, 3 * HP * P], F32R) for n in ("hi", "lo"))
        h_hi, h_lo = (sb("h_" + n, [P, DB, T], F32R) for n in ("hi", "lo"))
        wo = sb("wo", [P, H, D])
        v = sb("v", [P, TT, HP, 2, P])
        vw = sb("vw", [P, TT, HP, P])
        xk = sb("xk", [P, HP, TT, 2, P])
        kt = sb("kt", [P, HP, TT, P])
        qk = sb("qk", [P, HP, 2, T])
        sg = sb("sg", [P, HP, 2, T])
        neg = sb("neg", [P, 2, CH])
        z = sb("z", [P, 2, HP, PAD + NS])
        dk = sb("dk", [P, HP, TT])
        qz = sb("qz", [P, HP, T])
        rd = norm.rs
        sc = norm.sq[:].rearrange("p a (t q) -> p a t q", q=P)
        st = sb("st", [P, HP, 2, TT])
        pt = qz[:].rearrange("p a (t q) -> p a t q", q=P)
        a_neg = qk[:].rearrange("p a c (n q) -> p a (c n) q", q=P)
        mem = sb("mem", [P, HP, 8, P])
        att = k.h
        with nc.Block() as block:
            @block.sync
            def _(sp):
                sp.dma_start(beta[:], d["l3_betas"]).then_inc(s["betas_in"], 16)

                def load(i):
                    sp.dma_start(w[:], d["l3_w"][bass.ds(i, 1)].rearrange("u (b p) n -> p (u b) n", p=P)
                                 ).then_inc(s["w_in"], 16)

                load(0)
                sp.dma_start(wo[:], d["l3_wo"].rearrange("(j p) n -> p j n", p=P)).then_inc(s["wo_in"], 16)
                with sp.Fori(1, PAIRS) as i:
                    sp.wait_ge(s["qk_ready"], i * 8)
                    load(i)

            @block.gpsimd
            def _(pool):
                step = k.pool_chain
                step.link(pool, pool.memset(mask[:], 0.0))
                step.link(pool, pool.affine_select(out=mask[:], in_=mask[:], compare_op=ALU.is_ge, fill=NEG, base=0,
                                                   pattern=[[-1, P]], channel_multiplier=1))
                step.link(pool, pool.memset(mask[S:P, 0:S], NEG))
                step.link(pool, pool.memset(z[:], 0.0))
                step.link(pool, pool.memset(z[:, 0, :, PAD:PAD + 1], 1.0 / P))
                pool.sem_inc(s["const_ready"], 1)
                for a in range(HP):
                    for half in (v[ODD, :, a, 0, :], v[EVEN, :, a, 1, :], xk[ODD, a, :, 0, :], xk[EVEN, a, :, 1, :]):
                        step.link(pool, pool.memset(half, 0.0))
                pool.sem_inc(s["zeroed"], 1)

                def low_parts(i):
                    pool.wait_ge(s["w_hi_ready"], i + 1)
                    pool.tensor_tensor(w_lo[:], w[:], w_hi[:].bitcast(F32), ALU.subtract).then_inc(s["w_split"], 1)

                def pair(i):
                    pool.wait_ge(s["v_even_copied"], i + 1)
                    pool.wait_ge(s["v_odd_copied"], i + 1)
                    pool.tensor_tensor(vw[:], v[:, :, :, 0, :], v[:, :, :, 1, :], ALU.add).then_inc(s["v_whole"], 1)
                    for a in range(HP):
                        pool.wait_ge(s["sigma_ready"], i * 8 + (4 * a + 4))
                        pool.wait_ge(s["z_ready"], i * HP + (a + 1))
                        pool.tensor_tensor(qz[:, a].rearrange("p (g q) -> p g q", q=S),
                                           sg[:, a, 1].rearrange("p (g q) -> p g q", q=S),
                                           over(z[:, 0, a, PAD:], S, 2), ALU.mult).then_inc(s["qz_ready"], 1)

                low_parts(0)
                with pool.Fori(0, PAIRS - 1) as i:
                    pair(i)
                    low_parts(i + 1)
                pair(PAIRS - 1)

            @block.tensor
            def _(pe):
                norm.on_tensor(pe)
                norm.wait(pe)
                def project_out(turn):
                    pe.wait_ge(s["att_ready"], turn * HP)
                    for m in range(DB):
                        for j in range(H):
                            last = pe.matmul(k.bank[:, 7, m * P:(m + 1) * P], wo[:, j, tile(m)], att[:, :, j::H],
                                             start=(j == 0), stop=(j == H - 1))
                    last.then_inc(s["y_ready"], 1)

                def pair(i, first):
                    def keys_by_token(a):
                        pe.wait_ge(s["sigma_ready"], i * 8 + (4 * a + 2))
                        if a:
                            pe.wait_ge(s["kt_copied"], i * HP + 1)
                        for t in range(TT):
                            last = pe.transpose(k.bank[:, t // 4, (t % 4) * P:(t % 4 + 1) * P],
                                                sg[:, a, 0, tile(t)], k.ident[:])
                        last.then_inc(s["kt_ready"], 1)

                    def key_divisors(a):
                        pe.wait_ge(s["z_ready"], i * HP + (a + 1))
                        if a:
                            pe.wait_ge(s["qk_copied"], i * 8 + 5)
                        for t in range(TT):
                            last = pe.matmul(k.bank[:, 2 + 2 * a, 2 * t:2 * t + 2], sg[:, a, 0, tile(t)],
                                             z[:, 0, a, PAD + 2 * t:PAD + 2 * t + 2], start=True, stop=True)
                        last.then_inc(s["dk_ready"], 1)

                    def scores(a):
                        pe.wait_ge(s["qk_copied"], i * 8 + (4 + 4 * a))
                        for t in range(TT):
                            last = pe.matmul(k.bank[:, 2 + 3 * a + t // 4, (t % 4) * P:(t % 4 + 1) * P],
                                             qk[:, a, 1, tile(t)], qk[:, a, 0, tile(t)], start=True, stop=True)
                        last.then_inc(s["scores_ready"], 1)

                    def products_a(a):
                        pe.wait_ge(s["xk_ready"], i * HP + (a + 1))
                        for g in range(4):
                            if a:
                                pe.wait_ge(s["a_copied"], i * 8 + (g + 1))
                            elif g == 0:
                                pe.wait_ge(s["kt_copied"], i * HP + 2)
                            elif g == 2:
                                pe.wait_ge(s["dk_read"], i * HP + 2)
                            elif g == 3 and not first:
                                pe.wait_ge(s["x_added"], i)
                            for h in range(2):
                                last = pe.matmul(k.bank[:, A_BANKS[g], h * 256:(h + 1) * 256], kt[:, a, 2 * g + h, :],
                                                 xk[:, a, 2 * g + h].rearrange("p h q -> p (h q)"), start=True,
                                                 stop=True)
                            last.then_inc(s["a_ready"], 1)

                    def query_divisors(a):
                        pe.wait_ge(s["qz_ready"], i * HP + (a + 1))
                        if a:
                            pe.wait_ge(s["dq_ln"], i * HP + 1)
                        else:
                            pe.wait_ge(s["scores_read"], i * HP + 2)
                        for c in range(NCH):
                            last = pe.matmul(k.bank[:, 5 + c, :], k.ones[:], qz[:, a, chunk(c)], start=True,
                                             stop=True)
                        last.then_inc(s["dq_ready"], 1)

                    def read(n, a):
                        if n == 0:
                            pe.wait_ge(s["q_normed"], i * HP + (a + 1))
                            pe.wait_ge(s["a_copied"], i * 8 + 8)
                        bank = k.bank[:, A_BANKS[2 * a + n // 8], (n % 8) * S:(n % 8 + 1) * S]
                        lhs_t = mem[:, a, n % 8, :] if n else k.zeros[:, 0:P]
                        pe.matmul(bank, lhs_t, sg[:, a, 1, n * S:(n + 1) * S], start=True, stop=True
                                  ).then_inc(s["read_ready"], 1)

                    def memory_step(n, a):
                        t, odd = n // 2, n % 2
                        if n:
                            pe.wait_ge(s["mem_copied"], i * (HP * (NS - 1)) + (HP * (n - 1) + a + 1))
                        last = pe.matmul(k.bank[:, 2 + a, 0:P], kt[:, a, t, :], v[:, t, a, odd, :],
                                         start=(n == 0), stop=False, skip_group_check=True)
                        if n:
                            last = pe.matmul(k.bank[:, 2 + a, 0:P], a_neg[:, a, n, :], mem[:, a, n % 8, :],
                                             start=False, stop=False, skip_group_check=True)
                        last.then_inc(s["mem_ready"], 1)

                    def turn_probs(a):
                        pe.wait_ge(s["probs_ready"], i * HP + (a + 1))
                        for t in range(TT):
                            last = pe.transpose(k.bank[:, 5 - 3 * a + t // 4, (t % 4) * P:(t % 4 + 1) * P],
                                                sc[:, a, t, :], k.ident[:])
                        last.then_inc(s["pt_ready"], 1)

                    def local_attention(a):
                        pe.wait_ge(s["pt_copied"], i * HP + (a + 1))
                        for t in range(TT):
                            last = pe.matmul(k.bank[:, 5 - 3 * a + t // 4, (t % 4) * P:(t % 4 + 1) * P],
                                             vw[:, t, a, :], pt[:, a, t, :], start=True, stop=True)
                        last.then_inc(s["dot_ready"], 1)

                    pe.wait_ge(s["w_split"], i + 1)
                    for t in range(TT):
                        if not first and t == 0:
                            pe.wait_ge(s["att_ready"], i * HP - 1)
                        if not first and t == 4:
                            pe.wait_ge(s["dot_scaled"], i * HP)
                        for n, (b, hq, wq) in enumerate(parts):
                            last = pe.matmul(k.bank[:, t // 2, (t % 2) * 256:(t % 2 + 1) * 256], hq[:, b, tile(t)],
                                             wq[:, b, 4 * P:6 * P], start=(n == 0), stop=(n == len(parts) - 1))
                    last.then_inc(s["v_ready"], 1)
                    if not first:
                        pe.wait_ge(s["att_ready"], i * HP)
                    for a in range(HP):
                        for n in range(4):
                            if a:
                                pe.wait_ge(s["qk_copied"], i * 8 + (n + 1))
                            for q, (b, hq, wq) in enumerate(parts):
                                last = pe.matmul(k.bank[:, 4 + n, :], wq[:, b, tile(2 * a + 1 - n // 2)],
                                                 hq[:, b, chunk(n % 2)], start=(q == 0), stop=(q == len(parts) - 1))
                            last.then_inc(s["qk_ready"], 1)
                            if (a, n) == (1, 0):
                                pe.wait_ge(s["v_even_copied"], i + 1)
                                pe.wait_ge(s["v_odd_copied"], i + 1)
                                keys_by_token(0)
                            if (a, n) == (1, 1):
                                key_divisors(0)
                    pe.wait_ge(s["dk_read"], i * HP + 1)
                    scores(0)
                    if not first:
                        pe.wait_ge(s["qk_copied"], i * 8 + 8)
                        project_out(i)
                    keys_by_token(1)
                    key_divisors(1)
                    scores(1)
                    products_a(0)
                    query_divisors(0)
                    products_a(1)
                    pe.wait_ge(s["scores_read"], i * HP + 1)
                    for a in range(HP):
                        memory_step(0, a)
                    query_divisors(1)
                    for n in range(1, NS - 1):
                        for a in range(HP):
                            memory_step(n, a)
                            if n >= LAG:
                                read(n - LAG, a)
                        if n == NS - 4:
                            pe.wait_ge(s["dq_ln"], i * HP + 2)
                            turn_probs(0)
                    pe.wait_ge(s["v_whole"], i + 1)
                    local_attention(0)
                    pe.wait_ge(s["mem_copied"], i * (HP * (NS - 1)) + HP * (NS - 1))
                    for a in range(HP):
                        for n in range(NS - 1 - LAG, NS):
                            read(n, a)
                        if a == 0:
                            turn_probs(1)
                    local_attention(1)

                parts = [(b, hq, wq) for b in range(DB) for hq, wq in ((h_hi, w_hi), (h_hi, w_lo), (h_lo, w_hi))]
                pe.wait_ge(s["zeroed"], 1)
                pe.wait_ge(s["h_split"], 1)
                pair(0, True)
                pe.wait_ge(s["wo_in"], 16)
                with pe.Fori(1, PAIRS) as i:
                    pair(i, False)
                project_out(PAIRS)

            @block.scalar
            def _(act):
                norm.on_scalar(act)
                act.preload_act_table(ACT.Sigmoid)
                act.wait_ge(s["betas_in"], 16)
                act.activation(beta[:], beta[:], ACT.Sigmoid).then_inc(s["betas_ready"], 1)
                act.preload_act_table_set(EXP_LN)
                act.wait_ge(s["zeroed"], 1)
                norm.wait(act)
                act.activation(h_hi[:], k.h[:], ACT.Identity).then_inc(s["h_hi_ready"], 1)

                def high_parts(i):
                    act.wait_ge(s["w_in"], i * 16 + 16)
                    act.activation(w_hi[:], w[:], ACT.Identity).then_inc(s["w_hi_ready"], 1)

                def pair(i, final):
                    def two_banks(n):
                        return k.bank[:, n:n + 2, :].rearrange("p n q -> p (n q)")

                    def keys_copy(a):
                        act.wait_ge(s["kt_ready"], i * HP + (a + 1))
                        act.activation(kt[:, a].rearrange("p t q -> p (t q)"), two_banks(0), ACT.Identity
                                       ).then_inc(s["kt_copied"], 1)

                    def mem_copy(n, a):
                        act.wait_ge(s["mem_ready"], i * (HP * (NS - 1)) + (HP * n + a + 1))
                        if n >= 7:
                            act.wait_ge(s["read_ready"], i * (HP * NS) + (HP * (n + 1 - 8) + a + 1))
                        act.activation(mem[:, a, (n + 1) % 8, :], k.bank[:, 2 + a, 0:P], ACT.Identity
                                       ).then_inc(s["mem_copied"], 1)

                    def exponential(a):
                        act.wait_ge(s["shifted"], i * HP + (a + 1))
                        act.activation(sc[:, a], sc[:, a], ACT.Exp).then_inc(s["probs_exp"], 1)

                    act.wait_ge(s["v_ready"], i + 1)
                    act.activation(v[EVEN, :, :, 0, :], k.bank[EVEN, 0:4, :].rearrange(
                        "p n (t a q) -> p (n t) a q", t=2, a=HP), ACT.Identity).then_inc(s["v_even_copied"], 1)
                    for j in range(8):
                        a, n = j // 4, j % 4
                        act.wait_ge(s["qk_ready"], i * 8 + (j + 1))
                        if j >= 2:
                            act.wait_ge(s["sigma_ready"], i * 8 + (j - 1))
                        act.activation(neg[:, n % 2, :], k.bank[:, 4 + n, :], ACT.Relu, scale=-1.0
                                       ).then_inc(s["neg_ready"], 1)
                        act.activation(qk[:, a, n // 2, chunk(n % 2)], k.bank[:, 4 + n, :], ACT.Identity
                                       ).then_inc(s["qk_copied"], 1)
                        act.wait_ge(s["neg_ready"], i * 8 + (j + 1))
                        act.activation(neg[:, n % 2, :], neg[:, n % 2, :], ACT.Exp, scale=-1.0
                                       ).then_inc(s["neg_exp"], 1)
                        if j == 4:
                            keys_copy(0)
                    keys_copy(1)
                    if not final:
                        high_parts(i + 1)
                    for a in range(HP):
                        for g in range(4):
                            act.wait_ge(s["a_ready"], i * 8 + (4 * a + g + 1))
                            act.activation(a_neg[:, a, 4 * g:4 * g + 4, :].rearrange("p n q -> p (n q)"),
                                           k.bank[:, A_BANKS[g], :], ACT.Identity, scale=-1.0
                                           ).then_inc(s["a_copied"], 1)
                        if a:
                            for both in range(HP):
                                mem_copy(0, both)
                        act.wait_ge(s["dq_ready"], i * HP + (a + 1))
                        if a:
                            act.wait_ge(s["q_normed"], i * HP + a)
                        act.activation(rd[:], two_banks(5), ACT.Ln).then_inc(s["dq_ln"], 1)
                        act.wait_ge(s["dq_ln"], i * HP + (a + 1))
                        act.activation(rd[:], rd[:], ACT.Exp, scale=-1.0).then_inc(s["rd_ready"], 1)
                        if a == 0:
                            exponential(0)
                    for n in range(1, NS - 1):
                        for a in range(HP):
                            mem_copy(n, a)
                        if n == 2:
                            exponential(1)
                        if n == NS - 3:
                            act.wait_ge(s["pt_ready"], i * HP + 1)
                            act.activation(pt[:, 0].rearrange("p t q -> p (t q)"), two_banks(5), ACT.Identity
                                           ).then_inc(s["pt_copied"], 1)
                    for a in range(HP):
                        if a:
                            act.wait_ge(s["pt_ready"], i * HP + 2)
                            act.activation(pt[:, 1].rearrange("p t q -> p (t q)"), two_banks(2), ACT.Identity
                                           ).then_inc(s["pt_copied"], 1)
                        act.wait_ge(s["dot_ready"], i * HP + (a + 1))
                        act.activation(att[:, a], two_banks(5 - 3 * a), ACT.Identity, scale=bt[:, 1, a:a + 1]
                                       ).then_inc(s["dot_scaled"], 1)

                high_parts(0)
                with act.Fori(0, PAIRS - 1) as i:
                    pair(i, False)
                pair(PAIRS - 1, True)

            @block.vector
            def _(dve):
                norm.on_vector(dve)
                step = k.dve_chain
                dve.wait_ge(s["const_ready"], 1)
                dve.wait_ge(s["zeroed"], 1)
                dve.wait_ge(s["betas_ready"], 1)
                dve.wait_ge(s["h_hi_ready"], 1)
                dve.tensor_tensor(h_lo[:], k.h[:], h_hi[:].bitcast(F32), ALU.subtract).then_inc(s["h_split"], 1)

                def add_projection(turn):
                    dve.wait_ge(s["y_ready"], turn)
                    for m in range(DB):
                        for a in range(HP):
                            xs = k.x[:, m, :].rearrange("p (g q) -> p g q", q=S)[:, :, bass.ds(
                                turn * (4 * HP) + (4 * a - 4 * HP), 4)]
                            last = dve.scalar_tensor_tensor(
                                xs, k.bank[:, 7, m * P + a * S:m * P + (a + 1) * S].rearrange(
                                    "p (g n) -> p g n", n=4), gate_col(k, 3, GATE_A)[:, m:m + 1], xs,
                                ALU.mult, ALU.add)
                    last.then_inc(s["x_added"], 1)

                def pair(i, first):
                    def sigma(j):
                        a, n = j // 4, j % 4
                        dve.wait_ge(s["qk_copied"], i * 8 + (j + 1))
                        dve.wait_ge(s["neg_exp"], i * 8 + (j + 1))
                        dve.scalar_tensor_tensor(sg[:, a, n // 2, chunk(n % 2)], qk[:, a, n // 2, chunk(n % 2)], 0.0,
                                                 neg[:, n % 2, :], ALU.max, ALU.add).then_inc(s["sigma_ready"], 1)

                    def key_sums(a):
                        dve.wait_ge(s["sigma_ready"], i * 8 + (4 * a + 2))
                        step.link(dve, dve.tensor_reduce(
                            z[:, 0, a, PAD + 1:], sg[:, a, 0, 0:T - S].rearrange("p (g q) -> p g q", q=S), AX.X,
                            ALU.add))
                        for n in range(4):
                            src, dst, by = z[:, n % 2, a], z[:, (n + 1) % 2, a], 1 << n
                            ins = dve.tensor_tensor(dst[:, PAD:], src[:, PAD:], src[:, PAD - by:PAD + NS - by],
                                                    ALU.add)
                            if n < 3:
                                step.link(dve, ins)
                            else:
                                ins.then_inc(s["z_ready"], 1)

                    def key_divisors(a):
                        dve.wait_ge(s["dk_ready"], i * HP + (a + 1))
                        dens = k.bank[:, 2 + 2 * a, 0:2 * TT].rearrange("p (t o) -> p t o", o=2)
                        dve.reciprocal(dk[EVEN, a, :], dens[EVEN, :, 0])
                        step.link(dve, dve.reciprocal(dk[ODD, a, :], dens[ODD, :, 1]))
                        dve.sem_inc(s["dk_read"], 1)

                    def divide_keys(a):
                        dve.wait_ge(s["kt_copied"], i * HP + (a + 1))
                        dve.tensor_tensor(xk[EVEN, a, :, 0, :], kt[EVEN, a], over(dk[EVEN, a, :], P, 2), ALU.mult)
                        dve.tensor_tensor(xk[ODD, a, :, 1, :], kt[ODD, a], over(dk[ODD, a, :], P, 2), ALU.mult
                                          ).then_inc(s["xk_ready"], 1)

                    def read_scores(a):
                        dve.wait_ge(s["scores_ready"], i * HP + (a + 1))
                        dve.scalar_tensor_tensor(sc[:, a], k.bank[:, 2 + 3 * a:4 + 3 * a, :].rearrange(
                            "p n (t q) -> p (n t) q", q=P), INV_SCALE, over(mask[:], TT), ALU.mult, ALU.add
                            ).then_inc(s["scores_read"], 1)

                    if not first:
                        dve.wait_ge(s["att_ready"], i * HP)
                    step.link(dve, dve.tensor_copy(bt[:, 0, :], beta[:, bass.ds(i * HP, HP)]))
                    step.link(dve, dve.tensor_scalar(bt[:, 1, :], bt[:, 0, :], -1.0, 1.0, ALU.mult, ALU.add))
                    dve.wait_ge(s["v_ready"], i + 1)
                    dve.tensor_copy(v[ODD, :, :, 1, :], k.bank[ODD, 0:4, :].rearrange(
                        "p n (t a q) -> p (n t) a q", t=2, a=HP)).then_inc(s["v_odd_copied"], 1)
                    for j in range(8):
                        sigma(j)
                        if j in (1, 5):
                            key_sums(j // 5)
                        if j == 4:
                            key_divisors(0)
                    divide_keys(0)
                    read_scores(0)
                    if not first:
                        add_projection(i)
                    key_divisors(1)
                    divide_keys(1)
                    read_scores(1)
                    for a in range(HP):
                        dve.wait_ge(s["scores_read"], i * HP + (a + 1))
                        step.link(dve, dve.tensor_reduce(st[:, a, 0, :], sc[:, a], AX.X, ALU.max))
                        dve.tensor_tensor(sc[:, a], sc[:, a], over(st[:, a, 0, :], P, 2), ALU.subtract
                                          ).then_inc(s["shifted"], 1)
                        dve.wait_ge(s["rd_ready"], i * HP + (a + 1))
                        dve.wait_ge(s["qz_ready"], i * HP + (a + 1))
                        dve.tensor_tensor(sg[:, a, 1], sg[:, a, 1], rd[:], ALU.mult).then_inc(s["q_normed"], 1)
                    for a in range(HP):
                        dve.wait_ge(s["probs_exp"], i * HP + (a + 1))
                        step.link(dve, dve.tensor_reduce(st[:, a, 0, :], sc[:, a], AX.X, ALU.add))
                        step.link(dve, dve.reciprocal(st[:, a, 1, :], st[:, a, 0, :]))
                        dve.tensor_tensor(sc[:, a], sc[:, a], over(st[:, a, 1, :], P, 2), ALU.mult
                                          ).then_inc(s["probs_ready"], 1)
                    for a in range(HP):
                        dve.wait_ge(s["read_ready"], i * (HP * NS) + (HP * NS - (1 - a) * (LAG + 1)))
                        dve.wait_ge(s["dot_scaled"], i * HP + (a + 1))
                        for c in range(NCH):
                            last = dve.scalar_tensor_tensor(att[:, a, chunk(c)], k.bank[:, A_BANKS[2 * a + c], :],
                                                            bt[:, 0, a:a + 1], att[:, a, chunk(c)], ALU.mult, ALU.add)
                        last.then_inc(s["att_ready"], 1)

                pair(0, True)
                with dve.Fori(1, PAIRS) as i:
                    step.enter(i - 1, 18)
                    pair(i, False)
                step.leave(PAIRS - 1)
                add_projection(PAIRS)


def l3_ffn(k, norm):
    nc, d = k.nc, k.dram
    E, A, N = 8, 64, 2048
    UNITS = N // P
    PAIRS = UNITS // 2
    names = ("w_in", "idx_in", "ea_in", "iota_ready", "logits_ready", "shifted", "probs_exp", "weights_ready",
             "rt_ready", "rt_copied", "ea_shifted", "ea_exp", "ea_ready", "eat_ready", "eat_copied", "imp_ready",
             "delta_ready", "values_ready", "index_ready", "pick_made", "put_made", "up_ready", "copied", "gated", "hi_ready",
             "lo_ready", "summed", "done", "h_hi_ready", "h_split")
    s = {n: k.sem("l3f_" + n) for n in names}
    with ExitStack() as ctx:
        def sb(n, shape, dt=F32):
            return ctx.enter_context(nc.sbuf_tensor("l3f_" + n, shape, dt))
        gw = sb("gw", [P, DB, E])
        wt = sb("wt", [P, DB, D])
        ea = sb("ea", [E, A])
        est = sb("est", [E, 2])
        eat = sb("eat", [A, E])
        atoms = sb("atoms", [A, N])
        imp = sb("imp", [E, N])
        idx = sb("idx", [P, N], I32)
        idx_s = sb("idx_s", [P, UNITS], I32)
        colf = sb("colf", [P, N])
        rowf = sb("rowf", [P, UNITS])
        feature = sb("feature", [P, DB])
        iota = sb("iota", [P, D])
        p = sb("p", [P, TT, E])
        m = sb("m", [P, TT, E])
        v8 = sb("v8", [P, TT, 8])
        st = sb("st", [P, 2, TT])
        rt = sb("rt", [E, T])
        pick = sb("pick", [P, 2, DB, P], F32R)
        val = sb("val", [E, 2, P])
        put = sb("put", [P, 2, D], F32R)
        g = sb("g", [P, NCH, CH])
        a = sb("a", [P, NCH, CH])
        a_hi, a_lo = (sb("a_" + n, [P, NCH, CH], F32R) for n in ("hi", "lo"))
        h_hi, h_lo = (sb("h_" + n, [P, DB, T], F32R) for n in ("hi", "lo"))
        with nc.Block() as block:
            @block.sync
            def _(sp):
                sp.dma_start(gw[:], d["l3f_gw"].rearrange("(b p) n -> p b n", p=P)).then_inc(s["w_in"], 16)
                sp.dma_start(wt[:], d["l3f_w"].rearrange("(b p) n -> p b n", p=P)).then_inc(s["w_in"], 16)
                sp.dma_start(ea[:], d["l3f_ea"]).then_inc(s["ea_in"], 16)
                sp.dma_start(atoms[:], d["l3f_atoms"]).then_inc(s["ea_in"], 16)
                sp.dma_start(imp[:], d["l3f_imp"]).then_inc(s["ea_in"], 16)
                sp.dma_start(idx[:], d["l3f_idx"].to_broadcast([P, N])).then_inc(s["idx_in"], 16)
                sp.dma_start(idx_s[:], d["l3f_idx_s"]).then_inc(s["idx_in"], 16)

            @block.gpsimd
            def _(pool):
                pool.iota(iota[:], pattern=[[1, D]], base=0, channel_multiplier=0,
                          allow_small_or_imprecise_dtypes=True)
                pool.iota(feature[:], pattern=[[P, DB]], base=0, channel_multiplier=1,
                          allow_small_or_imprecise_dtypes=True).then_inc(s["iota_ready"], 1)

            @block.tensor
            def _(pe):
                norm.on_tensor(pe)
                norm.wait(pe)
                pe.wait_ge(s["w_in"], 32)
                for t in range(TT):
                    for b in range(DB):
                        last = pe.matmul(k.bank[:, 0, t * E:(t + 1) * E], k.h[:, b, tile(t)], gw[:, b, :],
                                         start=(b == 0), stop=(b == DB - 1))
                last.then_inc(s["logits_ready"], 1)
                for mm in range(DB):
                    for c in range(NCH):
                        for b in range(DB):
                            pe.matmul(k.bank[:, 4 + 2 * mm + c, :], wt[:, b, tile(mm)], k.h[:, b, chunk(c)],
                                      start=(b == 0), stop=False, skip_group_check=True)
                pe.wait_ge(s["ea_ready"], 1)
                pe.transpose(k.bank[0:A, 1, 0:E], ea[:], k.ident[0:E, 0:E]).then_inc(s["eat_ready"], 1)
                pe.wait_ge(s["weights_ready"], 1)
                for t in range(TT):
                    last = pe.transpose(k.bank[0:E, 2 + t // 4, (t % 4) * P:(t % 4 + 1) * P], m[:, t, :], k.ident[:])
                last.then_inc(s["rt_ready"], 1)
                pe.wait_ge(s["eat_copied"], 1)
                for n in range(N // CH):
                    if n >= 2:
                        pe.wait_ge(s["values_ready"], n - 1)
                    pe.matmul(k.bank[0:E, n % 2, :], eat[:], atoms[:, chunk(n)], start=True, stop=True
                              ).then_inc(s["delta_ready"], 1)
                pe.wait_ge(s["values_ready"], N // CH)
                pe.wait_ge(s["rt_copied"], 1)

                pe.wait_ge(s["h_split"], NCH)

                def up(i, n, first=False):
                    half, c = n // 2, n % 2
                    if c == 0:
                        pe.wait_ge(s["pick_made"], i * 2 + (half + 1))
                    if not (first and n < 2):
                        pe.wait_ge(s["gated"], i * 4 + (n - 1))
                    for b in range(DB):
                        for part in (h_hi, h_lo):
                            pe.matmul(k.bank[:, 2 * c, :], pick[:, half, b, :], part[:, b, chunk(c)],
                                      start=(b == 0 and part is h_hi), stop=(b == DB - 1 and part is h_lo))
                    pe.matmul(k.bank[:, 2 * c + 1, :], val[:, half, :], rt[:, chunk(c)], start=True, stop=True
                              ).then_inc(s["up_ready"], 1)

                def down(i, n):
                    half, c = n // 2 % 2, n % 2
                    if c == 0:
                        pe.wait_ge(s["put_made"], i * 2 + (n // 2 + 1))
                    pe.wait_ge(s["lo_ready"], i * 4 + (n + 1))
                    for mm in range(DB):
                        for part in (a_hi, a_lo):
                            last = pe.matmul(k.bank[:, 4 + 2 * mm + c, :], put[:, half, tile(mm)], part[:, c, :],
                                             start=False, stop=False, skip_group_check=True)
                    last.then_inc(s["summed"], 1)

                up(0, 0, True)
                up(0, 1, True)
                for n in range(2, 4):
                    up(0, n, True)
                    down(0, n - 2)
                with pe.Fori(1, PAIRS) as i:
                    for n in range(4):
                        up(i, n)
                        down(i, n - 2)
                down(PAIRS, -2)
                down(PAIRS, -1)

            @block.scalar
            def _(act):
                norm.on_scalar(act)
                act.preload_act_table_set(EXP_LN)
                act.wait_ge(s["ea_shifted"], 1)
                act.activation(ea[:], ea[:], ACT.Exp).then_inc(s["ea_exp"], 1)
                act.wait_ge(s["shifted"], 1)
                act.activation(p[:], p[:], ACT.Exp).then_inc(s["probs_exp"], 1)
                act.wait_ge(s["eat_ready"], 1)
                act.activation(eat[:], k.bank[0:A, 1, 0:E], ACT.Identity).then_inc(s["eat_copied"], 1)
                act.wait_ge(s["rt_ready"], 1)
                act.activation(rt[:], k.bank[0:E, 2:4, :].rearrange("p n q -> p (n q)"), ACT.Identity
                               ).then_inc(s["rt_copied"], 1)
                act.wait_ge(s["ea_in"], 48)
                act.activation(imp[:], imp[:], ACT.Sigmoid).then_inc(s["imp_ready"], 1)
                norm.wait(act)
                for c in range(NCH):
                    act.activation(h_hi[:, :, chunk(c)], k.h[:, :, chunk(c)], ACT.Identity
                                   ).then_inc(s["h_hi_ready"], 1)

                def high(i, n, first=False):
                    act.wait_ge(s["gated"], i * 4 + (n + 1))
                    if not (first and n < 2):
                        act.wait_ge(s["summed"], i * 4 + (n - 1))
                    act.activation(a_hi[:, n % 2, :], a[:, n % 2, :], ACT.Identity).then_inc(s["hi_ready"], 1)

                def pair(i, first):
                    for n in range(4):
                        act.wait_ge(s["up_ready"], i * 4 + (n + 1))
                        act.activation(g[:, n % 2, :], k.bank[:, 2 * (n % 2), :], ACT.Identity
                                       ).then_inc(s["copied"], 1)
                        if not (first and n == 0):
                            high(i, n - 1, first)

                pair(0, True)
                with act.Fori(1, PAIRS) as i:
                    pair(i, False)
                high(PAIRS, -1)

            @block.vector
            def _(dve):
                norm.on_vector(dve)
                step = k.dve_chain
                dve.wait_ge(s["ea_in"], 48)
                step.link(dve, dve.tensor_reduce(est[:, 0:1], ea[:], AX.X, ALU.max))
                dve.tensor_scalar(ea[:], ea[:], est[:, 0:1], None, ALU.subtract).then_inc(s["ea_shifted"], 1)
                dve.wait_ge(s["logits_ready"], 1)
                step.link(dve, dve.tensor_scalar(p[:], k.bank[:, 0, 0:TT * E].rearrange("p (t e) -> p t e", t=TT),
                                                 -50.0, 50.0, ALU.max, ALU.min))
                for t in range(TT):
                    last = dve.max(v8[:, t, :], p[:, t, :])
                step.link(dve, last)
                step.link(dve, dve.tensor_tensor(m[:], p[:], over(v8[:, :, 1], E, 2), ALU.is_ge))
                dve.tensor_tensor(p[:], p[:], over(v8[:, :, 0], E, 2), ALU.subtract).then_inc(s["shifted"], 1)
                dve.wait_ge(s["ea_exp"], 1)
                step.link(dve, dve.tensor_reduce(est[:, 0:1], ea[:], AX.X, ALU.add))
                step.link(dve, dve.reciprocal(est[:, 1:2], est[:, 0:1]))
                dve.tensor_scalar(ea[:], ea[:], est[:, 1:2], None, ALU.mult).then_inc(s["ea_ready"], 1)
                dve.wait_ge(s["probs_exp"], 1)
                step.link(dve, dve.tensor_tensor(m[:], m[:], p[:], ALU.mult))
                step.link(dve, dve.tensor_reduce(st[:, 0, :], m[:], AX.X, ALU.add))
                step.link(dve, dve.reciprocal(st[:, 1, :], st[:, 0, :]))
                dve.tensor_tensor(m[:], m[:], over(st[:, 1, :], E, 2), ALU.mult).then_inc(s["weights_ready"], 1)
                dve.wait_ge(s["idx_in"], 32)
                step.link(dve, dve.tensor_single_scalar(idx[:], idx[:], D - 1, ALU.bitwise_and))
                step.link(dve, dve.tensor_single_scalar(idx_s[:], idx_s[:], 8, ALU.logical_shift_right))
                dve.tensor_copy(colf[:], idx[:])
                step.link(dve, dve.tensor_copy(rowf[:], idx_s[:]))
                dve.wait_ge(s["imp_ready"], 1)
                for n in range(N // CH):
                    dve.wait_ge(s["delta_ready"], n + 1)
                    dve.tensor_tensor(imp[:, chunk(n)], imp[:, chunk(n)], k.bank[0:E, n % 2, :], ALU.mult
                                      ).then_inc(s["values_ready"], 1)
                dve.wait_ge(s["values_ready"], N // CH)
                dve.wait_ge(s["iota_ready"], 1)

                for c in range(NCH):
                    dve.wait_ge(s["h_hi_ready"], c + 1)
                    dve.tensor_tensor(h_lo[:, :, chunk(c)], k.h[:, :, chunk(c)], h_hi[:, :, chunk(c)].bitcast(F32),
                                      ALU.subtract).then_inc(s["h_split"], 1)

                def make_pick(i, unit):
                    at, half = i * (2 * P) + unit * P, unit % 2
                    for b in range(DB):
                        dve.tensor_scalar(pick[:, half, b, :], colf[:, bass.ds(at, P)], feature[:, b:b + 1], None,
                                          ALU.is_equal)
                    dve.tensor_copy(val[:, half, :], imp[:, bass.ds(at, P)]).then_inc(s["pick_made"], 1)

                def make_put(i, unit, first):
                    if not first:
                        dve.wait_ge(s["summed"], i * 4 + (2 * unit - 2))
                    dve.tensor_scalar(put[:, unit, :], iota[:], rowf[:, bass.ds(i * 2 + unit, 1)], None,
                                      ALU.is_equal).then_inc(s["put_made"], 1)

                def low(i, n, first=False):
                    dve.wait_ge(s["hi_ready"], i * 4 + (n + 1))
                    if not (first and n < 2):
                        dve.wait_ge(s["summed"], i * 4 + (n - 1))
                    dve.tensor_tensor(a_lo[:, n % 2, :], a[:, n % 2, :], a_hi[:, n % 2, :].bitcast(F32), ALU.subtract
                                      ).then_inc(s["lo_ready"], 1)

                def pair(i, first, final):
                    for n in range(4):
                        unit, c = n // 2, n % 2
                        if not (first and n < 2):
                            dve.wait_ge(s["lo_ready"], i * 4 + (n - 1))
                        dve.wait_ge(s["copied"], i * 4 + (n + 1))
                        dve.tensor_tensor(a[:, c, :], g[:, c, :], k.bank[:, 2 * c + 1, :], ALU.mult
                                          ).then_inc(s["gated"], 1)
                        if not (first and n == 0):
                            low(i, n - 1, first)
                        if c == 0:
                            make_put(i, unit, first)
                            if not (final and unit):
                                make_pick(i, unit + 1)

                make_pick(0, 0)
                pair(0, True, False)
                with dve.Fori(1, PAIRS - 1) as i:
                    pair(i, False, False)
                pair(PAIRS - 1, False, True)
                low(PAIRS, -1)
                dve.wait_ge(s["summed"], 4 * PAIRS)
                for mm in range(DB):
                    for c in range(NCH):
                        xs = k.x[:, mm, chunk(c)]
                        last = dve.scalar_tensor_tensor(xs, k.bank[:, 4 + 2 * mm + c, :],
                                                        gate_col(k, 3, GATE_B)[:, mm:mm + 1], xs, ALU.mult, ALU.add)
                last.then_inc(s["done"], 1)


def store(k, out):
    nc = k.nc
    stored = k.sem("x_stored")
    with nc.Block() as block:
        @block.sync
        def _(sp):
            sp.dma_start(out.rearrange("(b p) t -> p b t", p=P), k.x[:]).then_inc(stored, 16)
            sp.wait_ge(stored, 16)


def gate_col(k, layer, at):
    return k.mod[:, layer, at:at + DB]


def late_modulations(k, mods):
    with k.nc.Block() as block:
        @block.scalar
        def _(act):
            mods.on_scalar(act, range(1, 4))

        @block.vector
        def _(dve):
            mods.add_blocks(dve, range(1, 4))
            mods.finish(dve, range(1, 4))

        @block.tensor
        def _(pe):
            mods.on_tensor(pe, range(1, 4))


def build(nc, dram, out, only=None):
    halves = ((0, l0_attention, l0_ffn), (1, l1_attention, l1_ffn), (2, l2_attention, l2_ffn), (3, l3_attention, l3_ffn))
    steps = [(layer, part, half) for layer, *parts in halves for half, part in enumerate(parts)]
    with ExitStack() as ctx:
        k = Core(nc, ctx, dram)
        mod_ctx = ExitStack()
        with k.stage():
            constants(k)
            mods = Modulations(k, mod_ctx)
            mods.start()
        for n, (layer, part, half) in enumerate(steps):
            if only is not None and n not in only:
                if n == 0:
                    late_modulations(k, mods)
                    mod_ctx.close()
                continue
            with k.stage(), ExitStack() as norm_ctx:
                norm = adaln(k, norm_ctx, layer, *((SHIFT_B, SCALE_B) if half else (SHIFT_A, SCALE_A)))
                if n == 0:
                    part(k, norm, mods)
                else:
                    part(k, norm)
            if n == 0:
                mod_ctx.close()
        store(k, out)


def laid_out(i):
    def t(a):
        return np.swapaxes(np.asarray(a), -1, -2)

    def cat(*a, axis=-1):
        return np.concatenate([np.asarray(x) for x in a], axis=axis)

    H0 = 8
    wq = t(i["L0_attn_Wq"]).reshape(D, H0, P).transpose(1, 0, 2)
    wkv = t(i["L0_attn_Wkv"])
    wk = wkv[:, :H0 * P].reshape(D, H0, P).transpose(1, 0, 2)
    a = {
        "x": t(np.asarray(i["L0_attn_x"])[0]),
        "cs": np.stack([np.asarray(i[f"L{n}_c"]).reshape(DB, P).T for n in range(4)], 1).reshape(P, 4 * DB),
        "wmod": np.stack([np.asarray(i[f"L{n}_wmod"]) for n in range(4)]),
        "l0_wqk": cat(wq, wk),
        "l0_wv": wkv[:, H0 * P:],
        "l0_wg": t(i["L0_attn_Wg"]),
        "l0_bg": np.asarray(i["L0_attn_bg"])[None],
        "l0_scales": np.stack([np.asarray(i["L0_attn_q_scale"]), np.asarray(i["L0_attn_k_scale"])], 1),
        "l0_wo": t(i["L0_attn_Wo"]),
    }
    def in_blocks(w):
        w = np.asarray(w)
        if w.ndim == 3:
            w = w.transpose(1, 0, 2).reshape(D, -1)
        w = np.pad(w, ((0, 0), (0, -w.shape[1] % P)))
        return w.reshape(D, -1, P).transpose(1, 0, 2)

    def units(gate, up, down):
        w = cat(in_blocks(gate), in_blocks(up))
        down = np.asarray(down).reshape(-1, D)
        down = np.pad(down, ((0, -down.shape[0] % P), (0, 0))).reshape(-1, P, D)
        return w.reshape(-1, DB, P, 2 * P).transpose(0, 2, 1, 3).reshape(-1, P, DB * 2 * P), down

    a["l0f_wq"] = np.asarray(i["L0_ffn_W_q"])
    a["l0f_keys"] = np.asarray(i["L0_ffn_keys"])
    a["l0f_de"] = t(i["L0_ffn_down_embed"])
    a["l0f_ue"] = np.asarray(i["L0_ffn_up_embed"])
    a["l0f_win"], a["l0f_wout"] = units(i["L0_ffn_gate_w"], i["L0_ffn_up_w"], i["L0_ffn_down_w"])
    a["l1_w"] = cat(i["L1_attn_Wq"], i["L1_attn_Wk"], i["L1_attn_Wv"])
    a["l1_b"] = cat(i["L1_attn_bq"], i["L1_attn_bk"], i["L1_attn_bv"])[None]
    a["l1_wz"] = cat(i["L1_attn_Wbeta"], i["L1_attn_Walpha"])
    a["l1_bz"] = cat(i["L1_attn_bbeta"], i["L1_attn_balpha"])[None]
    a["l1f_gw"] = t(i["L1_ffn_gate_weight"])
    a["l1f_sim"] = np.asarray(i["L1_ffn_similarity"])
    gu = t(i["L1_ffn_gate_up_proj"])
    F1 = gu.shape[-1] // 2
    a["l1f_win"], a["l1f_wout"] = units(gu[..., :F1], gu[..., F1:], t(i["L1_ffn_down_proj"]))
    def cols2(v):
        v = np.asarray(v)
        return np.tile(v, D // v.shape[0]).reshape(DB, P).T

    conv = np.asarray(i["L2_attn_conv_w"])[:, 0]
    two = [i["L2_attn_" + n] for n in ("ln1w", "ln1b", "ln2w", "ln2b", "vnw", "vnb", "mnw", "mnb", "gnw", "gnb",
                                       "conv_b")]
    two += [conv[:, j] for j in range(4)]
    two += [i["L2_attn_big"], np.repeat(np.asarray(i["L2_attn_bg"]), 16), i["L2_attn_bog"]]
    a["l2_cols"] = np.stack([cols2(v) for v in two], 1)
    a["l2_w"] = cat(i["L2_attn_Wq"], i["L2_attn_Wk"], i["L2_attn_Wv"], i["L2_attn_Wig"],
                    np.repeat(np.asarray(i["L2_attn_Wg"]), 16, axis=1), i["L2_attn_Wog"])
    a["l2_wo"] = np.asarray(i["L2_attn_Wo"])
    a["l2_win"], a["l2_wout"] = units(i["L2_attn_Wgate"], i["L2_attn_Wval"], i["L2_attn_Wout"])
    a["l2f_gw"] = t(i["L2_ffn_gate_weight"])

    wi, wo = units(t(i["L2_ffn_gate_w"]), t(i["L2_ffn_up_w"]), t(i["L2_ffn_down_w"]))
    si, so = units(t(i["L2_ffn_sh_gate_w"]), t(i["L2_ffn_sh_up_w"]), t(i["L2_ffn_sh_down_w"]))
    a["l2f_win"], a["l2f_wout"] = cat(wi, si, axis=0), cat(wo, so, axis=0)
    PR3 = 8
    q3, k3, v3 = (np.asarray(i["L3_attn_" + n]).reshape(D, PR3, 2, P).transpose(1, 0, 2, 3) for n in ("Wq", "Wk", "Wv"))
    a["l3_w"] = cat(np.stack([q3, k3], 3).reshape(PR3, D, 4 * P), v3.reshape(PR3, D, 2 * P))
    a["l3_wo"] = np.asarray(i["L3_attn_Wo"])
    a["l3_betas"] = np.asarray(i["L3_attn_betas"]).reshape(16, P).T
    idx = np.asarray(i["L3_ffn_mask_idx"])
    a["l3f_gw"], a["l3f_w"] = t(i["L3_ffn_gate_w"]), t(i["L3_ffn_W"])
    a["l3f_ea"], a["l3f_atoms"] = np.asarray(i["L3_ffn_expert_atom_weights"]), np.asarray(i["L3_ffn_atoms"])
    a["l3f_imp"] = np.asarray(i["L3_ffn_importance"])
    a["l3f_idx"], a["l3f_idx_s"] = idx[None], idx.reshape(-1, P).T
    return a


def kernel(**inputs):
    import concourse.bacc as _bacc
    from concourse.bass_utils import run_bass_kernel_spmd as _run

    arrays = {"in_" + n: np.ascontiguousarray(a) for n, a in laid_out(inputs).items()}
    nc = _bacc.Bacc("TRN2", target_bir_lowering=False, num_devices=1)
    dram = {n[3:]: nc.dram_tensor(n, a.shape, mybir.dt.from_np(a.dtype), kind="ExternalInput").ap()
            for n, a in arrays.items()}
    out = nc.dram_tensor("out", (D, T), F32, kind="ExternalOutput").ap()
    build(nc, dram, out)
    r = _run(nc, [arrays], core_ids=[0])
    return np.ascontiguousarray(r.results[0]["out"].T)[None]
```

```python
from contextlib import ExitStack, contextmanager

import numpy as np

import concourse.bass as bass
import concourse.mybir as mybir

F32 = mybir.dt.float32
F32R = mybir.dt.float32r
I32 = mybir.dt.int32
ACT = mybir.ActivationFunctionType
ALU = mybir.AluOpType
AX = mybir.AxisListType

P = 128
T = 1024
D = 256
DB = D // P
CH = 512
NCH = T // CH
TT = T // P
NEG = -1.0e30
EXP_LN = "natural_log_exp_and_others"

SHIFT_A, SCALE_A, GATE_A, SHIFT_B, SCALE_B, GATE_B = range(0, 6 * DB, DB)


class Chain:

    def __init__(self, sem):
        self.sem, self.done, self.turn, self.each, self.k = sem, 0, None, 0, 0

    def link(self, eng, ins):
        ins.then_inc(self.sem, 1)
        self.k += 1
        if self.turn is None:
            self.done, self.k = self.done + 1, 0
            eng.wait_ge(self.sem, self.done)
        else:
            eng.wait_ge(self.sem, self.turn * self.each + (self.done + self.k))

    def enter(self, turn, each):
        self.turn, self.each, self.k = turn, each, 0

    def leave(self, turns):
        assert self.k == self.each, (self.k, self.each)
        self.done, self.turn, self.k = self.done + turns * self.each, None, 0


class Core:

    def __init__(self, nc, ctx, dram):
        self.nc, self.ctx, self.dram, self.local = nc, ctx, dram, None
        self.x = ctx.enter_context(nc.sbuf_tensor("x_stream", [P, DB, T], F32))
        self.h = ctx.enter_context(nc.sbuf_tensor("h_modulated", [P, DB, T], F32))
        self.mod = ctx.enter_context(nc.sbuf_tensor("modulation", [P, 4, 6 * DB], F32))
        self.ident = ctx.enter_context(nc.sbuf_tensor("ident", [P, P], F32))
        self.ones = ctx.enter_context(nc.sbuf_tensor("ones", [P, P], F32))
        self.zeros = ctx.enter_context(nc.sbuf_tensor("zeros", [P, CH], F32))
        self.mean_w = ctx.enter_context(nc.sbuf_tensor("mean_w", [P, P], F32))
        self.eps = ctx.enter_context(nc.sbuf_tensor("eps", [P, 4], F32))
        self.bank = ctx.enter_context(nc.psum_tensor("bank", [P, 8, CH], F32))
        self.dve_chain = Chain(self.sem("dve_step"))
        self.act_chain = Chain(self.sem("act_step"))
        self.pool_chain = Chain(self.sem("pool_step"))
        self.calls = {}

    def sem(self, name):
        if self.local is None:
            return self.ctx.enter_context(self.nc.semaphore(name))
        self.local.append(self.nc.alloc_semaphore(name=name))
        return self.local[-1]

    @contextmanager
    def stage(self):
        self.local = []
        yield
        self.nc.clear_and_free_semaphores(self.local)
        self.nc.all_engine_barrier()
        self.local = None

    def shared(self, name):
        if name not in self.calls:
            self.calls[name] = self.ctx.enter_context(self.nc.semaphore(name))
        return self.calls[name]


def over(ap, n, axis=1):
    a = ap.unsqueeze(axis)
    shape = list(a.shape)
    shape[axis] = n
    return a.to_broadcast(shape)


def chunk(c):
    return slice(c * CH, (c + 1) * CH)


def tile(t):
    return slice(t * P, (t + 1) * P)


EPS_LN, EPS_L2 = 1.0e-5, 1.0e-12


def constants(k):
    nc = k.nc
    with nc.Block() as block:
        @block.gpsimd
        def _(pool):
            step = k.pool_chain
            pool.memset(k.ones[:], 1.0)
            pool.memset(k.zeros[:], 0.0)
            pool.memset(k.mean_w[:], 1.0 / D)
            pool.memset(k.eps[:, 0:1], EPS_LN)
            pool.memset(k.eps[:, 1:2], EPS_L2)
            pool.memset(k.eps[:, 2:3], 1.0)
            pool.memset(k.eps[:, 3:4], 1.0e-6)
            step.link(pool, pool.memset(k.ident[:], 0.0))
            step.link(pool, pool.affine_select(out=k.ident[:], in_=k.ident[:], compare_op=ALU.not_equal, fill=1.0,
                                               base=0, pattern=[[-1, P]], channel_multiplier=1))


class Modulations:

    def __init__(self, k, ctx):
        self.k = k
        self.cs = ctx.enter_context(k.nc.sbuf_tensor("cs", [P, 4 * DB], F32))
        self.w = {}
        self.tmp = ctx.enter_context(k.nc.sbuf_tensor("mod_tmp", [P, 3, DB], F32))
        self.w_in = [k.shared(f"wmod_in{n}") for n in range(4)]
        self.scaled, self.added, self.summed, self.copied = (
            k.shared("mod_" + n) for n in ("scaled", "added", "summed", "copied"))

    def hold(self, ctx, layers):
        for n in layers:
            self.w[n] = ctx.enter_context(self.k.nc.sbuf_tensor(f"wmod{n}", [P, DB, 6 * D], F32))

    def on_sync(self, sp, layers):
        for n in layers:
            sp.dma_start(self.w[n][:], self.k.dram["wmod"][n].rearrange("(b p) n -> p b n", p=P)
                         ).then_inc(self.w_in[n], 16)

    def on_scalar(self, act, layers):
        for n in layers:
            act.wait_ge(self.w_in[n], 16)
            for b in range(DB):
                act.activation(self.w[n][:, b], self.w[n][:, b], ACT.Identity,
                               scale=self.cs[:, n * DB + b:n * DB + b + 1]).then_inc(self.scaled, 1)

    def add_blocks(self, eng, layers):
        for n in layers:
            w = self.w[n]
            eng.wait_ge(self.scaled, DB * (n + 1))
            eng.tensor_tensor(w[:, 0], w[:, 0], w[:, 1], ALU.add).then_inc(self.added, 1)

    def on_tensor(self, pe, layers, bank):
        for n in layers:
            pe.wait_ge(self.added, n + 1)
            for j in range(6 * DB):
                last = pe.matmul(self.k.bank[:, bank, n * 16 + j:n * 16 + j + 1], self.w[n][:, 0, tile(j)],
                                 self.k.ones[:, 0:1], start=True, stop=True)
            last.then_inc(self.summed, 1)

    def finish(self, dve, layers, bank):
        k, step, first, count = self.k, self.k.dve_chain, layers[0], len(layers)
        mod, tmp = k.mod[:, first:first + count], self.tmp[:, 0:count]
        dve.wait_ge(self.summed, first + count)
        cols = k.bank[:, bank, 0:64].rearrange("p (l j) -> p l j", l=4)
        step.link(dve, dve.tensor_copy(mod, cols[:, first:first + count, 0:6 * DB]))
        dve.sem_inc(self.copied, 1)
        for at in (SCALE_A, SCALE_B):
            s = mod[:, :, at:at + DB]
            step.link(dve, dve.tensor_scalar(s, s, 1.0, None, ALU.add))
        for at in (GATE_A, GATE_B):
            g = mod[:, :, at:at + DB]
            step.link(dve, dve.tensor_scalar(tmp, g, 0.0, 2.0, ALU.is_ge, ALU.mult))
            step.link(dve, dve.tensor_scalar(tmp, tmp, -1.0, None, ALU.add))
            step.link(dve, dve.tensor_tensor(g, g, tmp, ALU.mult))
            step.link(dve, dve.tensor_scalar(g, g, 0.25, None, ALU.max))
            step.link(dve, dve.tensor_tensor(g, g, tmp, ALU.mult))

    def start(self):
        k, nc, d = self.k, self.k.nc, self.k.dram
        x_in, c_in, c_ready = (k.sem(n) for n in ("x_in", "c_in", "silu_c_ready"))
        with ExitStack() as ctx, nc.Block() as block:
            self.hold(ctx, [0])

            @block.sync
            def _(sp):
                sp.dma_start(self.cs[:], d["cs"]).then_inc(c_in, 16)
                self.on_sync(sp, [0])
                sp.dma_start(k.x[:], d["x"].rearrange("(b p) t -> p b t", p=P)).then_inc(x_in, 16)
                sp.wait_ge(x_in, 16)

            @block.scalar
            def _(act):
                act.wait_ge(c_in, 16)
                act.activation(self.cs[:], self.cs[:], ACT.Silu).then_inc(c_ready, 1)
                act.wait_ge(c_ready, 1)
                self.on_scalar(act, [0])

            @block.tensor
            def _(pe):
                self.on_tensor(pe, [0], 3)

            @block.vector
            def _(dve):
                dve.wait_ge(c_ready, 1)
                self.add_blocks(dve, [0])
                self.finish(dve, [0], 3)


class LayerNorm:

    def __init__(self, k, ctx, src, dst, scale, shift):
        self.k, self.src, self.dst, self.scale, self.shift = k, src, dst, scale, shift
        self.at = NCH * k.calls.setdefault("layernorms", 0)
        k.calls["layernorms"] += 1
        self.s = {n: k.shared("ln_" + n) for n in ("mean_ready", "centered", "squared", "var_ready", "root_ready",
                                                   "normed", "out_ready")}
        self.sq = ctx.enter_context(k.nc.sbuf_tensor(f"ln_square{self.at}", [P, DB, T], F32))
        self.rs = ctx.enter_context(k.nc.sbuf_tensor(f"ln_rstd{self.at}", [P, T], F32))

    def wait(self, eng):
        eng.wait_ge(self.s["out_ready"], self.at + NCH)

    def on_tensor(self, pe):
        k, s = self.k, self.s
        for c in range(NCH):
            for b in range(DB):
                last = pe.matmul(k.bank[:, c, :], k.mean_w[:], self.src[:, b, chunk(c)], start=(b == 0),
                                 stop=(b == DB - 1))
            last.then_inc(s["mean_ready"], 1)
        for c in range(NCH):
            pe.wait_ge(s["squared"], self.at + c + 1)
            for b in range(DB):
                last = pe.matmul(k.bank[:, 2 + c, :], k.mean_w[:], self.sq[:, b, chunk(c)], start=(b == 0),
                                 stop=(b == DB - 1))
            last.then_inc(s["var_ready"], 1)

    def on_vector(self, dve):
        k, s, dst = self.k, self.s, self.dst
        for c in range(NCH):
            dve.wait_ge(s["mean_ready"], self.at + c + 1)
            dve.tensor_tensor(dst[:, :, chunk(c)], self.src[:, :, chunk(c)], over(k.bank[:, c, :], DB), ALU.subtract
                              ).then_inc(s["centered"], 1)
        for c in range(NCH):
            dve.wait_ge(s["root_ready"], self.at + c + 1)
            dve.tensor_tensor(dst[:, :, chunk(c)], dst[:, :, chunk(c)], over(self.rs[:, chunk(c)], DB), ALU.mult
                              ).then_inc(s["normed"], 1)
            dve.wait_ge(s["normed"], self.at + c + 1)
            for b in range(DB):
                last = dve.tensor_scalar(dst[:, b, chunk(c)], dst[:, b, chunk(c)], self.scale[:, b:b + 1],
                                         self.shift[:, b:b + 1], ALU.mult, ALU.add)
            last.then_inc(s["out_ready"], 1)

    def on_scalar(self, act):
        k, s, rs = self.k, self.s, self.rs
        act.preload_act_table_set(EXP_LN)
        for c in range(NCH):
            act.wait_ge(s["centered"], self.at + c + 1)
            act.activation(self.sq[:, :, chunk(c)], self.dst[:, :, chunk(c)], ACT.Square).then_inc(s["squared"], 1)
        for c in range(NCH):
            act.wait_ge(s["var_ready"], self.at + c + 1)
            k.act_chain.link(act, act.activation(rs[:, chunk(c)], k.bank[:, 2 + c, :], ACT.Ln, bias=k.eps[:, 0:1]))
            act.activation(rs[:, chunk(c)], rs[:, chunk(c)], ACT.Exp, scale=-0.5).then_inc(s["root_ready"], 1)


def layernorm(k, src, dst, scale, shift):
    with ExitStack() as ctx:
        norm = LayerNorm(k, ctx, src, dst, scale, shift)
        with k.nc.Block() as block:
            block.tensor(norm.on_tensor)
            block.vector(norm.on_vector)
            block.scalar(norm.on_scalar)


def adaln(k, ctx, layer, shift, scale):
    return LayerNorm(k, ctx, k.x, k.h, k.mod[:, layer, scale:scale + DB], k.mod[:, layer, shift:shift + DB])


class UnitWeights:
    IN, OUT = slice(0, DB * 2 * P), slice(DB * 2 * P, DB * 2 * P + D)

    def __init__(self, k, ctx, name, w_in, w_out):
        self.w_in, self.w_out = w_in, w_out
        self.w = ctx.enter_context(k.nc.sbuf_tensor(f"{name}_w", [P, 2, self.OUT.stop], F32))
        self.loaded = [k.sem(f"{name}_w_in{n}") for n in range(2)]

    def load(self, sp, u, half):
        sp.dma_start(self.w[:, half, self.IN], self.w_in[bass.ds(u, 1)].rearrange("u p n -> p (u n)")
                     ).then_inc(self.loaded[half], 16)
        sp.dma_start(self.w[:, half, self.OUT], self.w_out[bass.ds(u, 1)].rearrange("u f n -> f (u n)")
                     ).then_inc(self.loaded[half], 16)

    def load_first(self, sp):
        for half in range(2):
            self.load(sp, half, half)


def gated_units(k, name, weights, units, gate, src=None, rows=None, turn=1, rows_per_turn=0, owner=None,
                extra=None):
    nc = k.nc
    src = k.h if src is None else src
    pairs = units // 2
    weighted = rows is not None
    w, loaded = weights.w, weights.loaded
    rows_in = [k.sem(f"{name}_rows_in{n}") for n in range(2)]
    src_hi_ready, src_split, in_hi_ready, in_split, out_hi_ready, out_split, up_ready, act_ready, up_used, gated, hi_ready, lo_ready, summed, done = (
        k.sem(f"{name}_{n}") for n in ("src_hi_ready", "src_split", "in_hi_ready", "in_split", "out_hi_ready",
                                       "out_split", "up_ready", "act_ready", "up_used", "gated", "hi_ready",
                                       "lo_ready", "summed", "done"))
    w_in_part, w_out_part = weights.IN, weights.OUT
    WI, WU = w_out_part.start, w_out_part.stop
    with ExitStack() as ctx:
        def sb(n, shape, dt=F32):
            return ctx.enter_context(nc.sbuf_tensor(f"{name}_{n}", shape, dt))
        w_hi, w_lo = (sb("w_" + n, [P, 2, WU], F32R) for n in ("hi", "lo"))
        src_hi, src_lo = (sb("src_" + n, [P, DB, T], F32R) for n in ("hi", "lo"))
        s = sb("s", [P, NCH, CH])
        a = sb("a", [P, NCH, CH])
        a_hi, a_lo = (sb("a_" + n, [P, NCH, CH], F32R) for n in ("hi", "lo"))
        wr = sb("wr", [P, 2, T]) if weighted else None
        with nc.Block() as block:
            @block.sync
            def _(sp):
                def load_rows(g, j):
                    for p0, p1, r in owner(j):
                        sp.dma_start(wr[p0:p1, j % 2], rows[bass.ds(g * rows_per_turn + r, 1)].to_broadcast(
                            [p1 - p0, T])).then_inc(rows_in[j % 2], 16)

                def do_turn(g, first):
                    for j in range(turn):
                        if not (first and j < 2):
                            sp.wait_ge(out_split, g * turn + (j - 1))
                            weights.load(sp, g * turn + j, j % 2)
                        if weighted:
                            if not (first and j < 2):
                                sp.wait_ge(gated, g * (2 * turn) + (2 * j - 2))
                            load_rows(g, j)

                do_turn(0, True)
                if units > turn:
                    with sp.Fori(1, units // turn) as g:
                        do_turn(g, False)

            @block.gpsimd
            def _(pool):
                def low_parts(i, half):
                    for part, hi_ready_, split_ in ((w_in_part, in_hi_ready, in_split),
                                                    (w_out_part, out_hi_ready, out_split)):
                        pool.wait_ge(hi_ready_, i * 2 + (half + 1))
                        pool.tensor_tensor(w_lo[:, half, part], w[:, half, part], w_hi[:, half, part].bitcast(F32),
                                           ALU.subtract).then_inc(split_, 1)

                with pool.Fori(0, pairs) as i:
                    for half in range(2):
                        low_parts(i, half)

            @block.tensor
            def _(pe):
                for n, (lhs_t, rhs) in enumerate(extra or []):
                    for m in range(DB):
                        for c in range(NCH):
                            pe.matmul(k.bank[:, 4 + 2 * m + c, :], lhs_t[:, tile(m)], rhs[:, chunk(c)],
                                      start=(n == 0), stop=False, skip_group_check=True)
                passes = ((w_hi, src_hi, a_hi), (w_hi, src_lo, a_lo), (w_lo, src_hi, a_hi))

                def up(i, n, first=False):
                    half, c = n // 2, n % 2
                    if c == 0:
                        pe.wait_ge(in_split, i * 2 + (half + 1))
                    if not (first and n < 2):
                        pe.wait_ge(up_used, i * 4 + (n - 1))
                    if first and n < 2:
                        pe.wait_ge(src_split, n + 1)
                    for part in range(2):
                        for b in range(DB):
                            at = b * 2 * P + part * P
                            for q, (wq, xq, _) in enumerate(passes):
                                last = pe.matmul(k.bank[:, 2 * c + part, :], wq[:, half, at:at + P],
                                                 xq[:, b, chunk(c)], start=(b == 0 and q == 0),
                                                 stop=(b == DB - 1 and q == 2))
                    last.then_inc(up_ready, 1)

                def down(i, n, first=False):
                    half, c = n // 2 % 2, n % 2
                    if c == 0:
                        pe.wait_ge(out_split, i * 2 + (n // 2 + 1))
                    pe.wait_ge(lo_ready, i * 4 + (n + 1))
                    for m in range(DB):
                        at = WI + m * P
                        for q, (wq, _, aq) in enumerate(passes):
                            last = pe.matmul(k.bank[:, 4 + 2 * m + c, :], wq[:, half, at:at + P], aq[:, c, :],
                                             start=(first and q == 0 and not extra), stop=False,
                                             skip_group_check=True)
                    last.then_inc(summed, 1)

                up(0, 0, True)
                up(0, 1, True)
                for n in range(2, 4):
                    up(0, n, True)
                    down(0, n - 2, True)
                with pe.Fori(1, pairs) as i:
                    for n in range(4):
                        up(i, n)
                        down(i, n - 2)
                down(pairs, -2)
                down(pairs, -1)

            @block.scalar
            def _(act):
                def high(i, unit, part, ready):
                    half = unit % 2
                    act.wait_ge(loaded[half], i * 32 + (32 + 32 * (unit // 2)))
                    act.activation(w_hi[:, half, part], w[:, half, part], ACT.Identity).then_inc(ready, 1)

                def pair(i, first, last):
                    for n in range(4):
                        half, c = n // 2, n % 2
                        if c == 0:
                            high(i, half, w_out_part, out_hi_ready)
                            if not (last and half):
                                high(i, half + 1, w_in_part, in_hi_ready)
                        act.wait_ge(up_ready, i * 4 + (n + 1))
                        act.activation(s[:, c, :], k.bank[:, 2 * c, :], ACT.Silu).then_inc(act_ready, 1)
                        act.wait_ge(gated, i * 4 + (n + 1))
                        if not (first and n < 2):
                            act.wait_ge(summed, i * 4 + (n - 1))
                        act.activation(a_hi[:, c, :], a[:, c, :], ACT.Identity).then_inc(hi_ready, 1)

                high(0, 0, w_in_part, in_hi_ready)
                for c in range(NCH):
                    act.activation(src_hi[:, :, chunk(c)], src[:, :, chunk(c)], ACT.Identity
                                   ).then_inc(src_hi_ready, 1)
                act.preload_act_table(ACT.Silu)
                pair(0, True, False)
                with act.Fori(1, pairs - 1) as i:
                    pair(i, False, False)
                pair(pairs - 1, False, True)

            @block.vector
            def _(dve):
                for c in range(NCH):
                    dve.wait_ge(src_hi_ready, c + 1)
                    dve.tensor_tensor(src_lo[:, :, chunk(c)], src[:, :, chunk(c)], src_hi[:, :, chunk(c)].bitcast(F32),
                                      ALU.subtract).then_inc(src_split, 1)

                def pair(i, first):
                    for n in range(4):
                        half, c = n // 2, n % 2
                        dve.wait_ge(act_ready, i * 4 + (n + 1))
                        last = dve.tensor_tensor(a[:, c, :], s[:, c, :], k.bank[:, 2 * c + 1, :], ALU.mult)
                        last.then_inc(up_used, 1)
                        if weighted:
                            dve.wait_ge(up_used, i * 4 + (n + 1))
                            if c == 0:
                                dve.wait_ge(rows_in[half], i * 32 + 32)
                            last = dve.tensor_tensor(a[:, c, :], a[:, c, :], wr[:, half, chunk(c)], ALU.mult)
                            last.then_inc(gated, 1)
                        else:
                            dve.wait_ge(up_used, i * 4 + (n + 1))
                            dve.sem_inc(gated, 1)
                        dve.wait_ge(hi_ready, i * 4 + (n + 1))
                        if not (first and n < 2):
                            dve.wait_ge(summed, i * 4 + (n - 1))
                        dve.tensor_tensor(a_lo[:, c, :], a[:, c, :], a_hi[:, c, :].bitcast(F32), ALU.subtract
                                          ).then_inc(lo_ready, 1)

                pair(0, True)
                with dve.Fori(1, pairs) as i:
                    pair(i, False)
                dve.wait_ge(summed, 4 * pairs)
                for m in range(DB):
                    for c in range(NCH):
                        last = dve.scalar_tensor_tensor(k.x[:, m, chunk(c)], k.bank[:, 4 + 2 * m + c, :],
                                                        gate[:, m:m + 1], k.x[:, m, chunk(c)], ALU.mult, ALU.add)
                last.then_inc(done, 1)


def owners(f, count=2):
    def pieces(j):
        out, at = [], j * P
        while at < (j + 1) * P:
            end = min((at // f + 1) * f, (j + 1) * P)
            out.append((at - j * P, end - j * P, at // f))
            at = end
        if len(out) == 1:
            out = [(0, P // 2, out[0][2]), (P // 2, P, out[0][2])]
        assert len(out) == count
        return out
    return pieces


def l0_attention(k, norm):
    nc, d = k.nc, k.dram
    H, W, KW = 8, 64, 192
    SCALE = 8.0
    w_in = k.sem("l0_w_in")
    v_w_in, v_ready, v_copied, g_ready, gate_exp, gate_one, gates_ready, mask_ready, qscale_in = (
        k.sem("l0_" + n) for n in ("v_w_in", "v_ready", "v_copied", "g_ready", "gate_exp", "gate_one", "gates_ready",
                                   "mask_ready", "qscale_in"))
    qk_ready, sq_ready, ss_ready, ss_clamped, rn_ready, qk_normed, scores_ready, scores_read, best_ready, probs_exp, probs_ready = (
        k.sem("l0_" + n) for n in ("qk_ready", "sq_ready", "ss_ready", "ss_clamped", "rn_ready", "qk_normed",
                                   "scores_ready", "scores_read", "best_ready", "probs_exp", "probs_ready"))
    h_hi_ready, h_split, wv_hi_ready, wv_split, w_hi_ready, w_split = (
        k.sem("l0_" + n) for n in ("h_hi_ready", "h_split", "wv_hi_ready", "wv_split", "w_hi_ready", "w_split"))
    pt_ready, pt_copied, pt_odd_copied, o_ready, o_copied, vh_ready, y_ready, y_done = (
        k.sem("l0_" + n) for n in ("pt_ready", "pt_copied", "pt_odd_copied", "o_ready", "o_copied", "vh_ready", "y_ready", "y_done"))
    with ExitStack() as ctx:
        def sb(n, shape, dt=F32):
            return ctx.enter_context(nc.sbuf_tensor("l0_" + n, shape, dt))
        wv = sb("wv", [P, DB, H * P])
        wv_hi, wv_lo = (sb("wv_" + n, [P, DB, H * P], F32R) for n in ("hi", "lo"))
        h_hi, h_lo = (sb("h_" + n, [P, DB, T], F32R) for n in ("hi", "lo"))
        wqk_hi, wqk_lo = (sb("wqk_" + n, [P, DB, 2 * P], F32R) for n in ("hi", "lo"))
        wo = sb("wo", [P, H, D])
        wg = sb("wg", [P, DB, H])
        bg = sb("bg", [P, H])
        scales = sb("scales", [P, 2])
        wqk = sb("wqk", [P, DB, 2 * P])
        v = sb("v", [P, TT, H * P])
        vh = sb("vh", [P, TT, P])
        gates = sb("gates", [P, TT, H])
        qk = sb("qk", [P, 2, W + T])
        sq = norm.sq[:].rearrange("p b (c q) -> p (b c) q", q=CH)
        rn = sb("rn", [P, 4, CH])
        mask = sb("mask", [P, 2, KW])
        sc = sb("sc", [P, TT, P + P])
        st = sb("st", [P, 4, TT])
        pt = sb("pt", [P, TT, 2, P])
        o = sb("o", [P, H, T])

        def turned(n):
            return k.bank[:, 2 + n, :].rearrange("p (t a q) -> p t a q", t=2, a=2)

        with nc.Block() as block:
            @block.sync
            def _(sp):
                sp.dma_start(wv[:], d["l0_wv"].rearrange("(b p) n -> p b n", p=P)).then_inc(v_w_in, 16)
                sp.dma_start(wg[:], d["l0_wg"].rearrange("(b p) n -> p b n", p=P)).then_inc(v_w_in, 16)
                sp.dma_start(bg[:], d["l0_bg"].to_broadcast([P, H])).then_inc(v_w_in, 16)
                sp.dma_start(scales[:], d["l0_scales"]).then_inc(qscale_in, 16)
                sp.dma_start(wqk[:], d["l0_wqk"][0].rearrange("(b p) n -> p b n", p=P)).then_inc(w_in, 16)
                sp.dma_start(wo[:], d["l0_wo"].rearrange("(h p) n -> p h n", p=P)).then_inc(qscale_in, 16)
                with sp.Fori(1, H) as h:
                    sp.wait_ge(w_split, h)
                    sp.dma_start(wqk[:], d["l0_wqk"][bass.ds(h, 1)].rearrange("u (b p) n -> p (u b) n", p=P)
                                 ).then_inc(w_in, 16)

            @block.gpsimd
            def _(pool):
                step = k.pool_chain
                pool.memset(qk[:, :, 0:W], 0.0)
                pool.memset(sc[:, :, 0:W], 0.0)
                step.link(pool, pool.memset(mask[:], 0.0))
                m0, m1 = mask[:, 0, :], mask[:, 1, :]
                for m in (m0, m1):
                    step.link(pool, pool.affine_select(out=m, in_=m, compare_op=ALU.is_ge, fill=NEG, base=W,
                                                       pattern=[[-1, KW]], channel_multiplier=1))
                    step.link(pool, pool.affine_select(out=m, in_=m, compare_op=ALU.is_ge, fill=NEG, base=0,
                                                       pattern=[[1, KW]], channel_multiplier=-1))
                pool.memset(mask[:, 0, 0:W], NEG).then_inc(mask_ready, 1)

                def values(h):
                    pool.wait_ge(o_copied, h * 2 + 2)
                    pool.tensor_copy(vh[:], v[:, :, bass.ds(h * P, P)]).then_inc(vh_ready, 1)

                def low_parts(h):
                    pool.wait_ge(w_hi_ready, h + 1)
                    pool.tensor_tensor(wqk_lo[:], wqk[:], wqk_hi[:].bitcast(F32), ALU.subtract).then_inc(w_split, 1)

                pool.wait_ge(wv_hi_ready, 1)
                pool.tensor_tensor(wv_lo[:], wv[:], wv_hi[:].bitcast(F32), ALU.subtract).then_inc(wv_split, 1)
                low_parts(0)
                pool.wait_ge(v_copied, 2 * TT)
                with pool.Fori(0, H - 1) as h:
                    low_parts(h + 1)
                    values(h)
                values(H - 1)

            @block.tensor
            def _(pe):
                norm.on_tensor(pe)
                norm.wait(pe)
                pe.wait_ge(v_w_in, 48)
                for t in range(TT):
                    for b in range(DB):
                        last = pe.matmul(k.bank[:, 2, t * H:(t + 1) * H], k.h[:, b, tile(t)], wg[:, b, :],
                                         start=(b == 0), stop=(b == DB - 1))
                last.then_inc(g_ready, 1)
                pe.wait_ge(wv_split, 1)
                for t in range(TT):
                    if t % (TT // NCH) == 0:
                        pe.wait_ge(h_split, t // (TT // NCH) + 1)
                    for n in range(2):
                        j = 2 * t + n
                        if j >= 2:
                            pe.wait_ge(v_copied, j - 1)
                        passes = [(hq, wq, b) for hq, wq in ((h_hi, wv_hi), (h_hi, wv_lo), (h_lo, wv_hi))
                                  for b in range(DB)]
                        for q, (hq, wq, b) in enumerate(passes):
                            last = pe.matmul(k.bank[:, j % 2, :], hq[:, b, tile(t)], wq[:, b, chunk(n)],
                                             start=(q == 0), stop=(q == len(passes) - 1))
                        last.then_inc(v_ready, 1)

                def project(h):
                    pe.wait_ge(w_split, h + 1)
                    for j in range(4):
                        passes = [(wq, hq, b) for wq, hq in ((wqk_hi, h_hi), (wqk_hi, h_lo), (wqk_lo, h_hi))
                                  for b in range(DB)]
                        for q, (wq, hq, b) in enumerate(passes):
                            last = pe.matmul(k.bank[:, 4 + j, :], wq[:, b, tile(j // 2)], hq[:, b, chunk(j % 2)],
                                             start=(q == 0), stop=(q == len(passes) - 1))
                        last.then_inc(qk_ready, 1)

                def square_sums(h):
                    for j in range(4):
                        pe.wait_ge(sq_ready, h * 4 + (j + 1))
                        if j >= 2:
                            pe.wait_ge(ss_clamped, h * 4 + (j - 1))
                        pe.matmul(k.bank[:, j % 2, :], k.ones[:], sq[:, j, :], start=True, stop=True
                                  ).then_inc(ss_ready, 1)

                def turn_probs(h, part):
                    pe.wait_ge(probs_ready, h * 2 + (part + 1))
                    if part:
                        pe.wait_ge(pt_copied, h * 2 + 1)
                        pe.wait_ge(pt_odd_copied, h * 2 + 1)
                    for t in range(4 * part, 4 * part + 4):
                        for side in range(2):
                            at = (t % 2) * 256 + side * P
                            last = pe.transpose(k.bank[:, 2 + t // 2 % 2, at:at + P], sc[:, t, tile(side)],
                                                k.ident[:])
                        if t % 2:
                            last.then_inc(pt_ready, 1)

                def mix_values(h, part):
                    pe.wait_ge(pt_copied, h * 2 + (part + 1))
                    pe.wait_ge(pt_odd_copied, h * 2 + (part + 1))
                    for t in range(4 * part, 4 * part + 4):
                        out = k.bank[:, part, (t % 4) * P:(t % 4 + 1) * P]
                        if t:
                            pe.matmul(out, vh[:, t - 1, :], pt[:, t, 0, :], start=True, stop=False)
                        last = pe.matmul(out, vh[:, t, :], pt[:, t, 1, :], start=(t == 0), stop=True)
                    last.then_inc(o_ready, 1)

                def head(h, final):
                    pe.wait_ge(qk_normed, h * 4 + 4)
                    pe.wait_ge(ss_clamped, h * 4 + 4)
                    for n, t in enumerate((4, 5, 6, 7, 0, 1, 2, 3)):
                        if n == 4:
                            pe.wait_ge(o_copied, h * 2 + 2)
                        last = pe.matmul(k.bank[:, t // 2, (t % 2) * 256:(t % 2) * 256 + KW],
                                         qk[:, 0, W + t * P:W + (t + 1) * P], qk[:, 1, t * P:t * P + KW],
                                         start=True, stop=True)
                    last.then_inc(scores_ready, 1)
                    if not final:
                        project(h + 1)
                        pe.wait_ge(scores_read, h + 1)
                        square_sums(h + 1)
                    turn_probs(h, 0)
                    turn_probs(h, 1)
                    if not final:
                        pe.wait_ge(ss_clamped, h * 4 + 8)
                    pe.wait_ge(vh_ready, h + 1)
                    mix_values(h, 0)
                    mix_values(h, 1)

                project(0)
                pe.wait_ge(v_copied, 2 * TT)
                square_sums(0)
                pe.wait_ge(gates_ready, 1)
                with pe.Fori(0, H - 1) as h:
                    head(h, False)
                head(H - 1, True)
                pe.wait_ge(qscale_in, 32)
                pe.wait_ge(o_copied, 2 * H + 2)
                for m in range(DB):
                    for c in range(NCH):
                        for h in range(H):
                            last = pe.matmul(k.bank[:, 2 * m + c, :], wo[:, h, tile(m)], o[:, h, chunk(c)],
                                             start=(h == 0), stop=(h == H - 1))
                        last.then_inc(y_ready, 1)

            @block.scalar
            def _(act):
                act.wait_ge(v_w_in, 48)
                act.activation(wv_hi[:], wv[:], ACT.Identity).then_inc(wv_hi_ready, 1)
                norm.on_scalar(act)
                step = k.act_chain
                act.preload_act_table_set(EXP_LN)

                def high_parts(h):
                    act.wait_ge(w_in, h * 16 + 16)
                    act.activation(wqk_hi[:], wqk[:], ACT.Identity).then_inc(w_hi_ready, 1)

                norm.wait(act)
                for c in range(NCH):
                    act.activation(h_hi[:, :, chunk(c)], k.h[:, :, chunk(c)], ACT.Identity).then_inc(h_hi_ready, 1)
                high_parts(0)
                for j in range(2 * TT):
                    act.wait_ge(v_ready, j + 1)
                    act.activation(v[:, j // 2, chunk(j % 2)], k.bank[:, j % 2, :], ACT.Identity
                                   ).then_inc(v_copied, 1)
                act.wait_ge(gate_one, 1)
                act.activation(gates[:], gates[:], ACT.Exp, scale=-1.0).then_inc(gate_exp, 1)
                act.sem_inc(o_copied, 2)

                def square(h, j):
                    act.wait_ge(qk_ready, h * 4 + (j + 1))
                    act.activation(sq[:, j, :], k.bank[:, 4 + j, :], ACT.Square).then_inc(sq_ready, 1)

                def factors(h, n):
                    both = rn[:, 2 * n:2 * n + 2, :]
                    act.wait_ge(ss_clamped, h * 4 + (2 * n + 2))
                    step.link(act, act.activation(both, both, ACT.Ln, scale=65536.0))
                    act.activation(both, both, ACT.Exp, scale=-0.5).then_inc(rn_ready, 1)

                def head(h, final):
                    if not final:
                        high_parts(h + 1)
                        for j in range(3):
                            square(h + 1, j)
                    act.wait_ge(best_ready, h + 1)
                    for t in range(TT):
                        act.activation(sc[:, t, W:W + KW], sc[:, t, W:W + KW], ACT.Exp, bias=st[:, 0, t:t + 1],
                                       accum_out=st[:, 1, t:t + 1]).then_inc(probs_exp, 1)
                    if not final:
                        square(h + 1, 3)
                    for n in range(2):
                        if not final:
                            factors(h + 1, n)
                        act.wait_ge(pt_ready, h * 4 + (2 * n + 1))
                        act.activation(pt[:, 4 * n:4 * n + 2], turned(0), ACT.Identity).then_inc(pt_copied, 1)
                    for c in range(2):
                        act.wait_ge(o_ready, h * 2 + (c + 1))
                        act.activation(o[:, bass.ds(h, 1), chunk(c)], k.bank[:, c:c + 1, :], ACT.Identity
                                       ).then_inc(o_copied, 1)

                for j in range(4):
                    square(0, j)
                for n in range(2):
                    factors(0, n)
                with act.Fori(0, H - 1) as h:
                    step.enter(h, 2)
                    head(h, False)
                step.leave(H - 1)
                head(H - 1, True)

            @block.vector
            def _(dve):
                norm.on_vector(dve)
                step = k.dve_chain
                for c in range(NCH):
                    dve.wait_ge(h_hi_ready, c + 1)
                    dve.tensor_tensor(h_lo[:, :, chunk(c)], k.h[:, :, chunk(c)], h_hi[:, :, chunk(c)].bitcast(F32),
                                      ALU.subtract).then_inc(h_split, 1)
                dve.wait_ge(v_w_in, 48)
                dve.wait_ge(g_ready, 1)
                dve.tensor_tensor(gates[:], k.bank[:, 2, 0:TT * H].rearrange("p (t h) -> p t h", t=TT),
                                  over(bg[:], TT), ALU.add).then_inc(gate_one, 1)
                dve.wait_ge(gate_exp, 1)
                step.link(dve, dve.tensor_scalar(gates[:], gates[:], 1.0, None, ALU.add))
                dve.reciprocal(gates[:], gates[:]).then_inc(gates_ready, 1)
                dve.wait_ge(gates_ready, 1)
                dve.wait_ge(qscale_in, 32)
                step.link(dve, dve.tensor_scalar(scales[:], scales[:], 256.0, None, ALU.mult))
                step.link(dve, dve.tensor_scalar(scales[:, 0:1], scales[:, 0:1], SCALE, None, ALU.mult))
                dve.wait_ge(mask_ready, 1)

                def clamp(h, j):
                    dve.wait_ge(ss_ready, h * 4 + (j + 1))
                    dve.tensor_scalar(rn[:, j, :], k.bank[:, j % 2, :], 1.0e-24, None, ALU.max
                                      ).then_inc(ss_clamped, 1)

                def normalise(h, n):
                    dve.wait_ge(rn_ready, h * 2 + (n + 1))
                    for c in range(NCH):
                        j = 2 * n + c
                        dve.scalar_tensor_tensor(qk[:, n, W + c * CH:W + (c + 1) * CH], k.bank[:, 4 + j, :],
                                                 scales[:, n:n + 1], rn[:, j, :], ALU.mult, ALU.mult
                                                 ).then_inc(qk_normed, 1)

                def head(h, final):
                    dve.wait_ge(scores_ready, h + 1)
                    banks = k.bank[:, 0:4, :].rearrange("p n (a q) -> p (n a) q", a=2)
                    s = sc[:, :, W:W + KW]
                    dve.tensor_tensor(s[:, 0:1], banks[:, 0:1, 0:KW], mask[:, 0:1], ALU.add)
                    step.link(dve, dve.tensor_tensor(s[:, 1:TT], banks[:, 1:TT, 0:KW], over(mask[:, 1, :], TT - 1),
                                                     ALU.add))
                    dve.sem_inc(scores_read, 1)
                    step.link(dve, dve.tensor_reduce(st[:, 2, :], s, AX.X, ALU.max))
                    dve.tensor_scalar(st[:, 0, :], st[:, 2, :], -1.0, None, ALU.mult).then_inc(best_ready, 1)
                    step.link(dve, dve.tensor_copy(st[:, 3, :], gates[:, :, bass.ds(h, 1)].rearrange(
                        "p t h -> p (t h)")))
                    if not final:
                        clamp(h + 1, 0)
                        clamp(h + 1, 1)
                    for part in range(2):
                        four = slice(4 * part, 4 * part + 4)
                        dve.wait_ge(probs_exp, h * TT + (4 * part + 4))
                        step.link(dve, dve.reciprocal(st[:, 2, four], st[:, 1, four]))
                        step.link(dve, dve.tensor_tensor(st[:, 2, four], st[:, 2, four], st[:, 3, four], ALU.mult))
                        dve.tensor_tensor(s[:, four], s[:, four], over(st[:, 2, four], KW, 2), ALU.mult
                                          ).then_inc(probs_ready, 1)
                        if not final:
                            clamp(h + 1, 2 + part)
                    for n in range(2):
                        dve.wait_ge(pt_ready, h * 4 + (2 * n + 2))
                        dve.tensor_copy(pt[:, 4 * n + 2:4 * n + 4], turned(1)).then_inc(pt_odd_copied, 1)
                        if not final:
                            normalise(h + 1, n)

                for j in range(4):
                    clamp(0, j)
                for n in range(2):
                    normalise(0, n)
                with dve.Fori(0, H - 1) as h:
                    step.enter(h, 7)
                    head(h, False)
                step.leave(H - 1)
                head(H - 1, True)
                for j in range(4):
                    dve.wait_ge(y_ready, j + 1)
                    m, c = j // 2, j % 2
                    last = dve.scalar_tensor_tensor(k.x[:, m, chunk(c)], k.bank[:, j, :],
                                                    k.mod[:, 0, GATE_A + m:GATE_A + m + 1], k.x[:, m, chunk(c)],
                                                    ALU.mult, ALU.add)
                last.then_inc(y_done, 1)


def l0_ffn(k, norm, mods):
    nc, d = k.nc, k.dram
    TOP, KEYS, E, EB = 8, 64, 512, 4
    w_in, q_ready, q_copied, route_ready, route_copied = (
        k.sem("l0f_" + n) for n in ("w_in", "q_ready", "q_copied", "route_ready", "route_copied"))
    best_ready, best_exp, total_ready, total_ln, shift_ready, sums_ready, pair_exp, weights_ready, wt_ready = (
        k.sem("l0f_" + n) for n in ("best_ready", "best_exp", "total_ready", "total_ln", "shift_ready", "sums_ready",
                                    "pair_exp", "weights_ready", "wt_ready"))
    s_ready, s_act, s_gated = (k.sem("l0f_" + n) for n in ("s_ready", "s_act", "s_gated"))
    INNER = [(e, 0, 6 + e % 2) for e in range(EB)] + [(e, 1, e) for e in range(EB)]
    WT_BANKS = (4, 5, 4, 5, 4, 5, 6, 7)
    with ExitStack() as outer:
        ar = outer.enter_context(nc.sbuf_tensor("l0f_ar", [P, EB, T], F32))
        ue = outer.enter_context(nc.sbuf_tensor("l0f_ue", [P, EB, D], F32))
        weights = UnitWeights(k, outer, "l0m", d["l0f_win"], d["l0f_wout"])
        with ExitStack() as ctx:
            def sb(n, shape):
                return ctx.enter_context(nc.sbuf_tensor("l0f_" + n, shape, F32))
            wq = sb("wq", [P, DB, P])
            keys = sb("keys", [KEYS, 2, KEYS])
            de = sb("de", [P, DB, E])
            q = sb("q", [KEYS, 2, T])
            r = sb("r", [P, TT, 2, KEYS])
            s8 = sb("s8", [P, 2, TT, TOP])
            pairs = sb("pairs", [P, TT, TOP, TOP])
            best = sb("best", [P, TT, TOP])
            be = sb("be", [P, TT, TOP])
            st = sb("st", [P, 4, TT])
            f = sb("f", [P, 2, TOP, KEYS])
            fe = sb("fe", [P, 2, E])
            w = sb("w", [P, 2, E])
            later = range(1, 4)
            mods.hold(ctx, later)
            with nc.Block() as block:
                @block.gpsimd
                def _(pool):
                    mods.add_blocks(pool, later)

                @block.sync
                def _(sp):
                    sp.dma_start(wq[:], d["l0f_wq"].rearrange("(b p) n -> p b n", p=P)).then_inc(w_in, 16)
                    sp.dma_start(keys[:], d["l0f_keys"].rearrange("g p n -> p g n")).then_inc(w_in, 16)
                    sp.dma_start(de[:], d["l0f_de"].rearrange("(b p) n -> p b n", p=P)).then_inc(w_in, 16)
                    sp.dma_start(ue[:], d["l0f_ue"].rearrange("(b p) n -> p b n", p=P)).then_inc(w_in, 16)
                    weights.load_first(sp)
                    mods.on_sync(sp, later)

                @block.tensor
                def _(pe):
                    norm.on_tensor(pe)
                    norm.wait(pe)
                    pe.wait_ge(w_in, 64)
                    for g in range(2):
                        for b in range(DB):
                            last = pe.matmul(k.bank[:, g, :], wq[:, b, :], k.h[:, b, chunk(g)],
                                             start=(b == 0), stop=(b == DB - 1))
                        last.then_inc(q_ready, 1)
                    pe.wait_ge(q_copied, 2)
                    for t in range(TT):
                        for g in range(2):
                            last = pe.matmul(k.bank[:, 2 + t // 4, (t % 4) * P + g * KEYS:(t % 4) * P + (g + 1) * KEYS],
                                             q[:, g, tile(t)], keys[:, g, :], start=True, stop=True)
                    last.then_inc(route_ready, 1)
                    for n, (e, c, bank) in enumerate(INNER):
                        if n in (2, 3):
                            pe.wait_ge(s_act, n - 1)
                        if bank == 2:
                            pe.wait_ge(route_copied, 1)
                        for b in range(DB):
                            last = pe.matmul(k.bank[:, bank, :], de[:, b, tile(e)], k.h[:, b, chunk(c)],
                                             start=(b == 0), stop=(b == DB - 1))
                        last.then_inc(s_ready, 1)
                    pe.wait_ge(s_act, 4)
                    mods.on_tensor(pe, later, 6)
                    for t in range(TT):
                        pe.wait_ge(weights_ready, t + 1)
                        if WT_BANKS[t] < 6 and t >= 2:
                            pe.wait_ge(s_gated, t - 1)
                        elif t == 6:
                            pe.wait_ge(mods.copied, 2)
                        for e in range(EB):
                            last = pe.transpose(k.bank[:, WT_BANKS[t], tile(e)], w[:, t % 2, tile(e)], k.ident[:])
                        last.then_inc(wt_ready, 1)

                @block.scalar
                def _(act):
                    norm.on_scalar(act)
                    act.preload_act_table_set(EXP_LN)
                    act.wait_ge(route_ready, 1)
                    act.activation(r[:].rearrange("p t g e -> p (t g e)"),
                                   k.bank[:, 2:4, :].rearrange("p b n -> p (b n)"), ACT.Identity
                                   ).then_inc(route_copied, 1)

                    def inner(n):
                        e, c, bank = INNER[n]
                        act.wait_ge(s_ready, n + 1)
                        act.activation(ar[:, e, chunk(c)], k.bank[:, bank, :], ACT.Silu).then_inc(s_act, 1)

                    act.preload_act_table(ACT.Silu)
                    for n in range(4):
                        inner(n)
                    act.preload_act_table_set(EXP_LN)
                    mods.on_scalar(act, later)
                    act.wait_ge(best_ready, 1)
                    act.activation(be[:], be[:], ACT.Exp).then_inc(best_exp, 1)
                    act.wait_ge(total_ready, 1)
                    act.activation(st[:, 2, :], st[:, 1, :], ACT.Ln).then_inc(total_ln, 1)
                    act.wait_ge(shift_ready, 1)
                    for t in range(TT):
                        act.wait_ge(sums_ready, t + 1)
                        act.activation(fe[:, t % 2, :], f[:, t % 2].rearrange("p i j -> p (i j)"), ACT.Exp,
                                       bias=st[:, 0, t:t + 1]).then_inc(pair_exp, 1)
                    act.preload_act_table(ACT.Silu)
                    for n in range(4, 8):
                        inner(n)

                @block.vector
                def _(dve):
                    norm.on_vector(dve)
                    step = k.dve_chain
                    for g in range(2):
                        dve.wait_ge(q_ready, g + 1)
                        view = q[:, g, :].rearrange("p (t o) -> p t o", o=2)
                        dve.tensor_copy(view[:, :, 0], k.bank[0:KEYS, g, :])
                        dve.tensor_copy(view[:, :, 1], k.bank[KEYS:P, g, :]).then_inc(q_copied, 1)
                    dve.wait_ge(route_copied, 1)
                    for t in range(TT):
                        for g in range(2):
                            last = dve.max(s8[:, g, t, :], r[:, t, g, :])
                    step.link(dve, last)
                    step.link(dve, dve.tensor_tensor(pairs[:], over(s8[:, 0], TOP, 3), over(s8[:, 1], TOP, 2), ALU.add))
                    for t in range(TT):
                        last = dve.max(best[:, t, :], pairs[:, t].rearrange("p i j -> p (i j)"))
                    step.link(dve, last)
                    dve.tensor_tensor(be[:], best[:], over(best[:, :, 0], TOP, 2), ALU.subtract
                                      ).then_inc(best_ready, 1)

                    def pair_scores(t):
                        if t >= 2:
                            dve.wait_ge(pair_exp, t - 1)
                        dve.tensor_tensor(f[:, t % 2], over(r[:, t, 0, 0:TOP], KEYS, 2), over(r[:, t, 1, :], TOP, 1),
                                          ALU.add).then_inc(sums_ready, 1)

                    def gate(t):
                        dve.wait_ge(wt_ready, t + 1)
                        dve.wait_ge(s_act, 4 + t // 4 * 4)
                        xs = ar[:, :, tile(t)]
                        dve.tensor_tensor(xs, xs, k.bank[:, WT_BANKS[t], :].rearrange("p (e q) -> p e q", e=EB), ALU.mult
                                          ).then_inc(s_gated, 1)

                    dve.wait_ge(best_exp, 1)
                    dve.tensor_reduce(st[:, 1, :], be[:], AX.X, ALU.add).then_inc(total_ready, 1)
                    pair_scores(0)
                    dve.wait_ge(total_ln, 1)
                    dve.scalar_tensor_tensor(st[:, 0, :], best[:, :, 0], -1.0, st[:, 2, :], ALU.mult, ALU.subtract
                                             ).then_inc(shift_ready, 1)
                    for t in range(TT):
                        if t + 1 < TT:
                            pair_scores(t + 1)
                        dve.wait_ge(pair_exp, t + 1)
                        dve.wait_ge(sums_ready, t + 1)
                        if t >= 2:
                            dve.wait_ge(wt_ready, t - 1)
                        wv = w[:, t % 2, :]
                        step.link(dve, dve.scalar_tensor_tensor(wv, f[:, t % 2].rearrange("p i j -> p (i j)"),
                                                                best[:, t, TOP - 1:TOP], fe[:, t % 2, :],
                                                                ALU.is_ge, ALU.mult))
                        step.link(dve, dve.tensor_reduce(st[:, 3, t:t + 1], wv[:, 0:E - 1], AX.X, ALU.add))
                        dve.tensor_scalar(wv[:, E - 1:E], st[:, 3, t:t + 1], -1.0, 1.0, ALU.mult, ALU.add
                                          ).then_inc(weights_ready, 1)
                        if 1 <= t <= 4:
                            gate(t - 1)
                        if t == 2:
                            mods.finish(dve, later, 6)
                    for t in range(4, TT):
                        gate(t)
        gated_units(k, "l0m", weights, 8, gate_col(k, 0, GATE_B), turn=2,
                    extra=[(ue[:, e, :], ar[:, e, :]) for e in range(EB)])


def l1_attention(k, norm):
    nc, d = k.nc, k.dram
    H = 2
    names = ("w_in", "z_ready", "z_abs_ready", "z_exp", "one_plus_ready", "z_ln", "gates_ready", "alpha_ready",
             "alpha_ln", "cla_ready", "qkv_ready", "qkv_biased", "k_squared", "k_sum_ready", "k_rn_ready", "k_normed",
             "la_tri_ready", "row_ready", "row_exp", "dt_ready", "dt_exp", "decay_ready", "to_end_ready", "to_end_exp",
             "kw_ready", "qk_turned", "qt_copied", "qg_ready", "st_ready", "attn_ready", "y_ready", "delta_ready",
             "state_ready", "x_added", "const_ready")
    s = {n: k.sem("l1_" + n) for n in names}
    with ExitStack() as ctx:
        def sb(n, shape):
            return ctx.enter_context(nc.sbuf_tensor("l1_" + n, shape, F32))
        w = sb("w", [P, DB, 3 * D])
        wz = sb("wz", [P, DB, 4])
        bias = sb("bias", [P, 3 * D])
        bz = sb("bz", [P, 4])
        tri = sb("tri", [P, P])
        late = sb("late", [P, P])
        z = sb("z", [P, TT, 4])
        beta = sb("beta", [P, TT, H])
        zt = sb("zt", [P, 2, TT, 4])
        la = sb("la", [P, TT, H])
        cla = sb("cla", [P, TT, H])
        qkv = sb("qkv", [P, TT, 3, H, P])
        sq = sb("sq", [P, P])
        rn = sb("rn", [P, TT, H])
        la_tri = sb("la_tri", [P, TT, H, P])
        dt = sb("dt", [P, TT, H, P])
        ecr = sb("ecr", [P, TT, H, P])
        te = sb("te", [P, TT, H])
        kw = sb("kw", [P, TT, H, P])
        qkt = sb("qkt", [P, TT, 2, H, P])
        qg = sb("qg", [P, TT, H, P])
        at = sb("at", [P, TT, H, P])
        state = sb("state", [P, TT, H, P])

        def all_of(m):
            return m[:].rearrange("p t h q -> p (t h) q")

        def banks(first):
            return k.bank[:, first:first + 4, :].rearrange("p n (u q) -> p (n u) q", q=P)

        def each(m):
            return over(m.rearrange("p t h -> p (t h)"), P, 2)

        with nc.Block() as block:
            @block.sync
            def _(sp):
                sp.dma_start(wz[:], d["l1_wz"].rearrange("(b p) n -> p b n", p=P)).then_inc(s["w_in"], 16)
                sp.dma_start(bz[:], d["l1_bz"].to_broadcast([P, 4])).then_inc(s["w_in"], 16)
                sp.dma_start(w[:], d["l1_w"].rearrange("(b p) n -> p b n", p=P)).then_inc(s["w_in"], 16)
                sp.dma_start(bias[:], d["l1_b"].to_broadcast([P, 3 * D])).then_inc(s["w_in"], 16)

            @block.gpsimd
            def _(pool):
                step = k.pool_chain
                pool.memset(tri[:], 1.0)
                step.link(pool, pool.memset(late[:], 0.0))
                step.link(pool, pool.affine_select(out=tri[:], in_=tri[:], compare_op=ALU.is_ge, fill=0.0, base=0,
                                                   pattern=[[1, P]], channel_multiplier=-1))
                pool.affine_select(out=late[:], in_=late[:], compare_op=ALU.is_ge, fill=NEG, base=0,
                                   pattern=[[1, P]], channel_multiplier=-1).then_inc(s["const_ready"], 1)
                pool.wait_ge(s["alpha_ln"], 1)
                pool.tensor_tensor(all_of(la_tri), over(tri[:], TT * H), each(la[:]), ALU.mult
                                   ).then_inc(s["la_tri_ready"], 1)
                pool.wait_ge(s["dt_exp"], 1)
                pool.wait_ge(s["qkv_biased"], 4)
                pool.tensor_tensor(dt[:], dt[:], over(beta[:], P, 3), ALU.mult).then_inc(s["decay_ready"], 1)
                pool.wait_ge(s["row_exp"], 1)
                for part in range(2):
                    four = slice(4 * part, 4 * part + 4)
                    pool.wait_ge(s["qt_copied"], 4 * part + 4)
                    pool.tensor_tensor(qg[:, four], qkt[:, four, 0], ecr[:, four], ALU.mult).then_inc(s["qg_ready"], 1)

            @block.tensor
            def _(pe):
                norm.on_tensor(pe)
                norm.wait(pe)
                pe.wait_ge(s["w_in"], 64)
                for t in range(TT):
                    for b in range(DB):
                        last = pe.matmul(k.bank[:, 7, t * 4:t * 4 + 4], k.h[:, b, tile(t)], wz[:, b, :],
                                         start=(b == 0), stop=(b == DB - 1))
                last.then_inc(s["z_ready"], 1)
                for t in range(TT):
                    if t >= 2:
                        pe.wait_ge(s["qkv_biased"], t - 1)
                    for part, width in ((0, 2 * D), (1, D)):
                        for b in range(DB):
                            last = pe.matmul(k.bank[:, t % 2 * 2 + part, 0:width], k.h[:, b, tile(t)],
                                             w[:, b, part * 2 * D:part * 2 * D + width], start=(b == 0),
                                             stop=(b == DB - 1))
                    last.then_inc(s["qkv_ready"], 1)
                    if t == 3:
                        pe.wait_ge(s["const_ready"], 1)
                        pe.wait_ge(s["alpha_ln"], 1)
                        pe.matmul(k.bank[:, 7, 64:64 + TT * H], tri[:], la[:].rearrange("p t h -> p (t h)"),
                                  start=True, stop=True).then_inc(s["cla_ready"], 1)
                    if t == 5:
                        pe.wait_ge(s["la_tri_ready"], 1)
                        pe.wait_ge(s["gates_ready"], 1)
                        for n in range(4):
                            last = pe.matmul(k.bank[:, 4 + n, :], k.ones[:], la_tri[:, 2 * n:2 * n + 2].rearrange(
                                "p t h q -> p (t h q)"), start=True, stop=True)
                        last.then_inc(s["row_ready"], 1)
                pe.wait_ge(s["k_normed"], 1)

                def scores(t):
                    pe.wait_ge(s["qt_copied"], t + 1)
                    for h in range(H):
                        last = pe.matmul(k.bank[:, 4 + t // 2, (t % 2 * 2 + h) * P:(t % 2 * 2 + h + 1) * P],
                                         qkt[:, t, 1, h, :], qkt[:, t, 0, h, :], start=True, stop=True)
                    last.then_inc(s["st_ready"], 1)

                for t in range(TT):
                    if t >= 4:
                        pe.wait_ge(s["qt_copied"], t - 3)
                    for a in range(2):
                        for h in range(H):
                            last = pe.transpose(k.bank[:, t % 4, tile(2 * a + h)], qkv[:, t, a, h, :], k.ident[:])
                    last.then_inc(s["qk_turned"], 1)
                    if t == 2:
                        pe.wait_ge(s["dt_ready"], 1)
                        pe.wait_ge(s["row_exp"], 1)
                    if t >= 2:
                        scores(t - 2)
                scores(TT - 2)
                scores(TT - 1)
                pe.wait_ge(s["kw_ready"], 1)
                for t in range(TT - 1):
                    for h in range(H):
                        last = pe.matmul(k.bank[:, t // 2, (t % 2 * 2 + h) * P:(t % 2 * 2 + h + 1) * P],
                                         kw[:, t, h, :], qkv[:, t, 2, h, :], start=True, stop=True)
                    if t % 2 or t == TT - 2:
                        last.then_inc(s["delta_ready"], 1)
                pe.wait_ge(s["attn_ready"], 1)
                for c in range(NCH):
                    pe.wait_ge(s["qg_ready"], c + 1)
                    for t in range(4 * c, 4 * c + 4):
                        if t:
                            pe.wait_ge(s["state_ready"], t)
                        for h in range(H):
                            out = k.bank[:, 4 + 2 * c + h, (t % 4) * P:(t % 4 + 1) * P]
                            last = pe.matmul(out, qkv[:, t, 2, h, :], at[:, t, h, :], start=True, stop=(t == 0))
                            if t:
                                last = pe.matmul(out, state[:, t, h, :], qg[:, t, h, :], start=False, stop=True)
                    last.then_inc(s["y_ready"], 1)

            @block.scalar
            def _(act):
                norm.on_scalar(act)
                step = k.act_chain
                act.wait_ge(s["z_abs_ready"], 1)
                act.activation(zt[:, 0], zt[:, 0], ACT.Exp, scale=-1.0).then_inc(s["z_exp"], 1)
                act.wait_ge(s["one_plus_ready"], 1)
                act.activation(zt[:, 1, :, 0:H], zt[:, 0, :, 0:H], ACT.Ln).then_inc(s["z_ln"], 1)
                act.wait_ge(s["alpha_ready"], 1)
                act.activation(la[:], zt[:, 0, :, H:2 * H], ACT.Ln, bias=k.eps[:, 3:4]).then_inc(s["alpha_ln"], 1)
                for t in range(TT):
                    act.wait_ge(s["qkv_biased"], t + 1)
                    for h in range(H):
                        last = act.activation(sq[:], qkv[:, t, 1, h, :], ACT.Square, accum_out=rn[:, t, h:h + 1])
                        step.link(act, last)
                act.sem_inc(s["k_squared"], 1)
                act.wait_ge(s["k_sum_ready"], 1)
                step.link(act, act.activation(rn[:], rn[:], ACT.Ln, scale=65536.0))
                act.activation(rn[:], rn[:], ACT.Exp, scale=-0.5).then_inc(s["k_rn_ready"], 1)
                act.wait_ge(s["row_ready"], 1)
                act.activation(ecr[:].rearrange("p t h q -> p (t h q)"), k.bank[:, 4:8, :].rearrange(
                    "p n q -> p (n q)"), ACT.Exp).then_inc(s["row_exp"], 1)
                act.wait_ge(s["to_end_ready"], 1)
                act.activation(te[:], te[:], ACT.Exp).then_inc(s["to_end_exp"], 1)
                act.wait_ge(s["dt_ready"], 1)
                act.activation(dt[:].rearrange("p t h q -> p (t h q)"), dt[:].rearrange("p t h q -> p (t h q)"),
                               ACT.Exp).then_inc(s["dt_exp"], 1)
                for t in range(TT):
                    act.wait_ge(s["qk_turned"], t + 1)
                    act.activation(qkt[:, t].rearrange("p a h q -> p (a h q)"), k.bank[:, t % 4, :], ACT.Identity
                                   ).then_inc(s["qt_copied"], 1)

            @block.vector
            def _(dve):
                norm.on_vector(dve)
                step = k.dve_chain

                def add_bias(t):
                    dve.wait_ge(s["qkv_ready"], t + 1)
                    dve.tensor_tensor(qkv[:, t].rearrange("p a h q -> p (a h q)"),
                                      k.bank[:, t % 2 * 2:t % 2 * 2 + 2, :].rearrange("p n q -> p (n q)")[:, 0:3 * D],
                                      bias[:], ALU.add).then_inc(s["qkv_biased"], 1)

                dve.wait_ge(s["w_in"], 64)
                dve.wait_ge(s["z_ready"], 1)
                step.link(dve, dve.tensor_tensor(z[:], k.bank[:, 7, 0:TT * 4].rearrange("p (t n) -> p t n", t=TT),
                                                 over(bz[:], TT), ALU.add))
                step.link(dve, dve.tensor_scalar(zt[:, 1], z[:], -1.0, None, ALU.mult))
                dve.tensor_tensor(zt[:, 0, :, 0:H], z[:, :, 0:H], zt[:, 1, :, 0:H], ALU.max)
                dve.tensor_copy(zt[:, 0, :, H:], z[:, :, H:]).then_inc(s["z_abs_ready"], 1)
                dve.wait_ge(s["z_exp"], 1)
                dve.tensor_scalar(zt[:, 0], zt[:, 0], 1.0, None, ALU.add).then_inc(s["one_plus_ready"], 1)
                dve.wait_ge(s["one_plus_ready"], 1)
                dve.reciprocal(zt[:, 0, :, H:], zt[:, 0, :, H:]).then_inc(s["alpha_ready"], 1)
                add_bias(0)
                dve.wait_ge(s["z_ln"], 1)
                step.link(dve, dve.scalar_tensor_tensor(beta[:], z[:, :, 0:H], 0.0, zt[:, 1, :, 0:H], ALU.max,
                                                        ALU.add))
                for t in range(1, 4):
                    add_bias(t)
                dve.wait_ge(s["cla_ready"], 1)
                dve.tensor_copy(cla[:].rearrange("p t h -> p (t h)"), k.bank[:, 7, 64:64 + TT * H]
                                ).then_inc(s["gates_ready"], 1)
                for t in range(4, TT):
                    add_bias(t)
                dve.wait_ge(s["k_squared"], 1)
                dve.tensor_scalar(rn[:], rn[:], 1.0e-24, None, ALU.max).then_inc(s["k_sum_ready"], 1)
                dve.wait_ge(s["row_exp"], 1)
                dve.wait_ge(s["gates_ready"], 1)
                dve.wait_ge(s["const_ready"], 1)
                dve.tensor_tensor(te[:].rearrange("p t h -> p (t h)"), banks(4)[:, :, P - 1],
                                  cla[:].rearrange("p t h -> p (t h)"), ALU.subtract).then_inc(s["to_end_ready"], 1)
                dve.wait_ge(s["k_rn_ready"], 1)
                step.link(dve, dve.tensor_scalar(rn[:], rn[:], 256.0, None, ALU.mult))
                keys = qkv[:, :, 1]
                dve.tensor_tensor(keys, keys, over(rn[:], P, 3), ALU.mult).then_inc(s["k_normed"], 1)
                step.link(dve, dve.tensor_tensor(all_of(dt), banks(4), each(cla[:]), ALU.subtract))
                dve.tensor_tensor(all_of(dt), all_of(dt), over(late[:], TT * H), ALU.add).then_inc(s["dt_ready"], 1)
                dve.wait_ge(s["to_end_exp"], 1)
                dve.wait_ge(s["k_normed"], 1)
                step.link(dve, dve.tensor_tensor(te[:], te[:], beta[:], ALU.mult))
                dve.tensor_tensor(kw[:], keys, over(te[:], P, 3), ALU.mult).then_inc(s["kw_ready"], 1)
                for t in range(TT - 1):
                    if t % 2 == 0:
                        dve.wait_ge(s["delta_ready"], t // 2 + 1)
                    for h in range(H):
                        delta = k.bank[:, t // 2, (t % 2 * 2 + h) * P:(t % 2 * 2 + h + 1) * P]
                        if t:
                            last = dve.scalar_tensor_tensor(state[:, t + 1, h, :], state[:, t, h, :],
                                                            ecr[:, t, h, P - 1:P], delta, ALU.mult, ALU.add)
                        else:
                            last = dve.tensor_copy(state[:, t + 1, h, :], delta)
                    last.then_inc(s["state_ready"], 1)
                    dve.wait_ge(s["state_ready"], t + 1)
                dve.wait_ge(s["decay_ready"], 1)
                dve.wait_ge(s["st_ready"], TT)
                dve.tensor_tensor(all_of(at), banks(4), all_of(dt), ALU.mult).then_inc(s["attn_ready"], 1)
                for c in range(NCH):
                    dve.wait_ge(s["y_ready"], c + 1)
                    for h in range(H):
                        xs = k.x[:, h, chunk(c)]
                        last = dve.scalar_tensor_tensor(xs, k.bank[:, 4 + 2 * c + h, :],
                                                        k.mod[:, 1, GATE_A + h:GATE_A + h + 1], xs, ALU.mult, ALU.add)
                last.then_inc(s["x_added"], 1)


def l1_ffn(k, norm):
    nc, d = k.nc, k.dram
    E, TOP, SEL, THRESH = 64, 8, 4, 0.5
    names = ("w_in", "sim_in", "logits_ready", "shifted", "probs_exp", "weights_ready", "masks_ready", "wt_ready",
             "wt_copied", "counts_ready", "sim_ready", "map_ready", "eff_ready", "eff_copied", "stored")
    s = {n: k.sem("l1f_" + n) for n in names}
    rows = nc.dram_tensor("l1f_token_weights", (E, T), F32, kind="Internal").ap()
    with ExitStack() as outer:
        weights = UnitWeights(k, outer, "l1m", d["l1f_win"], d["l1f_wout"])
        with ExitStack() as ctx:
            def sb(n, shape, dt=F32):
                return ctx.enter_context(nc.sbuf_tensor("l1f_" + n, shape, dt))
            gw = sb("gw", [P, DB, E])
            sim = sb("sim", [E, E])
            iota = sb("iota", [E, E])
            p = sb("p", [P, TT, E])
            st = sb("st", [P, 2, TT])
            v8 = sb("v8", [P, TT, TOP])
            w = sb("w", [P, 2, TT, E])
            mask = sb("mask", [P, 2, TT, E])
            wt = sb("wt", [E, 2, T])
            cnt = sb("cnt", [E, 2])
            m8 = sb("m8", [E, TOP])
            i8 = sb("i8", [E, TOP], mybir.dt.uint32)
            bi = sb("bi", [E, 2])
            mp = sb("mp", [E, E])
            eff = sb("eff", [E, T])
            with nc.Block() as block:
                @block.sync
                def _(sp):
                    sp.dma_start(gw[:], d["l1f_gw"].rearrange("(b p) n -> p b n", p=P)).then_inc(s["w_in"], 16)
                    sp.dma_start(sim[:], d["l1f_sim"]).then_inc(s["sim_in"], 16)
                    weights.load_first(sp)
                    sp.wait_ge(s["eff_copied"], 2)
                    sp.dma_start(rows, eff[:]).then_inc(s["stored"], 16)
                    sp.wait_ge(s["stored"], 16)

                @block.gpsimd
                def _(pool):
                    pool.iota(iota[:], pattern=[[1, E]], base=0, channel_multiplier=0,
                              allow_small_or_imprecise_dtypes=True)
                    pool.wait_ge(s["sim_in"], 16)
                    pool.affine_select(out=sim[:], in_=sim[:], compare_op=ALU.not_equal, fill=1.0, base=0,
                                       pattern=[[-1, E]], channel_multiplier=1).then_inc(s["sim_ready"], 1)

                @block.tensor
                def _(pe):
                    norm.on_tensor(pe)
                    norm.wait(pe)
                    pe.wait_ge(s["w_in"], 16)
                    for t in range(TT):
                        for b in range(DB):
                            last = pe.matmul(k.bank[:, 0, t * E:(t + 1) * E], k.h[:, b, tile(t)], gw[:, b, :],
                                             start=(b == 0), stop=(b == DB - 1))
                    last.then_inc(s["logits_ready"], 1)
                    pe.wait_ge(s["masks_ready"], 1)
                    for a in range(2):
                        for t in range(TT):
                            pe.matmul(k.bank[0:E, 1, a:a + 1], mask[:, a, t, :], k.ones[:, 0:1], start=(t == 0),
                                      stop=(t == TT - 1))
                    for t in range(TT):
                        last = pe.matmul(k.bank[0:E, 1, E:2 * E], k.ones[:, 0:E], mask[:, 0, t, :], start=(t == 0),
                                         stop=(t == TT - 1))
                    last.then_inc(s["counts_ready"], 1)
                    pe.wait_ge(s["weights_ready"], 1)
                    for a in range(2):
                        for t in range(TT):
                            last = pe.transpose(k.bank[0:E, 2 + 2 * a + t // 4, (t % 4) * P:(t % 4 + 1) * P],
                                                w[:, a, t, :], k.ident[:])
                        last.then_inc(s["wt_ready"], 1)
                    pe.wait_ge(s["wt_copied"], 2)
                    pe.wait_ge(s["map_ready"], 1)
                    for c in range(NCH):
                        pe.matmul(k.bank[0:E, 6 + c, :], k.ident[0:E, 0:E], wt[:, 0, chunk(c)], start=True, stop=False)
                        pe.matmul(k.bank[0:E, 6 + c, :], mp[:], wt[:, 1, chunk(c)], start=False, stop=True
                                  ).then_inc(s["eff_ready"], 1)

                @block.scalar
                def _(act):
                    norm.on_scalar(act)
                    act.preload_act_table_set(EXP_LN)
                    act.wait_ge(s["shifted"], 1)
                    act.activation(p[:], p[:], ACT.Exp).then_inc(s["probs_exp"], 1)
                    for a in range(2):
                        act.wait_ge(s["wt_ready"], a + 1)
                        act.activation(wt[:, a, :], k.bank[0:E, 2 + 2 * a:4 + 2 * a, :].rearrange("p n q -> p (n q)"),
                                       ACT.Identity).then_inc(s["wt_copied"], 1)
                    for c in range(NCH):
                        act.wait_ge(s["eff_ready"], c + 1)
                        act.activation(eff[:, chunk(c)], k.bank[0:E, 6 + c, :], ACT.Identity).then_inc(s["eff_copied"], 1)

                @block.vector
                def _(dve):
                    norm.on_vector(dve)
                    step = k.dve_chain
                    dve.wait_ge(s["logits_ready"], 1)
                    logits = k.bank[:, 0, :].rearrange("p (t e) -> p t e", t=TT)
                    step.link(dve, dve.tensor_reduce(st[:, 0, :], logits, AX.X, ALU.max))
                    dve.tensor_tensor(p[:], logits, over(st[:, 0, :], E, 2), ALU.subtract).then_inc(s["shifted"], 1)
                    dve.wait_ge(s["probs_exp"], 1)
                    step.link(dve, dve.tensor_reduce(st[:, 0, :], p[:], AX.X, ALU.add))
                    step.link(dve, dve.reciprocal(st[:, 1, :], st[:, 0, :]))
                    step.link(dve, dve.tensor_tensor(p[:], p[:], over(st[:, 1, :], E, 2), ALU.mult))
                    for t in range(TT):
                        last = dve.max(v8[:, t, :], p[:, t, :])
                    step.link(dve, last)
                    step.link(dve, dve.tensor_reduce(st[:, 0, :], v8[:], AX.X, ALU.add))
                    step.link(dve, dve.tensor_scalar(st[:, 0, :], st[:, 0, :], 1.0e-12, None, ALU.max))
                    step.link(dve, dve.reciprocal(st[:, 1, :], st[:, 0, :]))
                    dve.tensor_tensor(mask[:, 0], p[:], over(v8[:, :, SEL - 1], E, 2), ALU.is_ge)
                    step.link(dve, dve.tensor_tensor(mask[:, 1], p[:], over(v8[:, :, TOP - 1], E, 2), ALU.is_ge))
                    step.link(dve, dve.tensor_tensor(mask[:, 1], mask[:, 1], mask[:, 0], ALU.subtract))
                    dve.sem_inc(s["masks_ready"], 1)
                    step.link(dve, dve.tensor_tensor(p[:], p[:], over(st[:, 1, :], E, 2), ALU.mult))
                    for a in range(2):
                        last = dve.tensor_tensor(w[:, a], p[:], mask[:, a], ALU.mult)
                    last.then_inc(s["weights_ready"], 1)
                    dve.wait_ge(s["counts_ready"], 1)
                    dve.wait_ge(s["sim_ready"], 1)
                    step.link(dve, dve.tensor_scalar(mp[:], k.bank[0:E, 1, E:2 * E], 0.5, NEG, ALU.is_lt, ALU.mult))
                    step.link(dve, dve.tensor_tensor(mp[:], mp[:], sim[:], ALU.add))
                    step.link(dve, dve.max(m8[:], mp[:]))
                    step.link(dve, dve.max_index(i8[:], m8[:], mp[:]))
                    step.link(dve, dve.tensor_copy(bi[:, 0:1], i8[:, 0:1]))
                    step.link(dve, dve.tensor_scalar(cnt[:, 0:1], k.bank[0:E, 1, 0:1], 0.5, None, ALU.is_lt))
                    step.link(dve, dve.tensor_scalar(cnt[:, 1:2], k.bank[0:E, 1, 1:2], 0.5, None, ALU.is_ge))
                    step.link(dve, dve.tensor_tensor(cnt[:, 0:1], cnt[:, 0:1], cnt[:, 1:2], ALU.mult))
                    step.link(dve, dve.tensor_scalar(cnt[:, 1:2], m8[:, 0:1], THRESH, None, ALU.is_ge))
                    step.link(dve, dve.tensor_tensor(cnt[:, 0:1], cnt[:, 0:1], cnt[:, 1:2], ALU.mult))
                    step.link(dve, dve.scalar_tensor_tensor(mp[:], iota[:], bi[:, 0:1], k.ident[0:E, 0:E], ALU.is_equal,
                                                            ALU.subtract))
                    dve.scalar_tensor_tensor(mp[:], mp[:], cnt[:, 0:1], k.ident[0:E, 0:E], ALU.mult, ALU.add
                                             ).then_inc(s["map_ready"], 1)
        gated_units(k, "l1m", weights, E * 96 // P, gate_col(k, 1, GATE_B), rows=rows, turn=6,
                    rows_per_turn=8, owner=owners(96))


class HeadNorm:

    TILES = [(b, c) for b in range(DB) for c in range(NCH)]

    def __init__(self, k, ctx, name, buf, group, eps, var_bank, mean_bank=None, like=None):
        self.k, self.buf, self.group, self.eps = k, buf, group, eps
        self.var_bank, self.mean_bank = var_bank, mean_bank
        self.sq, self.rs = (like.sq, like.rs) if like else (
            ctx.enter_context(k.nc.sbuf_tensor(f"{name}_{n}", [P, DB, T], F32)) for n in ("square", "root"))
        self.mean_ready, self.centered, self.squared, self.var_ready, self.root_ready = (
            k.sem(f"{name}_{n}") for n in ("mean_ready", "centered", "squared", "var_ready", "root_ready"))

    def tile(self, m, n):
        b, c = self.TILES[n]
        return m[:, b, chunk(c)]

    def mean(self, pe, n):
        pe.matmul(self.k.bank[:, self.mean_bank + n, :], self.group[:], self.tile(self.buf, n), start=True, stop=True
                  ).then_inc(self.mean_ready, 1)

    def center(self, dve, n):
        dve.wait_ge(self.mean_ready, n + 1)
        xs = self.tile(self.buf, n)
        dve.tensor_tensor(xs, xs, self.k.bank[:, self.mean_bank + n, :], ALU.subtract).then_inc(self.centered, 1)

    def square(self, act, n):
        if self.mean_bank is not None:
            act.wait_ge(self.centered, n + 1)
        act.activation(self.tile(self.sq, n), self.tile(self.buf, n), ACT.Square).then_inc(self.squared, 1)

    def var(self, pe, n):
        pe.wait_ge(self.squared, n + 1)
        pe.matmul(self.k.bank[:, self.var_bank + n, :], self.group[:], self.tile(self.sq, n), start=True, stop=True
                  ).then_inc(self.var_ready, 1)

    def root(self, act, n):
        act.wait_ge(self.var_ready, n + 1)
        r = self.tile(self.rs, n)
        self.k.act_chain.link(act, act.activation(r, self.k.bank[:, self.var_bank + n, :], ACT.Ln,
                                                  bias=self.k.eps[:, self.eps:self.eps + 1]))
        act.activation(r, r, ACT.Exp, scale=-0.5).then_inc(self.root_ready, 1)


def l2_attention(k, norm):
    nc, d = k.nc, k.dram
    HD, TAPS, PROJ = 16, 4, 6
    Q, K, V, IG, G, OG = range(PROJ)
    names = ("cols_in", "w_in", "wo_in", "pad_ready", "conv_ready", "silu_ready", "proj_ready",
             "proj_copied", "scanned", "mixed", "gated", "y_ready", "x_added", "w_hi_ready",
             "w_split", "h_hi_ready", "h_split", "xc_hi_ready", "xc_split")
    s = {n: k.sem("l2_" + n) for n in names}
    with ExitStack() as outer:
        h2 = outer.enter_context(nc.sbuf_tensor("l2_h2", [P, DB, T], F32))
        COLS = ["ln1w", "ln1b", "ln2w", "ln2b", "vnw", "vnb", "mnw", "mnb", "gnw", "gnb", "conv_b", "tap0", "tap1",
                "tap2", "tap3", "big", "bg", "bog"]
        cols = outer.enter_context(nc.sbuf_tensor("l2_cols", [P, len(COLS), DB], F32))
        weights = UnitWeights(k, outer, "l2m", d["l2_win"], d["l2_wout"])

        def col(name):
            return cols[:, COLS.index(name), :]

        with ExitStack() as ctx:
            def sb(n, shape):
                return ctx.enter_context(nc.sbuf_tensor("l2_" + n, shape, F32))
            w = sb("w", [P, DB, PROJ * D])
            wo = sb("wo", [P, DB, D])
            hp = sb("hp", [P, DB, TAPS - 1 + T])
            xc = sb("xc", [P, DB, T])
            pr = sb("pr", [P, PROJ, DB, T])
            hsum = sb("hsum", [P, P])
            hmean = sb("hmean", [P, P])
            with nc.Block() as block:
                @block.sync
                def _(sp):
                    sp.dma_start(cols[:], d["l2_cols"]).then_inc(s["cols_in"], 16)
                    sp.dma_start(w[:], d["l2_w"].rearrange("(b p) n -> p b n", p=P)).then_inc(s["w_in"], 16)
                    sp.dma_start(wo[:], d["l2_wo"].rearrange("(b p) n -> p b n", p=P)).then_inc(s["wo_in"], 16)
                    weights.load_first(sp)
                    sp.wait_ge(s["cols_in"], 16)

                block.tensor(norm.on_tensor)
                block.vector(norm.on_vector)
                block.scalar(norm.on_scalar)

                @block.gpsimd
                def _(pool):
                    step = k.pool_chain
                    pool.memset(hp[:, :, 0:TAPS - 1], 0.0).then_inc(s["pad_ready"], 1)
                    for m, v in ((hsum, 1.0), (hmean, 1.0 / HD)):
                        groups = m[:].rearrange("p (g e) -> p g e", e=HD)
                        step.link(pool, pool.memset(m[:], v))
                        step.link(pool, pool.affine_select(out=groups, in_=groups, compare_op=ALU.is_ge, fill=0.0,
                                                           base=0, pattern=[[-HD, P // HD], [0, HD]],
                                                           channel_multiplier=1))
                        step.link(pool, pool.affine_select(out=groups, in_=groups, compare_op=ALU.is_ge, fill=0.0,
                                                           base=HD - 1, pattern=[[HD, P // HD], [0, HD]],
                                                           channel_multiplier=-1))
            split = ctx.enter_context(ExitStack())
            w_hi, w_lo = (split.enter_context(nc.sbuf_tensor("l2_w_" + n, [P, DB, PROJ * D], F32R))
                          for n in ("hi", "lo"))
            h_hi, h_lo, xc_hi, xc_lo = (split.enter_context(nc.sbuf_tensor("l2_" + n, [P, DB, T], F32R))
                                        for n in ("h_hi", "h_lo", "xc_hi", "xc_lo"))
            with ExitStack() as inner:
                norm1 = LayerNorm(k, inner, k.h, hp[:, :, TAPS - 1:], col("ln1w"), col("ln1b"))
                with nc.Block() as block:
                    block.tensor(norm1.on_tensor)
                    block.vector(norm1.on_vector)

                    @block.scalar
                    def _(act):
                        act.wait_ge(s["w_in"], 16)
                        act.activation(w_hi[:], w[:], ACT.Identity).then_inc(s["w_hi_ready"], 1)
                        norm1.on_scalar(act)

                    @block.gpsimd
                    def _(pool):
                        pool.wait_ge(s["w_hi_ready"], 1)
                        pool.tensor_tensor(w_lo[:], w[:], w_hi[:].bitcast(F32), ALU.subtract
                                           ).then_inc(s["w_split"], 1)
            with nc.Block() as block:
                @block.tensor
                def _(pe):
                    pe.wait_ge(s["w_split"], 1)
                    for n in range(PROJ * 4):
                        j, m, c = n // 4, n // 2 % 2, n % 2
                        if n == IG * 4:
                            pe.wait_ge(s["xc_split"], DB)
                        if n >= 8:
                            pe.wait_ge(s["proj_copied"], n - 7)
                        src_hi, src_lo = (h_hi, h_lo) if j < IG else (xc_hi, xc_lo)
                        passes = [(wq, xq, b) for wq, xq in ((w_hi, src_hi), (w_lo, src_hi), (w_hi, src_lo))
                                  for b in range(DB)]
                        for q, (wq, xq, b) in enumerate(passes):
                            if n < NCH and q == 0:
                                pe.wait_ge(s["h_hi_ready"], n + 1)
                            if n < NCH and q == 2 * DB:
                                pe.wait_ge(s["h_split"], n + 1)
                            last = pe.matmul(k.bank[:, n % 8, :], wq[:, b, j * D + m * P:j * D + (m + 1) * P],
                                             xq[:, b, chunk(c)], start=(q == 0), stop=(q == len(passes) - 1))
                        last.then_inc(s["proj_ready"], 1)

                @block.vector
                def _(dve):
                    step = k.dve_chain
                    for c in range(NCH):
                        dve.wait_ge(s["h_hi_ready"], c + 1)
                        dve.tensor_tensor(h_lo[:, :, chunk(c)], hp[:, :, TAPS - 1 + c * CH:TAPS - 1 + (c + 1) * CH],
                                          h_hi[:, :, chunk(c)].bitcast(F32), ALU.subtract).then_inc(s["h_split"], 1)
                    for b in range(DB):
                        step.link(dve, dve.tensor_scalar(xc[:, b, :], hp[:, b, TAPS - 1:TAPS - 1 + T],
                                                         col("tap3")[:, b:b + 1], col("conv_b")[:, b:b + 1],
                                                         ALU.mult, ALU.add))
                        for j in range(TAPS - 1):
                            step.link(dve, dve.scalar_tensor_tensor(xc[:, b, :], hp[:, b, j:j + T],
                                                                    col(f"tap{j}")[:, b:b + 1], xc[:, b, :],
                                                                    ALU.mult, ALU.add))
                        dve.sem_inc(s["conv_ready"], 1)
                    for b in range(DB):
                        dve.wait_ge(s["xc_hi_ready"], b + 1)
                        dve.wait_ge(s["silu_ready"], b + 1)
                        dve.tensor_tensor(xc_lo[:, b, :], xc[:, b, :], xc_hi[:, b, :].bitcast(F32), ALU.subtract
                                          ).then_inc(s["xc_split"], 1)

                @block.scalar
                def _(act):
                    for c in range(NCH):
                        act.activation(h_hi[:, :, chunk(c)], hp[:, :, TAPS - 1 + c * CH:TAPS - 1 + (c + 1) * CH],
                                       ACT.Identity).then_inc(s["h_hi_ready"], 1)
                    act.preload_act_table(ACT.Silu)
                    for n in range(PROJ * 4):
                        j, m, c = n // 4, n // 2 % 2, n % 2
                        if n in (6, 8):
                            b = n // 2 - 3
                            act.wait_ge(s["conv_ready"], b + 1)
                            act.activation(xc_hi[:, b, :], xc[:, b, :], ACT.Silu).then_inc(s["xc_hi_ready"], 1)
                            act.activation(xc[:, b, :], xc[:, b, :], ACT.Silu).then_inc(s["silu_ready"], 1)
                        act.wait_ge(s["proj_ready"], n + 1)
                        if j < IG:
                            act.activation(pr[:, j, m, chunk(c)], k.bank[:, n % 8, :], ACT.Identity
                                           ).then_inc(s["proj_copied"], 1)
                        else:
                            bias = col(("big", "bg", "bog")[j - IG])[:, m:m + 1]
                            act.activation(pr[:, j, m, chunk(c)], k.bank[:, n % 8, :], ACT.Sigmoid, bias=bias
                                           ).then_inc(s["proj_copied"], 1)
            split.close()
            tiles = range(len(HeadNorm.TILES))
            keys = HeadNorm(k, ctx, "l2_keys", pr[:, K], hsum, 1, 4)
            values = HeadNorm(k, ctx, "l2_values", pr[:, V], hmean, 0, 0, 0)
            queries = HeadNorm(k, ctx, "l2_queries", pr[:, Q], hsum, 1, 4)
            memory = HeadNorm(k, ctx, "l2_memory", pr[:, V], hmean, 0, 4, 0, like=values)
            output = HeadNorm(k, ctx, "l2_output", pr[:, V], hmean, 0, 4, 0, like=values)
            with nc.Block() as block:
                @block.tensor
                def _(pe):
                    for n in tiles:
                        values.mean(pe, n)
                    for n in tiles:
                        keys.var(pe, n)
                    for n in tiles:
                        values.var(pe, n)
                    for n in tiles:
                        pe.wait_ge(keys.root_ready, n + 1)
                        queries.var(pe, n)
                    for n in tiles:
                        pe.wait_ge(s["scanned"], n // NCH + 1)
                        memory.mean(pe, n)
                    for n in tiles:
                        pe.wait_ge(queries.root_ready, n + 1)
                        memory.var(pe, n)
                    for n in tiles:
                        pe.wait_ge(s["mixed"], n + 1)
                        output.mean(pe, n)
                    for n in tiles:
                        output.var(pe, n)
                    pe.wait_ge(s["wo_in"], 16)
                    for n in range(4):
                        c, m = n // 2, n % 2
                        pe.wait_ge(s["gated"], 3 + c)
                        for b in range(DB):
                            last = pe.matmul(k.bank[:, n, :], wo[:, b, tile(m)], pr[:, V, b, chunk(c)],
                                             start=(b == 0), stop=(b == DB - 1))
                        last.then_inc(s["y_ready"], 1)

                @block.scalar
                def _(act):
                    act.preload_act_table_set(EXP_LN)
                    for n in tiles:
                        keys.square(act, n)
                    for n in tiles:
                        values.square(act, n)
                    for norm_of in (keys, values):
                        for n in tiles:
                            norm_of.root(act, n)
                    for n in tiles:
                        queries.square(act, n)
                    for n in tiles:
                        queries.root(act, n)
                    for norm_of in (memory, output):
                        for n in tiles:
                            norm_of.square(act, n)
                        for n in tiles:
                            norm_of.root(act, n)

                @block.vector
                def _(dve):
                    step = k.dve_chain

                    def times_root(of, n, scale):
                        dve.wait_ge(of.root_ready, n + 1)
                        xs = of.tile(of.buf, n)
                        b = n // NCH
                        step.link(dve, dve.scalar_tensor_tensor(xs, xs, col(scale)[:, b:b + 1], of.tile(of.rs, n),
                                                                ALU.mult, ALU.mult))

                    def plus_times(of, n, shift, factor, out):
                        b = n // NCH
                        return dve.scalar_tensor_tensor(of.tile(out, n), of.tile(of.buf, n), col(shift)[:, b:b + 1],
                                                        of.tile(factor, n), ALU.add, ALU.mult)

                    for n in tiles:
                        values.center(dve, n)
                    for n in tiles:
                        dve.wait_ge(keys.root_ready, n + 1)
                        xs = keys.tile(keys.buf, n)
                        step.link(dve, dve.tensor_tensor(xs, xs, keys.tile(keys.rs, n), ALU.mult))
                        step.link(dve, dve.tensor_tensor(xs, xs, keys.tile(pr[:, IG], n), ALU.mult))
                    for b in range(DB):
                        for n in range(b * NCH, (b + 1) * NCH):
                            times_root(values, n, "vnw")
                            step.link(dve, plus_times(values, n, "vnb", pr[:, K], pr[:, K]))
                        step.link(dve, dve.tensor_tensor_scan(pr[:, V, b, :], pr[:, G, b, :], pr[:, K, b, :], 0.0,
                                                              ALU.mult, ALU.add))
                        dve.sem_inc(s["scanned"], 1)
                    for n in tiles:
                        dve.wait_ge(queries.root_ready, n + 1)
                        xs = queries.tile(queries.buf, n)
                        step.link(dve, dve.tensor_tensor(xs, xs, queries.tile(queries.rs, n), ALU.mult))
                    for n in tiles:
                        memory.center(dve, n)
                    for n in tiles:
                        times_root(memory, n, "mnw")
                        plus_times(memory, n, "mnb", pr[:, Q], pr[:, V]).then_inc(s["mixed"], 1)
                    for n in tiles:
                        output.center(dve, n)
                    for n in tiles:
                        times_root(output, n, "gnw")
                        plus_times(output, n, "gnb", pr[:, OG], pr[:, V]).then_inc(s["gated"], 1)
                    for n in range(4):
                        c, m = n // 2, n % 2
                        dve.wait_ge(s["y_ready"], n + 1)
                        r, x = k.h[:, m, chunk(c)], k.x[:, m, chunk(c)]
                        step.link(dve, dve.tensor_tensor(r, r, k.bank[:, n, :], ALU.add))
                        last = dve.scalar_tensor_tensor(x, r, gate_col(k, 2, GATE_A)[:, m:m + 1], x, ALU.mult, ALU.add)
                    last.then_inc(s["x_added"], 1)
        layernorm(k, k.h, h2, col("ln2w"), col("ln2b"))
        gated_units(k, "l2m", weights, 8, gate_col(k, 2, GATE_A), src=h2, turn=2)


def l2_ffn(k, norm):
    nc, d = k.nc, k.dram
    E, GROUPS, F, UNITS = 8, 4, 176, 14
    names = ("w_in", "logits_ready", "shifted", "probs_exp", "weights_ready", "wt_ready", "wt_copied", "stored")
    s = {n: k.sem("l2f_" + n) for n in names}
    rows = nc.dram_tensor("l2f_token_weights", (E + 1, T), F32, kind="Internal").ap()
    with ExitStack() as outer:
        weights = UnitWeights(k, outer, "l2e", d["l2f_win"], d["l2f_wout"])
        with ExitStack() as ctx:
            def sb(n, shape):
                return ctx.enter_context(nc.sbuf_tensor("l2f_" + n, shape, F32))
            gw = sb("gw", [P, DB, E])
            p = sb("p", [P, TT, E])
            g = sb("g", [P, 2, TT, GROUPS])
            m = sb("m", [P, 2, TT, E])
            st = sb("st", [P, 2, TT])
            w = sb("w", [P, TT, E + 1])
            wt = sb("wt", [E + 1, T])
            with nc.Block() as block:
                @block.sync
                def _(sp):
                    sp.dma_start(gw[:], d["l2f_gw"].rearrange("(b p) n -> p b n", p=P)).then_inc(s["w_in"], 16)
                    weights.load_first(sp)
                    sp.wait_ge(s["wt_copied"], 1)
                    sp.dma_start(rows, wt[:]).then_inc(s["stored"], 16)
                    sp.wait_ge(s["stored"], 16)

                @block.tensor
                def _(pe):
                    norm.on_tensor(pe)
                    norm.wait(pe)
                    pe.wait_ge(s["w_in"], 16)
                    for t in range(TT):
                        for b in range(DB):
                            last = pe.matmul(k.bank[:, 0, t * E:(t + 1) * E], k.h[:, b, tile(t)], gw[:, b, :],
                                             start=(b == 0), stop=(b == DB - 1))
                    last.then_inc(s["logits_ready"], 1)
                    pe.wait_ge(s["weights_ready"], 1)
                    for t in range(TT):
                        last = pe.transpose(k.bank[0:E + 1, 1 + t // 4, (t % 4) * P:(t % 4 + 1) * P], w[:, t, :],
                                            k.ident[:])
                    last.then_inc(s["wt_ready"], 1)

                @block.scalar
                def _(act):
                    norm.on_scalar(act)
                    act.preload_act_table_set(EXP_LN)
                    act.wait_ge(s["shifted"], 1)
                    act.activation(p[:], p[:], ACT.Exp).then_inc(s["probs_exp"], 1)
                    act.wait_ge(s["wt_ready"], 1)
                    act.activation(wt[:], k.bank[0:E + 1, 1:3, :].rearrange("p n q -> p (n q)"), ACT.Identity
                                   ).then_inc(s["wt_copied"], 1)

                @block.vector
                def _(dve):
                    norm.on_vector(dve)
                    step = k.dve_chain
                    dve.memset(w[:, :, E:], 1.0)
                    dve.wait_ge(s["logits_ready"], 1)
                    logits = k.bank[:, 0, 0:TT * E].rearrange("p (t e) -> p t e", t=TT)
                    step.link(dve, dve.tensor_reduce(st[:, 0, :], logits, AX.X, ALU.max))
                    dve.tensor_tensor(p[:], logits, over(st[:, 0, :], E, 2), ALU.subtract).then_inc(s["shifted"], 1)
                    dve.wait_ge(s["probs_exp"], 1)
                    step.link(dve, dve.tensor_reduce(st[:, 0, :], p[:], AX.X, ALU.add))
                    step.link(dve, dve.reciprocal(st[:, 1, :], st[:, 0, :]))
                    step.link(dve, dve.tensor_tensor(p[:], p[:], over(st[:, 1, :], E, 2), ALU.mult))

                    def second_best(of, n, tmp):
                        step.link(dve, dve.tensor_reduce(st[:, 0, :], of, AX.X, ALU.max))
                        step.link(dve, dve.tensor_tensor(tmp, of, over(st[:, 0, :], n, 2), ALU.is_ge))
                        step.link(dve, dve.scalar_tensor_tensor(tmp, tmp, -4.0, of, ALU.mult, ALU.add))
                        step.link(dve, dve.tensor_reduce(st[:, 1, :], tmp, AX.X, ALU.max))

                    step.link(dve, dve.tensor_reduce(g[:, 0], p[:].rearrange("p t (g e) -> p t g e", g=GROUPS), AX.X,
                                                     ALU.max))
                    second_best(g[:, 0], GROUPS, g[:, 1])
                    step.link(dve, dve.tensor_tensor(g[:, 1], g[:, 0], over(st[:, 1, :], GROUPS, 2), ALU.is_ge))
                    by_group = m[:, 0].rearrange("p t (g e) -> p t g e", g=GROUPS)
                    step.link(dve, dve.tensor_tensor(by_group, p[:].rearrange("p t (g e) -> p t g e", g=GROUPS),
                                                     over(g[:, 1], E // GROUPS, 3), ALU.mult))
                    second_best(m[:, 0], E, m[:, 1])
                    step.link(dve, dve.tensor_tensor(m[:, 1], m[:, 0], over(st[:, 1, :], E, 2), ALU.is_ge))
                    dve.tensor_tensor(w[:, :, 0:E], m[:, 0], m[:, 1], ALU.mult).then_inc(s["weights_ready"], 1)
        routed, shared = owners(F), [(0, P // 2, E), (P // 2, P, E)]
        gated_units(k, "l2e", weights, UNITS, gate_col(k, 2, GATE_B), rows=rows, turn=UNITS,
                    owner=lambda j: routed(j) if j * P < E * F else shared)


def l3_attention(k, norm):
    nc, d = k.nc, k.dram
    H, HP, S, PAD = 16, 2, 64, 8
    PAIRS, NS, LAG = H // HP, T // S, 4
    INV_SCALE = float(P) ** -0.5
    EVEN, ODD = slice(0, S), slice(S, P)
    A_BANKS = (0, 1, 4, 7)
    GROUPS = [(a, g) for a in range(HP) for g in range(4)]
    names = ("betas_in", "betas_ready", "wo_in", "w_in", "const_ready", "zeroed", "v_ready", "v_even_copied",
             "v_odd_copied", "qk_ready", "qk_copied", "neg_ready", "neg_exp", "sigma_ready", "z_ready", "dk_ready", "dk_read",
             "kt_ready", "kt_copied", "xk_ready", "a_ready", "a_copied", "scores_ready", "scores_read", "shifted",
             "probs_exp", "probs_ready", "pt_ready", "pt_copied", "qz_ready", "dq_ready", "dq_ln", "rd_ready",
             "q_normed", "mem_ready", "mem_copied", "read_ready", "dot_ready", "dot_scaled", "att_ready", "y_ready",
             "x_added", "h_hi_ready", "h_split", "w_hi_ready", "w_split", "v_whole",
             "ones_ready", "qz_hi_ready", "qz_split")
    s = {n: k.sem("l3_" + n) for n in names}
    with ExitStack() as ctx:
        def sb(n, shape, dt=F32):
            return ctx.enter_context(nc.sbuf_tensor("l3_" + n, shape, dt))
        beta = sb("beta", [P, H])
        bt = sb("bt", [P, 2, HP])
        mask = sb("mask", [P, P])
        w = sb("w", [P, DB, 3 * HP * P])
        w_hi, w_lo = (sb("w_" + n, [P, DB, 3 * HP * P], F32R) for n in ("hi", "lo"))
        h_hi, h_lo = (sb("h_" + n, [P, DB, T], F32R) for n in ("hi", "lo"))
        wo = sb("wo", [P, H, D])
        v = sb("v", [P, TT, HP, 2, P])
        vw = sb("vw", [P, TT, HP, P])
        xk = sb("xk", [P, HP, TT, 2, P])
        kt = sb("kt", [P, HP, TT, P])
        qk = sb("qk", [P, HP, 2, T])
        sg = sb("sg", [P, HP, 2, T])
        neg = sb("neg", [P, 2, CH])
        z = sb("z", [P, 2, HP, PAD + NS])
        dk = sb("dk", [P, HP, TT])
        qz = sb("qz", [P, HP, T])
        qz_hi, qz_lo = (sb("qz_" + n, [P, T], F32R) for n in ("hi", "lo"))
        ones_r = sb("ones_r", [P, P], F32R)
        rd = norm.rs
        sc = norm.sq[:].rearrange("p a (t q) -> p a t q", q=P)
        st = sb("st", [P, HP, 2, TT])
        pt = qz[:].rearrange("p a (t q) -> p a t q", q=P)
        a_neg = qk[:].rearrange("p a c (n q) -> p a (c n) q", q=P)
        mem = sb("mem", [P, HP, 8, P])
        att = k.h
        with nc.Block() as block:
            @block.sync
            def _(sp):
                sp.dma_start(beta[:], d["l3_betas"]).then_inc(s["betas_in"], 16)

                def load(i):
                    sp.dma_start(w[:], d["l3_w"][bass.ds(i, 1)].rearrange("u (b p) n -> p (u b) n", p=P)
                                 ).then_inc(s["w_in"], 16)

                load(0)
                sp.dma_start(wo[:], d["l3_wo"].rearrange("(j p) n -> p j n", p=P)).then_inc(s["wo_in"], 16)
                with sp.Fori(1, PAIRS) as i:
                    sp.wait_ge(s["qk_ready"], i * 8)
                    load(i)

            @block.gpsimd
            def _(pool):
                step = k.pool_chain
                step.link(pool, pool.memset(mask[:], 0.0))
                step.link(pool, pool.affine_select(out=mask[:], in_=mask[:], compare_op=ALU.is_ge, fill=NEG, base=0,
                                                   pattern=[[-1, P]], channel_multiplier=1))
                step.link(pool, pool.memset(mask[S:P, 0:S], NEG))
                step.link(pool, pool.memset(z[:], 0.0))
                step.link(pool, pool.memset(z[:, 0, :, PAD:PAD + 1], 1.0 / P))
                pool.sem_inc(s["const_ready"], 1)
                for a in range(HP):
                    for half in (v[ODD, :, a, 0, :], v[EVEN, :, a, 1, :], xk[ODD, a, :, 0, :], xk[EVEN, a, :, 1, :]):
                        step.link(pool, pool.memset(half, 0.0))
                pool.sem_inc(s["zeroed"], 1)

                def low_parts(i):
                    pool.wait_ge(s["w_hi_ready"], i + 1)
                    pool.tensor_tensor(w_lo[:], w[:], w_hi[:].bitcast(F32), ALU.subtract).then_inc(s["w_split"], 1)

                def pair(i):
                    pool.wait_ge(s["v_even_copied"], i + 1)
                    pool.wait_ge(s["v_odd_copied"], i + 1)
                    pool.tensor_tensor(vw[:], v[:, :, :, 0, :], v[:, :, :, 1, :], ALU.add).then_inc(s["v_whole"], 1)
                    for a in range(HP):
                        pool.wait_ge(s["sigma_ready"], i * 8 + (4 * a + 4))
                        pool.wait_ge(s["z_ready"], i * HP + (a + 1))
                        pool.tensor_tensor(qz[:, a].rearrange("p (g q) -> p g q", q=S),
                                           sg[:, a, 1].rearrange("p (g q) -> p g q", q=S),
                                           over(z[:, 0, a, PAD:], S, 2), ALU.mult).then_inc(s["qz_ready"], 1)
                        if a:
                            pool.wait_ge(s["dq_ready"], i * HP + 1)
                        pool.tensor_tensor(qz_hi[:].rearrange("p (g q) -> p g q", q=S),
                                           sg[:, a, 1].rearrange("p (g q) -> p g q", q=S),
                                           over(z[:, 0, a, PAD:], S, 2), ALU.mult).then_inc(s["qz_hi_ready"], 1)
                        pool.wait_ge(s["qz_ready"], i * HP + (a + 1))
                        pool.wait_ge(s["qz_hi_ready"], i * HP + (a + 1))
                        pool.tensor_tensor(qz_lo[:], qz[:, a], qz_hi[:].bitcast(F32), ALU.subtract
                                           ).then_inc(s["qz_split"], 1)

                low_parts(0)
                with pool.Fori(0, PAIRS - 1) as i:
                    pair(i)
                    low_parts(i + 1)
                pair(PAIRS - 1)

            @block.tensor
            def _(pe):
                norm.on_tensor(pe)
                norm.wait(pe)
                def project_out(turn):
                    pe.wait_ge(s["att_ready"], turn * HP)
                    for m in range(DB):
                        for j in range(H):
                            last = pe.matmul(k.bank[:, 7, m * P:(m + 1) * P], wo[:, j, tile(m)], att[:, :, j::H],
                                             start=(j == 0), stop=(j == H - 1))
                    last.then_inc(s["y_ready"], 1)

                def pair(i, first):
                    def keys_by_token(a):
                        pe.wait_ge(s["sigma_ready"], i * 8 + (4 * a + 2))
                        if a:
                            pe.wait_ge(s["kt_copied"], i * HP + 1)
                        for t in range(TT):
                            last = pe.transpose(k.bank[:, t // 4, (t % 4) * P:(t % 4 + 1) * P],
                                                sg[:, a, 0, tile(t)], k.ident[:])
                        last.then_inc(s["kt_ready"], 1)

                    def key_divisors(a):
                        pe.wait_ge(s["z_ready"], i * HP + (a + 1))
                        if a:
                            pe.wait_ge(s["qk_copied"], i * 8 + 5)
                        for t in range(TT):
                            last = pe.matmul(k.bank[:, 2 + 2 * a, 2 * t:2 * t + 2], sg[:, a, 0, tile(t)],
                                             z[:, 0, a, PAD + 2 * t:PAD + 2 * t + 2], start=True, stop=True)
                        last.then_inc(s["dk_ready"], 1)

                    def scores(a):
                        pe.wait_ge(s["qk_copied"], i * 8 + (4 + 4 * a))
                        for t in range(TT):
                            last = pe.matmul(k.bank[:, 2 + 3 * a + t // 4, (t % 4) * P:(t % 4 + 1) * P],
                                             qk[:, a, 1, tile(t)], qk[:, a, 0, tile(t)], start=True, stop=True)
                        last.then_inc(s["scores_ready"], 1)

                    def products_a(a):
                        pe.wait_ge(s["xk_ready"], i * HP + (a + 1))
                        for g in range(4):
                            if a:
                                pe.wait_ge(s["a_copied"], i * 8 + (g + 1))
                            elif g == 0:
                                pe.wait_ge(s["kt_copied"], i * HP + 2)
                            elif g == 2:
                                pe.wait_ge(s["dk_read"], i * HP + 2)
                            elif g == 3 and not first:
                                pe.wait_ge(s["x_added"], i)
                            for h in range(2):
                                last = pe.matmul(k.bank[:, A_BANKS[g], h * 256:(h + 1) * 256], kt[:, a, 2 * g + h, :],
                                                 xk[:, a, 2 * g + h].rearrange("p h q -> p (h q)"), start=True,
                                                 stop=True)
                            last.then_inc(s["a_ready"], 1)

                    def query_divisors(a):
                        pe.wait_ge(s["qz_split"], i * HP + (a + 1))
                        if a:
                            pe.wait_ge(s["dq_ln"], i * HP + 1)
                        else:
                            pe.wait_ge(s["scores_read"], i * HP + 2)
                        for c in range(NCH):
                            for q, part in enumerate((qz_hi, qz_lo)):
                                last = pe.matmul(k.bank[:, 5 + c, :], ones_r[:], part[:, chunk(c)], start=(q == 0),
                                                 stop=(q == 1))
                        last.then_inc(s["dq_ready"], 1)

                    def read(n, a):
                        if n == 0:
                            pe.wait_ge(s["q_normed"], i * HP + (a + 1))
                            pe.wait_ge(s["a_copied"], i * 8 + 8)
                        bank = k.bank[:, A_BANKS[2 * a + n // 8], (n % 8) * S:(n % 8 + 1) * S]
                        lhs_t = mem[:, a, n % 8, :] if n else k.zeros[:, 0:P]
                        pe.matmul(bank, lhs_t, sg[:, a, 1, n * S:(n + 1) * S], start=True, stop=True
                                  ).then_inc(s["read_ready"], 1)

                    def memory_step(n, a):
                        t, odd = n // 2, n % 2
                        if n:
                            pe.wait_ge(s["mem_copied"], i * (HP * (NS - 1)) + (HP * (n - 1) + a + 1))
                        last = pe.matmul(k.bank[:, 2 + a, 0:P], kt[:, a, t, :], v[:, t, a, odd, :],
                                         start=(n == 0), stop=False, skip_group_check=True)
                        if n:
                            last = pe.matmul(k.bank[:, 2 + a, 0:P], a_neg[:, a, n, :], mem[:, a, n % 8, :],
                                             start=False, stop=False, skip_group_check=True)
                        last.then_inc(s["mem_ready"], 1)

                    def turn_probs(a):
                        pe.wait_ge(s["probs_ready"], i * HP + (a + 1))
                        for t in range(TT):
                            last = pe.transpose(k.bank[:, 5 - 3 * a + t // 4, (t % 4) * P:(t % 4 + 1) * P],
                                                sc[:, a, t, :], k.ident[:])
                        last.then_inc(s["pt_ready"], 1)

                    def local_attention(a):
                        pe.wait_ge(s["pt_copied"], i * HP + (a + 1))
                        for t in range(TT):
                            last = pe.matmul(k.bank[:, 5 - 3 * a + t // 4, (t % 4) * P:(t % 4 + 1) * P],
                                             vw[:, t, a, :], pt[:, a, t, :], start=True, stop=True)
                        last.then_inc(s["dot_ready"], 1)

                    pe.wait_ge(s["w_split"], i + 1)
                    for t in range(TT):
                        if not first and t == 0:
                            pe.wait_ge(s["att_ready"], i * HP - 1)
                        if not first and t == 4:
                            pe.wait_ge(s["dot_scaled"], i * HP)
                        for n, (b, hq, wq) in enumerate(parts):
                            last = pe.matmul(k.bank[:, t // 2, (t % 2) * 256:(t % 2 + 1) * 256], hq[:, b, tile(t)],
                                             wq[:, b, 4 * P:6 * P], start=(n == 0), stop=(n == len(parts) - 1))
                    last.then_inc(s["v_ready"], 1)
                    if not first:
                        pe.wait_ge(s["att_ready"], i * HP)
                    for a in range(HP):
                        for n in range(4):
                            if a:
                                pe.wait_ge(s["qk_copied"], i * 8 + (n + 1))
                            for q, (b, hq, wq) in enumerate(parts):
                                last = pe.matmul(k.bank[:, 4 + n, :], wq[:, b, tile(2 * a + 1 - n // 2)],
                                                 hq[:, b, chunk(n % 2)], start=(q == 0), stop=(q == len(parts) - 1))
                            last.then_inc(s["qk_ready"], 1)
                            if (a, n) == (1, 0):
                                pe.wait_ge(s["v_even_copied"], i + 1)
                                pe.wait_ge(s["v_odd_copied"], i + 1)
                                keys_by_token(0)
                            if (a, n) == (1, 1):
                                key_divisors(0)
                    pe.wait_ge(s["dk_read"], i * HP + 1)
                    scores(0)
                    if not first:
                        pe.wait_ge(s["qk_copied"], i * 8 + 8)
                        project_out(i)
                    keys_by_token(1)
                    key_divisors(1)
                    scores(1)
                    products_a(0)
                    query_divisors(0)
                    products_a(1)
                    pe.wait_ge(s["scores_read"], i * HP + 1)
                    for a in range(HP):
                        memory_step(0, a)
                    query_divisors(1)
                    for n in range(1, NS - 1):
                        for a in range(HP):
                            memory_step(n, a)
                            if n >= LAG:
                                read(n - LAG, a)
                        if n == NS - 4:
                            pe.wait_ge(s["dq_ln"], i * HP + 2)
                            turn_probs(0)
                    pe.wait_ge(s["v_whole"], i + 1)
                    local_attention(0)
                    pe.wait_ge(s["mem_copied"], i * (HP * (NS - 1)) + HP * (NS - 1))
                    for a in range(HP):
                        for n in range(NS - 1 - LAG, NS):
                            read(n, a)
                        if a == 0:
                            turn_probs(1)
                    local_attention(1)

                parts = [(b, hq, wq) for b in range(DB) for hq, wq in ((h_hi, w_hi), (h_hi, w_lo), (h_lo, w_hi))]
                pe.wait_ge(s["zeroed"], 1)
                pe.wait_ge(s["h_split"], 1)
                pe.wait_ge(s["ones_ready"], 1)
                pair(0, True)
                pe.wait_ge(s["wo_in"], 16)
                with pe.Fori(1, PAIRS) as i:
                    pair(i, False)
                project_out(PAIRS)

            @block.scalar
            def _(act):
                norm.on_scalar(act)
                act.preload_act_table(ACT.Sigmoid)
                act.wait_ge(s["betas_in"], 16)
                act.activation(beta[:], beta[:], ACT.Sigmoid).then_inc(s["betas_ready"], 1)
                act.activation(ones_r[:], k.ones[:], ACT.Identity).then_inc(s["ones_ready"], 1)
                act.preload_act_table_set(EXP_LN)
                act.wait_ge(s["zeroed"], 1)
                norm.wait(act)
                act.activation(h_hi[:], k.h[:], ACT.Identity).then_inc(s["h_hi_ready"], 1)

                def high_parts(i):
                    act.wait_ge(s["w_in"], i * 16 + 16)
                    act.activation(w_hi[:], w[:], ACT.Identity).then_inc(s["w_hi_ready"], 1)

                def pair(i, final):
                    def two_banks(n):
                        return k.bank[:, n:n + 2, :].rearrange("p n q -> p (n q)")

                    def keys_copy(a):
                        act.wait_ge(s["kt_ready"], i * HP + (a + 1))
                        act.activation(kt[:, a].rearrange("p t q -> p (t q)"), two_banks(0), ACT.Identity
                                       ).then_inc(s["kt_copied"], 1)

                    def mem_copy(n, a):
                        act.wait_ge(s["mem_ready"], i * (HP * (NS - 1)) + (HP * n + a + 1))
                        if n >= 7:
                            act.wait_ge(s["read_ready"], i * (HP * NS) + (HP * (n + 1 - 8) + a + 1))
                        act.activation(mem[:, a, (n + 1) % 8, :], k.bank[:, 2 + a, 0:P], ACT.Identity
                                       ).then_inc(s["mem_copied"], 1)

                    def exponential(a):
                        act.wait_ge(s["shifted"], i * HP + (a + 1))
                        act.activation(sc[:, a], sc[:, a], ACT.Exp).then_inc(s["probs_exp"], 1)

                    act.wait_ge(s["v_ready"], i + 1)
                    act.activation(v[EVEN, :, :, 0, :], k.bank[EVEN, 0:4, :].rearrange(
                        "p n (t a q) -> p (n t) a q", t=2, a=HP), ACT.Identity).then_inc(s["v_even_copied"], 1)
                    for j in range(8):
                        a, n = j // 4, j % 4
                        act.wait_ge(s["qk_ready"], i * 8 + (j + 1))
                        if j >= 2:
                            act.wait_ge(s["sigma_ready"], i * 8 + (j - 1))
                        act.activation(neg[:, n % 2, :], k.bank[:, 4 + n, :], ACT.Relu, scale=-1.0
                                       ).then_inc(s["neg_ready"], 1)
                        act.activation(qk[:, a, n // 2, chunk(n % 2)], k.bank[:, 4 + n, :], ACT.Identity
                                       ).then_inc(s["qk_copied"], 1)
                        act.wait_ge(s["neg_ready"], i * 8 + (j + 1))
                        act.activation(neg[:, n % 2, :], neg[:, n % 2, :], ACT.Exp, scale=-1.0
                                       ).then_inc(s["neg_exp"], 1)
                        if j == 4:
                            keys_copy(0)
                    keys_copy(1)
                    if not final:
                        high_parts(i + 1)
                    for a in range(HP):
                        for g in range(4):
                            act.wait_ge(s["a_ready"], i * 8 + (4 * a + g + 1))
                            act.activation(a_neg[:, a, 4 * g:4 * g + 4, :].rearrange("p n q -> p (n q)"),
                                           k.bank[:, A_BANKS[g], :], ACT.Identity, scale=-1.0
                                           ).then_inc(s["a_copied"], 1)
                        if a:
                            for both in range(HP):
                                mem_copy(0, both)
                        act.wait_ge(s["dq_ready"], i * HP + (a + 1))
                        if a:
                            act.wait_ge(s["q_normed"], i * HP + a)
                        act.activation(rd[:], two_banks(5), ACT.Ln).then_inc(s["dq_ln"], 1)
                        act.wait_ge(s["dq_ln"], i * HP + (a + 1))
                        act.activation(rd[:], rd[:], ACT.Exp, scale=-1.0).then_inc(s["rd_ready"], 1)
                        if a == 0:
                            exponential(0)
                    for n in range(1, NS - 1):
                        for a in range(HP):
                            mem_copy(n, a)
                        if n == 2:
                            exponential(1)
                        if n == NS - 3:
                            act.wait_ge(s["pt_ready"], i * HP + 1)
                            act.activation(pt[:, 0].rearrange("p t q -> p (t q)"), two_banks(5), ACT.Identity
                                           ).then_inc(s["pt_copied"], 1)
                    for a in range(HP):
                        if a:
                            act.wait_ge(s["pt_ready"], i * HP + 2)
                            act.activation(pt[:, 1].rearrange("p t q -> p (t q)"), two_banks(2), ACT.Identity
                                           ).then_inc(s["pt_copied"], 1)
                        act.wait_ge(s["dot_ready"], i * HP + (a + 1))
                        act.activation(att[:, a], two_banks(5 - 3 * a), ACT.Identity, scale=bt[:, 1, a:a + 1]
                                       ).then_inc(s["dot_scaled"], 1)

                high_parts(0)
                with act.Fori(0, PAIRS - 1) as i:
                    pair(i, False)
                pair(PAIRS - 1, True)

            @block.vector
            def _(dve):
                norm.on_vector(dve)
                step = k.dve_chain
                dve.wait_ge(s["const_ready"], 1)
                dve.wait_ge(s["zeroed"], 1)
                dve.wait_ge(s["betas_ready"], 1)
                dve.wait_ge(s["h_hi_ready"], 1)
                dve.tensor_tensor(h_lo[:], k.h[:], h_hi[:].bitcast(F32), ALU.subtract).then_inc(s["h_split"], 1)

                def add_projection(turn):
                    dve.wait_ge(s["y_ready"], turn)
                    for m in range(DB):
                        for a in range(HP):
                            xs = k.x[:, m, :].rearrange("p (g q) -> p g q", q=S)[:, :, bass.ds(
                                turn * (4 * HP) + (4 * a - 4 * HP), 4)]
                            last = dve.scalar_tensor_tensor(
                                xs, k.bank[:, 7, m * P + a * S:m * P + (a + 1) * S].rearrange(
                                    "p (g n) -> p g n", n=4), gate_col(k, 3, GATE_A)[:, m:m + 1], xs,
                                ALU.mult, ALU.add)
                    last.then_inc(s["x_added"], 1)

                def pair(i, first):
                    def sigma(j):
                        a, n = j // 4, j % 4
                        dve.wait_ge(s["qk_copied"], i * 8 + (j + 1))
                        dve.wait_ge(s["neg_exp"], i * 8 + (j + 1))
                        dve.scalar_tensor_tensor(sg[:, a, n // 2, chunk(n % 2)], qk[:, a, n // 2, chunk(n % 2)], 0.0,
                                                 neg[:, n % 2, :], ALU.max, ALU.add).then_inc(s["sigma_ready"], 1)

                    def key_sums(a):
                        dve.wait_ge(s["sigma_ready"], i * 8 + (4 * a + 2))
                        step.link(dve, dve.tensor_reduce(
                            z[:, 0, a, PAD + 1:], sg[:, a, 0, 0:T - S].rearrange("p (g q) -> p g q", q=S), AX.X,
                            ALU.add))
                        for n in range(4):
                            src, dst, by = z[:, n % 2, a], z[:, (n + 1) % 2, a], 1 << n
                            ins = dve.tensor_tensor(dst[:, PAD:], src[:, PAD:], src[:, PAD - by:PAD + NS - by],
                                                    ALU.add)
                            if n < 3:
                                step.link(dve, ins)
                            else:
                                ins.then_inc(s["z_ready"], 1)

                    def key_divisors(a):
                        dve.wait_ge(s["dk_ready"], i * HP + (a + 1))
                        dens = k.bank[:, 2 + 2 * a, 0:2 * TT].rearrange("p (t o) -> p t o", o=2)
                        dve.reciprocal(dk[EVEN, a, :], dens[EVEN, :, 0])
                        step.link(dve, dve.reciprocal(dk[ODD, a, :], dens[ODD, :, 1]))
                        dve.sem_inc(s["dk_read"], 1)

                    def divide_keys(a):
                        dve.wait_ge(s["kt_copied"], i * HP + (a + 1))
                        dve.tensor_tensor(xk[EVEN, a, :, 0, :], kt[EVEN, a], over(dk[EVEN, a, :], P, 2), ALU.mult)
                        dve.tensor_tensor(xk[ODD, a, :, 1, :], kt[ODD, a], over(dk[ODD, a, :], P, 2), ALU.mult
                                          ).then_inc(s["xk_ready"], 1)

                    def read_scores(a):
                        dve.wait_ge(s["scores_ready"], i * HP + (a + 1))
                        dve.scalar_tensor_tensor(sc[:, a], k.bank[:, 2 + 3 * a:4 + 3 * a, :].rearrange(
                            "p n (t q) -> p (n t) q", q=P), INV_SCALE, over(mask[:], TT), ALU.mult, ALU.add
                            ).then_inc(s["scores_read"], 1)

                    if not first:
                        dve.wait_ge(s["att_ready"], i * HP)
                    step.link(dve, dve.tensor_copy(bt[:, 0, :], beta[:, bass.ds(i * HP, HP)]))
                    step.link(dve, dve.tensor_scalar(bt[:, 1, :], bt[:, 0, :], -1.0, 1.0, ALU.mult, ALU.add))
                    dve.wait_ge(s["v_ready"], i + 1)
                    dve.tensor_copy(v[ODD, :, :, 1, :], k.bank[ODD, 0:4, :].rearrange(
                        "p n (t a q) -> p (n t) a q", t=2, a=HP)).then_inc(s["v_odd_copied"], 1)
                    for j in range(8):
                        sigma(j)
                        if j in (1, 5):
                            key_sums(j // 5)
                        if j == 4:
                            key_divisors(0)
                    divide_keys(0)
                    read_scores(0)
                    if not first:
                        add_projection(i)
                    key_divisors(1)
                    divide_keys(1)
                    read_scores(1)
                    for a in range(HP):
                        dve.wait_ge(s["scores_read"], i * HP + (a + 1))
                        step.link(dve, dve.tensor_reduce(st[:, a, 0, :], sc[:, a], AX.X, ALU.max))
                        dve.tensor_tensor(sc[:, a], sc[:, a], over(st[:, a, 0, :], P, 2), ALU.subtract
                                          ).then_inc(s["shifted"], 1)
                        dve.wait_ge(s["rd_ready"], i * HP + (a + 1))
                        dve.wait_ge(s["qz_hi_ready"], i * HP + (a + 1))
                        dve.tensor_tensor(sg[:, a, 1], sg[:, a, 1], rd[:], ALU.mult).then_inc(s["q_normed"], 1)
                    for a in range(HP):
                        dve.wait_ge(s["probs_exp"], i * HP + (a + 1))
                        step.link(dve, dve.tensor_reduce(st[:, a, 0, :], sc[:, a], AX.X, ALU.add))
                        step.link(dve, dve.reciprocal(st[:, a, 1, :], st[:, a, 0, :]))
                        dve.tensor_tensor(sc[:, a], sc[:, a], over(st[:, a, 1, :], P, 2), ALU.mult
                                          ).then_inc(s["probs_ready"], 1)
                    for a in range(HP):
                        dve.wait_ge(s["read_ready"], i * (HP * NS) + (HP * NS - (1 - a) * (LAG + 1)))
                        dve.wait_ge(s["dot_scaled"], i * HP + (a + 1))
                        for c in range(NCH):
                            last = dve.scalar_tensor_tensor(att[:, a, chunk(c)], k.bank[:, A_BANKS[2 * a + c], :],
                                                            bt[:, 0, a:a + 1], att[:, a, chunk(c)], ALU.mult, ALU.add)
                        last.then_inc(s["att_ready"], 1)

                pair(0, True)
                with dve.Fori(1, PAIRS) as i:
                    step.enter(i - 1, 18)
                    pair(i, False)
                step.leave(PAIRS - 1)
                add_projection(PAIRS)


def l3_ffn(k, norm):
    nc, d = k.nc, k.dram
    E, A, N = 8, 64, 2048
    UNITS = N // P
    PAIRS = UNITS // 2
    names = ("w_in", "idx_in", "ea_in", "iota_ready", "logits_ready", "shifted", "probs_exp", "weights_ready",
             "rt_ready", "rt_copied", "ea_shifted", "ea_exp", "ea_ready", "eat_ready", "eat_copied", "imp_ready",
             "delta_ready", "values_ready", "pick_made", "put_made", "up_ready", "copied", "gated", "hi_ready",
             "lo_ready", "summed", "done", "h_hi_ready", "h_split")
    s = {n: k.sem("l3f_" + n) for n in names}
    with ExitStack() as ctx:
        def sb(n, shape, dt=F32):
            return ctx.enter_context(nc.sbuf_tensor("l3f_" + n, shape, dt))
        gw = sb("gw", [P, DB, E])
        wt = sb("wt", [P, DB, D])
        ea = sb("ea", [E, A])
        est = sb("est", [E, 2])
        eat = sb("eat", [A, E])
        atoms = sb("atoms", [A, N])
        imp = sb("imp", [E, N])
        idx = sb("idx", [P, N], I32)
        idx_s = sb("idx_s", [P, UNITS], I32)
        colf = sb("colf", [P, N])
        rowf = sb("rowf", [P, UNITS])
        feature = sb("feature", [P, DB])
        iota = sb("iota", [P, D])
        p = sb("p", [P, TT, E])
        m = sb("m", [P, TT, E])
        v8 = sb("v8", [P, TT, 8])
        st = sb("st", [P, 2, TT])
        rt = sb("rt", [E, T])
        pick = sb("pick", [P, 2, DB, P], F32R)
        val = sb("val", [E, 2, P])
        put = sb("put", [P, 2, D], F32R)
        g = sb("g", [P, NCH, CH])
        a = sb("a", [P, NCH, CH])
        a_hi, a_lo = (sb("a_" + n, [P, NCH, CH], F32R) for n in ("hi", "lo"))
        h_hi, h_lo = (sb("h_" + n, [P, DB, T], F32R) for n in ("hi", "lo"))
        with nc.Block() as block:
            @block.sync
            def _(sp):
                sp.dma_start(gw[:], d["l3f_gw"].rearrange("(b p) n -> p b n", p=P)).then_inc(s["w_in"], 16)
                sp.dma_start(wt[:], d["l3f_w"].rearrange("(b p) n -> p b n", p=P)).then_inc(s["w_in"], 16)
                sp.dma_start(ea[:], d["l3f_ea"]).then_inc(s["ea_in"], 16)
                sp.dma_start(atoms[:], d["l3f_atoms"]).then_inc(s["ea_in"], 16)
                sp.dma_start(imp[:], d["l3f_imp"]).then_inc(s["ea_in"], 16)
                sp.dma_start(idx[:], d["l3f_idx"].to_broadcast([P, N])).then_inc(s["idx_in"], 16)
                sp.dma_start(idx_s[:], d["l3f_idx_s"]).then_inc(s["idx_in"], 16)

            @block.gpsimd
            def _(pool):
                pool.iota(iota[:], pattern=[[1, D]], base=0, channel_multiplier=0,
                          allow_small_or_imprecise_dtypes=True)
                pool.iota(feature[:], pattern=[[P, DB]], base=0, channel_multiplier=1,
                          allow_small_or_imprecise_dtypes=True).then_inc(s["iota_ready"], 1)

            @block.tensor
            def _(pe):
                norm.on_tensor(pe)
                norm.wait(pe)
                pe.wait_ge(s["w_in"], 32)
                for t in range(TT):
                    for b in range(DB):
                        last = pe.matmul(k.bank[:, 0, t * E:(t + 1) * E], k.h[:, b, tile(t)], gw[:, b, :],
                                         start=(b == 0), stop=(b == DB - 1))
                last.then_inc(s["logits_ready"], 1)

                def dense(n):
                    mm, c = n // NCH, n % NCH
                    for b in range(DB):
                        pe.matmul(k.bank[:, 4 + n, :], wt[:, b, tile(mm)], k.h[:, b, chunk(c)],
                                  start=(b == 0), stop=False, skip_group_check=True)

                def deltas(n):
                    if n >= 2:
                        pe.wait_ge(s["values_ready"], n - 1)
                    pe.matmul(k.bank[0:E, n % 2, :], eat[:], atoms[:, chunk(n)], start=True, stop=True
                              ).then_inc(s["delta_ready"], 1)

                dense(0)
                pe.wait_ge(s["ea_ready"], 1)
                pe.transpose(k.bank[0:A, 1, 0:E], ea[:], k.ident[0:E, 0:E]).then_inc(s["eat_ready"], 1)
                dense(1)
                pe.wait_ge(s["weights_ready"], 1)
                for t in range(TT):
                    last = pe.transpose(k.bank[0:E, 2 + t // 4, (t % 4) * P:(t % 4 + 1) * P], m[:, t, :], k.ident[:])
                last.then_inc(s["rt_ready"], 1)
                pe.wait_ge(s["eat_copied"], 1)
                deltas(0)
                deltas(1)
                dense(2)
                deltas(2)
                deltas(3)
                dense(3)
                pe.wait_ge(s["values_ready"], N // CH)
                pe.wait_ge(s["rt_copied"], 1)

                pe.wait_ge(s["h_split"], NCH)

                def up(i, n, first=False):
                    half, c = n // 2, n % 2
                    if c == 0:
                        pe.wait_ge(s["pick_made"], i * 2 + (half + 1))
                    if not (first and n < 2):
                        pe.wait_ge(s["gated"], i * 4 + (n - 1))
                    for b in range(DB):
                        for part in (h_hi, h_lo):
                            pe.matmul(k.bank[:, 2 * c, :], pick[:, half, b, :], part[:, b, chunk(c)],
                                      start=(b == 0 and part is h_hi), stop=(b == DB - 1 and part is h_lo))
                    pe.matmul(k.bank[:, 2 * c + 1, :], val[:, half, :], rt[:, chunk(c)], start=True, stop=True
                              ).then_inc(s["up_ready"], 1)

                def down(i, n):
                    half, c = n // 2 % 2, n % 2
                    if c == 0:
                        pe.wait_ge(s["put_made"], i * 2 + (n // 2 + 1))
                    pe.wait_ge(s["lo_ready"], i * 4 + (n + 1))
                    for mm in range(DB):
                        for part in (a_hi, a_lo):
                            last = pe.matmul(k.bank[:, 4 + 2 * mm + c, :], put[:, half, tile(mm)], part[:, c, :],
                                             start=False, stop=False, skip_group_check=True)
                    last.then_inc(s["summed"], 1)

                up(0, 0, True)
                up(0, 1, True)
                for n in range(2, 4):
                    up(0, n, True)
                    down(0, n - 2)
                with pe.Fori(1, PAIRS) as i:
                    for n in range(4):
                        up(i, n)
                        down(i, n - 2)
                down(PAIRS, -2)
                down(PAIRS, -1)

            @block.scalar
            def _(act):
                norm.on_scalar(act)
                norm.wait(act)
                for c in range(NCH):
                    act.activation(h_hi[:, :, chunk(c)], k.h[:, :, chunk(c)], ACT.Identity
                                   ).then_inc(s["h_hi_ready"], 1)
                act.preload_act_table(ACT.Sigmoid)
                act.wait_ge(s["ea_in"], 48)
                act.activation(imp[:], imp[:], ACT.Sigmoid).then_inc(s["imp_ready"], 1)
                act.preload_act_table_set(EXP_LN)
                act.wait_ge(s["ea_shifted"], 1)
                act.activation(ea[:], ea[:], ACT.Exp).then_inc(s["ea_exp"], 1)
                act.wait_ge(s["shifted"], 1)
                act.activation(p[:], p[:], ACT.Exp).then_inc(s["probs_exp"], 1)
                act.wait_ge(s["eat_ready"], 1)
                act.activation(eat[:], k.bank[0:A, 1, 0:E], ACT.Identity).then_inc(s["eat_copied"], 1)
                act.wait_ge(s["rt_ready"], 1)
                act.activation(rt[:], k.bank[0:E, 2:4, :].rearrange("p n q -> p (n q)"), ACT.Identity
                               ).then_inc(s["rt_copied"], 1)

                def high(i, n, first=False):
                    act.wait_ge(s["gated"], i * 4 + (n + 1))
                    if not (first and n < 2):
                        act.wait_ge(s["summed"], i * 4 + (n - 1))
                    act.activation(a_hi[:, n % 2, :], a[:, n % 2, :], ACT.Identity).then_inc(s["hi_ready"], 1)

                def pair(i, first):
                    for n in range(4):
                        act.wait_ge(s["up_ready"], i * 4 + (n + 1))
                        act.activation(g[:, n % 2, :], k.bank[:, 2 * (n % 2), :], ACT.Identity
                                       ).then_inc(s["copied"], 1)
                        if not (first and n == 0):
                            high(i, n - 1, first)

                pair(0, True)
                with act.Fori(1, PAIRS) as i:
                    pair(i, False)
                high(PAIRS, -1)

            @block.vector
            def _(dve):
                norm.on_vector(dve)
                step = k.dve_chain
                dve.wait_ge(s["ea_in"], 48)
                step.link(dve, dve.tensor_reduce(est[:, 0:1], ea[:], AX.X, ALU.max))
                dve.tensor_scalar(ea[:], ea[:], est[:, 0:1], None, ALU.subtract).then_inc(s["ea_shifted"], 1)
                dve.wait_ge(s["idx_in"], 32)
                step.link(dve, dve.tensor_single_scalar(idx[:], idx[:], D - 1, ALU.bitwise_and))
                step.link(dve, dve.tensor_single_scalar(idx_s[:], idx_s[:], 8, ALU.logical_shift_right))
                dve.tensor_copy(colf[:], idx[:])
                step.link(dve, dve.tensor_copy(rowf[:], idx_s[:]))
                for c in range(NCH):
                    dve.wait_ge(s["h_hi_ready"], c + 1)
                    dve.tensor_tensor(h_lo[:, :, chunk(c)], k.h[:, :, chunk(c)], h_hi[:, :, chunk(c)].bitcast(F32),
                                      ALU.subtract).then_inc(s["h_split"], 1)
                dve.wait_ge(s["logits_ready"], 1)
                step.link(dve, dve.tensor_scalar(p[:], k.bank[:, 0, 0:TT * E].rearrange("p (t e) -> p t e", t=TT),
                                                 -50.0, 50.0, ALU.max, ALU.min))
                for t in range(TT):
                    last = dve.max(v8[:, t, :], p[:, t, :])
                step.link(dve, last)
                step.link(dve, dve.tensor_tensor(m[:], p[:], over(v8[:, :, 1], E, 2), ALU.is_ge))
                dve.tensor_tensor(p[:], p[:], over(v8[:, :, 0], E, 2), ALU.subtract).then_inc(s["shifted"], 1)
                dve.wait_ge(s["ea_exp"], 1)
                step.link(dve, dve.tensor_reduce(est[:, 0:1], ea[:], AX.X, ALU.add))
                step.link(dve, dve.reciprocal(est[:, 1:2], est[:, 0:1]))
                dve.tensor_scalar(ea[:], ea[:], est[:, 1:2], None, ALU.mult).then_inc(s["ea_ready"], 1)
                dve.wait_ge(s["probs_exp"], 1)
                step.link(dve, dve.tensor_tensor(m[:], m[:], p[:], ALU.mult))
                step.link(dve, dve.tensor_reduce(st[:, 0, :], m[:], AX.X, ALU.add))
                step.link(dve, dve.reciprocal(st[:, 1, :], st[:, 0, :]))
                dve.tensor_tensor(m[:], m[:], over(st[:, 1, :], E, 2), ALU.mult).then_inc(s["weights_ready"], 1)
                dve.wait_ge(s["imp_ready"], 1)
                for n in range(N // CH):
                    dve.wait_ge(s["delta_ready"], n + 1)
                    dve.tensor_tensor(imp[:, chunk(n)], imp[:, chunk(n)], k.bank[0:E, n % 2, :], ALU.mult
                                      ).then_inc(s["values_ready"], 1)
                dve.wait_ge(s["values_ready"], N // CH)
                dve.wait_ge(s["iota_ready"], 1)

                def make_pick(i, unit):
                    at, half = i * (2 * P) + unit * P, unit % 2
                    for b in range(DB):
                        dve.tensor_scalar(pick[:, half, b, :], colf[:, bass.ds(at, P)], feature[:, b:b + 1], None,
                                          ALU.is_equal)
                    dve.tensor_copy(val[:, half, :], imp[:, bass.ds(at, P)]).then_inc(s["pick_made"], 1)

                def make_put(i, unit, first):
                    if not first:
                        dve.wait_ge(s["summed"], i * 4 + (2 * unit - 2))
                    dve.tensor_scalar(put[:, unit, :], iota[:], rowf[:, bass.ds(i * 2 + unit, 1)], None,
                                      ALU.is_equal).then_inc(s["put_made"], 1)

                def low(i, n, first=False):
                    dve.wait_ge(s["hi_ready"], i * 4 + (n + 1))
                    if not (first and n < 2):
                        dve.wait_ge(s["summed"], i * 4 + (n - 1))
                    dve.tensor_tensor(a_lo[:, n % 2, :], a[:, n % 2, :], a_hi[:, n % 2, :].bitcast(F32), ALU.subtract
                                      ).then_inc(s["lo_ready"], 1)

                def pair(i, first, final):
                    for n in range(4):
                        unit, c = n // 2, n % 2
                        if not (first and n < 2):
                            dve.wait_ge(s["lo_ready"], i * 4 + (n - 1))
                        dve.wait_ge(s["copied"], i * 4 + (n + 1))
                        dve.tensor_tensor(a[:, c, :], g[:, c, :], k.bank[:, 2 * c + 1, :], ALU.mult
                                          ).then_inc(s["gated"], 1)
                        if not (first and n == 0):
                            low(i, n - 1, first)
                        if c == 0:
                            make_put(i, unit, first)
                            if not (final and unit):
                                make_pick(i, unit + 1)

                make_pick(0, 0)
                pair(0, True, False)
                with dve.Fori(1, PAIRS - 1) as i:
                    pair(i, False, False)
                pair(PAIRS - 1, False, True)
                low(PAIRS, -1)
                dve.wait_ge(s["summed"], 4 * PAIRS)
                for mm in range(DB):
                    for c in range(NCH):
                        xs = k.x[:, mm, chunk(c)]
                        last = dve.scalar_tensor_tensor(xs, k.bank[:, 4 + 2 * mm + c, :],
                                                        gate_col(k, 3, GATE_B)[:, mm:mm + 1], xs, ALU.mult, ALU.add)
                last.then_inc(s["done"], 1)


def store(k, out):
    nc = k.nc
    stored = k.sem("x_stored")
    with nc.Block() as block:
        @block.sync
        def _(sp):
            sp.dma_start(out.rearrange("(b p) t -> p b t", p=P), k.x[:]).then_inc(stored, 16)
            sp.wait_ge(stored, 16)


def gate_col(k, layer, at):
    return k.mod[:, layer, at:at + DB]


def build(nc, dram, out):
    halves = ((0, l0_attention, l0_ffn), (1, l1_attention, l1_ffn), (2, l2_attention, l2_ffn), (3, l3_attention, l3_ffn))
    steps = [(layer, part, half) for layer, *parts in halves for half, part in enumerate(parts)]
    with ExitStack() as ctx:
        k = Core(nc, ctx, dram)
        mod_ctx = ExitStack()
        with k.stage():
            constants(k)
            mods = Modulations(k, mod_ctx)
            mods.start()
        for n, (layer, part, half) in enumerate(steps):
            with k.stage(), ExitStack() as norm_ctx:
                norm = adaln(k, norm_ctx, layer, *((SHIFT_B, SCALE_B) if half else (SHIFT_A, SCALE_A)))
                if n == 1:
                    part(k, norm, mods)
                else:
                    part(k, norm)
            if n == 1:
                mod_ctx.close()
        store(k, out)


def laid_out(i):
    def t(a):
        return np.swapaxes(np.asarray(a), -1, -2)

    def cat(*a, axis=-1):
        return np.concatenate([np.asarray(x) for x in a], axis=axis)

    H0 = 8
    wq = t(i["L0_attn_Wq"]).reshape(D, H0, P).transpose(1, 0, 2)
    wkv = t(i["L0_attn_Wkv"])
    wk = wkv[:, :H0 * P].reshape(D, H0, P).transpose(1, 0, 2)
    a = {
        "x": t(np.asarray(i["L0_attn_x"])[0]),
        "cs": np.stack([np.asarray(i[f"L{n}_c"]).reshape(DB, P).T for n in range(4)], 1).reshape(P, 4 * DB),
        "wmod": np.stack([np.asarray(i[f"L{n}_wmod"]) for n in range(4)]),
        "l0_wqk": cat(wq, wk),
        "l0_wv": wkv[:, H0 * P:],
        "l0_wg": t(i["L0_attn_Wg"]),
        "l0_bg": np.asarray(i["L0_attn_bg"])[None],
        "l0_scales": np.stack([np.asarray(i["L0_attn_q_scale"]), np.asarray(i["L0_attn_k_scale"])], 1),
        "l0_wo": t(i["L0_attn_Wo"]),
    }
    def in_blocks(w):
        w = np.asarray(w)
        if w.ndim == 3:
            w = w.transpose(1, 0, 2).reshape(D, -1)
        w = np.pad(w, ((0, 0), (0, -w.shape[1] % P)))
        return w.reshape(D, -1, P).transpose(1, 0, 2)

    def units(gate, up, down):
        w = cat(in_blocks(gate), in_blocks(up))
        down = np.asarray(down).reshape(-1, D)
        down = np.pad(down, ((0, -down.shape[0] % P), (0, 0))).reshape(-1, P, D)
        return w.reshape(-1, DB, P, 2 * P).transpose(0, 2, 1, 3).reshape(-1, P, DB * 2 * P), down

    a["l0f_wq"] = np.asarray(i["L0_ffn_W_q"])
    a["l0f_keys"] = np.asarray(i["L0_ffn_keys"])
    a["l0f_de"] = t(i["L0_ffn_down_embed"])
    a["l0f_ue"] = np.asarray(i["L0_ffn_up_embed"])
    a["l0f_win"], a["l0f_wout"] = units(i["L0_ffn_gate_w"], i["L0_ffn_up_w"], i["L0_ffn_down_w"])
    a["l1_w"] = cat(i["L1_attn_Wq"], i["L1_attn_Wk"], i["L1_attn_Wv"])
    a["l1_b"] = cat(i["L1_attn_bq"], i["L1_attn_bk"], i["L1_attn_bv"])[None]
    a["l1_wz"] = cat(i["L1_attn_Wbeta"], i["L1_attn_Walpha"])
    a["l1_bz"] = cat(i["L1_attn_bbeta"], i["L1_attn_balpha"])[None]
    a["l1f_gw"] = t(i["L1_ffn_gate_weight"])
    a["l1f_sim"] = np.asarray(i["L1_ffn_similarity"])
    gu = t(i["L1_ffn_gate_up_proj"])
    F1 = gu.shape[-1] // 2
    a["l1f_win"], a["l1f_wout"] = units(gu[..., :F1], gu[..., F1:], t(i["L1_ffn_down_proj"]))
    def cols2(v):
        v = np.asarray(v)
        return np.tile(v, D // v.shape[0]).reshape(DB, P).T

    conv = np.asarray(i["L2_attn_conv_w"])[:, 0]
    two = [i["L2_attn_" + n] for n in ("ln1w", "ln1b", "ln2w", "ln2b", "vnw", "vnb", "mnw", "mnb", "gnw", "gnb",
                                       "conv_b")]
    two += [conv[:, j] for j in range(4)]
    two += [i["L2_attn_big"], np.repeat(np.asarray(i["L2_attn_bg"]), 16), i["L2_attn_bog"]]
    a["l2_cols"] = np.stack([cols2(v) for v in two], 1)
    a["l2_w"] = cat(i["L2_attn_Wq"], i["L2_attn_Wk"], i["L2_attn_Wv"], i["L2_attn_Wig"],
                    np.repeat(np.asarray(i["L2_attn_Wg"]), 16, axis=1), i["L2_attn_Wog"])
    a["l2_wo"] = np.asarray(i["L2_attn_Wo"])
    a["l2_win"], a["l2_wout"] = units(i["L2_attn_Wgate"], i["L2_attn_Wval"], i["L2_attn_Wout"])
    a["l2f_gw"] = t(i["L2_ffn_gate_weight"])

    wi, wo = units(t(i["L2_ffn_gate_w"]), t(i["L2_ffn_up_w"]), t(i["L2_ffn_down_w"]))
    si, so = units(t(i["L2_ffn_sh_gate_w"]), t(i["L2_ffn_sh_up_w"]), t(i["L2_ffn_sh_down_w"]))
    a["l2f_win"], a["l2f_wout"] = cat(wi, si, axis=0), cat(wo, so, axis=0)
    PR3 = 8
    q3, k3, v3 = (np.asarray(i["L3_attn_" + n]).reshape(D, PR3, 2, P).transpose(1, 0, 2, 3) for n in ("Wq", "Wk", "Wv"))
    a["l3_w"] = cat(np.stack([q3, k3], 3).reshape(PR3, D, 4 * P), v3.reshape(PR3, D, 2 * P))
    a["l3_wo"] = np.asarray(i["L3_attn_Wo"])
    a["l3_betas"] = np.asarray(i["L3_attn_betas"]).reshape(16, P).T
    idx = np.asarray(i["L3_ffn_mask_idx"])
    a["l3f_gw"], a["l3f_w"] = t(i["L3_ffn_gate_w"]), t(i["L3_ffn_W"])
    a["l3f_ea"], a["l3f_atoms"] = np.asarray(i["L3_ffn_expert_atom_weights"]), np.asarray(i["L3_ffn_atoms"])
    a["l3f_imp"] = np.asarray(i["L3_ffn_importance"])
    a["l3f_idx"], a["l3f_idx_s"] = idx[None], idx.reshape(-1, P).T
    return a


def kernel(**inputs):
    import concourse.bacc as _bacc
    from concourse.bass_utils import run_bass_kernel_spmd as _run

    arrays = {"in_" + n: np.ascontiguousarray(a) for n, a in laid_out(inputs).items()}
    nc = _bacc.Bacc("TRN2", target_bir_lowering=False, num_devices=1)
    dram = {n[3:]: nc.dram_tensor(n, a.shape, mybir.dt.from_np(a.dtype), kind="ExternalInput").ap()
            for n, a in arrays.items()}
    out = nc.dram_tensor("out", (D, T), F32, kind="ExternalOutput").ap()
    build(nc, dram, out)
    r = _run(nc, [arrays], core_ids=[0])
    return np.ascontiguousarray(r.results[0]["out"].T)[None]
```
